# Optimizing a Trainium2 kernel written in Bass

```python
import numpy as np
import jax
import jax.numpy as jnp

def _softmax(x, axis=-1):
    return jax.nn.softmax(x, axis=axis)

def _gelu(x):
    return jax.nn.gelu(x, approximate=True)

def _silu(x):
    return jax.nn.silu(x)

def _sigmoid(x):
    return jax.nn.sigmoid(x)

def _layernorm(x, axis=-1, eps=1e-05):
    m = jnp.mean(x, axis=axis, keepdims=True)
    v = jnp.var(x, axis=axis, keepdims=True)
    return (x - m) / jnp.sqrt(v + eps)

def _scatter_add(tgt, idx, src, axis=0):
    return tgt.at[idx].add(src)

def _segment_sum(src, seg, n):
    return jax.ops.segment_sum(src, seg, n)
kernel_name = 'mk_perceiver_d4_seqx_r4_8c3366'

def setup_inputs(seed: int=0):
    np.random.seed(seed)
    _w = jnp.asarray

    def _rec_inputs():
        import jax
        import jax.numpy as jnp
        _rk = jax.random.key(seed)
        x = -0.0002928 + 1 * jax.random.normal(jax.random.fold_in(_rk, 1), (1, 128, 256), jnp.float32)
        _lenS = 128 - jax.random.randint(jax.random.fold_in(_rk, 7), (1,), 0, max(1, 128 // 4) + 1, jnp.int32)
        _lenS2 = 12544 - jax.random.randint(jax.random.fold_in(_rk, 8), (1,), 0, max(1, 12544 // 4) + 1, jnp.int32)
        _ctx_1024P = jax.random.normal(jax.random.fold_in(_rk, 11), (1, 16, 256), jnp.float32)
        _ctx_1024c = jax.random.dirichlet(jax.random.fold_in(_rk, 511), 0.3 * jnp.ones((16,), jnp.float32), (1, 12544))
        _ctx_1024t = jnp.einsum('bsk,bkd->bsd', _ctx_1024c, _ctx_1024P)
        _ctx_1024t = _ctx_1024t * jax.lax.rsqrt(jnp.mean(jnp.square(_ctx_1024t)) + 1e-12) * 0.953939
        ctx_1024 = -1.39393e-06 + 0.999914 * (_ctx_1024t + 0.3 * jax.random.normal(jax.random.fold_in(_rk, 611), (1, 12544, 256), jnp.float32))
        return (x, ctx_1024)
    x, ctx_1024 = _rec_inputs()

    def _L0_xattn_setup():
        import jax, jax.numpy as jnp
        import numpy as np
        D_MODEL = 256
        NUM_HEADS = 16
        HEAD_DIM = D_MODEL // NUM_HEADS
        key = jax.random.key(seed)
        ks = jax.random.split(key, 10)
        B, SQ, SK = (2, 512, 512)
        scale = 1.0 / np.sqrt(D_MODEL)
        inp = {'x1': jax.random.normal(ks[0], (B, SQ, D_MODEL), jnp.float32), 'x2': jax.random.normal(ks[1], (B, SK, D_MODEL), jnp.float32), 'Wq': jax.random.normal(ks[2], (D_MODEL, D_MODEL), jnp.float32) * scale, 'bq': jnp.zeros((D_MODEL,), jnp.float32), 'Wk': jax.random.normal(ks[3], (D_MODEL, D_MODEL), jnp.float32) * scale, 'bk': jnp.zeros((D_MODEL,), jnp.float32), 'Wv': jax.random.normal(ks[4], (D_MODEL, D_MODEL), jnp.float32) * scale, 'bv': jnp.zeros((D_MODEL,), jnp.float32), 'Wo': jax.random.normal(ks[5], (D_MODEL, D_MODEL), jnp.float32) * scale, 'bo': jnp.zeros((D_MODEL,), jnp.float32)}
        return inp
    _L0_xattn_all = _L0_xattn_setup()
    _L0_xattn_in = {k: v for k, v in _L0_xattn_all.items() if k in ('Wq', 'bq', 'Wk', 'bk', 'Wv', 'bv', 'Wo', 'bo')}
    del _L0_xattn_all

    def _L0_attn_setup():
        import jax, jax.numpy as jnp
        import numpy as np
        HEADS = 16
        DIM_HEAD = 64
        SCALE = 8.0
        NUM_NULL_KV = 2
        NON_CAUSAL_PREFIX = 64
        LN_EPS = 1e-05

        def _l2norm(t):
            n = jnp.sqrt(jnp.sum(t * t, axis=-1, keepdims=True))
            return t / jnp.maximum(n, 1e-12)

        def _layer_norm(x, gamma):
            mu = jnp.mean(x, axis=-1, keepdims=True)
            var = jnp.mean((x - mu) ** 2, axis=-1, keepdims=True)
            return (x - mu) * jax.lax.rsqrt(var + LN_EPS) * gamma
        key = jax.random.key(seed)
        ks = jax.random.split(key, 6)
        b, n, dim = (2, 512, 256)
        inner = HEADS * DIM_HEAD
        return {'x': jax.random.normal(ks[0], (b, n, dim), jnp.float32), 'gamma': jnp.ones((dim,), jnp.float32), 'Wq': jax.random.normal(ks[1], (dim, inner), jnp.float32) * dim ** (-0.5), 'Wkv': jax.random.normal(ks[2], (dim, 2 * DIM_HEAD), jnp.float32) * dim ** (-0.5), 'q_scale': jnp.ones((DIM_HEAD,), jnp.float32), 'k_scale': jnp.ones((DIM_HEAD,), jnp.float32), 'null_kv': jax.random.normal(ks[3], (2, NUM_NULL_KV, DIM_HEAD), jnp.float32), 'Wout': jax.random.normal(ks[4], (inner, dim), jnp.float32) * inner ** (-0.5)}
    _L0_attn_all = _L0_attn_setup()
    _L0_attn_in = {k: v for k, v in _L0_attn_all.items() if k in ('gamma', 'Wq', 'Wkv', 'q_scale', 'k_scale', 'null_kv', 'Wout')}
    del _L0_attn_all

    def _L0_ffn_setup():
        import jax, jax.numpy as jnp
        import numpy as np
        DIM = 256

        def _reference_tuple_inner(x, W_r, W_k, W_v, mu_r, mu_k):
            B, T, C = x.shape
            x_prev = jnp.concatenate([jnp.zeros((B, 1, C), x.dtype), x[:, :-1, :]], axis=1)
            xr = mu_r * x + (1.0 - mu_r) * x_prev
            xk = mu_k * x + (1.0 - mu_k) * x_prev
            r = jax.nn.sigmoid(jnp.einsum('btc,dc->btd', xr, W_r))
            k = jnp.einsum('btc,dc->btd', xk, W_k)
            k_act = jnp.square(jax.nn.relu(k))
            out = r * jnp.einsum('btc,dc->btd', k_act, W_v)
            new_state = x[:, -1, :]
            return (out, new_state)
        key = jax.random.key(seed)
        ks = jax.random.split(key, 6)
        B, T, C = (8, 512, DIM)
        x = jax.random.normal(ks[0], (B, T, C), dtype=jnp.float32)
        s = 1.0 / np.sqrt(C)
        W_r = jax.random.uniform(ks[1], (C, C), jnp.float32, -s, s)
        W_k = jax.random.uniform(ks[2], (C, C), jnp.float32, -s, s)
        W_v = jax.random.uniform(ks[3], (C, C), jnp.float32, -s, s)
        mu_r = jax.random.uniform(ks[4], (C,), jnp.float32)
        mu_k = jax.random.uniform(ks[5], (C,), jnp.float32)
        return {'x': x, 'W_r': W_r, 'W_k': W_k, 'W_v': W_v, 'mu_r': mu_r, 'mu_k': mu_k}
    _L0_ffn_all = _L0_ffn_setup()
    _L0_ffn_in = {k: v for k, v in _L0_ffn_all.items() if k in ('W_r', 'W_k', 'W_v', 'mu_r', 'mu_k')}
    del _L0_ffn_all

    def _L1_xattn_setup():
        import jax, jax.numpy as jnp
        import numpy as np
        D_MODEL = 256
        NUM_HEADS = 16
        D_HEAD = D_MODEL // NUM_HEADS

        def _split_heads(x):
            B, L, _ = x.shape
            return x.reshape(B, L, NUM_HEADS, D_HEAD).transpose(0, 2, 1, 3)
        key = jax.random.key(seed)
        ks = jax.random.split(key, 10)
        B, L = (2, 512)
        s = 1.0 / np.sqrt(D_MODEL)
        inp = {'x_q': jax.random.normal(ks[0], (B, L, D_MODEL), jnp.float32), 'x_kv': jax.random.normal(ks[1], (B, L, D_MODEL), jnp.float32), 'wq': jax.random.normal(ks[2], (D_MODEL, D_MODEL), jnp.float32) * s, 'bq': jnp.zeros((D_MODEL,), jnp.float32), 'wk': jax.random.normal(ks[3], (D_MODEL, D_MODEL), jnp.float32) * s, 'bk': jnp.zeros((D_MODEL,), jnp.float32), 'wv': jax.random.normal(ks[4], (D_MODEL, D_MODEL), jnp.float32) * s, 'bv': jnp.zeros((D_MODEL,), jnp.float32), 'wo': jax.random.normal(ks[5], (D_MODEL, D_MODEL), jnp.float32) * s, 'bo': jnp.zeros((D_MODEL,), jnp.float32)}
        return inp
    _L1_xattn_all = _L1_xattn_setup()
    _L1_xattn_in = {k: v for k, v in _L1_xattn_all.items() if k in ('wq', 'bq', 'wk', 'bk', 'wv', 'bv', 'wo', 'bo')}
    del _L1_xattn_all

    def _L1_attn_setup():
        import jax, jax.numpy as jnp
        import numpy as np
        NUM_HEADS = 4
        CHUNK = 64
        GATE_NORM = 16.0
        EPS = 1e-05

        def _xavier(key, fan_in, fan_out):
            gain = 2.0 ** (-2.5)
            limit = gain * np.sqrt(6.0 / (fan_in + fan_out))
            return jax.random.uniform(key, (fan_in, fan_out), jnp.float32, -limit, limit)

        def _to_chunks(t, B, H, NC, C):
            d = t.shape[-1]
            return t.reshape(B, H, NC, C, d).transpose(2, 0, 1, 3, 4)

        def _gla_forward(x, Wq, Wk, Wv, Wg, gk_w1, gk_w2, gk_b2, g_norm_w, Wo):
            B, L, D = x.shape
            H = NUM_HEADS
            C = CHUNK
            NC = L // C
            q = x @ Wq
            k = x @ Wk
            v = x @ Wv
            gk = jax.nn.log_sigmoid(x @ gk_w1 @ gk_w2 + gk_b2) / GATE_NORM

            def split_heads(t):
                return t.reshape(B, L, H, -1).transpose(0, 2, 1, 3)
            q, k, v, gk = map(split_heads, (q, k, v, gk))
            dk = q.shape[-1]
            scale = dk ** (-0.5)
            qc = _to_chunks(q, B, H, NC, C)
            kc = _to_chunks(k, B, H, NC, C)
            vc = _to_chunks(v, B, H, NC, C)
            gc = _to_chunks(gk, B, H, NC, C)
            Bcum = jnp.cumsum(gc, axis=3)
            causal = jnp.tril(jnp.ones((C, C), jnp.float32))

            def step(Hst, inp):
                qi, ki, vi, bi = inp
                qg = qi * jnp.exp(bi) * scale
                kg = ki * jnp.exp(-bi)
                o_inter = jnp.einsum('bhcd,bhde->bhce', qg, Hst)
                A = jnp.einsum('bhtd,bhsd->bhts', qg, kg) * causal
                o_intra = jnp.einsum('bhts,bhse->bhte', A, vi)
                b_last = bi[:, :, -1:, :]
                kH = ki * jnp.exp(b_last - bi)
                H_new = jnp.exp(b_last).transpose(0, 1, 3, 2) * Hst + jnp.einsum('bhcd,bhce->bhde', kH, vi)
                return (H_new, o_inter + o_intra)
            dv = v.shape[-1]
            H0 = jnp.zeros((B, H, dk, dv), jnp.float32)
            _, oc = jax.lax.scan(step, H0, (qc, kc, vc, Bcum))
            o = oc.transpose(1, 2, 0, 3, 4).reshape(B, H, L, dv)
            o = o.transpose(0, 2, 1, 3)
            rms = jnp.sqrt(jnp.mean(o * o, axis=-1, keepdims=True) + EPS)
            o_n = o / rms * g_norm_w
            g = (x @ Wg).reshape(B, L, H, dv)
            o = o_n * g * jax.nn.sigmoid(g)
            return o.reshape(B, L, H * dv) @ Wo
        key = jax.random.key(seed)
        ks = jax.random.split(key, 8)
        B, L, D = (4, 512, 256)
        Dk, Dv, R = (256, 512, 16)
        x = jax.random.normal(ks[0], (B, L, D), jnp.float32)
        return {'x': x, 'Wq': _xavier(ks[1], D, Dk), 'Wk': _xavier(ks[2], D, Dk), 'Wv': _xavier(ks[3], D, Dv), 'Wg': _xavier(ks[4], D, Dv), 'gk_w1': _xavier(ks[5], D, R), 'gk_w2': _xavier(ks[6], R, Dk), 'gk_b2': jnp.zeros((Dk,), jnp.float32), 'g_norm_w': jnp.ones((Dv // NUM_HEADS,), jnp.float32), 'Wo': _xavier(ks[7], Dv, D)}
    _L1_attn_all = _L1_attn_setup()
    _L1_attn_in = {k: v for k, v in _L1_attn_all.items() if k in ('Wq', 'Wk', 'Wv', 'Wg', 'gk_w1', 'gk_w2', 'gk_b2', 'g_norm_w', 'Wo')}
    del _L1_attn_all

    def _L1_ffn_setup():
        import jax, jax.numpy as jnp
        import numpy as np
        E, G, TOPK = (32, 16, 2)
        HID, INTER, A_INTER = (256, 512, 128)
        CAP_FACTOR = 1.25
        SCALE = 0.05

        def _stats(x):
            mean = x.mean(-1, keepdims=True)
            std = jnp.std(x, axis=-1, keepdims=True, ddof=1)
            mn = x.min(-1, keepdims=True)
            mx = x.max(-1, keepdims=True)
            l2 = jnp.linalg.norm(x, axis=-1, keepdims=True)
            sp = (jnp.abs(x) < 1e-06).astype(x.dtype).mean(-1, keepdims=True)
            return jnp.concatenate([mean, std, mn, mx, l2, sp], -1)
        key = jax.random.key(seed)
        ks = jax.random.split(key, 8)
        B, N = (4, 256)
        s = lambda k, shape, sc: jax.random.normal(k, shape, jnp.float32) * sc
        return {'x': jax.random.normal(ks[0], (B, N, HID), jnp.float32), 'r1_w': s(ks[1], (HID // 2, HID + 6), 0.02), 'r1_b': jnp.zeros((HID // 2,), jnp.float32), 'r2_w': s(ks[2], (E, HID // 2), 0.02), 'w_up': s(ks[3], (E, 2 * INTER, HID), 0.02), 'w_down': s(ks[4], (E, HID, INTER), 0.02), 'a_up': s(ks[5], (G, 2 * A_INTER, HID), 0.02), 'a_down': s(ks[6], (G, HID, A_INTER), 0.02)}
    _L1_ffn_all = _L1_ffn_setup()
    _L1_ffn_in = {k: v for k, v in _L1_ffn_all.items() if k in ('r1_w', 'r1_b', 'r2_w', 'w_up', 'w_down', 'a_up', 'a_down')}
    del _L1_ffn_all

    def _L2_xattn_setup():
        import jax, jax.numpy as jnp
        import numpy as np
        DIM = 256
        key = jax.random.key(seed)
        ks = jax.random.split(key, 9)
        B, S, D = (8, 512, DIM)
        inv = 1.0 / np.sqrt(D)
        return {'image_emb': jax.random.normal(ks[0], (B, S, D), dtype=jnp.float32), 'text_emb': jax.random.normal(ks[1], (B, S, D), dtype=jnp.float32), 'edge_index': jax.random.randint(ks[2], (2, 16), 0, 512, dtype=jnp.int64), 'Wq': jax.random.normal(ks[3], (D, D), dtype=jnp.float32) * inv, 'bq': jnp.zeros((D,), dtype=jnp.float32), 'Wk': jax.random.normal(ks[4], (D, D), dtype=jnp.float32) * inv, 'bk': jnp.zeros((D,), dtype=jnp.float32), 'Wv': jax.random.normal(ks[5], (D, D), dtype=jnp.float32) * inv, 'bv': jnp.zeros((D,), dtype=jnp.float32)}
    _L2_xattn_all = _L2_xattn_setup()
    _L2_xattn_in = {k: v for k, v in _L2_xattn_all.items() if k in ('edge_index', 'Wq', 'bq', 'Wk', 'bk', 'Wv', 'bv')}
    del _L2_xattn_all

    def _L2_attn_setup():
        import jax, jax.numpy as jnp
        import numpy as np
        B, S, E = (4, 512, 256)
        H, KVH = (16, 4)
        D = E // H
        QL, KVL = (64, 32)
        ROPE_BASE = 10000.0

        def _rope(x):
            d = x.shape[-1]
            inv_freq = 1.0 / ROPE_BASE ** (jnp.arange(0, d, 2, dtype=jnp.float32) / d)
            t = jnp.arange(x.shape[1], dtype=jnp.float32)
            freqs = jnp.outer(t, inv_freq)
            cos = jnp.cos(freqs)[None, :, None, :].astype(x.dtype)
            sin = jnp.sin(freqs)[None, :, None, :].astype(x.dtype)
            x1, x2 = (x[..., ::2], x[..., 1::2])
            r1 = x1 * cos - x2 * sin
            r2 = x1 * sin + x2 * cos
            return jnp.stack([r1, r2], axis=-1).reshape(x.shape)
        key = jax.random.key(seed)
        ks = jax.random.split(key, 7)
        s = 0.02
        return {'x': jax.random.normal(ks[0], (B, S, E), dtype=jnp.float32), 'Wqa': jax.random.normal(ks[1], (E, QL), dtype=jnp.float32) * s, 'Wqb': jax.random.normal(ks[2], (QL, E), dtype=jnp.float32) * s, 'Wkva': jax.random.normal(ks[3], (E, KVL), dtype=jnp.float32) * s, 'Wkvb': jax.random.normal(ks[4], (KVL, KVH * D * 2), dtype=jnp.float32) * s, 'Wout': jax.random.normal(ks[5], (E, E), dtype=jnp.float32) * s, 'bout': jax.random.normal(ks[6], (E,), dtype=jnp.float32) * s}
    _L2_attn_all = _L2_attn_setup()
    _L2_attn_in = {k: v for k, v in _L2_attn_all.items() if k in ('Wqa', 'Wqb', 'Wkva', 'Wkvb', 'Wout', 'bout')}
    del _L2_attn_all

    def _L2_ffn_setup():
        import jax, jax.numpy as jnp
        import numpy as np
        B, S, N_EMBD = (4, 1024, 256)
        HIDDEN = 4 * N_EMBD
        M_BITS_FC = 3
        M_BITS_PROJ = 3
        BLOCK_K = 32

        def block_quant(v, m_bits, bk):
            *lead, K = v.shape
            vb = v.reshape(*lead, K // bk, bk)
            amax = jnp.max(jnp.abs(vb), axis=-1, keepdims=True)
            tiny = jnp.asarray(2.0 ** (-126), v.dtype)
            e = jnp.floor(jnp.log2(jnp.maximum(amax, tiny)))
            scale = jnp.exp2(e - m_bits)
            q = jnp.round(vb / scale) * scale
            q = vb + jax.lax.stop_gradient(q - vb)
            return q.reshape(v.shape)

        def lowprec_linear(x, w, b, m_bits, bk):
            xq = block_quant(x, m_bits, bk)
            wq = block_quant(w, m_bits, bk)
            return jnp.einsum('bsk,nk->bsn', xq, wq) + b
        key = jax.random.key(seed)
        k0, k1, k2 = jax.random.split(key, 3)
        x = jax.random.normal(k0, (B, S, N_EMBD), jnp.float32)
        w_fc = jax.random.normal(k1, (HIDDEN, N_EMBD), jnp.float32) * (1.0 / np.sqrt(N_EMBD))
        b_fc = jnp.zeros((HIDDEN,), jnp.float32)
        w_proj = jax.random.normal(k2, (N_EMBD, HIDDEN), jnp.float32) * (1.0 / np.sqrt(HIDDEN))
        b_proj = jnp.zeros((N_EMBD,), jnp.float32)
        return {'x': x, 'w_fc': w_fc, 'b_fc': b_fc, 'w_proj': w_proj, 'b_proj': b_proj}
    _L2_ffn_all = _L2_ffn_setup()
    _L2_ffn_in = {k: v for k, v in _L2_ffn_all.items() if k in ('w_fc', 'b_fc', 'w_proj', 'b_proj')}
    del _L2_ffn_all

    def _L3_xattn_setup():
        import jax, jax.numpy as jnp
        import numpy as np
        DIM = 256
        H = 16
        DH = 64
        INNER = H * DH
        SCALE = DH ** (-0.5)
        key = jax.random.key(seed)
        ks = jax.random.split(key, 6)
        B, L, R = (4, 1024, 128)
        x = jax.random.normal(ks[0], (B, L, DIM), dtype=jnp.float32)
        context = jax.random.normal(ks[1], (B, R, DIM), dtype=jnp.float32)
        s = DIM ** (-0.5)
        Wq = jax.random.normal(ks[2], (DIM, INNER), dtype=jnp.float32) * s
        Wk = jax.random.normal(ks[3], (DIM, INNER), dtype=jnp.float32) * s
        Wv = jax.random.normal(ks[4], (DIM, INNER), dtype=jnp.float32) * s
        Wo = jax.random.normal(ks[5], (INNER, DIM), dtype=jnp.float32) * INNER ** (-0.5)
        return {'x': x, 'context': context, 'Wq': Wq, 'Wk': Wk, 'Wv': Wv, 'Wo': Wo}
    _L3_xattn_all = _L3_xattn_setup()
    _L3_xattn_in = {k: v for k, v in _L3_xattn_all.items() if k in ('Wq', 'Wk', 'Wv', 'Wo')}
    del _L3_xattn_all

    def _L3_attn_setup():
        import math
        import jax, jax.numpy as jnp
        import numpy as np
        B, L, DIM, HEADS = (4, 512, 256, 8)
        HEAD = DIM // HEADS
        SCALE_BASE = 512.0
        EPS = 1e-05

        def _xpos(x, downscale=False):
            l, dh = (x.shape[-2], x.shape[-1])
            half = dh // 2
            pos = jnp.arange(l, dtype=x.dtype)
            base = (jnp.arange(0, dh, 2, dtype=x.dtype) + 0.4 * dh) / (1.4 * dh)
            scale = base[None, :] ** (pos[:, None] / SCALE_BASE)
            inv_freq = 1.0 / 10000.0 ** (jnp.arange(half, dtype=x.dtype) / half)
            sinusoid = pos[:, None] * inv_freq[None, :]
            sin, cos = (jnp.sin(sinusoid), jnp.cos(sinusoid))
            if downscale:
                scale = 1.0 / scale
            s = jnp.repeat(sin * scale, 2, axis=-1)
            c = jnp.repeat(cos * scale, 2, axis=-1)
            x1, x2 = (x[..., ::2], x[..., 1::2])
            rot = jnp.stack([-x2, x1], axis=-1).reshape(x.shape)
            return x * c + rot * s

        def _decay_mask(l, gammas):
            n = jnp.arange(l)[:, None]
            m = jnp.arange(l)[None, :]
            lg = jnp.log(gammas)
            expo = (n - m).astype(jnp.float32)[None, :, :] * lg[:, None, None]
            return jnp.where((n >= m)[None], jnp.exp(expo), 0.0)
        key = jax.random.key(seed)
        ks = jax.random.split(key, 6)
        d = DIM
        return {'X': jax.random.normal(ks[0], (B, L, DIM), dtype=jnp.float32), 'W_Q': jax.random.normal(ks[1], (HEADS, DIM, HEAD), dtype=jnp.float32) / d, 'W_K': jax.random.normal(ks[2], (HEADS, DIM, HEAD), dtype=jnp.float32) / d, 'W_V': jax.random.normal(ks[3], (HEADS, DIM, HEAD), dtype=jnp.float32) / d, 'W_G': jax.random.normal(ks[4], (DIM, DIM), dtype=jnp.float32) / d, 'W_O': jax.random.normal(ks[5], (DIM, DIM), dtype=jnp.float32) / d, 'gn_weight': jnp.ones((DIM,), dtype=jnp.float32), 'gn_bias': jnp.zeros((DIM,), dtype=jnp.float32)}
    _L3_attn_all = _L3_attn_setup()
    _L3_attn_in = {k: v for k, v in _L3_attn_all.items() if k in ('W_Q', 'W_K', 'W_V', 'W_G', 'W_O', 'gn_weight', 'gn_bias')}
    del _L3_attn_all

    def _L3_ffn_setup():
        import jax, jax.numpy as jnp
        import numpy as np
        from jax import lax
        B, N, D, H, E, K = (16, 256, 256, 1024, 8, 2)
        key = jax.random.key(seed)
        ks = jax.random.split(key, 12)
        s = 0.02
        return {'x': jax.random.normal(ks[0], (B, N, D), jnp.float32), 'alpha': jnp.asarray(0.9, jnp.float32), 'w_gate': jax.random.normal(ks[1], (D, E), jnp.float32) * s, 'b_gate': jnp.zeros((E,), jnp.float32), 'W1m': jax.random.normal(ks[2], (D, H), jnp.float32) * s, 'b1m': jnp.zeros((H,), jnp.float32), 'W2m': jax.random.normal(ks[3], (H, D), jnp.float32) * s, 'b2m': jnp.zeros((D,), jnp.float32), 'W1e': jax.random.normal(ks[4], (E, D, H), jnp.float32) * s, 'b1e': jnp.zeros((E, H), jnp.float32), 'W2e': jax.random.normal(ks[5], (E, H, D), jnp.float32) * s, 'b2e': jnp.zeros((E, D), jnp.float32)}
    _L3_ffn_all = _L3_ffn_setup()
    _L3_ffn_in = {k: v for k, v in _L3_ffn_all.items() if k in ('alpha', 'w_gate', 'b_gate', 'W1m', 'b1m', 'W2m', 'b2m', 'W1e', 'b1e', 'W2e', 'b2e')}
    del _L3_ffn_all
    return {'x': x, 'ctx_1024': ctx_1024, 'L0_xattn_Wq': _L0_xattn_in['Wq'], 'L0_xattn_bq': _L0_xattn_in['bq'], 'L0_xattn_Wk': _L0_xattn_in['Wk'], 'L0_xattn_bk': _L0_xattn_in['bk'], 'L0_xattn_Wv': _L0_xattn_in['Wv'], 'L0_xattn_bv': _L0_xattn_in['bv'], 'L0_xattn_Wo': _L0_xattn_in['Wo'], 'L0_xattn_bo': _L0_xattn_in['bo'], 'L0_attn_gamma': _L0_attn_in['gamma'], 'L0_attn_Wq': _L0_attn_in['Wq'], 'L0_attn_Wkv': _L0_attn_in['Wkv'], 'L0_attn_q_scale': _L0_attn_in['q_scale'], 'L0_attn_k_scale': _L0_attn_in['k_scale'], 'L0_attn_null_kv': _L0_attn_in['null_kv'], 'L0_attn_Wout': _L0_attn_in['Wout'], 'L0_ffn_W_r': _L0_ffn_in['W_r'], 'L0_ffn_W_k': _L0_ffn_in['W_k'], 'L0_ffn_W_v': _L0_ffn_in['W_v'], 'L0_ffn_mu_r': _L0_ffn_in['mu_r'], 'L0_ffn_mu_k': _L0_ffn_in['mu_k'], 'L1_xattn_wq': _L1_xattn_in['wq'], 'L1_xattn_bq': _L1_xattn_in['bq'], 'L1_xattn_wk': _L1_xattn_in['wk'], 'L1_xattn_bk': _L1_xattn_in['bk'], 'L1_xattn_wv': _L1_xattn_in['wv'], 'L1_xattn_bv': _L1_xattn_in['bv'], 'L1_xattn_wo': _L1_xattn_in['wo'], 'L1_xattn_bo': _L1_xattn_in['bo'], 'L1_attn_Wq': _L1_attn_in['Wq'], 'L1_attn_Wk': _L1_attn_in['Wk'], 'L1_attn_Wv': _L1_attn_in['Wv'], 'L1_attn_Wg': _L1_attn_in['Wg'], 'L1_attn_gk_w1': _L1_attn_in['gk_w1'], 'L1_attn_gk_w2': _L1_attn_in['gk_w2'], 'L1_attn_gk_b2': _L1_attn_in['gk_b2'], 'L1_attn_g_norm_w': _L1_attn_in['g_norm_w'], 'L1_attn_Wo': _L1_attn_in['Wo'], 'L1_ffn_r1_w': _L1_ffn_in['r1_w'], 'L1_ffn_r1_b': _L1_ffn_in['r1_b'], 'L1_ffn_r2_w': _L1_ffn_in['r2_w'], 'L1_ffn_w_up': _L1_ffn_in['w_up'], 'L1_ffn_w_down': _L1_ffn_in['w_down'], 'L1_ffn_a_up': _L1_ffn_in['a_up'], 'L1_ffn_a_down': _L1_ffn_in['a_down'], 'L2_xattn_edge_index': _L2_xattn_in['edge_index'], 'L2_xattn_Wq': _L2_xattn_in['Wq'], 'L2_xattn_bq': _L2_xattn_in['bq'], 'L2_xattn_Wk': _L2_xattn_in['Wk'], 'L2_xattn_bk': _L2_xattn_in['bk'], 'L2_xattn_Wv': _L2_xattn_in['Wv'], 'L2_xattn_bv': _L2_xattn_in['bv'], 'L2_attn_Wqa': _L2_attn_in['Wqa'], 'L2_attn_Wqb': _L2_attn_in['Wqb'], 'L2_attn_Wkva': _L2_attn_in['Wkva'], 'L2_attn_Wkvb': _L2_attn_in['Wkvb'], 'L2_attn_Wout': _L2_attn_in['Wout'], 'L2_attn_bout': _L2_attn_in['bout'], 'L2_ffn_w_fc': _L2_ffn_in['w_fc'], 'L2_ffn_b_fc': _L2_ffn_in['b_fc'], 'L2_ffn_w_proj': _L2_ffn_in['w_proj'], 'L2_ffn_b_proj': _L2_ffn_in['b_proj'], 'L3_xattn_Wq': _L3_xattn_in['Wq'], 'L3_xattn_Wk': _L3_xattn_in['Wk'], 'L3_xattn_Wv': _L3_xattn_in['Wv'], 'L3_xattn_Wo': _L3_xattn_in['Wo'], 'L3_attn_W_Q': _L3_attn_in['W_Q'], 'L3_attn_W_K': _L3_attn_in['W_K'], 'L3_attn_W_V': _L3_attn_in['W_V'], 'L3_attn_W_G': _L3_attn_in['W_G'], 'L3_attn_W_O': _L3_attn_in['W_O'], 'L3_attn_gn_weight': _L3_attn_in['gn_weight'], 'L3_attn_gn_bias': _L3_attn_in['gn_bias'], 'L3_ffn_alpha': _L3_ffn_in['alpha'], 'L3_ffn_w_gate': _L3_ffn_in['w_gate'], 'L3_ffn_b_gate': _L3_ffn_in['b_gate'], 'L3_ffn_W1m': _L3_ffn_in['W1m'], 'L3_ffn_b1m': _L3_ffn_in['b1m'], 'L3_ffn_W2m': _L3_ffn_in['W2m'], 'L3_ffn_b2m': _L3_ffn_in['b2m'], 'L3_ffn_W1e': _L3_ffn_in['W1e'], 'L3_ffn_b1e': _L3_ffn_in['b1e'], 'L3_ffn_W2e': _L3_ffn_in['W2e'], 'L3_ffn_b2e': _L3_ffn_in['b2e']}

def reference(x, ctx_1024, L0_xattn_Wq, L0_xattn_bq, L0_xattn_Wk, L0_xattn_bk, L0_xattn_Wv, L0_xattn_bv, L0_xattn_Wo, L0_xattn_bo, L0_attn_gamma, L0_attn_Wq, L0_attn_Wkv, L0_attn_q_scale, L0_attn_k_scale, L0_attn_null_kv, L0_attn_Wout, L0_ffn_W_r, L0_ffn_W_k, L0_ffn_W_v, L0_ffn_mu_r, L0_ffn_mu_k, L1_xattn_wq, L1_xattn_bq, L1_xattn_wk, L1_xattn_bk, L1_xattn_wv, L1_xattn_bv, L1_xattn_wo, L1_xattn_bo, L1_attn_Wq, L1_attn_Wk, L1_attn_Wv, L1_attn_Wg, L1_attn_gk_w1, L1_attn_gk_w2, L1_attn_gk_b2, L1_attn_g_norm_w, L1_attn_Wo, L1_ffn_r1_w, L1_ffn_r1_b, L1_ffn_r2_w, L1_ffn_w_up, L1_ffn_w_down, L1_ffn_a_up, L1_ffn_a_down, L2_xattn_edge_index, L2_xattn_Wq, L2_xattn_bq, L2_xattn_Wk, L2_xattn_bk, L2_xattn_Wv, L2_xattn_bv, L2_attn_Wqa, L2_attn_Wqb, L2_attn_Wkva, L2_attn_Wkvb, L2_attn_Wout, L2_attn_bout, L2_ffn_w_fc, L2_ffn_b_fc, L2_ffn_w_proj, L2_ffn_b_proj, L3_xattn_Wq, L3_xattn_Wk, L3_xattn_Wv, L3_xattn_Wo, L3_attn_W_Q, L3_attn_W_K, L3_attn_W_V, L3_attn_W_G, L3_attn_W_O, L3_attn_gn_weight, L3_attn_gn_bias, L3_ffn_alpha, L3_ffn_w_gate, L3_ffn_b_gate, L3_ffn_W1m, L3_ffn_b1m, L3_ffn_W2m, L3_ffn_b2m, L3_ffn_W1e, L3_ffn_b1e, L3_ffn_W2e, L3_ffn_b2e):
    import jax
    import jax.numpy as jnp

    def _L0_xattn_ref(x1, x2, Wq, bq, Wk, bk, Wv, bv, Wo, bo):
        import jax, jax.numpy as jnp
        import numpy as np
        D_MODEL = 256
        NUM_HEADS = 16
        HEAD_DIM = D_MODEL // NUM_HEADS
        B, SQ, _ = x1.shape
        SK = x2.shape[1]

        def split_heads(t, S):
            return t.reshape(B, S, NUM_HEADS, HEAD_DIM).transpose(0, 2, 1, 3)
        Q = split_heads(x1 @ Wq + bq, SQ)
        K = split_heads(x2 @ Wk + bk, SK)
        V = split_heads(x2 @ Wv + bv, SK)
        scores = jnp.einsum('bhqd,bhkd->bhqk', Q, K) / jnp.sqrt(jnp.asarray(HEAD_DIM, Q.dtype))
        attn = jax.nn.softmax(scores, axis=-1)
        ctx = jnp.einsum('bhqk,bhkd->bhqd', attn, V)
        ctx = ctx.transpose(0, 2, 1, 3).reshape(B, SQ, D_MODEL)
        return ctx @ Wo + bo

    def _L0_attn_ref(x, gamma, Wq, Wkv, q_scale, k_scale, null_kv, Wout):
        import jax, jax.numpy as jnp
        import numpy as np
        HEADS = 16
        DIM_HEAD = 64
        SCALE = 8.0
        NUM_NULL_KV = 2
        NON_CAUSAL_PREFIX = 64
        LN_EPS = 1e-05

        def _l2norm(t):
            n = jnp.sqrt(jnp.sum(t * t, axis=-1, keepdims=True))
            return t / jnp.maximum(n, 1e-12)

        def _layer_norm(x, gamma):
            mu = jnp.mean(x, axis=-1, keepdims=True)
            var = jnp.mean((x - mu) ** 2, axis=-1, keepdims=True)
            return (x - mu) * jax.lax.rsqrt(var + LN_EPS) * gamma
        b, n, dim = x.shape
        kv = jnp.einsum('bnd,de->bne', x, Wkv)
        k, v = (kv[..., :DIM_HEAD], kv[..., DIM_HEAD:])
        xn = _layer_norm(x, gamma)
        q = jnp.einsum('bnd,de->bne', xn, Wq)
        null_k = jnp.broadcast_to(null_kv[0], (b, NUM_NULL_KV, DIM_HEAD))
        null_v = jnp.broadcast_to(null_kv[1], (b, NUM_NULL_KV, DIM_HEAD))
        k = jnp.concatenate([null_k, k], axis=1)
        v = jnp.concatenate([null_v, v], axis=1)
        q = q.reshape(b, n, HEADS, DIM_HEAD).transpose(0, 2, 1, 3)
        q = _l2norm(q) * q_scale
        k = _l2norm(k) * k_scale
        sim = jnp.einsum('bhid,bjd->bhij', q, k) * SCALE
        i, j = (n, k.shape[1])
        rows = jnp.arange(i)[:, None]
        cols = jnp.arange(j)[None, :]
        causal_mask = cols > rows + (j - i)
        prefix_free = (rows < NON_CAUSAL_PREFIX) & (cols < NON_CAUSAL_PREFIX + (j - i))
        causal_mask = causal_mask & ~prefix_free
        neg = -jnp.finfo(sim.dtype).max
        sim = jnp.where(causal_mask, neg, sim)
        attn = jax.nn.softmax(sim, axis=-1)
        out = jnp.einsum('bhij,bjd->bhid', attn, v)
        out = out.transpose(0, 2, 1, 3).reshape(b, n, HEADS * DIM_HEAD)
        return jnp.einsum('bne,ed->bnd', out, Wout)

    def _L0_ffn_ref(x, W_r, W_k, W_v, mu_r, mu_k):
        import jax, jax.numpy as jnp
        import numpy as np
        DIM = 256

        def _reference_tuple_inner(x, W_r, W_k, W_v, mu_r, mu_k):
            B, T, C = x.shape
            x_prev = jnp.concatenate([jnp.zeros((B, 1, C), x.dtype), x[:, :-1, :]], axis=1)
            xr = mu_r * x + (1.0 - mu_r) * x_prev
            xk = mu_k * x + (1.0 - mu_k) * x_prev
            r = jax.nn.sigmoid(jnp.einsum('btc,dc->btd', xr, W_r))
            k = jnp.einsum('btc,dc->btd', xk, W_k)
            k_act = jnp.square(jax.nn.relu(k))
            out = r * jnp.einsum('btc,dc->btd', k_act, W_v)
            new_state = x[:, -1, :]
            return (out, new_state)
        return _reference_tuple_inner(x, W_r, W_k, W_v, mu_r, mu_k)[0]

    def _L1_xattn_ref(x_q, x_kv, wq, bq, wk, bk, wv, bv, wo, bo):
        import jax, jax.numpy as jnp
        import numpy as np
        D_MODEL = 256
        NUM_HEADS = 16
        D_HEAD = D_MODEL // NUM_HEADS

        def _split_heads(x):
            B, L, _ = x.shape
            return x.reshape(B, L, NUM_HEADS, D_HEAD).transpose(0, 2, 1, 3)
        q = _split_heads(x_q @ wq.T + bq)
        k = _split_heads(x_kv @ wk.T + bk)
        v = _split_heads(x_kv @ wv.T + bv)
        scale = 1.0 / jnp.sqrt(jnp.asarray(D_HEAD, q.dtype))
        scores = jnp.einsum('bhqd,bhkd->bhqk', q, k) * scale
        attn = jax.nn.softmax(scores, axis=-1)
        out = jnp.einsum('bhqk,bhkd->bhqd', attn, v)
        B, H, Lq, Dh = out.shape
        out = out.transpose(0, 2, 1, 3).reshape(B, Lq, H * Dh)
        return out @ wo.T + bo

    def _L1_attn_ref(x, Wq, Wk, Wv, Wg, gk_w1, gk_w2, gk_b2, g_norm_w, Wo):
        import jax, jax.numpy as jnp
        import numpy as np
        NUM_HEADS = 4
        CHUNK = 64
        GATE_NORM = 16.0
        EPS = 1e-05

        def _xavier(key, fan_in, fan_out):
            gain = 2.0 ** (-2.5)
            limit = gain * np.sqrt(6.0 / (fan_in + fan_out))
            return jax.random.uniform(key, (fan_in, fan_out), jnp.float32, -limit, limit)

        def _to_chunks(t, B, H, NC, C):
            d = t.shape[-1]
            return t.reshape(B, H, NC, C, d).transpose(2, 0, 1, 3, 4)

        def _gla_forward(x, Wq, Wk, Wv, Wg, gk_w1, gk_w2, gk_b2, g_norm_w, Wo):
            B, L, D = x.shape
            H = NUM_HEADS
            C = CHUNK
            NC = L // C
            q = x @ Wq
            k = x @ Wk
            v = x @ Wv
            gk = jax.nn.log_sigmoid(x @ gk_w1 @ gk_w2 + gk_b2) / GATE_NORM

            def split_heads(t):
                return t.reshape(B, L, H, -1).transpose(0, 2, 1, 3)
            q, k, v, gk = map(split_heads, (q, k, v, gk))
            dk = q.shape[-1]
            scale = dk ** (-0.5)
            qc = _to_chunks(q, B, H, NC, C)
            kc = _to_chunks(k, B, H, NC, C)
            vc = _to_chunks(v, B, H, NC, C)
            gc = _to_chunks(gk, B, H, NC, C)
            Bcum = jnp.cumsum(gc, axis=3)
            causal = jnp.tril(jnp.ones((C, C), jnp.float32))

            def step(Hst, inp):
                qi, ki, vi, bi = inp
                qg = qi * jnp.exp(bi) * scale
                kg = ki * jnp.exp(-bi)
                o_inter = jnp.einsum('bhcd,bhde->bhce', qg, Hst)
                A = jnp.einsum('bhtd,bhsd->bhts', qg, kg) * causal
                o_intra = jnp.einsum('bhts,bhse->bhte', A, vi)
                b_last = bi[:, :, -1:, :]
                kH = ki * jnp.exp(b_last - bi)
                H_new = jnp.exp(b_last).transpose(0, 1, 3, 2) * Hst + jnp.einsum('bhcd,bhce->bhde', kH, vi)
                return (H_new, o_inter + o_intra)
            dv = v.shape[-1]
            H0 = jnp.zeros((B, H, dk, dv), jnp.float32)
            _, oc = jax.lax.scan(step, H0, (qc, kc, vc, Bcum))
            o = oc.transpose(1, 2, 0, 3, 4).reshape(B, H, L, dv)
            o = o.transpose(0, 2, 1, 3)
            rms = jnp.sqrt(jnp.mean(o * o, axis=-1, keepdims=True) + EPS)
            o_n = o / rms * g_norm_w
            g = (x @ Wg).reshape(B, L, H, dv)
            o = o_n * g * jax.nn.sigmoid(g)
            return o.reshape(B, L, H * dv) @ Wo
        return _gla_forward(x, Wq, Wk, Wv, Wg, gk_w1, gk_w2, gk_b2, g_norm_w, Wo)

    def _L1_ffn_ref(x, r1_w, r1_b, r2_w, w_up, w_down, a_up, a_down):
        import jax, jax.numpy as jnp
        import numpy as np
        E, G, TOPK = (32, 16, 2)
        HID, INTER, A_INTER = (256, 512, 128)
        CAP_FACTOR = 1.25
        SCALE = 0.05

        def _stats(x):
            mean = x.mean(-1, keepdims=True)
            std = jnp.std(x, axis=-1, keepdims=True, ddof=1)
            mn = x.min(-1, keepdims=True)
            mx = x.max(-1, keepdims=True)
            l2 = jnp.linalg.norm(x, axis=-1, keepdims=True)
            sp = (jnp.abs(x) < 1e-06).astype(x.dtype).mean(-1, keepdims=True)
            return jnp.concatenate([mean, std, mn, mx, l2, sp], -1)
        B, N, C = x.shape
        xf = x.reshape(-1, C)
        T = xf.shape[0]
        cap = int(CAP_FACTOR * T / E)
        ri = jnp.concatenate([xf, _stats(xf)], -1)
        h = jax.nn.gelu(ri @ r1_w.T + r1_b, approximate=False)
        probs = jax.nn.softmax(h @ r2_w.T, -1)
        topp, topi = jax.lax.top_k(probs, TOPK)
        wnorm = topp / topp.sum(-1, keepdims=True)
        eids = jnp.arange(E)
        hit = topi[..., None] == eids
        routed = hit.any(1)
        Wc = jnp.where(hit, wnorm[..., None], 0.0).sum(1)
        score = jnp.where(routed, probs, -jnp.inf)
        idx = jnp.argsort(-score, axis=0)[:cap].T
        valid = jnp.take_along_axis(routed.T, idx, 1)
        w = jnp.take_along_axis(Wc.T, idx, 1) * valid
        xe = xf[idx]
        up = jnp.einsum('eci,eji->ecj', xe, w_up)
        gate, upv = jnp.split(up, 2, axis=-1)
        hact = jax.nn.silu(gate) * upv
        ye = jnp.einsum('ecj,eoj->eco', hact, w_down)
        out = jnp.zeros((T, C), xf.dtype).at[idx.reshape(-1)].add((w[..., None] * ye).reshape(-1, C))
        Wmask = jnp.zeros((T, E), xf.dtype).at[idx, eids[:, None]].add(w)
        gw = SCALE * Wmask.reshape(T, G, E // G).sum(-1)
        aup = jnp.einsum('tc,gjc->tgj', xf, a_up)
        ag, av = jnp.split(aup, 2, axis=-1)
        ah = jax.nn.silu(ag) * av
        ay = jnp.einsum('tgj,goj->tgo', ah, a_down)
        out = out + jnp.einsum('tg,tgo->to', gw, ay)
        return out.reshape(B, N, C)

    def _L2_xattn_ref(image_emb, text_emb, edge_index, Wq, bq, Wk, bk, Wv, bv):
        import jax, jax.numpy as jnp
        import numpy as np
        DIM = 256
        D = image_emb.shape[-1]
        scale = D ** (-0.5)
        q = jnp.einsum('bsd,ed->bse', image_emb, Wq) + bq
        k = jnp.einsum('bsd,ed->bse', text_emb, Wk) + bk
        v = jnp.einsum('bsd,ed->bse', text_emb, Wv) + bv
        scores = jnp.einsum('bqd,bkd->bqk', q, k) * scale
        probs = jax.nn.softmax(scores, axis=-1)
        attended = jnp.einsum('bqk,bkd->bqd', probs, v)
        return attended

    def _L2_attn_ref(x, Wqa, Wqb, Wkva, Wkvb, Wout, bout):
        import jax, jax.numpy as jnp
        import numpy as np
        B, S, E = (4, 512, 256)
        H, KVH = (16, 4)
        D = E // H
        QL, KVL = (64, 32)
        ROPE_BASE = 10000.0

        def _rope(x):
            d = x.shape[-1]
            inv_freq = 1.0 / ROPE_BASE ** (jnp.arange(0, d, 2, dtype=jnp.float32) / d)
            t = jnp.arange(x.shape[1], dtype=jnp.float32)
            freqs = jnp.outer(t, inv_freq)
            cos = jnp.cos(freqs)[None, :, None, :].astype(x.dtype)
            sin = jnp.sin(freqs)[None, :, None, :].astype(x.dtype)
            x1, x2 = (x[..., ::2], x[..., 1::2])
            r1 = x1 * cos - x2 * sin
            r2 = x1 * sin + x2 * cos
            return jnp.stack([r1, r2], axis=-1).reshape(x.shape)
        b, s, _ = x.shape
        scale = D ** (-0.5)
        q = (x @ Wqa @ Wqb).reshape(b, s, H, D)
        kv = (x @ Wkva @ Wkvb).reshape(b, s, KVH, D, 2)
        k, v = (kv[..., 0], kv[..., 1])
        q = _rope(q)
        k = _rope(k)
        g = H // KVH
        k = jnp.repeat(k, g, axis=2)
        v = jnp.repeat(v, g, axis=2)
        scores = jnp.einsum('bqhd,bkhd->bhqk', q, k) * scale
        causal = jnp.triu(jnp.ones((s, s), dtype=bool), k=1)
        scores = jnp.where(causal[None, None], -jnp.inf, scores)
        w = jax.nn.softmax(scores, axis=-1)
        out = jnp.einsum('bhqk,bkhd->bqhd', w, v).reshape(b, s, E)
        return out @ Wout + bout

    def _L2_ffn_ref(x, w_fc, b_fc, w_proj, b_proj):
        import jax, jax.numpy as jnp
        import numpy as np
        B, S, N_EMBD = (4, 1024, 256)
        HIDDEN = 4 * N_EMBD
        M_BITS_FC = 3
        M_BITS_PROJ = 3
        BLOCK_K = 32

        def block_quant(v, m_bits, bk):
            *lead, K = v.shape
            vb = v.reshape(*lead, K // bk, bk)
            amax = jnp.max(jnp.abs(vb), axis=-1, keepdims=True)
            tiny = jnp.asarray(2.0 ** (-126), v.dtype)
            e = jnp.floor(jnp.log2(jnp.maximum(amax, tiny)))
            scale = jnp.exp2(e - m_bits)
            q = jnp.round(vb / scale) * scale
            q = vb + jax.lax.stop_gradient(q - vb)
            return q.reshape(v.shape)

        def lowprec_linear(x, w, b, m_bits, bk):
            xq = block_quant(x, m_bits, bk)
            wq = block_quant(w, m_bits, bk)
            return jnp.einsum('bsk,nk->bsn', xq, wq) + b
        h = lowprec_linear(x, w_fc, b_fc, M_BITS_FC, BLOCK_K)
        h = jax.nn.gelu(h, approximate=False)
        return lowprec_linear(h, w_proj, b_proj, M_BITS_PROJ, BLOCK_K)

    def _L3_xattn_ref(x, context, Wq, Wk, Wv, Wo):
        import jax, jax.numpy as jnp
        import numpy as np
        DIM = 256
        H = 16
        DH = 64
        INNER = H * DH
        SCALE = DH ** (-0.5)
        B, L, _ = x.shape
        R = context.shape[1]
        q = (x @ Wq).reshape(B, L, H, DH).transpose(0, 2, 1, 3)
        k = (context @ Wk).reshape(B, R, H, DH).transpose(0, 2, 1, 3)
        v = (context @ Wv).reshape(B, R, H, DH).transpose(0, 2, 1, 3)
        scores = jnp.einsum('bhld,bhrd->bhlr', q, k) * SCALE
        attn = jax.nn.softmax(scores, axis=-1)
        out = jnp.einsum('bhlr,bhrd->bhld', attn, v)
        out = out.transpose(0, 2, 1, 3).reshape(B, L, INNER)
        return out @ Wo

    def _L3_attn_ref(X, W_Q, W_K, W_V, W_G, W_O, gn_weight, gn_bias):
        import math
        import jax, jax.numpy as jnp
        import numpy as np
        B, L, DIM, HEADS = (4, 512, 256, 8)
        HEAD = DIM // HEADS
        SCALE_BASE = 512.0
        EPS = 1e-05

        def _xpos(x, downscale=False):
            l, dh = (x.shape[-2], x.shape[-1])
            half = dh // 2
            pos = jnp.arange(l, dtype=x.dtype)
            base = (jnp.arange(0, dh, 2, dtype=x.dtype) + 0.4 * dh) / (1.4 * dh)
            scale = base[None, :] ** (pos[:, None] / SCALE_BASE)
            inv_freq = 1.0 / 10000.0 ** (jnp.arange(half, dtype=x.dtype) / half)
            sinusoid = pos[:, None] * inv_freq[None, :]
            sin, cos = (jnp.sin(sinusoid), jnp.cos(sinusoid))
            if downscale:
                scale = 1.0 / scale
            s = jnp.repeat(sin * scale, 2, axis=-1)
            c = jnp.repeat(cos * scale, 2, axis=-1)
            x1, x2 = (x[..., ::2], x[..., 1::2])
            rot = jnp.stack([-x2, x1], axis=-1).reshape(x.shape)
            return x * c + rot * s

        def _decay_mask(l, gammas):
            n = jnp.arange(l)[:, None]
            m = jnp.arange(l)[None, :]
            lg = jnp.log(gammas)
            expo = (n - m).astype(jnp.float32)[None, :, :] * lg[:, None, None]
            return jnp.where((n >= m)[None], jnp.exp(expo), 0.0)
        b, l, d = X.shape
        h = W_Q.shape[0]
        gammas = 1.0 - jnp.exp(jnp.linspace(math.log(1.0 / 32.0), math.log(1.0 / 512.0), h)).astype(jnp.float32)
        Q = jnp.einsum('bld,hde->bhle', X, W_Q)
        K = jnp.einsum('bld,hde->bhle', X, W_K)
        V = jnp.einsum('bld,hdv->bhlv', X, W_V)
        Q = _xpos(Q)
        K = _xpos(K, downscale=True)
        D = _decay_mask(l, gammas).astype(X.dtype)
        scores = jnp.einsum('bhle,bhme->bhlm', Q, K) * D[None]
        Y = jnp.einsum('bhlm,bhmv->bhlv', scores, V)
        mean = Y.mean(axis=-1, keepdims=True)
        var = Y.var(axis=-1, keepdims=True)
        Yn = (Y - mean) * jax.lax.rsqrt(var + EPS)
        Yn = jnp.transpose(Yn, (0, 2, 1, 3)).reshape(b, l, -1)
        Yn = Yn * gn_weight + gn_bias
        G = X @ W_G
        out = G * jax.nn.sigmoid(G) * Yn @ W_O
        return out

    def _L3_ffn_ref(x, alpha, w_gate, b_gate, W1m, b1m, W2m, b2m, W1e, b1e, W2e, b2e):
        import jax, jax.numpy as jnp
        import numpy as np
        from jax import lax
        B, N, D, H, E, K = (16, 256, 256, 1024, 8, 2)
        main = jax.nn.gelu(x @ W1m + b1m) @ W2m + b2m
        logits = jnp.mean(x, axis=1) @ w_gate + b_gate
        probs = jax.nn.softmax(logits, axis=-1)
        top_vals, top_idx = lax.top_k(probs, K)
        gate_w = top_vals / jnp.sum(top_vals, axis=-1, keepdims=True)
        W1g = W1e[top_idx]
        b1g = b1e[top_idx]
        W2g = W2e[top_idx]
        b2g = b2e[top_idx]
        h = jax.nn.gelu(jnp.einsum('bnd,bkdh->bknh', x, W1g) + b1g[:, :, None, :])
        eo = jnp.einsum('bknh,bkhd->bknd', h, W2g) + b2g[:, :, None, :]
        expert_out = jnp.einsum('bk,bknd->bnd', gate_w, eo)
        a = jnp.clip(alpha, 0.1, 1.0)
        return a * main + (1.0 - a) * expert_out
    x = x + _L0_xattn_ref(_layernorm(x, axis=-1), ctx_1024, L0_xattn_Wq, L0_xattn_bq, L0_xattn_Wk, L0_xattn_bk, L0_xattn_Wv, L0_xattn_bv, L0_xattn_Wo, L0_xattn_bo)
    x = x + _L0_attn_ref(_layernorm(x, axis=-1), L0_attn_gamma, L0_attn_Wq, L0_attn_Wkv, L0_attn_q_scale, L0_attn_k_scale, L0_attn_null_kv, L0_attn_Wout)
    x = x + _L0_ffn_ref(_layernorm(x, axis=-1), L0_ffn_W_r, L0_ffn_W_k, L0_ffn_W_v, L0_ffn_mu_r, L0_ffn_mu_k)
    x = x + _L1_xattn_ref(_layernorm(x, axis=-1), ctx_1024, L1_xattn_wq, L1_xattn_bq, L1_xattn_wk, L1_xattn_bk, L1_xattn_wv, L1_xattn_bv, L1_xattn_wo, L1_xattn_bo)
    x = x + _L1_attn_ref(_layernorm(x, axis=-1), L1_attn_Wq, L1_attn_Wk, L1_attn_Wv, L1_attn_Wg, L1_attn_gk_w1, L1_attn_gk_w2, L1_attn_gk_b2, L1_attn_g_norm_w, L1_attn_Wo)
    x = x + _L1_ffn_ref(_layernorm(x, axis=-1), L1_ffn_r1_w, L1_ffn_r1_b, L1_ffn_r2_w, L1_ffn_w_up, L1_ffn_w_down, L1_ffn_a_up, L1_ffn_a_down)
    x = x + _L2_xattn_ref(_layernorm(x, axis=-1), ctx_1024, L2_xattn_edge_index, L2_xattn_Wq, L2_xattn_bq, L2_xattn_Wk, L2_xattn_bk, L2_xattn_Wv, L2_xattn_bv)
    x = x + _L2_attn_ref(_layernorm(x, axis=-1), L2_attn_Wqa, L2_attn_Wqb, L2_attn_Wkva, L2_attn_Wkvb, L2_attn_Wout, L2_attn_bout)
    x = x + _L2_ffn_ref(_layernorm(x, axis=-1), L2_ffn_w_fc, L2_ffn_b_fc, L2_ffn_w_proj, L2_ffn_b_proj)
    x = x + _L3_xattn_ref(_layernorm(x, axis=-1), ctx_1024, L3_xattn_Wq, L3_xattn_Wk, L3_xattn_Wv, L3_xattn_Wo)
    x = x + _L3_attn_ref(_layernorm(x, axis=-1), L3_attn_W_Q, L3_attn_W_K, L3_attn_W_V, L3_attn_W_G, L3_attn_W_O, L3_attn_gn_weight, L3_attn_gn_bias)
    x = x + _L3_ffn_ref(_layernorm(x, axis=-1), L3_ffn_alpha, L3_ffn_w_gate, L3_ffn_b_gate, L3_ffn_W1m, L3_ffn_b1m, L3_ffn_W2m, L3_ffn_b2m, L3_ffn_W1e, L3_ffn_b1e, L3_ffn_W2e, L3_ffn_b2e)
    return x

_drawn_inputs = setup_inputs


def setup_inputs(seed=0):
    import zlib

    import numpy as np

    out = dict(_drawn_inputs(seed))
    spreads = {'L0_xattn_bq': (0.0, 0.1),
     'L0_xattn_bk': (0.0, 2.0),
     'L0_xattn_bv': (0.0, 0.1),
     'L0_xattn_bo': (0.0, 0.1),
     'L0_attn_gamma': (1.0, 0.2),
     'L0_attn_q_scale': (1.0, 0.2),
     'L0_attn_k_scale': (1.0, 0.2),
     'L1_xattn_bq': (0.0, 0.1),
     'L1_xattn_bk': (0.0, 2.0),
     'L1_xattn_bv': (0.0, 0.1),
     'L1_xattn_bo': (0.0, 0.1),
     'L1_attn_gk_b2': (0.0, 0.529),
     'L1_attn_g_norm_w': (1.0, 0.6),
     'L1_ffn_r1_b': (0.0, 0.478),
     'L2_xattn_bq': (0.0, 0.1),
     'L2_xattn_bk': (0.0, 2.0),
     'L2_xattn_bv': (0.0, 0.1),
     'L2_ffn_b_fc': (0.0, 0.1),
     'L2_ffn_b_proj': (0.0, 0.1),
     'L3_attn_gn_weight': (1.0, 0.6),
     'L3_attn_gn_bias': (0.0, 0.8),
     'L3_ffn_b_gate': (0.0, 0.8),
     'L3_ffn_b1m': (0.0, 0.466),
     'L3_ffn_b2m': (0.0, 0.1),
     'L3_ffn_b1e': (0.0, 0.8),
     'L3_ffn_b2e': (0.0, 2.0)}
    factors = {'L1_attn_gk_w1': 8.0,
     'L1_attn_gk_w2': 8.0,
     'L1_ffn_r1_w': 2.68,
     'L1_ffn_r2_w': 2.72,
     'L1_ffn_w_up': 3.21,
     'L1_ffn_w_down': 3.129,
     'L1_ffn_a_up': 8.0,
     'L1_ffn_a_down': 8.0,
     'L2_attn_Wqa': 64.0,
     'L2_attn_Wqb': 64.0,
     'L3_attn_W_Q': 8.0,
     'L3_attn_W_K': 8.0,
     'L3_attn_W_V': 8.0,
     'L3_attn_W_G': 8.0,
     'L3_attn_W_O': 8.0,
     'L3_ffn_w_gate': 8.0,
     'L3_ffn_W1e': 8.0,
     'L3_ffn_W2e': 8.0}
    for name, (base, spread) in spreads.items():
        noise = np.random.default_rng([zlib.crc32(name.encode()), seed]).standard_normal(out[name].shape)
        drawn = base * np.exp(spread * noise) if base else spread * noise
        out[name] = jnp.asarray(drawn.astype(out[name].dtype))
    for name, factor in factors.items():
        out[name] = (out[name] * factor).astype(out[name].dtype)
    return out
```

```python
from contextlib import ExitStack

import numpy as np

import concourse.bass as bass
from concourse import mybir

F32 = mybir.dt.float32
BF16 = mybir.dt.bfloat16
I32 = mybir.dt.int32
U32 = mybir.dt.uint32
ALU = mybir.AluOpType
ACT = mybir.ActivationFunctionType
AX = mybir.AxisListType

P = 128
D = 256
DT = D // P
KEYS = 12544
CH = 896
BLK = CH // 2
TPC = CH // P
NCH = KEYS // CH
LN_EPS = 1e-5
FIRST, LAST = 0, 12


class Chain:

    def __init__(self, eng, sem):
        self.eng, self.sem, self.n = eng, sem, 0

    def __call__(self, ins):
        self.n += 1
        ins.then_inc(self.sem, 1)
        self.eng.wait_ge(self.sem, self.n)


class Core:

    def __init__(self, nc, ctx, dram, cols):
        self.nc, self.ctx, self.dram, self.cols = nc, ctx, dram, cols
        self.x = ctx.enter_context(nc.sbuf_tensor("rows", [P, D], F32))
        self.const = ctx.enter_context(nc.sbuf_tensor("consts", [P, cols["const"]["_"]], F32))
        self.psum = ctx.enter_context(nc.psum_tensor("psum", [P, 8, 512], F32))
        self.w = None

    def constant(self, name):
        a, b = self.cols["const"][name]
        return self.const[:, a:b]

    def weight(self, name):
        a, b = self.cols[self.layer][name]
        return self.w[:, a:b]

    def kxn(self, name, k=DT):
        return self.weight(name).rearrange("p (k n) -> p k n", k=k)

    def ident(self, n=P):
        return self.constant("ident")[0:n, 0:n]


class Scope:

    def __init__(self, core, name):
        self.nc, self.name, self.ctx, self.sems = core.nc, name, ExitStack(), []

    def __enter__(self):
        return self

    def __exit__(self, *e):
        self.ctx.__exit__(*e)
        if e[0] is None:
            self.nc.clear_and_free_semaphores(self.sems)
            self.nc.all_engine_barrier(sem_only=True)

    def sb(self, name, shape, dt=F32):
        return self.ctx.enter_context(self.nc.sbuf_tensor(f"{self.name}_{name}", shape, dt))

    def signals(self, names):
        made = [self.nc.alloc_semaphore(f"{self.name}_{n}") for n in names.split()]
        self.sems += made
        return made


class Norm:

    def __init__(self, core, scope, src=None, gamma=None, tag="ln"):
        self.nc, self.ident, self.gamma = core.nc, core.ident(), gamma
        self.src = core.x[:] if src is None else src
        self.stats = scope.sb(f"{tag}_stats", [P, 6])
        self.mv = scope.sb(f"{tag}_mv", [P, 2])
        self.std = scope.sb(f"{tag}_std", [P, 1])
        self.rstd = scope.sb(f"{tag}_rstd", [P, 1])
        self.xn = scope.sb(f"{tag}_xn", [P, D])
        self.xnT = scope.sb(f"{tag}_xnT", [P, DT, P])
        self.ps = core.psum[:, 7, 0:DT * P]
        self.var_ready, self.std_ready, self.xn_ready, self.xT_in_psum, self.xT_ready = scope.signals(
            f"{tag}_var_ready {tag}_std_ready {tag}_xn_ready {tag}_xT_in_psum {tag}_xT_ready")

    def vector(self, dve, chain):
        nc = self.nc
        chain(nc.vector.bn_stats(self.stats[:], self.src))
        chain(nc.vector.bn_aggr(self.mv[:], self.stats[:]))
        nc.vector.tensor_scalar(self.rstd[:], self.mv[:, 1:2], LN_EPS, None, ALU.add).then_inc(self.var_ready, 1)
        dve.wait_ge(self.std_ready, 1)
        chain(nc.vector.reciprocal(self.rstd[:], self.std[:]))
        last = nc.vector.tensor_scalar(self.xn[:], self.src, self.mv[:, 0:1], self.rstd[:], ALU.subtract, ALU.mult)
        if self.gamma is not None:
            chain(last)
            last = nc.vector.tensor_tensor(self.xn[:], self.xn[:], self.gamma, ALU.mult)
        last.then_inc(self.xn_ready, 1)
        dve.wait_ge(self.xT_in_psum, 1)
        nc.vector.tensor_copy(self.xnT[:].rearrange("p k t -> p (k t)"), self.ps).then_inc(self.xT_ready, 1)
        dve.wait_ge(self.xT_ready, 1)

    def scalar(self, act):
        act.wait_ge(self.var_ready, 1)
        self.nc.scalar.activation(self.std[:], self.rstd[:], ACT.Sqrt).then_inc(self.std_ready, 1)

    def tensor(self, pe):
        pe.wait_ge(self.xn_ready, 1)
        for k in range(DT):
            last = self.nc.tensor.transpose(self.ps[:, k * P:(k + 1) * P], self.xn[:, k * P:(k + 1) * P],
                                            self.ident)
        last.then_inc(self.xT_in_psum, 1)


def cross_attention(core, name, heads, groups, wq, wk, wv, wo, bq, bk, bv, bo, scale):
    nc = core.nc
    dh = D // heads
    per = max(1, heads // DT)
    hq = per * P
    units = 2 if heads == 16 else 1
    UW = heads * P // units
    VW = heads * (dh + 1)
    with Scope(core, name) as s:
        norm = Norm(core, s)
        ctxb = s.sb("ctx", [P, 2, DT, CH])
        kT = s.sb("kT", [P, 2, DT, CH])
        v = s.sb("v", [P, 2, TPC, heads, dh + 1])
        prob = s.sb("prob", [P, 2, heads * P])
        qT = s.sb("qT", [P, DT, P])
        qbd = s.sb("qbd", [P, DT, per, P])
        chunk_max = s.sb("chunk_max", [P, 2, heads])
        run_max = s.sb("run_max", [P, heads])
        neg = s.sb("neg", [P, 2, heads])
        m3b = s.sb("m3b", [P, 3, heads], BF16)
        m3f = s.sb("m3f", [P, 3 * heads])
        m3T = s.sb("m3T", [3 * heads, P], BF16)
        m3row = s.sb("m3row", [3, heads * P], BF16)
        ones3 = s.sb("ones3", [3, P], BF16)
        oacc = s.sb("oacc", [P, VW])
        rden = s.sb("rden", [P, heads, 1])
        o = s.sb("o", [P, D])
        oT = s.sb("oT", [P, DT, P])
        ps = core.psum
        ident = core.ident()
        m3_dram = nc.dram_tensor(f"{name}_m3", [3 * heads, P], BF16).ap()

        (ctx_free, k_in_psum, k_ready, q_in_psum, q_ready, s_full, s_free, neg_ready, m3_in_psum, m3T_ready,
         m3_rows, st_full, p_ready, pv_done, v_in_psum, v_ready, o_added, o_ready, oT_in_psum, oT_ready,
         y_in_psum, x_done, chain_sem, max_step, m3_stored) = s.signals(
            "ctx_free k_in_psum k_ready q_in_psum q_ready s_full s_free neg_ready m3_in_psum m3T_ready "
            "m3_rows st_full p_ready pv_done v_in_psum v_ready o_added o_ready oT_in_psum oT_ready "
            "y_in_psum x_done chain_sem max_step m3_stored")
        ctx_in = s.signals("ctx_in0 ctx_in1")
        K_RING, S_RING, ST_RING, V_RING, O_RING, CTX_RING = 2, 2, 2, 2, 2, 2
        S_CREDIT = heads + 1
        ST_CREDIT = TPC * units + 1
        PV_CREDIT = TPC * units + 1

        ctxT = core.dram["ctxT"].rearrange("(k p) n -> p k n", p=P)
        block = s.ctx.enter_context(nc.Block())

        @block.sync
        def _(sp):
            for g in range(groups):
                for ps_no in range(2):
                    base = (2 * g + ps_no) * NCH
                    with sp.Fori(0, NCH // 2) as i:
                        for b in range(2):
                            sp.wait_ge(ctx_free, i * 2 + (base + b + 1))
                            sp.dma_start(ctxb[:, b], ctxT[:, :, bass.ds(i * (2 * CH) + b * CH, CH)]).then_inc(
                                ctx_in[b], 16)

        @block.gpsimd
        def _(pool):
            pool.sem_inc(ctx_free, CTX_RING)
            pool.sem_inc(k_ready, K_RING)
            pool.sem_inc(s_full, S_CREDIT)
            pool.sem_inc(s_free, S_RING)
            pool.sem_inc(st_full, ST_CREDIT)
            pool.sem_inc(p_ready, ST_RING)
            pool.sem_inc(pv_done, PV_CREDIT)
            pool.sem_inc(v_ready, V_RING)
            pool.sem_inc(o_added, O_RING)

        @block.scalar
        def _(act):
            norm.scalar(act)
            for g in range(groups):
                def keys(i, b, base, k_free_wait):
                    k_free_wait()
                    for hb in range(4):
                        half, blk = hb // 2, hb % 2
                        act.wait_ge(k_in_psum, i * 8 + (4 * (base + b) + hb + 1))
                        nc.scalar.activation(kT[:, b, half, blk * BLK:(blk + 1) * BLK], ps[:, 6 + hb % 2, 0:BLK],
                                             ACT.Identity, bias=bk(g, half)).then_inc(k_ready, 1)

                base = 2 * g * NCH
                with act.Fori(0, NCH // 2) as i:
                    for b in range(2):
                        keys(i, b, base, lambda: act.wait_ge(
                            s_full, i * (2 * heads) + ((g * NCH + b) * heads + 1)))
                act.wait_ge(m3T_ready, g + 1)
                act.dma_start(m3_dram[:, :], m3T[:]).then_inc(m3_stored, 16)
                act.wait_ge(m3_stored, 16 * (g + 1))
                act.dma_start(m3row[:], m3_dram.rearrange("(k h) q -> k (h q)", k=3)).then_inc(m3_rows, 16)
                base = (2 * g + 1) * NCH
                with act.Fori(0, NCH // 2) as i:
                    for b in range(2):
                        cu = TPC * units
                        keys(i, b, base, lambda: act.wait_ge(
                            st_full, i * (2 * cu) + ((g * NCH + b) * cu + 1)))
                        for t in range(TPC):
                            for u in range(units):
                                at = (g * NCH + b) * cu + t * units + u
                                act.wait_ge(st_full, i * (2 * cu) + (at + 1 + ST_CREDIT))
                                act.wait_ge(pv_done, i * (2 * cu) + (at + 1 + PV_CREDIT - 2 * units))
                                slot = (b * TPC + t) % 2
                                bank = 2 * ((at if units == 1 else u) % 2)
                                src = ps[:, bank:bank + 2, :].rearrange("p a n -> p (a n)")[:, 0:UW]
                                nc.scalar.activation(prob[:, slot, u * UW:(u + 1) * UW], src,
                                                     ACT.Exp).then_inc(p_ready, 1)

        @block.vector
        def _(dve):
            chain = Chain(dve, chain_sem)
            chain(nc.vector.memset(ones3[:], 1.0))
            chain(nc.vector.memset(v[:, :, :, :, dh:dh + 1].rearrange("p a t h w -> p (a t h) w"), 1.0))
            norm.vector(dve, chain)
            for g in range(groups):
                chain(nc.vector.memset(run_max[:], -3.0e38))
                dve.wait_ge(q_in_psum, g + 1)
                for k in range(DT):
                    last = nc.vector.tensor_scalar(qT[:, k, :], ps[:, 4, k * P:(k + 1) * P], bq(g, k), scale,
                                                   ALU.add, ALU.mult)
                chain(last)
                for k in range(DT):
                    if heads == 1:
                        last = nc.vector.tensor_copy(qbd[:, k, 0, :], qT[:, k, :])
                    else:
                        mask = core.constant(f"head{dh}")
                        last = nc.vector.tensor_tensor(
                            qbd[:, k], qT[:, k, :].unsqueeze(1).to_broadcast([P, per, P]),
                            mask.unsqueeze(2).to_broadcast([P, per, P]), ALU.mult)
                last.then_inc(q_ready, 1)
                with dve.Fori(0, NCH // 2) as i:
                    for b in range(2):
                        for h in range(heads):
                            at = (g * NCH + b) * heads + h
                            dve.wait_ge(s_full, i * (2 * heads) + (at + 1 + S_CREDIT))
                            bank = 2 * (at % 2)
                            nc.vector.tensor_reduce(chunk_max[:, b, h:h + 1], ps[:, bank:bank + 2, 0:BLK],
                                                    AX.XY, ALU.max).then_inc(s_free, 1)
                        dve.wait_ge(s_free, i * (2 * heads) + ((g * NCH + b + 1) * heads + S_RING))
                        if b:
                            dve.wait_ge(max_step, i * 2 + (g * NCH + 1))
                        nc.vector.tensor_tensor(run_max[:], run_max[:], chunk_max[:, b], ALU.max).then_inc(
                            max_step, 1)
                        if b:
                            dve.wait_ge(max_step, i * 2 + (g * NCH + 2))
                chain(nc.vector.tensor_scalar(neg[:, 0], run_max[:], -1.0, None, ALU.mult))
                for k in range(3):
                    chain(nc.vector.tensor_copy(m3b[:, k], neg[:, k % 2]))
                    if k < 2:
                        chain(nc.vector.tensor_tensor(neg[:, (k + 1) % 2], neg[:, k % 2], m3b[:, k],
                                                      ALU.subtract))
                nc.vector.tensor_copy(m3f[:], m3b[:].rearrange("p a h -> p (a h)")).then_inc(neg_ready, 1)
                dve.wait_ge(m3_in_psum, g + 1)
                nc.vector.tensor_copy(m3T[:], ps[0:3 * heads, 5, 0:P]).then_inc(m3T_ready, 1)
                chain(nc.vector.memset(oacc[:], 0.0))
                cu = TPC * units
                with dve.Fori(0, NCH // 2) as i:
                    for b in range(2):
                        dve.wait_ge(pv_done, i * (2 * cu) + ((g * NCH + b) * cu + 1))
                        for t in range(TPC):
                            at = (g * NCH + b) * TPC + t
                            dve.wait_ge(v_in_psum, i * (2 * TPC) + (at + 1))
                            src = ps[:, 6 + at % 2, 0:D].rearrange("p (h w) -> p h w", h=heads)
                            nc.vector.tensor_tensor(v[:, b, t, :, 0:dh], src,
                                                    bv(g).rearrange("p (h w) -> p h w", h=heads),
                                                    ALU.add).then_inc(v_ready, 1)
                        dve.wait_ge(pv_done, i * (2 * cu) + ((g * NCH + b + 1) * cu + PV_CREDIT))
                        if b:
                            dve.wait_ge(o_added, i * 2 + (g * NCH + 1 + O_RING))
                        nc.vector.tensor_tensor(oacc[:], oacc[:], ps[:, 4 + b, 0:VW], ALU.add).then_inc(
                            o_added, 1)
                        if b:
                            dve.wait_ge(o_added, i * 2 + (g * NCH + 2 + O_RING))
                oa = oacc[:].rearrange("p (h w) -> p h w", h=heads)
                chain(nc.vector.reciprocal(rden[:], oa[:, :, dh:dh + 1]))
                nc.vector.tensor_tensor(o[:].rearrange("p (h w) -> p h w", h=heads), oa[:, :, 0:dh],
                                        rden[:].to_broadcast([P, heads, dh]), ALU.mult).then_inc(o_ready, 1)
                dve.wait_ge(oT_in_psum, g + 1)
                nc.vector.tensor_copy(oT[:].rearrange("p k t -> p (k t)"), ps[:, 4, 0:D]).then_inc(oT_ready, 1)
                if wo is None:
                    chain(nc.vector.tensor_tensor(core.x[:], core.x[:], o[:], ALU.add))
                else:
                    dve.wait_ge(y_in_psum, g + 1)
                    chain(nc.vector.tensor_tensor(core.x[:], core.x[:], ps[:, 5, 0:D], ALU.add))
                    if bo is not None and g == 0:
                        chain(nc.vector.tensor_tensor(core.x[:], core.x[:], bo, ALU.add))

        @block.tensor
        def _(pe):
            norm.tensor(pe)
            for g in range(groups):
                pe.wait_ge(norm.xT_ready, 1)
                if g:
                    pe.wait_ge(oT_ready, g)
                for half in range(DT):
                    for k in range(DT):
                        last = nc.tensor.matmul(ps[:, 4, half * P:(half + 1) * P], wq(g, k, half),
                                                norm.xnT[:, k, :], start=(k == 0), stop=(k == DT - 1))
                last.then_inc(q_in_psum, 1)

                def keys(i, b, base):
                    pe.wait_ge(ctx_in[b], i * 16 + (base // 2 + 1) * 16)
                    for hb in range(4):
                        half, blk = hb // 2, hb % 2
                        pe.wait_ge(k_ready, i * 8 + (4 * (base + b) + hb + 1))
                        for k in range(DT):
                            last = nc.tensor.matmul(ps[:, 6 + hb % 2, 0:BLK], wk(g, k, half),
                                                    ctxb[:, b, k, blk * BLK:(blk + 1) * BLK],
                                                    start=(k == 0), stop=(k == DT - 1))
                        if hb < 3:
                            last.then_inc(k_in_psum, 1)
                    return last

                pe.wait_ge(q_ready, g + 1)
                base = 2 * g * NCH
                with pe.Fori(0, NCH // 2) as i:
                    for b in range(2):
                        keys(i, b, base).then_inc(k_in_psum, 1)
                        pe.wait_ge(k_ready, i * 8 + (4 * (base + b) + 4 + K_RING))
                        pe.sem_inc(ctx_free, 1)
                        for h in range(heads):
                            at = (g * NCH + b) * heads + h
                            bank = 2 * (at % 2)
                            pe.wait_ge(s_free, i * (2 * heads) + (at + 1))
                            for blk in range(2):
                                if heads == 1:
                                    for k in range(DT):
                                        last = nc.tensor.matmul(ps[:, bank + blk, 0:BLK], qbd[:, k, 0, :],
                                                                kT[:, b, k, blk * BLK:(blk + 1) * BLK],
                                                                start=(k == 0), stop=(k == DT - 1))
                                else:
                                    last = nc.tensor.matmul(ps[:, bank + blk, 0:BLK],
                                                            qbd[:, h // per, h % per, :],
                                                            kT[:, b, h // per, blk * BLK:(blk + 1) * BLK],
                                                            start=True, stop=True)
                            last.then_inc(s_full, 1)
                pe.wait_ge(neg_ready, g + 1)
                nc.tensor.transpose(ps[0:3 * heads, 5, 0:P], m3f[:], ident).then_inc(m3_in_psum, 1)
                pe.wait_ge(m3_rows, 16 * (g + 1))

                base = (2 * g + 1) * NCH
                cu = TPC * units

                def scores(i, b, t):
                    for u in range(units):
                        at = (g * NCH + b) * cu + t * units + u
                        pe.wait_ge(p_ready, i * (2 * cu) + (at + 1))
                        slot = 2 * ((at if units == 1 else u) % 2)
                        flat = ps[:, slot:slot + 2, :].rearrange("p a n -> p (a n)")
                        for c0 in range(0, UW, 512):
                            w = min(512, UW)
                            nc.tensor.matmul(flat[:, c0:c0 + w], ones3[:],
                                             m3row[:, u * UW + c0:u * UW + c0 + w], start=True, stop=False,
                                             skip_group_check=True)
                        keys_of = kT[:, b, :, t * P:(t + 1) * P]
                        for k in range(DT) if units == 1 else [u]:
                            for c0 in range(0, hq, 512):
                                w = min(512, hq)
                                at0 = c0 + (k * hq if units == 1 and heads > 1 else 0)
                                q = qbd[:, k].rearrange("p j q -> p (j q)")
                                last = nc.tensor.matmul(flat[:, at0:at0 + w], keys_of[:, k, :],
                                                        q[:, c0:c0 + w], start=False, stop=True,
                                                        skip_group_check=True)
                        last.then_inc(st_full, 1)

                def values(i, b, t):
                    slot = (b * TPC + t) % 2
                    for u in range(units):
                        at = (g * NCH + b) * cu + t * units + u
                        pe.wait_ge(p_ready, i * (2 * cu) + (at + 1 + ST_RING))
                        for h in range(u * heads // units, (u + 1) * heads // units):
                            last = nc.tensor.matmul(ps[:, 4 + b, h * (dh + 1):(h + 1) * (dh + 1)],
                                                    prob[:, slot, h * P:(h + 1) * P], v[:, b, t, h, :],
                                                    start=(t == 0 and h == 0), stop=(t == TPC - 1),
                                                    skip_group_check=True)
                        last.then_inc(pv_done, 1)

                with pe.Fori(0, NCH // 2) as i:
                    for b in range(2):
                        keys(i, b, base).then_inc(k_in_psum, 1)
                        pe.wait_ge(k_ready, i * 8 + (4 * (base + b) + 4 + K_RING))
                        for t in range(TPC):
                            at = (g * NCH + b) * TPC + t
                            pe.wait_ge(v_ready, i * (2 * TPC) + (at + 1))
                            for k in range(DT):
                                last = nc.tensor.matmul(ps[:, 6 + at % 2, 0:D],
                                                        ctxb[:, b, k, t * P:(t + 1) * P], wv(g, k),
                                                        start=(k == 0), stop=(k == DT - 1))
                            last.then_inc(v_in_psum, 1)
                        pe.wait_ge(v_ready, i * (2 * TPC) + ((g * NCH + b + 1) * TPC + V_RING))
                        pe.sem_inc(ctx_free, 1)
                        pe.wait_ge(o_added, i * 2 + (g * NCH + b + 1))
                        scores(i, b, 0)
                        for t in range(1, TPC):
                            scores(i, b, t)
                            values(i, b, t - 1)
                        values(i, b, TPC - 1)
                pe.wait_ge(o_ready, g + 1)
                for k in range(DT):
                    last = nc.tensor.transpose(ps[:, 4, k * P:(k + 1) * P], o[:, k * P:(k + 1) * P], ident)
                last.then_inc(oT_in_psum, 1)
                if wo is not None:
                    pe.wait_ge(oT_ready, g + 1)
                    for k in range(DT):
                        last = nc.tensor.matmul(ps[:, 5, 0:D], oT[:, k, :], wo(g, k), start=(k == 0),
                                                stop=(k == DT - 1))
                    last.then_inc(y_in_psum, 1)


class RowSoftmax:

    def __init__(self, core, scope, heads, width, per_bank, scale, mask):
        self.nc, self.ps, self.ident = core.nc, core.psum, core.ident()
        self.heads, self.width, self.per_bank, self.scale, self.mask = heads, width, per_bank, scale, mask
        self.p = scope.sb("p", [P, heads, width])
        self.top = scope.sb("top", [P, heads])
        self.pT = scope.sb("pT", [P, heads, P])
        self.s_in_psum, self.shifted, self.exp_done, self.p_ready, self.pT_in_psum, self.pT_ready = scope.signals(
            "s_in_psum shifted exp_done p_ready pT_in_psum pT_ready")

    def bc(self, a, width):
        return a.unsqueeze(2).to_broadcast([P, self.heads, width])

    def vector(self, dve, chain):
        nc = self.nc
        dve.wait_ge(self.s_in_psum, 1)
        for h in range(0, self.heads, self.per_bank):
            n = min(self.per_bank, self.heads - h)
            src = self.ps[:, h // self.per_bank, 0:n * self.width].rearrange("p (h c) -> p h c", h=n)
            last = nc.vector.scalar_tensor_tensor(self.p[:, h:h + n], src, self.scale,
                                                  self.mask.unsqueeze(1).to_broadcast([P, n, self.width]),
                                                  ALU.mult, ALU.add)
        chain(last)
        chain(nc.vector.tensor_reduce(self.top[:], self.p[:], AX.X, ALU.max))
        nc.vector.tensor_tensor(self.p[:], self.p[:], self.bc(self.top[:], self.width), ALU.subtract).then_inc(
            self.shifted, 1)
        dve.wait_ge(self.exp_done, 1)
        chain(nc.vector.tensor_reduce(self.top[:], self.p[:], AX.X, ALU.add))
        chain(nc.vector.reciprocal(self.top[:], self.top[:]))
        nc.vector.tensor_tensor(self.p[:], self.p[:], self.bc(self.top[:], self.width), ALU.mult).then_inc(
            self.p_ready, 1)
        dve.wait_ge(self.pT_in_psum, 1)
        for b in range(0, self.heads // 4, 2):
            last = nc.vector.tensor_copy(self.pT[:, 4 * b:4 * b + 8].rearrange("p h q -> p (h q)"),
                                         self.ps[:, b:b + 2, :].rearrange("p b n -> p (b n)"))
        last.then_inc(self.pT_ready, 1)

    def scalar(self, act):
        act.wait_ge(self.shifted, 1)
        flat = self.p[:].rearrange("p h c -> p (h c)")
        self.nc.scalar.activation(flat, flat, ACT.Exp).then_inc(self.exp_done, 1)

    def tensor(self, pe):
        pe.wait_ge(self.p_ready, 1)
        for h in range(self.heads):
            last = self.nc.tensor.transpose(self.ps[:, h // 4, (h % 4) * P:(h % 4 + 1) * P],
                                            self.p[:, h, 0:P], self.ident)
        last.then_inc(self.pT_in_psum, 1)


def transposed(nc, ps, bank, src, tiles, ident, signal):
    for k in range(tiles):
        last = nc.tensor.transpose(ps[:, bank + k // 4, (k % 4) * P:(k % 4 + 1) * P],
                                   src[:, k * P:(k + 1) * P], ident)
    last.then_inc(signal, 1)


def projected(nc, out, xT, w, tiles, signal, start=True):
    for k in range(tiles):
        last = nc.tensor.matmul(out, xT[:, k, :], w[:, k], start=(k == 0), stop=(k == tiles - 1))
    if signal is not None:
        last.then_inc(signal, 1)


def l0_attn(core):
    nc, ps, ident = core.nc, core.psum, core.ident()
    H, DH = 16, 64
    with Scope(core, "l0a") as s:
        outer = Norm(core, s)
        inner = Norm(core, s, outer.xn[:], core.weight("gamma"), "inner")
        order = [h for n in range(2) for h in range(n, H, 2)]
        soft = RowSoftmax(core, s, H, P + 2, 2, 8.0, core.constant("prefix_mask"))
        q, sq, qT = s.sb("q", [P, H, DH]), s.sb("sq", [P, H, DH]), s.sb("qT", [P, 8, P])
        k, v = s.sb("k", [P, DH]), s.sb("v", [P, DH])
        kk, nk = s.sb("kk", [P, 2, DH]), s.sb("nk", [2, 2, DH])
        kT = s.sb("kT", [P, P + 2])
        ss, rn = s.sb("ss", [P, H + 2]), s.sb("rn", [P, H + 2])
        pn, pnT = s.sb("pn", [P, 2 * H]), s.sb("pnT", [2 * H, P])
        o, oT = s.sb("o", [P, H * DH]), s.sb("oT", [P, 8, P])
        (chain_sem, kv_in_psum, q_in_psum, squares, norms, qk_ready, qkT_in_psum, qkT_ready, pn_ready,
         pnT_in_psum, pnT_ready, o_in_psum, o_ready, oT_in_psum, oT_ready, y_in_psum) = s.signals(
            "chain_sem kv_in_psum q_in_psum squares norms qk_ready qkT_in_psum qkT_ready pn_ready "
            "pnT_in_psum pnT_ready o_in_psum o_ready oT_in_psum oT_ready y_in_psum")
        block = s.ctx.enter_context(nc.Block())

        @block.vector
        def _(dve):
            chain = Chain(dve, chain_sem)
            outer.vector(dve, chain)
            inner.vector(dve, chain)
            null_k = core.weight("null_k")[0:2, :]
            chain(nc.vector.memset(ss[:], 1.0))
            dve.wait_ge(kv_in_psum, 1)
            nc.vector.tensor_copy(k[:], ps[:, 0, 0:DH])
            chain(nc.vector.tensor_copy(v[:], ps[:, 0, DH:2 * DH]))
            dve.wait_ge(q_in_psum, 1)
            chain(nc.vector.tensor_copy(q[:].rearrange("p h d -> p (h d)"),
                                        ps[:, 1:3, :].rearrange("p b n -> p (b n)")))
            chain(nc.vector.tensor_tensor(sq[:], q[:], q[:], ALU.mult))
            chain(nc.vector.tensor_reduce(ss[:, 0:H], sq[:], AX.X, ALU.add))
            chain(nc.vector.tensor_tensor(sq[:, 0], k[:], k[:], ALU.mult))
            chain(nc.vector.tensor_reduce(ss[:, H:H + 1], sq[:, 0], AX.X, ALU.add))
            chain(nc.vector.tensor_tensor(sq[0:2, 1], null_k, null_k, ALU.mult))
            nc.vector.tensor_reduce(ss[0:2, H + 1:H + 2], sq[0:2, 1], AX.X, ALU.add).then_inc(squares, 1)
            dve.wait_ge(norms, 1)
            chain(nc.vector.tensor_scalar(rn[:], rn[:], 1e-12, None, ALU.max))
            chain(nc.vector.reciprocal(rn[:], rn[:]))
            chain(nc.vector.tensor_tensor(q[:], q[:], rn[:, 0:H].unsqueeze(2).to_broadcast([P, H, DH]), ALU.mult))
            nc.vector.tensor_tensor(q[:], q[:], core.weight("qs").unsqueeze(1).to_broadcast([P, H, DH]), ALU.mult)
            for n in range(2):
                nc.vector.scalar_tensor_tensor(kk[:, n], k[:], rn[:, H:H + 1], core.weight("ks"), ALU.mult, ALU.mult)
                last = nc.vector.scalar_tensor_tensor(nk[:, n], null_k, rn[0:2, H + 1:H + 2],
                                                      core.weight("ks")[0:2, :], ALU.mult, ALU.mult)
            last.then_inc(qk_ready, 1)
            dve.wait_ge(qkT_in_psum, 1)
            nc.vector.tensor_copy(qT[:].rearrange("p t n -> p (t n)"), ps[:, 0:2, :].rearrange("p b n -> p (b n)"))
            nc.vector.tensor_copy(kT[:], ps[:, 3, 0:P + 2]).then_inc(qkT_ready, 1)
            soft.vector(dve, chain)
            nc.vector.tensor_copy(pn[:].rearrange("p (h n) -> p h n", h=H), soft.p[:, :, P:P + 2]).then_inc(
                pn_ready, 1)
            dve.wait_ge(pnT_in_psum, 1)
            nc.vector.tensor_copy(pnT[:], ps[0:2 * H, 4, 0:P]).then_inc(pnT_ready, 1)
            dve.wait_ge(o_in_psum, 1)
            nc.vector.tensor_copy(o[:], ps[:, 5:7, :].rearrange("p b n -> p (b n)")).then_inc(o_ready, 1)
            dve.wait_ge(oT_in_psum, 1)
            nc.vector.tensor_copy(oT[:].rearrange("p t n -> p (t n)"),
                                  ps[:, 0:2, :].rearrange("p b n -> p (b n)")).then_inc(oT_ready, 1)
            dve.wait_ge(y_in_psum, 1)
            nc.vector.tensor_tensor(core.x[:], core.x[:], ps[:, 2, 0:D], ALU.add)

        @block.scalar
        def _(act):
            outer.scalar(act)
            inner.scalar(act)
            act.wait_ge(squares, 1)
            nc.scalar.activation(rn[:], ss[:], ACT.Sqrt).then_inc(norms, 1)
            soft.scalar(act)

        @block.tensor
        def _(pe):
            outer.tensor(pe)
            pe.wait_ge(outer.xT_ready, 1)
            projected(nc, ps[:, 0, 0:2 * DH], outer.xnT, core.kxn("akv"), DT, kv_in_psum)
            inner.tensor(pe)
            pe.wait_ge(inner.xT_ready, 1)
            wq = core.kxn("aq")
            for n in range(2):
                projected(nc, ps[:, 1 + n, :], inner.xnT, wq[:, :, n * 512:(n + 1) * 512], DT,
                          q_in_psum if n else None)
            pe.wait_ge(qk_ready, 1)
            for t in range(8):
                nc.tensor.transpose(ps[:, t // 4, (t % 4) * P:(t % 4 + 1) * P],
                                    q[:].rearrange("p h d -> p (h d)")[:, t * P:(t + 1) * P], ident)
            nc.tensor.transpose(ps[:, 3, 0:P], kk[:].rearrange("p n d -> p (n d)"), ident)
            nc.tensor.transpose(ps[:, 3, P:P + 2], nk[:].rearrange("p n d -> p (n d)"),
                                core.ident(2)).then_inc(qkT_in_psum, 1)
            pe.wait_ge(qkT_ready, 1)
            for n, h in enumerate(order):
                at = DH * (h % 2)
                last = nc.tensor.matmul(ps[:, n // 2, (n % 2) * (P + 2):(n % 2 + 1) * (P + 2)],
                                        qT[at:at + DH, h // 2, :], kT[at:at + DH, :], start=True, stop=True)
            last.then_inc(soft.s_in_psum, 1)
            soft.tensor(pe)
            pe.wait_ge(pn_ready, 1)
            nc.tensor.transpose(ps[0:2 * H, 4, 0:P], pn[:], ident).then_inc(pnT_in_psum, 1)
            pe.wait_ge(pnT_ready, 1)
            pe.wait_ge(soft.pT_ready, 1)
            nv = core.weight("null_v")[0:2 * H, :]
            for n in range(2):
                nc.tensor.matmul(ps[:, 5 + n, :], pnT[:], nv[:, n * 512:(n + 1) * 512], start=True, stop=False,
                                 skip_group_check=True)
                for h in range(8 * n, 8 * n + 8):
                    last = nc.tensor.matmul(ps[:, 5 + n, (h % 8) * DH:(h % 8 + 1) * DH], soft.pT[:, order.index(h), :], v[:],
                                            start=False, stop=(h % 8 == 7), skip_group_check=True)
            last.then_inc(o_in_psum, 1)
            pe.wait_ge(o_ready, 1)
            transposed(nc, ps, 0, o, 8, ident, oT_in_psum)
            pe.wait_ge(oT_ready, 1)
            projected(nc, ps[:, 2, 0:D], oT, core.kxn("ao", 8), 8, y_in_psum)


def l0_ffn(core):
    nc, ps = core.nc, core.psum
    with Scope(core, "l0f") as s:
        norm = Norm(core, s)
        mix = s.sb("mix", [P, 2, DT, P])
        omu = s.sb("omu", [P, 2 * DT])
        kact = s.sb("kact", [P, DT, P])
        r, y = s.sb("r", [P, D]), s.sb("y", [P, D])
        chain_sem, mixed, r_in_psum, k_in_psum, k_ready, r_ready, y_in_psum = s.signals(
            "chain_sem mixed r_in_psum k_in_psum k_ready r_ready y_in_psum")
        block = s.ctx.enter_context(nc.Block())

        @block.vector
        def _(dve):
            chain = Chain(dve, chain_sem)
            norm.vector(dve, chain)
            for n, mu in enumerate((core.weight("mu_r"), core.weight("mu_k"))):
                nc.vector.tensor_scalar(omu[:, 2 * n:2 * n + 2], mu, -1.0, 1.0, ALU.mult, ALU.add)
                for k in range(DT):
                    last = nc.vector.tensor_scalar(mix[:, n, k], norm.xnT[:, k], mu[:, k:k + 1], None, ALU.mult)
            chain(last)
            for n in range(2):
                for k in range(DT):
                    last = nc.vector.scalar_tensor_tensor(
                        mix[:, n, k, 1:P], norm.xnT[:, k, 0:P - 1], omu[:, 2 * n + k:2 * n + k + 1],
                        mix[:, n, k, 1:P], ALU.mult, ALU.add)
            last.then_inc(mixed, 1)
            dve.wait_ge(k_in_psum, 1)
            kflat = kact[:].rearrange("p k t -> p (k t)")
            chain(nc.vector.tensor_scalar(kflat, ps[:, 1, 0:D], 0.0, None, ALU.max))
            nc.vector.tensor_tensor(kflat, kflat, kflat, ALU.mult).then_inc(k_ready, 1)
            dve.wait_ge(y_in_psum, 1)
            dve.wait_ge(r_ready, 1)
            chain(nc.vector.tensor_tensor(y[:], ps[:, 2, 0:D], r[:], ALU.mult))
            nc.vector.tensor_tensor(core.x[:], core.x[:], y[:], ALU.add)

        @block.scalar
        def _(act):
            norm.scalar(act)
            act.wait_ge(r_in_psum, 1)
            nc.scalar.activation(r[:], ps[:, 0, 0:D], ACT.Sigmoid).then_inc(r_ready, 1)

        @block.tensor
        def _(pe):
            norm.tensor(pe)
            pe.wait_ge(mixed, 1)
            projected(nc, ps[:, 0, 0:D], mix[:, 0], core.kxn("fr"), DT, r_in_psum)
            wk = core.kxn("fk")
            for half in range(DT):
                for k in range(DT):
                    last = nc.tensor.matmul(ps[:, 1, half * P:(half + 1) * P], wk[:, k, half * P:(half + 1) * P],
                                            mix[:, 1, k], start=(k == 0), stop=(k == DT - 1))
            last.then_inc(k_in_psum, 1)
            pe.wait_ge(k_ready, 1)
            projected(nc, ps[:, 2, 0:D], kact, core.kxn("fv"), DT, y_in_psum)


def l1_attn(core):
    nc, ps, ident = core.nc, core.psum, core.ident()
    H, DK, DV, C = 4, 64, 128, 64
    with Scope(core, "l1a") as s:
        norm = Norm(core, s)
        qT, kT = s.sb("qT", [P, DT, P]), s.sb("kT", [P, DT, P])
        low = s.sb("low", [16, P])
        z, az, g = s.sb("z", [P, DT, P]), s.sb("az", [P, DT, P]), s.sb("g", [P, DT, P])
        b, eb, enb, blast = s.sb("b", [P, DT, P]), s.sb("eb", [P, DT, P]), s.sb("enb", [P, DT, P]), s.sb("bl", [P, DT, C])
        qg, kg, kh = s.sb("qg", [P, DT, P]), s.sb("kg", [P, DT, P]), s.sb("kh", [P, DT, C])
        ones = s.sb("ones", [P, C])
        v, gate, sig = s.sb("v", [P, H * DV]), s.sb("gate", [P, H * DV]), s.sb("sig", [P, H * DV])
        at = s.sb("at", [P, H, P])
        o, sq = s.sb("o", [P, H, DV]), s.sb("sq", [P, H, DV])
        ms, rms = s.sb("ms", [P, H]), s.sb("rms", [P, H])
        oT = s.sb("oT", [P, H, P])
        (chain_sem, low_in_psum, low_ready, z_in_psum, az_ready, soft_ready, b_ready, eb_ready, qk_in_psum, qk_ready,
         gates_ready, v_in_psum, v_ready, g_in_psum, g_ready, a_in_psum, a_ready, o_in_psum, ms_ready, rms_ready,
         o_ready, oT_in_psum, oT_ready, y_in_psum) = s.signals(
            "chain_sem low_in_psum low_ready z_in_psum az_ready soft_ready b_ready eb_ready qk_in_psum qk_ready "
            "gates_ready v_in_psum v_ready g_in_psum g_ready a_in_psum a_ready o_in_psum ms_ready rms_ready "
            "o_ready oT_in_psum oT_ready y_in_psum")
        flat = lambda t: t[:].rearrange("p k t -> p (k t)")
        block = s.ctx.enter_context(nc.Block())

        @block.vector
        def _(dve):
            chain = Chain(dve, chain_sem)
            norm.vector(dve, chain)
            chain(nc.vector.memset(ones[:], 1.0))
            dve.wait_ge(low_in_psum, 1)
            nc.vector.tensor_copy(low[:], ps[0:16, 0, 0:P]).then_inc(low_ready, 1)
            dve.wait_ge(z_in_psum, 1)
            for k in range(DT):
                last = nc.vector.tensor_scalar(z[:, k], ps[:, 1, k * P:(k + 1) * P], core.weight("gkb")[:, k:k + 1],
                                               None, ALU.add)
            chain(last)
            chain(nc.vector.tensor_scalar(az[:], z[:], -1.0, None, ALU.mult))
            nc.vector.tensor_tensor(az[:], az[:], z[:], ALU.min).then_inc(az_ready, 1)
            dve.wait_ge(az_ready, 1)
            chain(nc.vector.tensor_scalar(z[:], z[:], 0.0, None, ALU.min))
            dve.wait_ge(soft_ready, 1)
            chain(nc.vector.tensor_tensor(g[:], z[:], az[:], ALU.subtract))
            chain(nc.vector.tensor_scalar(g[:], g[:], 1.0 / 16.0, None, ALU.mult))
            for k in range(DT):
                for c in range(2):
                    last = nc.vector.tensor_tensor_scan(b[:, k, c * C:(c + 1) * C], ones[:],
                                                        g[:, k, c * C:(c + 1) * C], 0.0, ALU.mult, ALU.add)
            chain(last)
            for k in range(DT):
                last = nc.vector.tensor_scalar(blast[:, k], b[:, k, 0:C], -1.0, b[:, k, C - 1:C], ALU.mult, ALU.add)
            last.then_inc(b_ready, 1)
            dve.wait_ge(qk_in_psum, 1)
            chain(nc.vector.tensor_copy(flat(kT), ps[:, 3, 0:D]))
            dve.wait_ge(eb_ready, 1)
            chain(nc.vector.scalar_tensor_tensor(flat(qg), ps[:, 2, 0:D], DK ** -0.5, flat(eb), ALU.mult, ALU.mult))
            nc.vector.tensor_tensor(kg[:], kT[:], enb[:], ALU.mult)
            nc.vector.tensor_tensor(kh[:], kT[:, :, 0:C], blast[:], ALU.mult).then_inc(gates_ready, 1)
            dve.wait_ge(a_in_psum, 1)
            mask = core.constant("chunk_mask").unsqueeze(1).to_broadcast([P, 2, P])
            for n in range(2):
                last = nc.vector.tensor_tensor(at[:, n:H:2], ps[:, n, 0:2 * P].rearrange("p (h t) -> p h t", h=2),
                                               mask, ALU.mult)
            chain(last)
            for n in range(2):
                last = nc.vector.tensor_copy(at[0:C, n:H:2, C:P],
                                             ps[0:C, 2 + n, 0:2 * C].rearrange("p (h t) -> p h t", h=2))
            last.then_inc(a_ready, 1)
            dve.wait_ge(o_in_psum, 1)
            chain(nc.vector.tensor_copy(o[:].rearrange("p h d -> p (h d)"), ps[:, 6, :]))
            chain(nc.vector.tensor_tensor(sq[:], o[:], o[:], ALU.mult))
            chain(nc.vector.tensor_reduce(ms[:], sq[:], AX.X, ALU.add))
            nc.vector.tensor_scalar(ms[:], ms[:], 1.0 / DV, 1e-5, ALU.mult, ALU.add).then_inc(ms_ready, 1)
            dve.wait_ge(rms_ready, 1)
            chain(nc.vector.reciprocal(rms[:], rms[:]))
            chain(nc.vector.tensor_tensor(o[:], o[:], rms[:].unsqueeze(2).to_broadcast([P, H, DV]), ALU.mult))
            chain(nc.vector.tensor_tensor(o[:], o[:], core.weight("gn").unsqueeze(1).to_broadcast([P, H, DV]),
                                          ALU.mult))
            dve.wait_ge(g_ready, 2)
            oflat = o[:].rearrange("p h d -> p (h d)")
            chain(nc.vector.tensor_tensor(oflat, oflat, gate[:], ALU.mult))
            nc.vector.tensor_tensor(oflat, oflat, sig[:], ALU.mult).then_inc(o_ready, 1)
            dve.wait_ge(oT_in_psum, 1)
            nc.vector.tensor_copy(oT[:].rearrange("p h t -> p (h t)"), ps[:, 2, :]).then_inc(oT_ready, 1)
            dve.wait_ge(y_in_psum, 1)
            nc.vector.tensor_tensor(core.x[:], core.x[:], ps[:, 3, 0:D], ALU.add)

        @block.scalar
        def _(act):
            chain = Chain(act, qk_ready)
            norm.scalar(act)
            act.wait_ge(az_ready, 1)
            chain(nc.scalar.activation(az[:], az[:], ACT.Exp))
            nc.scalar.activation(az[:], az[:], ACT.Ln, bias=core.constant("one")).then_inc(soft_ready, 1)
            act.wait_ge(v_in_psum, 1)
            nc.scalar.activation(v[:], ps[:, 4, :], ACT.Copy).then_inc(v_ready, 1)
            act.wait_ge(g_in_psum, 1)
            nc.scalar.activation(gate[:], ps[:, 5, :], ACT.Copy).then_inc(g_ready, 1)
            act.wait_ge(b_ready, 1)
            chain(nc.scalar.activation(flat(eb), flat(b), ACT.Exp))
            nc.scalar.activation(flat(enb), flat(b), ACT.Exp, scale=-1.0)
            nc.scalar.activation(blast[:].rearrange("p k t -> p (k t)"), blast[:].rearrange("p k t -> p (k t)"),
                                 ACT.Exp).then_inc(eb_ready, 1)
            nc.scalar.activation(sig[:], ps[:, 5, :], ACT.Sigmoid).then_inc(g_ready, 1)
            act.wait_ge(ms_ready, 1)
            nc.scalar.activation(rms[:], ms[:], ACT.Sqrt).then_inc(rms_ready, 1)

        @block.tensor
        def _(pe):
            norm.tensor(pe)
            pe.wait_ge(norm.xT_ready, 1)
            for k in range(DT):
                last = nc.tensor.matmul(ps[0:16, 0, 0:P], core.kxn("gk1")[:, k, :], norm.xnT[:, k, :],
                                        start=(k == 0), stop=(k == DT - 1))
            last.then_inc(low_in_psum, 1)
            for name, bank in (("gq", 2), ("gk", 3)):
                w = core.kxn(name)
                for half in range(DT):
                    for k in range(DT):
                        last = nc.tensor.matmul(ps[:, bank, half * P:(half + 1) * P],
                                                w[:, k, half * P:(half + 1) * P], norm.xnT[:, k, :],
                                                start=(k == 0), stop=(k == DT - 1))
            last.then_inc(qk_in_psum, 1)
            projected(nc, ps[:, 4, :], norm.xnT, core.kxn("gv"), DT, v_in_psum)
            projected(nc, ps[:, 5, :], norm.xnT, core.kxn("gg"), DT, g_in_psum)
            pe.wait_ge(low_ready, 1)
            for half in range(DT):
                last = nc.tensor.matmul(ps[:, 1, half * P:(half + 1) * P],
                                        core.weight("gk2")[0:16, half * P:(half + 1) * P], low[:],
                                        start=True, stop=True)
            last.then_inc(z_in_psum, 1)
            pe.wait_ge(gates_ready, 1)
            for h in range(H):
                r = slice(DK * (h % 2), DK * (h % 2) + DK)
                nc.tensor.matmul(ps[:, h % 2, (h // 2) * P:(h // 2 + 1) * P], kg[r, h // 2, :], qg[r, h // 2, :],
                                 start=True, stop=True)
            for h in range(H):
                r = slice(DK * (h % 2), DK * (h % 2) + DK)
                last = nc.tensor.matmul(ps[0:C, 2 + h % 2, (h // 2) * C:(h // 2 + 1) * C], kh[r, h // 2, :], qg[r, h // 2, C:P],
                                        start=True, stop=True)
            last.then_inc(a_in_psum, 1)
            pe.wait_ge(a_ready, 1)
            pe.wait_ge(v_ready, 1)
            for h in range(H):
                last = nc.tensor.matmul(ps[:, 6, h * DV:(h + 1) * DV], at[:, h, :], v[:, h * DV:(h + 1) * DV],
                                        start=True, stop=True)
            last.then_inc(o_in_psum, 1)
            pe.wait_ge(o_ready, 1)
            transposed(nc, ps, 2, o[:].rearrange("p h d -> p (h d)"), H, ident, oT_in_psum)
            pe.wait_ge(oT_ready, 1)
            projected(nc, ps[:, 3, 0:D], oT, core.kxn("go", 4), 4, y_in_psum)


def l0_xattn(core):
    cross_attention(core, "l0x", 16, 1, *cross_weights(core, 1), 0.25)


def l1_xattn(core):
    cross_attention(core, "l1x", 16, 1, *cross_weights(core, 1), 0.25)


def l2_xattn(core):
    cross_attention(core, "l2x", 1, 1, *cross_weights(core, 1), 1.0 / 16.0)


def l3_xattn(core):
    cross_attention(core, "l3x", 4, 4, *cross_weights(core, 4), 0.125)


def cross_weights(core, groups):
    def columns(name):
        m = core.kxn(name)
        return lambda g, k, half=None: (m[:, k, g * D:(g + 1) * D] if half is None
                                        else m[:, k, g * D + half * P:g * D + (half + 1) * P])

    has = core.cols[core.layer]
    col = lambda name: (lambda g, k: core.weight(name)[:, k:k + 1]) if name in has else (
        lambda g, k: core.constant("zero")[:, 0:1])
    row = lambda name: (lambda g: core.weight(name)) if name in has else (lambda g: core.constant("zero"))
    wo = None
    if "xo" in has:
        rows = core.kxn("xo", DT * groups)
        wo = lambda g, k: rows[:, DT * g + k, :]
    return (columns("xq"), columns("xk"), columns("xv"), wo, col("xbq"), col("xbk"), row("xbv"),
            core.weight("xbo") if "xbo" in has else None)




def l1_ffn(core):
    nc, ps, ident = core.nc, core.psum, core.ident()
    E, G, CAP, SLOTS, INTER, AI = 32, 16, 5, 32, 512, 128
    PER = P // SLOTS
    GROUPS = E // PER
    RING = 6
    with Scope(core, "l1f") as s:
        norm = Norm(core, s)
        stats, sq = s.sb("stats", [P, 8]), s.sb("sq", [P, D])
        statsT = s.sb("statsT", [6, P])
        hT = s.sb("hT", [P, P])
        logits, probs = s.sb("logits", [P, E]), s.sb("probs", [P, E])
        top, topi, topf = s.sb("top", [P, 8]), s.sb("topi", [P, 8], U32), s.sb("topf", [P, 8])
        small = s.sb("small", [P, 4])
        hit, wc, score = s.sb("hit", [P, 2, E]), s.sb("wc", [P, E]), s.sb("score", [P, E])
        scoreT = s.sb("scoreT", [E, P])
        best, besti, bestf = s.sb("best", [E, 8]), s.sb("besti", [E, 8], U32), s.sb("bestf", [E, 8])
        pick = s.sb("pick", [E, CAP, P])
        sel, wsel = s.sb("sel", [P, E, SLOTS]), s.sb("wsel", [P, E, SLOTS])
        wmask, gw = s.sb("wmask", [P, E]), s.sb("gw", [P, G])
        xeT = s.sb("xeT", [P, DT, E * SLOTS])
        wselT = s.sb("wselT", [P, GROUPS, P])
        up = s.sb("up", [P, RING, DT, 2 * INTER])
        down = s.sb("down", [P, RING, INTER // P, D])
        sg, hact = s.sb("sg", [P, INTER]), s.sb("hact", [P, INTER])
        hactT = s.sb("hactT", [P, INTER // P, P])
        ye = s.sb("ye", [P, GROUPS, D])
        aup = s.sb("aup", [P, 2, DT, 2 * AI])
        adown = s.sb("adown", [P, 2, D])
        asg, ah = s.sb("asg", [P, 2, P]), s.sb("ah", [P, 2, P])
        acc = s.sb("acc", [P, D])
        (chain_sem, sums_ready, sqrt_ready, stats_ready, statsT_in_psum, statsT_ready, h_in_psum, h_ready,
         logits_in_psum, shifted, exp_done, score_ready, scoreT_in_psum, scoreT_ready, pick_ready, sel_in_psum,
         sel_ready, xe_in_psum, xe_ready, up_used, down_used, sig_done, hact_ready, hactT_in_psum,
         hactT_ready, ye_ready, a_in_psum, asig_done, ah_ready, ay_in_psum, ay_added,
         out_in_psum) = s.signals(
            "chain_sem sums_ready sqrt_ready stats_ready statsT_in_psum statsT_ready h_in_psum h_ready "
            "logits_in_psum shifted exp_done score_ready scoreT_in_psum scoreT_ready pick_ready sel_in_psum "
            "sel_ready xe_in_psum xe_ready up_used down_used sig_done hact_ready hactT_in_psum "
            "hactT_ready ye_ready a_in_psum asig_done ah_ready ay_in_psum ay_added out_in_psum")
        up_in = s.signals(" ".join(f"up_in{n}" for n in range(RING)))
        down_in = s.signals(" ".join(f"down_in{n}" for n in range(RING)))
        a_in = s.signals("a_in0 a_in1")
        block = s.ctx.enter_context(nc.Block())

        @block.sync
        def _(sp):
            for e in range(E):
                if e >= RING:
                    sp.wait_ge(up_used, e - RING + 1)
                sp.dma_start(up[:, e % RING], core.dram["w_up"][e]).then_inc(up_in[e % RING], 16)
                if e >= RING:
                    sp.wait_ge(down_used, e - RING + 1)
                sp.dma_start(down[:, e % RING], core.dram["w_down"][e]).then_inc(down_in[e % RING], 16)

        @block.gpsimd
        def _(pool):
            for n in range(G):
                if n >= 2:
                    pool.wait_ge(ay_in_psum, n - 1)
                pool.dma_start(aup[:, n % 2], core.dram["a_up"][n]).then_inc(a_in[n % 2], 16)
                pool.dma_start(adown[:, n % 2], core.dram["a_down"][n]).then_inc(a_in[n % 2], 16)

        @block.vector
        def _(dve):
            chain = Chain(dve, chain_sem)
            norm.vector(dve, chain)
            xn = norm.xn[:]
            chain(nc.vector.memset(stats[:], 0.0))
            chain(nc.vector.bn_stats(norm.stats[:], xn))
            chain(nc.vector.bn_aggr(norm.mv[:], norm.stats[:]))
            nc.vector.tensor_copy(stats[:, 0:1], norm.mv[:, 0:1])
            nc.vector.tensor_scalar(stats[:, 6:7], norm.mv[:, 1:2], D / (D - 1.0), None, ALU.mult)
            nc.vector.tensor_reduce(stats[:, 2:3], xn, AX.X, ALU.min)
            nc.vector.tensor_reduce(stats[:, 3:4], xn, AX.X, ALU.max)
            chain(nc.vector.tensor_tensor(sq[:], xn, xn, ALU.mult))
            nc.vector.tensor_reduce(stats[:, 7:8], sq[:], AX.X, ALU.add).then_inc(sums_ready, 1)
            dve.wait_ge(sums_ready, 1)
            chain(nc.vector.tensor_scalar(sq[:], xn, 1e-6, None, ALU.is_lt))
            chain(nc.vector.scalar_tensor_tensor(sq[:], xn, -1e-6, sq[:], ALU.is_gt, ALU.mult))
            chain(nc.vector.tensor_reduce(stats[:, 5:6], sq[:], AX.X, ALU.add))
            nc.vector.tensor_scalar(stats[:, 5:6], stats[:, 5:6], 1.0 / D, None, ALU.mult).then_inc(stats_ready, 1)
            dve.wait_ge(statsT_in_psum, 1)
            nc.vector.tensor_copy(statsT[:], ps[0:6, 0, 0:P]).then_inc(statsT_ready, 1)
            dve.wait_ge(logits_in_psum, 1)
            chain(nc.vector.tensor_reduce(small[:, 0:1], ps[:, 2, 0:E], AX.X, ALU.max))
            nc.vector.tensor_scalar(logits[:], ps[:, 2, 0:E], small[:, 0:1], None, ALU.subtract).then_inc(shifted, 1)
            dve.wait_ge(exp_done, 1)
            chain(nc.vector.tensor_reduce(small[:, 1:2], logits[:], AX.X, ALU.add))
            chain(nc.vector.reciprocal(small[:, 1:2], small[:, 1:2]))
            chain(nc.vector.tensor_scalar(probs[:], logits[:], small[:, 1:2], None, ALU.mult))
            chain(nc.vector.max(top[:], probs[:]))
            chain(nc.vector.max_index(topi[:], top[:], probs[:]))
            chain(nc.vector.tensor_copy(topf[:], topi[:]))
            chain(nc.vector.tensor_tensor(small[:, 0:1], top[:, 0:1], top[:, 1:2], ALU.add))
            chain(nc.vector.reciprocal(small[:, 0:1], small[:, 0:1]))
            for n in range(2):
                last = nc.vector.tensor_scalar(hit[:, n], core.constant("iota")[:, 0:E], topf[:, n:n + 1], None,
                                               ALU.is_equal)
            chain(last)
            chain(nc.vector.tensor_tensor(score[:], hit[:, 0], hit[:, 1], ALU.add))
            chain(nc.vector.tensor_scalar(wc[:], probs[:], small[:, 0:1], None, ALU.mult))
            chain(nc.vector.tensor_tensor(wc[:], wc[:], score[:], ALU.mult))
            chain(nc.vector.tensor_tensor(logits[:], probs[:], score[:], ALU.mult))
            chain(nc.vector.tensor_scalar(score[:], score[:], 1.0, None, ALU.subtract))
            nc.vector.tensor_tensor(score[:], score[:], logits[:], ALU.add).then_inc(score_ready, 1)
            dve.wait_ge(scoreT_in_psum, 1)
            nc.vector.tensor_copy(scoreT[:], ps[0:E, 3, 0:P]).then_inc(scoreT_ready, 1)
            dve.wait_ge(scoreT_ready, 1)
            chain(nc.vector.max(best[:], scoreT[:]))
            chain(nc.vector.max_index(besti[:], best[:], scoreT[:]))
            chain(nc.vector.tensor_copy(bestf[:], besti[:]))
            for c in range(CAP):
                last = nc.vector.tensor_scalar(pick[:, c], core.constant("iota")[0:E, :], bestf[:, c:c + 1], None,
                                               ALU.is_equal)
            last.then_inc(pick_ready, 1)
            chain(nc.vector.memset(sel[:], 0.0))
            dve.wait_ge(sel_in_psum, 1)
            chain(nc.vector.tensor_copy(sel[:, :, 0:CAP].rearrange("p e c -> p c e"),
                                        ps[:, 4, 0:CAP * E].rearrange("p (c e) -> p c e", c=CAP)))
            nc.vector.tensor_tensor(wsel[:], sel[:], wc[:].unsqueeze(2).to_broadcast([P, E, SLOTS]),
                                    ALU.mult).then_inc(sel_ready, 1)
            dve.wait_ge(sel_ready, 1)
            chain(nc.vector.tensor_reduce(wmask[:], wsel[:, :, 0:CAP], AX.X, ALU.add))
            chain(nc.vector.tensor_reduce(gw[:], wmask[:].rearrange("p (g e) -> p g e", g=G), AX.X, ALU.add))
            chain(nc.vector.tensor_scalar(gw[:], gw[:], 0.05, None, ALU.mult))
            chain(nc.vector.memset(acc[:], 0.0))
            dve.wait_ge(xe_in_psum, 1)
            nc.vector.tensor_copy(xeT[:].rearrange("p k n -> p (k n)"),
                                  ps[:, 0:4, :].rearrange("p b n -> p (b n)")).then_inc(xe_ready, 1)
            dve.wait_ge(xe_in_psum, 2)
            nc.vector.tensor_copy(wselT[:].rearrange("p g n -> p (g n)"),
                                  ps[:, 4:6, :].rearrange("p b n -> p (b n)")).then_inc(xe_ready, 1)
            for q in range(GROUPS):
                dve.wait_ge(sig_done, q + 1)
                chain(nc.vector.tensor_tensor(sg[:], sg[:], ps[:, 0, :], ALU.mult))
                if q:
                    dve.wait_ge(hactT_in_psum, q)
                nc.vector.tensor_tensor(hact[:], sg[:], ps[:, 1, :], ALU.mult).then_inc(hact_ready, 1)
                dve.wait_ge(hactT_in_psum, q + 1)
                nc.vector.tensor_copy(hactT[:].rearrange("p k n -> p (k n)"), ps[:, 2, :]).then_inc(hactT_ready, 1)
                for n in range(2 * q, 2 * q + 2):
                    dve.wait_ge(asig_done, n + 1)
                    chain(nc.vector.tensor_tensor(asg[:, n % 2], asg[:, n % 2], ps[:, 4, 0:P], ALU.mult))
                    nc.vector.tensor_tensor(ah[:, n % 2], asg[:, n % 2], ps[:, 4, P:2 * P], ALU.mult).then_inc(
                        ah_ready, 1)
                    dve.wait_ge(ay_in_psum, n + 1)
                    nc.vector.scalar_tensor_tensor(acc[:], ps[:, 5, 0:D], gw[:, n:n + 1], acc[:], ALU.mult,
                                                   ALU.add).then_inc(ay_added, 1)
                    dve.wait_ge(ay_added, n + 1)
                dve.wait_ge(down_used, PER * (q + 1))
                nc.vector.tensor_copy(ye[:, q], ps[:, 3, 0:D]).then_inc(ye_ready, 1)
            chain(nc.vector.tensor_tensor(core.x[:], core.x[:], acc[:], ALU.add))
            dve.wait_ge(out_in_psum, 1)
            nc.vector.tensor_tensor(core.x[:], core.x[:], ps[:, 7, 0:D], ALU.add)

        @block.scalar
        def _(act):
            norm.scalar(act)
            act.wait_ge(sums_ready, 1)
            nc.scalar.activation(stats[:, 1:2], stats[:, 6:7], ACT.Sqrt).then_inc(sqrt_ready, 1)
            nc.scalar.activation(stats[:, 4:5], stats[:, 7:8], ACT.Sqrt).then_inc(sqrt_ready, 1)
            act.wait_ge(h_in_psum, 1)
            nc.scalar.activation(hT[:], ps[:, 1, 0:P], ACT.Gelu, bias=core.weight("r1b")).then_inc(h_ready, 1)
            act.wait_ge(shifted, 1)
            nc.scalar.activation(logits[:], logits[:], ACT.Exp).then_inc(exp_done, 1)
            for q in range(GROUPS):
                act.wait_ge(up_used, PER * (q + 1))
                if q:
                    act.wait_ge(hact_ready, q)
                nc.scalar.activation(sg[:], ps[:, 0, :], ACT.Sigmoid).then_inc(sig_done, 1)
                for n in range(2 * q, 2 * q + 2):
                    act.wait_ge(a_in_psum, n + 1)
                    if n >= 2:
                        act.wait_ge(ah_ready, n - 1)
                    nc.scalar.activation(asg[:, n % 2], ps[:, 4, 0:P], ACT.Sigmoid).then_inc(asig_done, 1)

        @block.tensor
        def _(pe):
            norm.tensor(pe)
            pe.wait_ge(stats_ready, 1)
            pe.wait_ge(sqrt_ready, 2)
            nc.tensor.transpose(ps[0:6, 0, 0:P], stats[:, 0:6], ident).then_inc(statsT_in_psum, 1)
            pe.wait_ge(norm.xT_ready, 1)
            pe.wait_ge(statsT_ready, 1)
            r1 = core.kxn("r1")
            for k in range(DT):
                nc.tensor.matmul(ps[:, 1, 0:P], r1[:, k, :], norm.xnT[:, k, :], start=(k == 0), stop=False)
            nc.tensor.matmul(ps[:, 1, 0:P], core.weight("r1s")[0:6, :], statsT[:], start=False,
                             stop=True).then_inc(h_in_psum, 1)
            pe.wait_ge(h_ready, 1)
            nc.tensor.matmul(ps[:, 2, 0:E], hT[:], core.weight("r2"), start=True, stop=True).then_inc(
                logits_in_psum, 1)
            pe.wait_ge(score_ready, 1)
            nc.tensor.transpose(ps[0:E, 3, 0:P], score[:], ident).then_inc(scoreT_in_psum, 1)
            pe.wait_ge(pick_ready, 1)
            for c in range(CAP):
                last = nc.tensor.transpose(ps[:, 4, c * E:(c + 1) * E], pick[:, c], core.ident(E))
            last.then_inc(sel_in_psum, 1)
            pe.wait_ge(sel_ready, 1)
            flat = sel[:].rearrange("p e c -> p (e c)")
            for k in range(DT):
                for n in range(2):
                    last = nc.tensor.matmul(ps[:, 2 * k + n, :], norm.xn[:, k * P:(k + 1) * P],
                                            flat[:, n * 512:(n + 1) * 512], start=True, stop=True)
            last.then_inc(xe_in_psum, 1)
            transposed(nc, ps, 4, wsel[:].rearrange("p e c -> p (e c)"), GROUPS, ident, xe_in_psum)
            pe.wait_ge(xe_ready, 2)
            for q in range(GROUPS):
                for j in range(PER):
                    e = q * PER + j
                    pe.wait_ge(up_in[e % RING], 16 * (e // RING + 1))
                    if q and j == 0:
                        pe.wait_ge(hact_ready, q)
                    for n in range(2):
                        for k in range(DT):
                            last = nc.tensor.matmul(ps[j * SLOTS:(j + 1) * SLOTS, n, :],
                                                    xeT[:, k, e * SLOTS:(e + 1) * SLOTS],
                                                    up[:, e % RING, k, n * INTER:(n + 1) * INTER],
                                                    start=(k == 0), stop=(k == DT - 1))
                    last.then_inc(up_used, 1)
                pe.wait_ge(hact_ready, q + 1)
                if q:
                    pe.wait_ge(hactT_ready, q)
                transposed(nc, ps, 2, hact, INTER // P, ident, hactT_in_psum)
                for n in range(2 * q, 2 * q + 2):
                    pe.wait_ge(a_in[n % 2], 32 * (n // 2 + 1))
                    if n:
                        pe.wait_ge(ah_ready, n)
                    for m in range(2):
                        for k in range(DT):
                            last = nc.tensor.matmul(ps[:, 4, m * P:(m + 1) * P],
                                                    aup[:, n % 2, k, m * AI:(m + 1) * AI], norm.xnT[:, k, :],
                                                    start=(k == 0), stop=(k == DT - 1))
                    last.then_inc(a_in_psum, 1)
                    pe.wait_ge(ah_ready, n + 1)
                    if n:
                        pe.wait_ge(ay_added, n)
                    nc.tensor.matmul(ps[:, 5, 0:D], ah[:, n % 2], adown[:, n % 2], start=True,
                                     stop=True).then_inc(ay_in_psum, 1)
                pe.wait_ge(hactT_ready, q + 1)
                if q:
                    pe.wait_ge(ye_ready, q)
                for j in range(PER):
                    e = q * PER + j
                    pe.wait_ge(down_in[e % RING], 16 * (e // RING + 1))
                    for k in range(INTER // P):
                        last = nc.tensor.matmul(ps[j * SLOTS:(j + 1) * SLOTS, 3, 0:D],
                                                hactT[:, k, j * SLOTS:(j + 1) * SLOTS], down[:, e % RING, k, :],
                                                start=(k == 0), stop=(k == INTER // P - 1))
                    last.then_inc(down_used, 1)
            pe.wait_ge(ye_ready, GROUPS)
            for q in range(GROUPS):
                last = nc.tensor.matmul(ps[:, 7, 0:D], wselT[:, q, :], ye[:, q, :], start=(q == 0),
                                        stop=(q == GROUPS - 1))
            last.then_inc(out_in_psum, 1)


def rotary(nc, src, even, odd, cos, sin, tmp, chain):
    x1, x2 = src
    nc.vector.tensor_tensor(tmp[0], x1, cos, ALU.mult)
    nc.vector.tensor_tensor(tmp[1], x2, sin, ALU.mult)
    nc.vector.tensor_tensor(tmp[2], x1, sin, ALU.mult)
    chain(nc.vector.tensor_tensor(tmp[3], x2, cos, ALU.mult))
    nc.vector.tensor_tensor(even, tmp[0], tmp[1], ALU.subtract)
    return nc.vector.tensor_tensor(odd, tmp[2], tmp[3], ALU.add)


def l2_attn(core):
    nc, ps, ident = core.nc, core.psum, core.ident()
    H, KV, DH, QL, KL, PAD = 16, 4, 16, 64, 32, 32
    with Scope(core, "l2a") as s:
        norm = Norm(core, s)
        soft = RowSoftmax(core, s, H, P, 4, DH ** -0.5, core.constant("causal_mask"))
        qaT, kvaT = s.sb("qaT", [QL, P]), s.sb("kvaT", [KL, P])
        qk, v = s.sb("qk", [P, H + KV, DH]), s.sb("v", [P, KV * DH])
        tmp = s.sb("tmp", [P, 4, H + KV, DH // 2])
        rot = s.sb("rot", [P, H + KV, DH])
        qp, kp = s.sb("qp", [P, H // KV, KV, PAD]), s.sb("kp", [P, KV, PAD])
        qT, kT = s.sb("qT", [P, H // KV, P]), s.sb("kT", [P, P])
        o, oT = s.sb("o", [P, D]), s.sb("oT", [P, DT, P])
        (chain_sem, low_in_psum, low_ready, qkv_in_psum, qk_ready, qkT_in_psum, qkT_ready, o_in_psum, o_ready,
         oT_in_psum, oT_ready, y_in_psum) = s.signals(
            "chain_sem low_in_psum low_ready qkv_in_psum qk_ready qkT_in_psum qkT_ready o_in_psum o_ready "
            "oT_in_psum oT_ready y_in_psum")
        block = s.ctx.enter_context(nc.Block())

        @block.vector
        def _(dve):
            chain = Chain(dve, chain_sem)
            norm.vector(dve, chain)
            nc.vector.memset(qp[:], 0.0)
            chain(nc.vector.memset(kp[:], 0.0))
            dve.wait_ge(low_in_psum, 1)
            nc.vector.tensor_copy(qaT[:], ps[0:QL, 0, 0:P])
            nc.vector.tensor_copy(kvaT[:], ps[0:KL, 0, P:2 * P]).then_inc(low_ready, 1)
            dve.wait_ge(qkv_in_psum, 1)
            nc.vector.tensor_copy(qk[:, 0:H].rearrange("p h d -> p (h d)"), ps[:, 1, 0:D])
            nc.vector.tensor_copy(qk[:, H:].rearrange("p h d -> p (h d)"), ps[:, 2, 0:KV * DH])
            chain(nc.vector.tensor_copy(v[:], ps[:, 2, KV * DH:2 * KV * DH]))
            table = lambda n: core.constant(n).unsqueeze(1).to_broadcast([P, H + KV, DH // 2])
            chain(rotary(nc, (qk[:, :, 0::2], qk[:, :, 1::2]), rot[:, :, 0::2], rot[:, :, 1::2], table("rope_cos"),
                         table("rope_sin"), [tmp[:, n] for n in range(4)], chain))
            nc.vector.tensor_copy(qp[:, :, :, 0:DH].rearrange("p i g d -> p g i d"),
                                  rot[:, 0:H].rearrange("p (g i) d -> p g i d", g=KV))
            nc.vector.tensor_copy(kp[:, :, 0:DH], rot[:, H:]).then_inc(qk_ready, 1)
            dve.wait_ge(qkT_in_psum, 1)
            nc.vector.tensor_copy(qT[:].rearrange("p i q -> p (i q)"), ps[:, 3, :])
            nc.vector.tensor_copy(kT[:], ps[:, 4, 0:P]).then_inc(qkT_ready, 1)
            soft.vector(dve, chain)
            dve.wait_ge(o_in_psum, 1)
            nc.vector.tensor_copy(o[:], ps[:, 5, 0:D]).then_inc(o_ready, 1)
            dve.wait_ge(oT_in_psum, 1)
            nc.vector.tensor_copy(oT[:].rearrange("p k t -> p (k t)"), ps[:, 6, 0:D]).then_inc(oT_ready, 1)
            chain(nc.vector.tensor_tensor(core.x[:], core.x[:], core.weight("bout"), ALU.add))
            dve.wait_ge(y_in_psum, 1)
            nc.vector.tensor_tensor(core.x[:], core.x[:], ps[:, 4, 0:D], ALU.add)

        @block.scalar
        def _(act):
            norm.scalar(act)
            soft.scalar(act)

        @block.tensor
        def _(pe):
            norm.tensor(pe)
            pe.wait_ge(norm.xT_ready, 1)
            for k in range(DT):
                nc.tensor.matmul(ps[0:QL, 0, 0:P], core.kxn("qa")[:, k, :], norm.xnT[:, k, :], start=(k == 0),
                                 stop=(k == DT - 1))
            for k in range(DT):
                last = nc.tensor.matmul(ps[0:KL, 0, P:2 * P], core.kxn("kva")[:, k, :], norm.xnT[:, k, :],
                                        start=(k == 0), stop=(k == DT - 1))
            last.then_inc(low_in_psum, 1)
            pe.wait_ge(low_ready, 1)
            nc.tensor.matmul(ps[:, 1, 0:D], qaT[:], core.weight("qb")[0:QL, :], start=True, stop=True)
            nc.tensor.matmul(ps[:, 2, 0:2 * KV * DH], kvaT[:], core.weight("kvb")[0:KL, :], start=True,
                             stop=True).then_inc(qkv_in_psum, 1)
            pe.wait_ge(qk_ready, 1)
            for i in range(H // KV):
                nc.tensor.transpose(ps[:, 3, i * P:(i + 1) * P], qp[:, i].rearrange("p g d -> p (g d)"), ident)
            nc.tensor.transpose(ps[:, 4, 0:P], kp[:].rearrange("p g d -> p (g d)"), ident).then_inc(qkT_in_psum, 1)
            pe.wait_ge(qkT_ready, 1)
            for g in range(KV):
                for i in range(H // KV):
                    last = nc.tensor.matmul(ps[:, g, i * P:(i + 1) * P], qT[PAD * g:PAD * (g + 1), i, :],
                                            kT[PAD * g:PAD * (g + 1), :], start=True, stop=True)
            last.then_inc(soft.s_in_psum, 1)
            soft.tensor(pe)
            pe.wait_ge(soft.pT_ready, 1)
            for h in range(H):
                g = h // (H // KV)
                last = nc.tensor.matmul(ps[:, 5, h * DH:(h + 1) * DH], soft.pT[:, h, :], v[:, g * DH:(g + 1) * DH],
                                        start=True, stop=True)
            last.then_inc(o_in_psum, 1)
            pe.wait_ge(o_ready, 1)
            transposed(nc, ps, 6, o, DT, ident, oT_in_psum)
            pe.wait_ge(oT_ready, 1)
            projected(nc, ps[:, 4, 0:D], oT, core.kxn("aout"), DT, y_in_psum)


def quantised(nc, chain, src, out, blocks, top, inv, scaled):
    wide = [P, blocks, 32]
    top, inv = top[:, 0:blocks], inv[:, 0:blocks]
    chain(nc.vector.tensor_reduce(top, src, AX.X, ALU.max, apply_absolute_value=True))
    chain(nc.vector.tensor_scalar(top, top, 2.0 ** -120, None, ALU.max))
    chain(nc.vector.tensor_scalar(top.bitcast(I32), top.bitcast(I32), 0x7F800000, None, ALU.bitwise_and))
    chain(nc.vector.tensor_scalar(top, top, 0.125, None, ALU.mult))
    chain(nc.vector.reciprocal(inv, top))
    chain(nc.vector.tensor_tensor(scaled, src, inv.unsqueeze(2).to_broadcast(wide), ALU.mult))
    chain(nc.vector.tensor_scalar(scaled, scaled, 1.5 * 2.0 ** 23, None, ALU.add))
    chain(nc.vector.tensor_scalar(scaled, scaled, 1.5 * 2.0 ** 23, None, ALU.subtract))
    return nc.vector.tensor_tensor(out, scaled, top.unsqueeze(2).to_broadcast(wide), ALU.mult)


def l2_ffn(core):
    nc, ps = core.nc, core.psum
    F = 1024
    FT = F // P
    with Scope(core, "l2f") as s:
        norm = Norm(core, s)
        identb = s.sb("identb", [P, P], BF16)
        top, inv, scaled = s.sb("top", [P, 64]), s.sb("inv", [P, 64]), s.sb("scaled", [P, 64, 32])
        wfq, wpq = s.sb("wfq", [P, FT, D], BF16), s.sb("wpq", [P, DT, F], BF16)
        wfT, wpT = s.sb("wfT", [P, DT, F], BF16), s.sb("wpT", [P, FT, D], BF16)
        xq, xqT = s.sb("xq", [P, D], BF16), s.sb("xqT", [P, DT, P], BF16)
        h = s.sb("h", [P, F])
        hq, hqT = s.sb("hq", [P, F], BF16), s.sb("hqT", [P, FT, P], BF16)
        (chain_sem, wf_ready, wp_ready, wfT_in_psum, wpT_in_psum, wT_ready, xq_ready, xqT_in_psum, xqT_ready,
         h_in_psum, h_ready, gelu_done, hq_ready, hqT_in_psum, hqT_ready, y_in_psum) = s.signals(
            "chain_sem wf_ready wp_ready wfT_in_psum wpT_in_psum wT_ready xq_ready xqT_in_psum xqT_ready "
            "h_in_psum h_ready gelu_done hq_ready hqT_in_psum hqT_ready y_in_psum")
        blocks = lambda a: a.rearrange("p (b k) -> p b k", k=32)
        half_words = lambda bank, n: ps[:, bank, :].bitcast(BF16)[:, 0:n]
        block = s.ctx.enter_context(nc.Block())

        @block.vector
        def _(dve):
            chain = Chain(dve, chain_sem)
            nc.vector.tensor_copy(identb[:], core.ident())
            quantised(nc, chain, blocks(core.weight("fc")), blocks(wfq[:].rearrange("p n k -> p (n k)")), 64, top,
                      inv, scaled[:]).then_inc(wf_ready, 1)
            dve.wait_ge(wf_ready, 1)
            quantised(nc, chain, blocks(core.weight("proj")), blocks(wpq[:].rearrange("p n k -> p (n k)")), 64,
                      top, inv, scaled[:]).then_inc(wp_ready, 1)
            dve.wait_ge(wp_ready, 1)
            norm.vector(dve, chain)
            quantised(nc, chain, blocks(norm.xn[:]), blocks(xq[:]), 8, top, inv, scaled[:, 0:8]).then_inc(
                xq_ready, 1)
            dve.wait_ge(xq_ready, 1)
            dve.wait_ge(wfT_in_psum, 1)
            for k in range(DT):
                nc.vector.tensor_copy(wfT[:, k], half_words(k, F))
            dve.wait_ge(wpT_in_psum, 1)
            for n in range(2):
                last = nc.vector.tensor_copy(wpT[:, 4 * n:4 * n + 4].rearrange("p k o -> p (k o)"),
                                             half_words(2 + n, F))
            last.then_inc(wT_ready, 1)
            dve.wait_ge(xqT_in_psum, 1)
            nc.vector.tensor_copy(xqT[:].rearrange("p k t -> p (k t)"), half_words(4, D)).then_inc(xqT_ready, 1)
            dve.wait_ge(h_in_psum, 1)
            nc.vector.tensor_tensor(h[:], ps[:, 5:7, :].rearrange("p b n -> p (b n)"), core.weight("bfc"),
                                    ALU.add).then_inc(h_ready, 1)
            dve.wait_ge(gelu_done, 1)
            quantised(nc, chain, blocks(h[:]), blocks(hq[:]), 32, top, inv, scaled[:, 0:32]).then_inc(hq_ready, 1)
            dve.wait_ge(hqT_in_psum, 1)
            nc.vector.tensor_copy(hqT[:].rearrange("p k t -> p (k t)"), half_words(0, F)).then_inc(hqT_ready, 1)
            chain(nc.vector.tensor_tensor(core.x[:], core.x[:], core.weight("bproj"), ALU.add))
            dve.wait_ge(y_in_psum, 1)
            nc.vector.tensor_tensor(core.x[:], core.x[:], ps[:, 1, 0:D], ALU.add)

        @block.scalar
        def _(act):
            norm.scalar(act)
            act.wait_ge(h_ready, 1)
            nc.scalar.activation(h[:], h[:], ACT.Gelu).then_inc(gelu_done, 1)

        @block.tensor
        def _(pe):
            pe.wait_ge(wf_ready, 1)
            for k in range(DT):
                for n in range(FT):
                    last = nc.tensor.transpose(half_words(k, F)[:, n * P:(n + 1) * P],
                                               wfq[:, n, k * P:(k + 1) * P], identb[:])
            last.then_inc(wfT_in_psum, 1)
            pe.wait_ge(wp_ready, 1)
            for k in range(FT):
                for n in range(DT):
                    at = (k % 4) * D + n * P
                    last = nc.tensor.transpose(half_words(2 + k // 4, F)[:, at:at + P],
                                               wpq[:, n, k * P:(k + 1) * P], identb[:])
            last.then_inc(wpT_in_psum, 1)
            norm.tensor(pe)
            pe.wait_ge(xq_ready, 1)
            for k in range(DT):
                last = nc.tensor.transpose(half_words(4, D)[:, k * P:(k + 1) * P], xq[:, k * P:(k + 1) * P],
                                           identb[:])
            last.then_inc(xqT_in_psum, 1)
            pe.wait_ge(wT_ready, 1)
            pe.wait_ge(xqT_ready, 1)
            for n in range(2):
                projected(nc, ps[:, 5 + n, :], xqT, wfT[:, :, n * 512:(n + 1) * 512], DT, h_in_psum if n else None)
            pe.wait_ge(hq_ready, 1)
            for k in range(FT):
                last = nc.tensor.transpose(half_words(0, F)[:, k * P:(k + 1) * P], hq[:, k * P:(k + 1) * P],
                                           identb[:])
            last.then_inc(hqT_in_psum, 1)
            pe.wait_ge(hqT_ready, 1)
            projected(nc, ps[:, 1, 0:D], hqT, wpT, FT, y_in_psum)


def l3_attn(core):
    nc, ps, ident = core.nc, core.psum, core.ident()
    H, DH = 8, 32
    with Scope(core, "l3a") as s:
        norm = Norm(core, s)
        q, k, v = s.sb("q", [P, H, DH]), s.sb("k", [P, H, DH]), s.sb("v", [P, D])
        tmp = s.sb("tmp", [P, 4, H, DH // 2])
        qr, kr = s.sb("qr", [P, H, DH]), s.sb("kr", [P, H, DH])
        qT, kT = s.sb("qT", [P, DT, P]), s.sb("kT", [P, DT, P])
        st = s.sb("st", [P, H, P])
        y, sq = s.sb("y", [P, H, DH]), s.sb("sq", [P, H, DH])
        mean, var, std = s.sb("mean", [P, H]), s.sb("var", [P, H]), s.sb("std", [P, H])
        sig, gate = s.sb("sig", [P, D]), s.sb("gate", [P, D])
        yT = s.sb("yT", [P, DT, P])
        (chain_sem, qkv_in_psum, g_in_psum, gate_ready, rot_ready, qkT_in_psum, qkT_ready, s_in_psum, s_ready,
         y_in_psum, var_ready, std_ready, y_ready, yT_in_psum, yT_ready, out_in_psum) = s.signals(
            "chain_sem qkv_in_psum g_in_psum gate_ready rot_ready qkT_in_psum qkT_ready s_in_psum s_ready "
            "y_in_psum var_ready std_ready y_ready yT_in_psum yT_ready out_in_psum")
        flat = lambda t: t[:].rearrange("p h d -> p (h d)")
        wide = lambda t: t[:].unsqueeze(2).to_broadcast([P, H, DH])
        block = s.ctx.enter_context(nc.Block())

        @block.vector
        def _(dve):
            chain = Chain(dve, chain_sem)
            norm.vector(dve, chain)
            dve.wait_ge(qkv_in_psum, 1)
            nc.vector.tensor_copy(flat(q), ps[:, 0, 0:D])
            nc.vector.tensor_copy(flat(k), ps[:, 1, 0:D])
            chain(nc.vector.tensor_copy(v[:], ps[:, 2, 0:D]))
            for src, dst, tag in ((q, qr, "q"), (k, kr, "k")):
                table = lambda n: core.constant(n).unsqueeze(1).to_broadcast([P, H, DH // 2])
                last = rotary(nc, (src[:, :, 0::2], src[:, :, 1::2]), dst[:, :, 0::2], dst[:, :, 1::2],
                              table(f"xpos_cos_{tag}"), table(f"xpos_sin_{tag}"), [tmp[:, n] for n in range(4)],
                              chain)
                if tag == "q":
                    chain(last)
            last.then_inc(rot_ready, 1)
            dve.wait_ge(qkT_in_psum, 1)
            nc.vector.tensor_copy(flat(qT), ps[:, 4, 0:D])
            nc.vector.tensor_copy(flat(kT), ps[:, 5, 0:D]).then_inc(qkT_ready, 1)
            dve.wait_ge(s_in_psum, 1)
            decay = core.constant("decay").rearrange("p (h t) -> p h t", h=H)
            for g in range(4):
                last = nc.vector.tensor_tensor(st[:, g:H:4], ps[:, g, 0:2 * P].rearrange("p (h t) -> p h t", h=2),
                                               decay[:, g:H:4], ALU.mult)
            last.then_inc(s_ready, 1)
            dve.wait_ge(y_in_psum, 1)
            chain(nc.vector.tensor_copy(flat(y), ps[:, 4, 0:D]))
            chain(nc.vector.tensor_reduce(mean[:], y[:], AX.X, ALU.add))
            chain(nc.vector.tensor_scalar(mean[:], mean[:], 1.0 / DH, None, ALU.mult))
            chain(nc.vector.tensor_tensor(y[:], y[:], wide(mean), ALU.subtract))
            chain(nc.vector.tensor_tensor(sq[:], y[:], y[:], ALU.mult))
            chain(nc.vector.tensor_reduce(var[:], sq[:], AX.X, ALU.add))
            nc.vector.tensor_scalar(var[:], var[:], 1.0 / DH, LN_EPS, ALU.mult, ALU.add).then_inc(var_ready, 1)
            dve.wait_ge(std_ready, 1)
            chain(nc.vector.reciprocal(std[:], std[:]))
            chain(nc.vector.tensor_tensor(y[:], y[:], wide(std), ALU.mult))
            chain(nc.vector.tensor_tensor(flat(y), flat(y), core.weight("gnw"), ALU.mult))
            chain(nc.vector.tensor_tensor(flat(y), flat(y), core.weight("gnb"), ALU.add))
            dve.wait_ge(gate_ready, 2)
            chain(nc.vector.tensor_tensor(flat(y), flat(y), sig[:], ALU.mult))
            nc.vector.tensor_tensor(flat(y), flat(y), gate[:], ALU.mult).then_inc(y_ready, 1)
            dve.wait_ge(yT_in_psum, 1)
            nc.vector.tensor_copy(flat(yT), ps[:, 0, 0:D]).then_inc(yT_ready, 1)
            dve.wait_ge(out_in_psum, 1)
            nc.vector.tensor_tensor(core.x[:], core.x[:], ps[:, 1, 0:D], ALU.add)

        @block.scalar
        def _(act):
            norm.scalar(act)
            act.wait_ge(g_in_psum, 1)
            nc.scalar.activation(sig[:], ps[:, 3, 0:D], ACT.Sigmoid).then_inc(gate_ready, 1)
            nc.scalar.activation(gate[:], ps[:, 3, 0:D], ACT.Copy).then_inc(gate_ready, 1)
            act.wait_ge(var_ready, 1)
            nc.scalar.activation(std[:], var[:], ACT.Sqrt).then_inc(std_ready, 1)

        @block.tensor
        def _(pe):
            norm.tensor(pe)
            pe.wait_ge(norm.xT_ready, 1)
            for bank, name in enumerate(("rq", "rk", "rv")):
                projected(nc, ps[:, bank, 0:D], norm.xnT, core.kxn(name), DT, qkv_in_psum if bank == 2 else None)
            projected(nc, ps[:, 3, 0:D], norm.xnT, core.kxn("rg"), DT, g_in_psum)
            pe.wait_ge(rot_ready, 1)
            for bank, r in ((4, qr), (5, kr)):
                for n in range(DT):
                    last = nc.tensor.transpose(ps[:, bank, n * P:(n + 1) * P], flat(r)[:, n * P:(n + 1) * P], ident)
            last.then_inc(qkT_in_psum, 1)
            pe.wait_ge(qkT_ready, 1)
            pe.wait_ge(gate_ready, 2)
            for h in range(H):
                r = slice(DH * (h % 4), DH * (h % 4) + DH)
                last = nc.tensor.matmul(ps[:, h % 4, (h // 4) * P:(h // 4 + 1) * P], kT[r, h // 4, :],
                                        qT[r, h // 4, :], start=True, stop=True)
            last.then_inc(s_in_psum, 1)
            pe.wait_ge(s_ready, 1)
            for h in range(H):
                last = nc.tensor.matmul(ps[:, 4, h * DH:(h + 1) * DH], st[:, h, :], v[:, h * DH:(h + 1) * DH],
                                        start=True, stop=True)
            last.then_inc(y_in_psum, 1)
            pe.wait_ge(y_ready, 1)
            transposed(nc, ps, 0, flat(y), DT, ident, yT_in_psum)
            pe.wait_ge(yT_ready, 1)
            projected(nc, ps[:, 1, 0:D], yT, core.kxn("ro"), DT, out_in_psum)


def l3_ffn(core):
    nc, ps = core.nc, core.psum
    E, F = 8, 1024
    FT = F // P
    W1, W2, B1, B2 = 0, DT * F, DT * F + FT * D, DT * F + FT * D + FT
    WIDE = B2 + D
    with Scope(core, "l3f") as s:
        norm = Norm(core, s)
        w = s.sb("w", [P, 2, WIDE])
        hT = s.sb("hT", [P, 2, FT, P])
        mean, g = s.sb("mean", [P, DT, 1]), s.sb("g", [1, E])
        one = s.sb("one", [1, 4])
        top, topi = s.sb("top", [1, 8]), s.sb("topi", [1, 8], U32)
        pair, ones = s.sb("pair", [1, 2]), s.sb("ones", [1, P])
        coef = s.sb("coef", [P, 4])
        y, b2a = s.sb("y", [P, D]), s.sb("b2a", [P, D])
        (chain_sem, mean_ready, g_in_psum, shifted, exp_done, chosen, pair_ready, pair_in_psum, h_in_psum, h_ready,
         y_in_psum, y_added, coef_ready) = s.signals(
            "chain_sem mean_ready g_in_psum shifted exp_done chosen pair_ready pair_in_psum h_in_psum h_ready "
            "y_in_psum y_added coef_ready")
        w_in = s.signals("w_in0 w_in1")
        block = s.ctx.enter_context(nc.Block())

        @block.sync
        def _(sp):
            sp.dma_start(w[:, 0], core.dram["mlps"][E]).then_inc(w_in[0], 16)
            sp.wait_ge(chosen, 1)
            first = sp.value_load(topi[0:1, 0:1], min_val=0, max_val=E - 1)
            sp.dma_start(w[:, 1], core.dram["mlps"][bass.ds(first, 1)].squeeze(0)).then_inc(w_in[1], 16)
            second = sp.value_load(topi[0:1, 1:2], min_val=0, max_val=E - 1)
            sp.wait_ge(y_added, 1)
            sp.dma_start(w[:, 0], core.dram["mlps"][bass.ds(second, 1)].squeeze(0)).then_inc(w_in[0], 16)

        @block.vector
        def _(dve):
            chain = Chain(dve, chain_sem)
            nc.vector.memset(ones[:], 1.0)
            norm.vector(dve, chain)
            chain(nc.vector.tensor_reduce(mean[:], norm.xnT[:], AX.X, ALU.add))
            nc.vector.tensor_scalar(mean[:], mean[:], 1.0 / P, None, ALU.mult).then_inc(mean_ready, 1)
            dve.wait_ge(g_in_psum, 1)
            chain(nc.vector.tensor_tensor(g[:], ps[0:1, 0, 0:E], core.weight("bgate")[0:1, :], ALU.add))
            chain(nc.vector.tensor_reduce(one[:, 0:1], g[:], AX.X, ALU.max))
            nc.vector.tensor_scalar(g[:], g[:], one[:, 0:1], None, ALU.subtract).then_inc(shifted, 1)
            dve.wait_ge(exp_done, 1)
            chain(nc.vector.tensor_reduce(one[:, 1:2], g[:], AX.X, ALU.add))
            chain(nc.vector.reciprocal(one[:, 1:2], one[:, 1:2]))
            chain(nc.vector.tensor_scalar(g[:], g[:], one[:, 1:2], None, ALU.mult))
            chain(nc.vector.max(top[:], g[:]))
            nc.vector.max_index(topi[:], top[:], g[:]).then_inc(chosen, 1)
            chain(nc.vector.tensor_tensor(one[:, 2:3], top[:, 0:1], top[:, 1:2], ALU.add))
            chain(nc.vector.reciprocal(one[:, 2:3], one[:, 2:3]))
            nc.vector.tensor_scalar(pair[:], top[:, 0:2], one[:, 2:3], None, ALU.mult).then_inc(pair_ready, 1)
            chain(nc.vector.tensor_scalar(coef[:, 0:1], core.weight("alpha"), 0.1, 1.0, ALU.max, ALU.min))
            chain(nc.vector.tensor_scalar(coef[:, 3:4], coef[:, 0:1], -1.0, 1.0, ALU.mult, ALU.add))
            dve.wait_ge(pair_in_psum, 1)
            chain(nc.vector.tensor_scalar(coef[:, 1:3], ps[:, 1, 0:2], coef[:, 3:4], None, ALU.mult))
            for n in range(3):
                dve.wait_ge(y_in_psum, n + 1)
                chain(nc.vector.tensor_tensor(y[:], ps[:, 2, 0:D], w[:, n % 2, B2:B2 + D], ALU.add))
                nc.vector.scalar_tensor_tensor(core.x[:], y[:], coef[:, n:n + 1], core.x[:], ALU.mult,
                                               ALU.add).then_inc(y_added, 1)
                dve.wait_ge(y_added, n + 1)

        @block.scalar
        def _(act):
            norm.scalar(act)
            act.wait_ge(shifted, 1)
            nc.scalar.activation(g[:], g[:], ACT.Exp).then_inc(exp_done, 1)
            for n in range(3):
                for t in range(FT):
                    act.wait_ge(h_in_psum, n * FT + t + 1)
                    nc.scalar.activation(hT[:, n % 2, t], ps[:, 3 + t % 4, 0:P], ACT.Gelu_apprx_tanh,
                                         bias=w[:, n % 2, B1 + t:B1 + t + 1]).then_inc(h_ready, 1)

        @block.tensor
        def _(pe):
            norm.tensor(pe)
            pe.wait_ge(mean_ready, 1)
            wg = core.kxn("gate")
            for k in range(DT):
                last = nc.tensor.matmul(ps[0:1, 0, 0:E], mean[:, k, :], wg[:, k, :], start=(k == 0),
                                        stop=(k == DT - 1))
            last.then_inc(g_in_psum, 1)
            pe.wait_ge(pair_ready, 1)
            nc.tensor.matmul(ps[:, 1, 0:2], ones[:], pair[:], start=True, stop=True).then_inc(pair_in_psum, 1)
            for n in range(3):
                pe.wait_ge(w_in[n % 2], 16 * (n // 2 + 1))
                w1 = w[:, n % 2, W1:W2].rearrange("p (k f) -> p k f", k=DT)
                w2 = w[:, n % 2, W2:B1].rearrange("p (k o) -> p k o", k=FT)
                for t in range(FT):
                    if n * FT + t >= 4:
                        pe.wait_ge(h_ready, n * FT + t - 3)
                    for k in range(DT):
                        last = nc.tensor.matmul(ps[:, 3 + t % 4, 0:P], w1[:, k, t * P:(t + 1) * P],
                                                norm.xnT[:, k, :], start=(k == 0), stop=(k == DT - 1))
                    last.then_inc(h_in_psum, 1)
                if n:
                    pe.wait_ge(y_added, n)
                pe.wait_ge(h_ready, (n + 1) * FT)
                projected(nc, ps[:, 2, 0:D], hT[:, n % 2], w2, FT, y_in_psum)


LAYERS = [[l0_xattn, l0_attn, l0_ffn], [l1_xattn, l1_attn, l1_ffn], [l2_xattn, l2_attn, l2_ffn],
          [l3_xattn, l3_attn, l3_ffn]]


def program(nc, dram, cols, out):
    with ExitStack() as ctx:
        core = Core(nc, ctx, dram, cols)
        x_in = nc.alloc_semaphore("x_in")
        const_in = nc.alloc_semaphore("const_in")
        weights_in = nc.alloc_semaphore("weights_in")
        stored = nc.alloc_semaphore("stored")
        with nc.Block() as block:
            @block.sync
            def _(sp):
                sp.dma_start(core.x[:], dram["x"]).then_inc(x_in, 16)
                sp.dma_start(core.const[:], dram["const"]).then_inc(const_in, 16)
                sp.wait_ge(x_in, 16)
                sp.wait_ge(const_in, 16)
        for layer in range(4):
            if not FIRST < 3 * (layer + 1) or LAST <= 3 * layer:
                continue
            core.layer = f"w{layer}"
            with nc.sbuf_tensor(f"weights{layer}", [P, cols[core.layer]["_"]], F32) as w:
                core.w = w
                with nc.Block() as block:
                    @block.sync
                    def _(sp):
                        sp.dma_start(w[:], dram[core.layer]).then_inc(weights_in, 16)
                        sp.wait_ge(weights_in, 16 * (1 + sum(FIRST < 3 * (n + 1) for n in range(layer))))
                for n, sub in enumerate(LAYERS[layer]):
                    if FIRST <= 3 * layer + n < LAST:
                        sub(core)
        with nc.Block() as block:
            @block.sync
            def _(sp):
                sp.dma_start(out, core.x[:]).then_inc(stored, 16)
                sp.wait_ge(stored, 16)



def _constants():
    p = np.arange(P)
    t = {"ident": np.eye(P)}
    t["head16"] = (p[:, None] // 16 == np.arange(8)[None, :])
    t["head64"] = (p[:, None] // 64 == np.arange(2)[None, :])
    t["zero"] = np.zeros((P, D))
    t["one"] = np.ones((P, 1))
    i, j = p[:, None], p[None, :]
    masked = (j > i) & ~((i < 64) & (j < 64))
    t["prefix_mask"] = np.concatenate([np.where(masked, -1e30, 0.0), np.zeros((P, 2))], 1)
    t["causal_mask"] = np.where(j > i, -1e30, 0.0)
    t["chunk_mask"] = (j >= i) & (i // 64 == j // 64)
    t["iota"] = np.broadcast_to(p[None, :], (P, P))
    freq = p[:, None].astype(np.float32) * (1.0 / 10000.0 ** (np.arange(0, 16, 2, dtype=np.float32) / 16))[None, :]
    t["rope_cos"], t["rope_sin"] = np.cos(freq), np.sin(freq)
    pos = p.astype(np.float32)
    base = (np.arange(0, 32, 2, dtype=np.float32) + np.float32(0.4 * 32)) / np.float32(1.4 * 32)
    scale = base[None, :] ** (pos[:, None] / np.float32(512.0))
    turn = pos[:, None] * (1.0 / 10000.0 ** (np.arange(16, dtype=np.float32) / 16))[None, :]
    t["xpos_cos_q"], t["xpos_sin_q"] = np.cos(turn) * scale, np.sin(turn) * scale
    t["xpos_cos_k"], t["xpos_sin_k"] = np.cos(turn) / scale, np.sin(turn) / scale
    gamma = 1.0 - np.exp(np.linspace(np.log(1.0 / 32.0), np.log(1.0 / 512.0), 8))
    apart = (j - i)[:, None, :]
    t["decay"] = np.where(apart >= 0, np.exp(np.maximum(apart, 0) * np.log(gamma)[None, :, None]),
                          0.0).reshape(P, 8 * P)
    return t


def _kxn(w):
    k = w.shape[0] // P
    return w.reshape(k, P, -1).transpose(1, 0, 2).reshape(P, -1)


def _col(b):
    return b.reshape(-1, P).T


def _row(b):
    return np.broadcast_to(b.reshape(1, -1), (P, b.size))


def _pad(a):
    return np.concatenate([a, np.zeros((P - a.shape[0], a.shape[1]), a.dtype)], 0)


def _null_values(null_v, heads):
    z = np.zeros((P, heads * null_v.shape[1]), null_v.dtype)
    for n, h in enumerate([h for m in range(2) for h in range(m, heads, 2)]):
        z[2 * n:2 * n + 2, h * null_v.shape[1]:(h + 1) * null_v.shape[1]] = null_v
    return z


def _packs(a):
    w0 = {
        "xq": _kxn(a["L0_xattn_Wq"]), "xk": _kxn(a["L0_xattn_Wk"]), "xv": _kxn(a["L0_xattn_Wv"]),
        "xo": _kxn(a["L0_xattn_Wo"]), "xbq": _col(a["L0_xattn_bq"]), "xbk": _col(a["L0_xattn_bk"]),
        "xbv": _row(a["L0_xattn_bv"]), "xbo": _row(a["L0_xattn_bo"]),
        "gamma": _row(a["L0_attn_gamma"]), "aq": _kxn(a["L0_attn_Wq"]), "akv": _kxn(a["L0_attn_Wkv"]),
        "qs": _row(a["L0_attn_q_scale"]), "ks": _row(a["L0_attn_k_scale"]),
        "null_k": _pad(a["L0_attn_null_kv"][0]), "null_v": _null_values(a["L0_attn_null_kv"][1], 16),
        "ao": _kxn(a["L0_attn_Wout"]),
        "fr": _kxn(a["L0_ffn_W_r"].T), "fk": _kxn(a["L0_ffn_W_k"].T), "fv": _kxn(a["L0_ffn_W_v"].T),
        "mu_r": _col(a["L0_ffn_mu_r"]), "mu_k": _col(a["L0_ffn_mu_k"]),
    }
    w1 = {
        "xq": _kxn(a["L1_xattn_wq"].T), "xk": _kxn(a["L1_xattn_wk"].T), "xv": _kxn(a["L1_xattn_wv"].T),
        "xo": _kxn(a["L1_xattn_wo"].T), "xbq": _col(a["L1_xattn_bq"]), "xbk": _col(a["L1_xattn_bk"]),
        "xbv": _row(a["L1_xattn_bv"]), "xbo": _row(a["L1_xattn_bo"]),
        "gq": _kxn(a["L1_attn_Wq"]), "gk": _kxn(a["L1_attn_Wk"]), "gv": _kxn(a["L1_attn_Wv"]),
        "gg": _kxn(a["L1_attn_Wg"]), "gk1": _kxn(a["L1_attn_gk_w1"]), "gk2": _pad(a["L1_attn_gk_w2"]),
        "gkb": _col(a["L1_attn_gk_b2"]), "gn": _row(a["L1_attn_g_norm_w"]), "go": _kxn(a["L1_attn_Wo"]),
    }
    w1.update({
        "r1": _kxn(np.ascontiguousarray(a["L1_ffn_r1_w"].T)[0:D]), "r1s": _pad(a["L1_ffn_r1_w"].T[D:]),
        "r1b": _col(a["L1_ffn_r1_b"]), "r2": a["L1_ffn_r2_w"].T,
    })
    kvb = a["L2_attn_Wkvb"].reshape(32, 64, 2)
    w2 = {
        "xq": _kxn(a["L2_xattn_Wq"].T), "xk": _kxn(a["L2_xattn_Wk"].T), "xv": _kxn(a["L2_xattn_Wv"].T),
        "xbq": _col(a["L2_xattn_bq"]), "xbk": _col(a["L2_xattn_bk"]), "xbv": _row(a["L2_xattn_bv"]),
        "qa": _kxn(a["L2_attn_Wqa"]), "qb": _pad(a["L2_attn_Wqb"]), "kva": _kxn(a["L2_attn_Wkva"]),
        "kvb": _pad(np.concatenate([kvb[:, :, 0], kvb[:, :, 1]], 1)), "aout": _kxn(a["L2_attn_Wout"]),
        "bout": _row(a["L2_attn_bout"]),
        "fc": _kxn(a["L2_ffn_w_fc"]), "bfc": _row(a["L2_ffn_b_fc"]), "proj": _kxn(a["L2_ffn_w_proj"]),
        "bproj": _row(a["L2_ffn_b_proj"]),
    }
    heads = lambda m: _kxn(m.transpose(1, 0, 2).reshape(D, -1))
    w3 = {
        "xq": _kxn(a["L3_xattn_Wq"]), "xk": _kxn(a["L3_xattn_Wk"]), "xv": _kxn(a["L3_xattn_Wv"]),
        "xo": _kxn(a["L3_xattn_Wo"]),
        "rq": heads(a["L3_attn_W_Q"]), "rk": heads(a["L3_attn_W_K"]), "rv": heads(a["L3_attn_W_V"]),
        "rg": _kxn(a["L3_attn_W_G"]), "ro": _kxn(a["L3_attn_W_O"]), "gnw": _row(a["L3_attn_gn_weight"]),
        "gnb": _row(a["L3_attn_gn_bias"]),
        "gate": _kxn(a["L3_ffn_w_gate"]), "bgate": _row(a["L3_ffn_b_gate"]),
        "alpha": _row(a["L3_ffn_alpha"].reshape(1)),
    }
    return [w0, w1, w2, w3]


def _each(w):
    return np.stack([_kxn(m) for m in w])


def _big(a):
    mlp = lambda w1, w2, b1, b2: np.concatenate([_kxn(w1), _kxn(w2), _col(b1), _row(b2)], 1)
    mlps = [mlp(a["L3_ffn_W1e"][e], a["L3_ffn_W2e"][e], a["L3_ffn_b1e"][e], a["L3_ffn_b2e"][e]) for e in range(8)]
    mlps.append(mlp(a["L3_ffn_W1m"], a["L3_ffn_W2m"], a["L3_ffn_b1m"], a["L3_ffn_b2m"]))
    return {
        "w_up": _each(a["L1_ffn_w_up"].transpose(0, 2, 1)), "w_down": _each(a["L1_ffn_w_down"].transpose(0, 2, 1)),
        "a_up": _each(a["L1_ffn_a_up"].transpose(0, 2, 1)), "a_down": _each(a["L1_ffn_a_down"].transpose(0, 2, 1)),
        "mlps": np.stack(mlps),
    }


def kernel(**inputs):
    import concourse.bacc as bacc
    from concourse.bass_utils import run_bass_kernel_spmd

    a = {n: np.asarray(v) for n, v in inputs.items()}
    arrays, cols = {}, {}
    packs = {f"w{n}": pack for n, pack in enumerate(_packs(a))}
    packs["const"] = {n: t.astype(np.float32) for n, t in _constants().items()}
    for name, pack in packs.items():
        at, where = 0, {}
        for n, piece in pack.items():
            where[n] = (at, at + piece.shape[1])
            at += piece.shape[1]
        where["_"] = at
        cols[name] = where
        arrays[name] = np.ascontiguousarray(np.concatenate(list(pack.values()), 1))
    arrays["x"] = a["x"][0]
    arrays["ctxT"] = np.ascontiguousarray(a["ctx_1024"][0].T)
    arrays.update(_big(a))

    nc = bacc.Bacc("TRN2", target_bir_lowering=False, num_devices=1)
    dram = {n: nc.dram_tensor(n, v.shape, mybir.dt.from_np(v.dtype), kind="ExternalInput").ap()
            for n, v in arrays.items()}
    out = nc.dram_tensor("out_0_dram", (P, D), F32, kind="ExternalOutput").ap()
    program(nc, dram, cols, out)
    r = run_bass_kernel_spmd(nc, [arrays], core_ids=[0])
    return r.results[0]["out_0_dram"].reshape(1, P, D)
```

```python
from contextlib import ExitStack

import numpy as np

import concourse.bass as bass
from concourse import mybir

F32 = mybir.dt.float32
BF16 = mybir.dt.bfloat16
F16 = mybir.dt.float16
F32R = mybir.dt.float32r
I32 = mybir.dt.int32
U32 = mybir.dt.uint32
ALU = mybir.AluOpType
ACT = mybir.ActivationFunctionType
AX = mybir.AxisListType

P = 128
D = 256
DT = D // P
KEYS = 12544
CH = 896
BLK = CH // 2
TPC = CH // P
NCH = KEYS // CH
LN_EPS = 1e-5
P_SHIFT = float(8 * np.log(2))
AHEAD = 4


class Chain:

    def __init__(self, eng, sem):
        self.eng, self.sem, self.n = eng, sem, 0

    def __call__(self, ins):
        self.n += 1
        ins.then_inc(self.sem, 1)
        self.eng.wait_ge(self.sem, self.n)


class Core:

    def __init__(self, nc, ctx, dram, cols):
        self.nc, self.ctx, self.dram, self.cols = nc, ctx, dram, cols
        self.x = ctx.enter_context(nc.sbuf_tensor("rows", [P, D], F32))
        self.const = ctx.enter_context(nc.sbuf_tensor("consts", [P, cols["const"]["_"]], F32))
        self.psum = ctx.enter_context(nc.psum_tensor("psum", [P, 8, 512], F32))
        self.w = None

    def constant(self, name):
        a, b = self.cols["const"][name]
        return self.const[:, a:b]

    def weight(self, name):
        a, b = self.cols[self.layer][name]
        return self.w[:, a:b]

    def kxn(self, name, k=DT):
        return self.weight(name).rearrange("p (k n) -> p k n", k=k)

    def ident(self, n=P):
        return self.constant("ident")[0:n, 0:n]


class Scope:

    def __init__(self, core, name):
        self.nc, self.name, self.ctx, self.sems = core.nc, name, ExitStack(), []

    def __enter__(self):
        return self

    def __exit__(self, *e):
        self.ctx.__exit__(*e)
        if e[0] is None:
            self.nc.clear_and_free_semaphores(self.sems)
            self.nc.all_engine_barrier(sem_only=True)

    def sb(self, name, shape, dt=F32):
        return self.ctx.enter_context(self.nc.sbuf_tensor(f"{self.name}_{name}", shape, dt))

    def signals(self, names):
        made = [self.nc.alloc_semaphore(f"{self.name}_{n}") for n in names.split()]
        self.sems += made
        return made


class Norm:

    def __init__(self, core, scope, src=None, gamma=None, tag="ln"):
        self.nc, self.ident, self.gamma = core.nc, core.ident(), gamma
        self.src = core.x[:] if src is None else src
        self.stats = scope.sb(f"{tag}_stats", [P, 6])
        self.mv = scope.sb(f"{tag}_mv", [P, 2])
        self.std = scope.sb(f"{tag}_std", [P, 1])
        self.rstd = scope.sb(f"{tag}_rstd", [P, 1])
        self.xn = scope.sb(f"{tag}_xn", [P, D])
        self.xnT = scope.sb(f"{tag}_xnT", [P, DT, P])
        self.ps = core.psum[:, 7, 0:DT * P]
        self.var_ready, self.std_ready, self.xn_ready, self.xT_in_psum, self.xT_ready = scope.signals(
            f"{tag}_var_ready {tag}_std_ready {tag}_xn_ready {tag}_xT_in_psum {tag}_xT_ready")

    def vector(self, dve, chain):
        nc = self.nc
        chain(nc.vector.bn_stats(self.stats[:], self.src))
        chain(nc.vector.bn_aggr(self.mv[:], self.stats[:]))
        nc.vector.tensor_scalar(self.rstd[:], self.mv[:, 1:2], LN_EPS, None, ALU.add).then_inc(self.var_ready, 1)
        dve.wait_ge(self.std_ready, 1)
        chain(nc.vector.reciprocal(self.rstd[:], self.std[:]))
        last = nc.vector.tensor_scalar(self.xn[:], self.src, self.mv[:, 0:1], self.rstd[:], ALU.subtract, ALU.mult)
        if self.gamma is not None:
            chain(last)
            last = nc.vector.tensor_tensor(self.xn[:], self.xn[:], self.gamma, ALU.mult)
        last.then_inc(self.xn_ready, 1)
        dve.wait_ge(self.xT_in_psum, 1)
        nc.vector.tensor_copy(self.xnT[:].rearrange("p k t -> p (k t)"), self.ps).then_inc(self.xT_ready, 1)
        dve.wait_ge(self.xT_ready, 1)

    def scalar(self, act):
        act.wait_ge(self.var_ready, 1)
        self.nc.scalar.activation(self.std[:], self.rstd[:], ACT.Sqrt).then_inc(self.std_ready, 1)

    def tensor(self, pe):
        pe.wait_ge(self.xn_ready, 1)
        for k in range(DT):
            last = self.nc.tensor.transpose(self.ps[:, k * P:(k + 1) * P], self.xn[:, k * P:(k + 1) * P],
                                            self.ident)
        last.then_inc(self.xT_in_psum, 1)


def cross_attention_plain(core, name, heads, groups, wq, wk, wv, wo, bq, bk, bv, bo, scale):
    nc = core.nc
    dh = D // heads
    per = max(1, heads // DT)
    hq = per * P
    units = 2 if heads == 16 else 1
    UW = heads * P // units
    VW = heads * (dh + 1)
    with Scope(core, name) as s:
        norm = Norm(core, s)
        ctxb = s.sb("ctx", [P, 2, DT, CH])
        kT = s.sb("kT", [P, 2, DT, CH])
        v = s.sb("v", [P, 2, TPC, heads, dh + 1])
        prob = s.sb("prob", [P, 2, heads * P])
        qT = s.sb("qT", [P, DT, P])
        qbd = s.sb("qbd", [P, DT, per, P])
        chunk_max = s.sb("chunk_max", [P, 2, heads])
        run_max = s.sb("run_max", [P, heads])
        neg = s.sb("neg", [P, 2, heads])
        m3b = s.sb("m3b", [P, 3, heads], BF16)
        m3f = s.sb("m3f", [P, 3 * heads])
        m3T = s.sb("m3T", [3 * heads, P], BF16)
        m3row = s.sb("m3row", [3, heads * P], BF16)
        ones3 = s.sb("ones3", [3, P], BF16)
        oacc = s.sb("oacc", [P, VW])
        rden = s.sb("rden", [P, heads, 1])
        o = s.sb("o", [P, D])
        oT = s.sb("oT", [P, DT, P])
        ps = core.psum
        ident = core.ident()
        m3_dram = nc.dram_tensor(f"{name}_m3", [3 * heads, P], BF16).ap()

        (ctx_free, k_in_psum, k_ready, q_in_psum, q_ready, s_full, s_free, neg_ready, m3_in_psum, m3T_ready,
         m3_rows, st_full, p_ready, pv_done, v_in_psum, v_ready, o_added, o_ready, oT_in_psum, oT_ready,
         y_in_psum, x_done, chain_sem, max_step, m3_stored) = s.signals(
            "ctx_free k_in_psum k_ready q_in_psum q_ready s_full s_free neg_ready m3_in_psum m3T_ready "
            "m3_rows st_full p_ready pv_done v_in_psum v_ready o_added o_ready oT_in_psum oT_ready "
            "y_in_psum x_done chain_sem max_step m3_stored")
        ctx_in = s.signals("ctx_in0 ctx_in1")
        K_RING, S_RING, ST_RING, V_RING, O_RING, CTX_RING = 2, 2, 2, 2, 2, 2
        S_CREDIT = heads + 1
        ST_CREDIT = TPC * units + 1
        PV_CREDIT = TPC * units + 1

        ctxT = core.dram["ctxT"].rearrange("(k p) n -> p k n", p=P)
        block = s.ctx.enter_context(nc.Block())

        @block.sync
        def _(sp):
            for g in range(groups):
                for ps_no in range(2):
                    base = (2 * g + ps_no) * NCH
                    with sp.Fori(0, NCH // 2) as i:
                        for b in range(2):
                            sp.wait_ge(ctx_free, i * 2 + (base + b + 1))
                            sp.dma_start(ctxb[:, b], ctxT[:, :, bass.ds(i * (2 * CH) + b * CH, CH)]).then_inc(
                                ctx_in[b], 16)

        @block.gpsimd
        def _(pool):
            pool.sem_inc(ctx_free, CTX_RING)
            pool.sem_inc(k_ready, K_RING)
            pool.sem_inc(s_full, S_CREDIT)
            pool.sem_inc(s_free, S_RING)
            pool.sem_inc(st_full, ST_CREDIT)
            pool.sem_inc(p_ready, ST_RING)
            pool.sem_inc(pv_done, PV_CREDIT)
            pool.sem_inc(v_ready, V_RING)
            pool.sem_inc(o_added, O_RING)

        @block.scalar
        def _(act):
            norm.scalar(act)
            for g in range(groups):
                def keys(i, b, base, k_free_wait):
                    k_free_wait()
                    for hb in range(4):
                        half, blk = hb // 2, hb % 2
                        act.wait_ge(k_in_psum, i * 8 + (4 * (base + b) + hb + 1))
                        nc.scalar.activation(kT[:, b, half, blk * BLK:(blk + 1) * BLK], ps[:, 6 + hb % 2, 0:BLK],
                                             ACT.Identity, bias=bk(g, half)).then_inc(k_ready, 1)

                base = 2 * g * NCH
                with act.Fori(0, NCH // 2) as i:
                    for b in range(2):
                        keys(i, b, base, lambda: act.wait_ge(
                            s_full, i * (2 * heads) + ((g * NCH + b) * heads + 1)))
                act.wait_ge(m3T_ready, g + 1)
                act.dma_start(m3_dram[:, :], m3T[:]).then_inc(m3_stored, 16)
                act.wait_ge(m3_stored, 16 * (g + 1))
                act.dma_start(m3row[:], m3_dram.rearrange("(k h) q -> k (h q)", k=3)).then_inc(m3_rows, 16)
                base = (2 * g + 1) * NCH
                with act.Fori(0, NCH // 2) as i:
                    for b in range(2):
                        cu = TPC * units
                        keys(i, b, base, lambda: act.wait_ge(
                            st_full, i * (2 * cu) + ((g * NCH + b) * cu + 1)))
                        for t in range(TPC):
                            for u in range(units):
                                at = (g * NCH + b) * cu + t * units + u
                                act.wait_ge(st_full, i * (2 * cu) + (at + 1 + ST_CREDIT))
                                act.wait_ge(pv_done, i * (2 * cu) + (at + 1 + PV_CREDIT - 2 * units))
                                slot = (b * TPC + t) % 2
                                bank = 2 * ((at if units == 1 else u) % 2)
                                src = ps[:, bank:bank + 2, :].rearrange("p a n -> p (a n)")[:, 0:UW]
                                nc.scalar.activation(prob[:, slot, u * UW:(u + 1) * UW], src,
                                                     ACT.Exp).then_inc(p_ready, 1)

        @block.vector
        def _(dve):
            chain = Chain(dve, chain_sem)
            chain(nc.vector.memset(ones3[:], 1.0))
            chain(nc.vector.memset(v[:, :, :, :, dh:dh + 1].rearrange("p a t h w -> p (a t h) w"), 1.0))
            norm.vector(dve, chain)
            for g in range(groups):
                chain(nc.vector.memset(run_max[:], -3.0e38))
                dve.wait_ge(q_in_psum, g + 1)
                for k in range(DT):
                    last = nc.vector.tensor_scalar(qT[:, k, :], ps[:, 4, k * P:(k + 1) * P], bq(g, k), scale,
                                                   ALU.add, ALU.mult)
                chain(last)
                for k in range(DT):
                    if heads == 1:
                        last = nc.vector.tensor_copy(qbd[:, k, 0, :], qT[:, k, :])
                    else:
                        mask = core.constant(f"head{dh}")
                        last = nc.vector.tensor_tensor(
                            qbd[:, k], qT[:, k, :].unsqueeze(1).to_broadcast([P, per, P]),
                            mask.unsqueeze(2).to_broadcast([P, per, P]), ALU.mult)
                last.then_inc(q_ready, 1)
                with dve.Fori(0, NCH // 2) as i:
                    for b in range(2):
                        for h in range(heads):
                            at = (g * NCH + b) * heads + h
                            dve.wait_ge(s_full, i * (2 * heads) + (at + 1 + S_CREDIT))
                            bank = 2 * (at % 2)
                            nc.vector.tensor_reduce(chunk_max[:, b, h:h + 1], ps[:, bank:bank + 2, 0:BLK],
                                                    AX.XY, ALU.max).then_inc(s_free, 1)
                        dve.wait_ge(s_free, i * (2 * heads) + ((g * NCH + b + 1) * heads + S_RING))
                        if b:
                            dve.wait_ge(max_step, i * 2 + (g * NCH + 1))
                        nc.vector.tensor_tensor(run_max[:], run_max[:], chunk_max[:, b], ALU.max).then_inc(
                            max_step, 1)
                        if b:
                            dve.wait_ge(max_step, i * 2 + (g * NCH + 2))
                chain(nc.vector.tensor_scalar(neg[:, 0], run_max[:], -1.0, None, ALU.mult))
                for k in range(3):
                    chain(nc.vector.tensor_copy(m3b[:, k], neg[:, k % 2]))
                    if k < 2:
                        chain(nc.vector.tensor_tensor(neg[:, (k + 1) % 2], neg[:, k % 2], m3b[:, k],
                                                      ALU.subtract))
                nc.vector.tensor_copy(m3f[:], m3b[:].rearrange("p a h -> p (a h)")).then_inc(neg_ready, 1)
                dve.wait_ge(m3_in_psum, g + 1)
                nc.vector.tensor_copy(m3T[:], ps[0:3 * heads, 5, 0:P]).then_inc(m3T_ready, 1)
                chain(nc.vector.memset(oacc[:], 0.0))
                cu = TPC * units
                with dve.Fori(0, NCH // 2) as i:
                    for b in range(2):
                        dve.wait_ge(pv_done, i * (2 * cu) + ((g * NCH + b) * cu + 1))
                        for t in range(TPC):
                            at = (g * NCH + b) * TPC + t
                            dve.wait_ge(v_in_psum, i * (2 * TPC) + (at + 1))
                            src = ps[:, 6 + at % 2, 0:D].rearrange("p (h w) -> p h w", h=heads)
                            nc.vector.tensor_tensor(v[:, b, t, :, 0:dh], src,
                                                    bv(g).rearrange("p (h w) -> p h w", h=heads),
                                                    ALU.add).then_inc(v_ready, 1)
                        dve.wait_ge(pv_done, i * (2 * cu) + ((g * NCH + b + 1) * cu + PV_CREDIT))
                        if b:
                            dve.wait_ge(o_added, i * 2 + (g * NCH + 1 + O_RING))
                        nc.vector.tensor_tensor(oacc[:], oacc[:], ps[:, 4 + b, 0:VW], ALU.add).then_inc(
                            o_added, 1)
                        if b:
                            dve.wait_ge(o_added, i * 2 + (g * NCH + 2 + O_RING))
                oa = oacc[:].rearrange("p (h w) -> p h w", h=heads)
                chain(nc.vector.reciprocal(rden[:], oa[:, :, dh:dh + 1]))
                nc.vector.tensor_tensor(o[:].rearrange("p (h w) -> p h w", h=heads), oa[:, :, 0:dh],
                                        rden[:].to_broadcast([P, heads, dh]), ALU.mult).then_inc(o_ready, 1)
                dve.wait_ge(oT_in_psum, g + 1)
                nc.vector.tensor_copy(oT[:].rearrange("p k t -> p (k t)"), ps[:, 4, 0:D]).then_inc(oT_ready, 1)
                if wo is None:
                    chain(nc.vector.tensor_tensor(core.x[:], core.x[:], o[:], ALU.add))
                else:
                    dve.wait_ge(y_in_psum, g + 1)
                    chain(nc.vector.tensor_tensor(core.x[:], core.x[:], ps[:, 5, 0:D], ALU.add))
                    if bo is not None and g == 0:
                        chain(nc.vector.tensor_tensor(core.x[:], core.x[:], bo, ALU.add))

        @block.tensor
        def _(pe):
            norm.tensor(pe)
            for g in range(groups):
                pe.wait_ge(norm.xT_ready, 1)
                if g:
                    pe.wait_ge(oT_ready, g)
                for half in range(DT):
                    for k in range(DT):
                        last = nc.tensor.matmul(ps[:, 4, half * P:(half + 1) * P], wq(g, k, half),
                                                norm.xnT[:, k, :], start=(k == 0), stop=(k == DT - 1))
                last.then_inc(q_in_psum, 1)

                def keys(i, b, base):
                    pe.wait_ge(ctx_in[b], i * 16 + (base // 2 + 1) * 16)
                    for hb in range(4):
                        half, blk = hb // 2, hb % 2
                        pe.wait_ge(k_ready, i * 8 + (4 * (base + b) + hb + 1))
                        for k in range(DT):
                            last = nc.tensor.matmul(ps[:, 6 + hb % 2, 0:BLK], wk(g, k, half),
                                                    ctxb[:, b, k, blk * BLK:(blk + 1) * BLK],
                                                    start=(k == 0), stop=(k == DT - 1))
                        if hb < 3:
                            last.then_inc(k_in_psum, 1)
                    return last

                pe.wait_ge(q_ready, g + 1)
                base = 2 * g * NCH
                with pe.Fori(0, NCH // 2) as i:
                    for b in range(2):
                        keys(i, b, base).then_inc(k_in_psum, 1)
                        pe.wait_ge(k_ready, i * 8 + (4 * (base + b) + 4 + K_RING))
                        pe.sem_inc(ctx_free, 1)
                        for h in range(heads):
                            at = (g * NCH + b) * heads + h
                            bank = 2 * (at % 2)
                            pe.wait_ge(s_free, i * (2 * heads) + (at + 1))
                            for blk in range(2):
                                if heads == 1:
                                    for k in range(DT):
                                        last = nc.tensor.matmul(ps[:, bank + blk, 0:BLK], qbd[:, k, 0, :],
                                                                kT[:, b, k, blk * BLK:(blk + 1) * BLK],
                                                                start=(k == 0), stop=(k == DT - 1))
                                else:
                                    last = nc.tensor.matmul(ps[:, bank + blk, 0:BLK],
                                                            qbd[:, h // per, h % per, :],
                                                            kT[:, b, h // per, blk * BLK:(blk + 1) * BLK],
                                                            start=True, stop=True)
                            last.then_inc(s_full, 1)
                pe.wait_ge(neg_ready, g + 1)
                nc.tensor.transpose(ps[0:3 * heads, 5, 0:P], m3f[:], ident).then_inc(m3_in_psum, 1)
                pe.wait_ge(m3_rows, 16 * (g + 1))

                base = (2 * g + 1) * NCH
                cu = TPC * units

                def scores(i, b, t):
                    for u in range(units):
                        at = (g * NCH + b) * cu + t * units + u
                        pe.wait_ge(p_ready, i * (2 * cu) + (at + 1))
                        slot = 2 * ((at if units == 1 else u) % 2)
                        flat = ps[:, slot:slot + 2, :].rearrange("p a n -> p (a n)")
                        for c0 in range(0, UW, 512):
                            w = min(512, UW)
                            nc.tensor.matmul(flat[:, c0:c0 + w], ones3[:],
                                             m3row[:, u * UW + c0:u * UW + c0 + w], start=True, stop=False,
                                             skip_group_check=True)
                        keys_of = kT[:, b, :, t * P:(t + 1) * P]
                        for k in range(DT) if units == 1 else [u]:
                            for c0 in range(0, hq, 512):
                                w = min(512, hq)
                                at0 = c0 + (k * hq if units == 1 and heads > 1 else 0)
                                q = qbd[:, k].rearrange("p j q -> p (j q)")
                                last = nc.tensor.matmul(flat[:, at0:at0 + w], keys_of[:, k, :],
                                                        q[:, c0:c0 + w], start=False, stop=True,
                                                        skip_group_check=True)
                        last.then_inc(st_full, 1)

                def values(i, b, t):
                    slot = (b * TPC + t) % 2
                    for u in range(units):
                        at = (g * NCH + b) * cu + t * units + u
                        pe.wait_ge(p_ready, i * (2 * cu) + (at + 1 + ST_RING))
                        for h in range(u * heads // units, (u + 1) * heads // units):
                            last = nc.tensor.matmul(ps[:, 4 + b, h * (dh + 1):(h + 1) * (dh + 1)],
                                                    prob[:, slot, h * P:(h + 1) * P], v[:, b, t, h, :],
                                                    start=(t == 0 and h == 0), stop=(t == TPC - 1),
                                                    skip_group_check=True)
                        last.then_inc(pv_done, 1)

                with pe.Fori(0, NCH // 2) as i:
                    for b in range(2):
                        keys(i, b, base).then_inc(k_in_psum, 1)
                        pe.wait_ge(k_ready, i * 8 + (4 * (base + b) + 4 + K_RING))
                        for t in range(TPC):
                            at = (g * NCH + b) * TPC + t
                            pe.wait_ge(v_ready, i * (2 * TPC) + (at + 1))
                            for k in range(DT):
                                last = nc.tensor.matmul(ps[:, 6 + at % 2, 0:D],
                                                        ctxb[:, b, k, t * P:(t + 1) * P], wv(g, k),
                                                        start=(k == 0), stop=(k == DT - 1))
                            last.then_inc(v_in_psum, 1)
                        pe.wait_ge(v_ready, i * (2 * TPC) + ((g * NCH + b + 1) * TPC + V_RING))
                        pe.sem_inc(ctx_free, 1)
                        pe.wait_ge(o_added, i * 2 + (g * NCH + b + 1))
                        scores(i, b, 0)
                        for t in range(1, TPC):
                            scores(i, b, t)
                            values(i, b, t - 1)
                        values(i, b, TPC - 1)
                pe.wait_ge(o_ready, g + 1)
                for k in range(DT):
                    last = nc.tensor.transpose(ps[:, 4, k * P:(k + 1) * P], o[:, k * P:(k + 1) * P], ident)
                last.then_inc(oT_in_psum, 1)
                if wo is not None:
                    pe.wait_ge(oT_ready, g + 1)
                    for k in range(DT):
                        last = nc.tensor.matmul(ps[:, 5, 0:D], oT[:, k, :], wo(g, k), start=(k == 0),
                                                stop=(k == DT - 1))
                    last.then_inc(y_in_psum, 1)


def split(nc, out_hi, out_lo, src, chain):
    chain(nc.vector.tensor_copy(out_hi, src))
    return nc.vector.tensor_tensor(out_lo, src, out_hi.bitcast(F32), ALU.subtract)


def cross_attention(core, name, heads, groups, wq, wk, wv, wo, bq, bk, bv, bo, scale):
    nc = core.nc
    dh = D // heads
    per = heads // DT
    hq = per * P
    units = 2 if heads == 16 else 1
    UW = heads * P // units
    HW = 3 * dh + 1
    BW = per * HW
    CU = TPC * units
    PAIRS = NCH // 2
    K_BANK, V_BANK = 7, 6
    with Scope(core, name) as s:
        norm = Norm(core, s)
        ctxb = s.sb("ctx", [P, 2, DT, CH])
        chi, clo = s.sb("chi", [P, 2, DT, CH], F32R), s.sb("clo", [P, 2, DT, CH], F32R)
        khi, klo = s.sb("khi", [P, 2, DT, CH], F32R), s.sb("klo", [P, 2, DT, CH], F32R)
        v = s.sb("v", [P, 2, TPC, heads, HW], BF16)
        vrest = s.sb("vrest", [P, 2, D])
        p32 = s.sb("p32", [P, 2, UW])
        phi, plo = s.sb("phi", [P, 2, heads * P], F16), s.sb("plo", [P, 2, heads * P], F16)
        wkh, wkl = s.sb("wkh", [P, DT, D], F32R), s.sb("wkl", [P, DT, D], F32R)
        wvh, wvl = s.sb("wvh", [P, DT, D], F32R), s.sb("wvl", [P, DT, D], F32R)
        qT = s.sb("qT", [P, DT, P])
        qh, ql = s.sb("qh", [P, DT, per * P], F32R), s.sb("ql", [P, DT, per * P], F32R)
        chunk_max = s.sb("chunk_max", [P, 2, heads])
        run_max = s.sb("run_max", [P, heads])
        neg = s.sb("neg", [P, 2, heads])
        m3b = s.sb("m3b", [P, 3, heads], BF16)
        m3f = s.sb("m3f", [P, 3 * heads])
        m3T = s.sb("m3T", [3 * heads, P], BF16)
        m3row = s.sb("m3row", [3, heads * P], BF16)
        ones3, zeros3 = s.sb("ones3", [3, P], BF16), s.sb("zeros3", [3, P], BF16)
        oa = s.sb("oa", [P, heads, HW])
        rden = s.sb("rden", [P, heads, 1])
        o = s.sb("o", [P, D])
        oT = s.sb("oT", [P, DT, P])
        ps = core.psum
        ident = core.ident()
        m3_dram = nc.dram_tensor(f"{name}_m3", [3 * heads, P], BF16).ap()

        (weights_split, hi_ready, lo_ready, k_in_psum, khi_ready, klo_ready, q_in_psum, q_ready, s_full,
         s_free, max_step, neg_ready, m3_in_psum, m3T_ready, m3_stored, m3_rows, v_in_psum, v1_ready,
         rest_ready, v2_ready, v_ready, st_full, p32_ready, phi_ready, plo_ready, pv_done, o_ready,
         oT_in_psum, oT_ready, y_in_psum, chain_sem) = s.signals(
            "weights_split hi_ready lo_ready k_in_psum khi_ready klo_ready q_in_psum q_ready s_full "
            "s_free max_step neg_ready m3_in_psum m3T_ready m3_stored m3_rows v_in_psum v1_ready "
            "rest_ready v2_ready v_ready st_full p32_ready phi_ready plo_ready pv_done o_ready "
            "oT_in_psum oT_ready y_in_psum chain_sem")
        ctx_in = s.signals("ctx_in0 ctx_in1")
        RING = 2

        ctxT = core.dram["ctxT"].rearrange("(k p) n -> p k n", p=P)
        block = s.ctx.enter_context(nc.Block())

        @block.sync
        def _(sp):
            def load(i, n0, b):
                sp.dma_start(ctxb[:, b], ctxT[:, :, bass.ds(i * (2 * CH) + (n0 + b) * CH, CH)]).then_inc(
                    ctx_in[b], 16)

            for g in range(groups):
                for b in range(2):
                    if g:
                        sp.wait_ge(lo_ready, g * NCH - 1 + b)
                    load(0, 0, b)
                with sp.Fori(0, PAIRS - 1) as i:
                    for b in range(2):
                        sp.wait_ge(hi_ready, i * 2 + (2 * g * NCH + b + 1))
                        load(i, 2, b)
                for b in range(2):
                    sp.wait_ge(hi_ready, (2 * g + 1) * NCH - 1 + b)
                    load(0, 0, b)
                with sp.Fori(0, PAIRS - 1) as i:
                    for b in range(2):
                        sp.wait_ge(lo_ready, i * 2 + (g * NCH + b + 1))
                        load(i, 2, b)

        @block.gpsimd
        def _(pool):
            for sem in (khi_ready, s_free, rest_ready, v_ready, phi_ready, plo_ready):
                pool.sem_inc(sem, RING)

            def lower(i, g, n0):
                b = n0 % 2
                if g or n0 > 1:
                    pool.wait_ge(v_in_psum, i * (2 * TPC) + TPC * (g * NCH + n0 - 1))
                pool.wait_ge(hi_ready, i * 2 + ((2 * g + 1) * NCH + n0 + 1))
                nc.gpsimd.tensor_tensor(clo[:, b], ctxb[:, b], chi[:, b].bitcast(F32), ALU.subtract).then_inc(
                    lo_ready, 1)

            def third(i, g, n0, t):
                at = (g * NCH + n0) * TPC + t
                b = n0 % 2
                rest = vrest[:, at % 2].rearrange("p (h w) -> p h w", h=heads)
                pool.wait_ge(v2_ready, i * (2 * TPC) + (at + 1))
                nc.gpsimd.tensor_tensor(v[:, b, t, :, 2 * dh + 1:HW], rest, v[:, b, t, :, dh + 1:2 * dh + 1],
                                        ALU.subtract).then_inc(v_ready, 1)

            for g in range(groups):
                lower(0, g, 0)
                lower(0, g, 1)
                for t in range(TPC):
                    third(0, g, 0, t)
                with pool.Fori(0, PAIRS - 1) as i:
                    for b in range(2):
                        for t in range(TPC):
                            if t == AHEAD:
                                lower(i, g, b + 2)
                            third(i, g, b + 1, t)
                for t in range(TPC):
                    third(PAIRS - 1, g, 1, t)

        @block.scalar
        def _(act):
            norm.scalar(act)

            def upper(i, load, freed, count):
                b = load % 2
                act.wait_ge(ctx_in[b], i * 16 + (load // 2 + 1) * 16)
                if freed is not None:
                    act.wait_ge(freed, count)
                nc.scalar.activation(chi[:, b], ctxb[:, b], ACT.Copy).then_inc(hi_ready, 1)

            def key(i, g, load, hb, bank):
                hf, blk = hb // 2, hb % 2
                act.wait_ge(k_in_psum, i * 8 + (4 * load + hb + 1))
                nc.scalar.activation(khi[:, load % 2, hf, blk * BLK:(blk + 1) * BLK], ps[:, bank, 0:BLK],
                                     ACT.Identity, bias=bk(g, hf)).then_inc(khi_ready, 1)

            def first(i, g, n0, t):
                at = (g * NCH + n0) * TPC + t
                act.wait_ge(v_in_psum, i * (2 * TPC) + (at + 1))
                nc.scalar.activation(v[:, n0 % 2, t, :, 0:dh],
                                     ps[:, V_BANK, 0:D].rearrange("p (h w) -> p h w", h=heads),
                                     ACT.Copy).then_inc(v1_ready, 1)

            def second(i, g, n0, t):
                at = (g * NCH + n0) * TPC + t
                act.wait_ge(rest_ready, i * (2 * TPC) + (at + 1 + RING))
                nc.scalar.activation(v[:, n0 % 2, t, :, dh + 1:2 * dh + 1],
                                     vrest[:, at % 2].rearrange("p (h w) -> p h w", h=heads),
                                     ACT.Copy).then_inc(v2_ready, 1)

            def probs(i, g, n0, t):
                for u in range(units):
                    at = (g * NCH + n0) * CU + t * units + u
                    tile = ((g * NCH + n0) * TPC + t) % 2
                    src = ps[:, 2 * (at % 2):2 * (at % 2) + 2, :].rearrange("p a n -> p (a n)")[:, 0:UW]
                    act.wait_ge(st_full, i * (2 * CU) + (at + 1))
                    act.wait_ge(plo_ready, i * (2 * CU) + (at + 1))
                    nc.scalar.activation(p32[:, at % 2], src, ACT.Exp).then_inc(p32_ready, 1)
                    nc.scalar.activation(phi[:, tile, u * UW:(u + 1) * UW], src, ACT.Exp).then_inc(phi_ready, 1)

            for g in range(groups):
                load0 = 2 * g * NCH
                if g == 0:
                    for b in range(2):
                        upper(0, b, None, 0)

                def body_a(i, b):
                    for hb in range(4):
                        if hb == 2:
                            upper(i, load0 + b + 2, k_in_psum, i * 8 + 4 * (load0 + b + 1))
                        key(i, g, load0 + b + 1, hb, 6 + hb % 2)

                for hb in range(4):
                    key(0, g, load0, hb, 6 + hb % 2)
                with act.Fori(0, PAIRS - 1) as i:
                    for b in range(2):
                        body_a(i, b)
                i = PAIRS - 1
                body_a(i, 0)
                upper(i, load0 + 3, k_in_psum, i * 8 + 4 * (load0 + 2))
                load0 = (2 * g + 1) * NCH
                act.wait_ge(m3T_ready, g + 1)
                act.dma_start(m3_dram[:, :], m3T[:]).then_inc(m3_stored, 16)
                for hb in range(4):
                    key(0, g, load0, hb, K_BANK)
                act.wait_ge(m3_stored, 16 * (g + 1))
                act.dma_start(m3row[:], m3_dram.rearrange("(k h) q -> k (h q)", k=3)).then_inc(m3_rows, 16)
                for t in range(TPC):
                    first(0, g, 0, t)
                    second(0, g, 0, t)
                probs(0, g, 0, 0)

                def body_b(i, b, split, project):
                    for t in range(TPC):
                        if split and t == AHEAD:
                            upper(i, load0 + b + 2, v_in_psum, i * (2 * TPC) + TPC * (g * NCH + b + 1))
                        if project:
                            if t < 4:
                                key(i, g, load0 + b + 1, t, K_BANK)
                            first(i, g, b + 1, t)
                        if t + 1 < TPC:
                            probs(i, g, b, t + 1)
                        elif project:
                            probs(i, g, b + 1, 0)
                        if project:
                            second(i, g, b + 1, t)

                with act.Fori(0, PAIRS - 1) as i:
                    for b in range(2):
                        body_b(i, b, True, True)
                body_b(PAIRS - 1, 0, g + 1 < groups, True)
                body_b(PAIRS - 1, 1, g + 1 < groups, False)

        @block.vector
        def _(dve):
            chain = Chain(dve, chain_sem)
            chain(nc.vector.memset(ones3[:], 1.0))
            chain(nc.vector.memset(zeros3[:], 0.0))
            chain(nc.vector.memset(v[:, :, :, :, dh:dh + 1].rearrange("p a t h w -> p (a t h) w"), 1.0))
            norm.vector(dve, chain)

            def key_rest(i, g, n0, hb):
                hf, cols = hb // 2, slice((hb % 2) * BLK, (hb % 2 + 1) * BLK)
                load = (2 * g + 1) * NCH + n0
                dve.wait_ge(khi_ready, i * 8 + (4 * load + hb + 1 + RING))
                nc.vector.scalar_tensor_tensor(klo[:, n0 % 2, hf, cols], ps[:, K_BANK, 0:BLK], bk(g, hf),
                                               khi[:, n0 % 2, hf, cols].bitcast(F32), ALU.add,
                                               ALU.subtract).then_inc(klo_ready, 1)

            def value_rest(i, g, n0, t):
                at = (g * NCH + n0) * TPC + t
                dve.wait_ge(v1_ready, i * (2 * TPC) + (at + 1))
                dve.wait_ge(v_ready, i * (2 * TPC) + (at + 1))
                nc.vector.tensor_tensor(vrest[:, at % 2].rearrange("p (h w) -> p h w", h=heads),
                                        ps[:, V_BANK, 0:D].rearrange("p (h w) -> p h w", h=heads),
                                        v[:, n0 % 2, t, :, 0:dh], ALU.subtract).then_inc(rest_ready, 1)

            def prob_rest(i, g, n0, t):
                for u in range(units):
                    at = (g * NCH + n0) * CU + t * units + u
                    tile = ((g * NCH + n0) * TPC + t) % 2
                    cols = slice(u * UW, (u + 1) * UW)
                    dve.wait_ge(phi_ready, i * (2 * CU) + (at + 1 + RING))
                    nc.vector.tensor_tensor(plo[:, tile, cols], p32[:, at % 2], phi[:, tile, cols],
                                            ALU.subtract).then_inc(plo_ready, 1)

            for g in range(groups):
                for hi, lo, w in ((wkh, wkl, wk), (wvh, wvl, wv)):
                    for k in range(DT):
                        last = split(nc, hi[:, k], lo[:, k], w(g, k), chain)
                    if w is wk:
                        chain(last)
                last.then_inc(weights_split, 1)
                chain(nc.vector.memset(run_max[:], -3.0e38))
                dve.wait_ge(q_in_psum, g + 1)
                for k in range(DT):
                    last = nc.vector.tensor_scalar(qT[:, k, :], ps[:, 4, k * P:(k + 1) * P], bq(g, k), scale,
                                                   ALU.add, ALU.mult)
                chain(last)
                mask = core.constant(f"head{dh}")
                for k in range(DT):
                    wide = p32[:, 0, 0:hq].rearrange("p (j q) -> p j q", j=per)
                    chain(nc.vector.tensor_tensor(wide, qT[:, k, :].unsqueeze(1).to_broadcast([P, per, P]),
                                                  mask.unsqueeze(2).to_broadcast([P, per, P]), ALU.mult))
                    last = split(nc, qh[:, k], ql[:, k], p32[:, 0, 0:hq], chain)
                    if k == 0:
                        chain(last)
                last.then_inc(q_ready, 1)
                with dve.Fori(0, PAIRS) as i:
                    for b in range(2):
                        for h in range(heads):
                            at = (g * NCH + b) * heads + h
                            dve.wait_ge(s_full, i * (2 * heads) + (at + 1))
                            bank = 2 * (at % 2)
                            nc.vector.tensor_reduce(chunk_max[:, b, h:h + 1], ps[:, bank:bank + 2, 0:BLK],
                                                    AX.XY, ALU.max).then_inc(s_free, 1)
                        dve.wait_ge(s_free, i * (2 * heads) + ((g * NCH + b + 1) * heads + RING))
                        if b:
                            dve.wait_ge(max_step, i * 2 + (g * NCH + 1))
                        nc.vector.tensor_tensor(run_max[:], run_max[:], chunk_max[:, b], ALU.max).then_inc(
                            max_step, 1)
                        if b:
                            dve.wait_ge(max_step, i * 2 + (g * NCH + 2))
                chain(nc.vector.tensor_scalar(neg[:, 0], run_max[:], -1.0, P_SHIFT, ALU.mult, ALU.add))
                for k in range(3):
                    chain(nc.vector.tensor_copy(m3b[:, k], neg[:, k % 2]))
                    if k < 2:
                        chain(nc.vector.tensor_tensor(neg[:, (k + 1) % 2], neg[:, k % 2], m3b[:, k],
                                                      ALU.subtract))
                nc.vector.tensor_copy(m3f[:], m3b[:].rearrange("p a h -> p (a h)")).then_inc(neg_ready, 1)
                dve.wait_ge(m3_in_psum, g + 1)
                nc.vector.tensor_copy(m3T[:], ps[0:3 * heads, 5, 0:P]).then_inc(m3T_ready, 1)
                for hb in range(4):
                    key_rest(0, g, 0, hb)
                for t in range(TPC):
                    value_rest(0, g, 0, t)
                prob_rest(0, g, 0, 0)

                def body_b(i, b, project):
                    for t in range(TPC):
                        if project:
                            if t < 4:
                                key_rest(i, g, b + 1, t)
                            value_rest(i, g, b + 1, t)
                        if t + 1 < TPC:
                            prob_rest(i, g, b, t + 1)
                        elif project:
                            prob_rest(i, g, b + 1, 0)

                with dve.Fori(0, PAIRS - 1) as i:
                    for b in range(2):
                        body_b(i, b, True)
                body_b(PAIRS - 1, 0, True)
                body_b(PAIRS - 1, 1, False)
                dve.wait_ge(pv_done, (g + 1) * NCH * CU)
                chain(nc.vector.tensor_copy(oa[:].rearrange("p (a j) w -> p a (j w)", a=DT), ps[:, 4:6, 0:BW]))
                o3 = o[:].rearrange("p (h w) -> p h w", h=heads)
                nc.vector.reciprocal(rden[:], oa[:, :, dh:dh + 1])
                chain(nc.vector.tensor_tensor(o3, oa[:, :, 0:dh], oa[:, :, dh + 1:2 * dh + 1], ALU.add))
                chain(nc.vector.tensor_tensor(o3, o3, oa[:, :, 2 * dh + 1:HW], ALU.add))
                last = nc.vector.tensor_tensor(o3, o3, rden[:].to_broadcast([P, heads, dh]), ALU.mult)
                if bv is not None:
                    chain(last)
                    last = nc.vector.tensor_tensor(o[:], o[:], bv(g), ALU.add)
                last.then_inc(o_ready, 1)
                dve.wait_ge(oT_in_psum, g + 1)
                nc.vector.tensor_copy(oT[:].rearrange("p k t -> p (k t)"), ps[:, 4, 0:D]).then_inc(oT_ready, 1)
                dve.wait_ge(y_in_psum, g + 1)
                chain(nc.vector.tensor_tensor(core.x[:], core.x[:], ps[:, 5, 0:D], ALU.add))
                if bo is not None and g == 0:
                    chain(nc.vector.tensor_tensor(core.x[:], core.x[:], bo, ALU.add))

        @block.tensor
        def _(pe):
            norm.tensor(pe)

            def products(out, pairs):
                for n, (lhsT, rhs) in enumerate(pairs):
                    last = nc.tensor.matmul(out, lhsT, rhs, start=(n == 0), stop=(n == len(pairs) - 1))
                return last

            def key_upper(i, load, hb):
                b = load % 2
                hf, cols = slice((hb // 2) * P, (hb // 2 + 1) * P), slice((hb % 2) * BLK, (hb % 2 + 1) * BLK)
                if hb == 0:
                    pe.wait_ge(hi_ready, i * 2 + (load + 1))
                pe.wait_ge(khi_ready, i * 8 + (4 * load + hb + 1))
                products(ps[:, 6 + hb % 2, 0:BLK],
                         [(wkh[:, k, hf], chi[:, b, k, cols]) for k in range(DT)]).then_inc(k_in_psum, 1)

            def score_upper(i, g, n0, h):
                at = (g * NCH + n0) * heads + h
                pe.wait_ge(s_free, i * (2 * heads) + (at + 1))
                for blk in range(2):
                    last = nc.tensor.matmul(ps[:, 2 * (at % 2) + blk, 0:BLK],
                                            qh[:, h // per, (h % per) * P:(h % per + 1) * P],
                                            khi[:, n0 % 2, h // per, blk * BLK:(blk + 1) * BLK],
                                            start=True, stop=True)
                last.then_inc(s_full, 1)

            def key(i, g, n0, hb):
                b = n0 % 2
                hf, cols = slice((hb // 2) * P, (hb // 2 + 1) * P), slice((hb % 2) * BLK, (hb % 2 + 1) * BLK)
                if hb == 0:
                    pe.wait_ge(lo_ready, i * 2 + (g * NCH + n0 + 1))
                if g or n0 or hb:
                    pe.wait_ge(klo_ready, i * 8 + (4 * (g * NCH + n0) + hb))
                pairs = []
                for k in range(DT):
                    pairs += [(wkh[:, k, hf], chi[:, b, k, cols]), (wkl[:, k, hf], chi[:, b, k, cols]),
                              (wkh[:, k, hf], clo[:, b, k, cols])]
                products(ps[:, K_BANK, 0:BLK], pairs).then_inc(k_in_psum, 1)

            def value(i, g, n0, t):
                at = (g * NCH + n0) * TPC + t
                b = n0 % 2
                rows = slice(t * P, (t + 1) * P)
                pe.wait_ge(rest_ready, i * (2 * TPC) + (at + RING))
                pairs = []
                for k in range(DT):
                    pairs += [(chi[:, b, k, rows], wvh[:, k]), (clo[:, b, k, rows], wvh[:, k]),
                              (chi[:, b, k, rows], wvl[:, k])]
                products(ps[:, V_BANK, 0:D], pairs).then_inc(v_in_psum, 1)

            def scores(i, g, n0, t):
                b = n0 % 2
                if t == 0:
                    pe.wait_ge(klo_ready, i * 8 + 4 * (g * NCH + n0 + 1))
                for u in range(units):
                    at = (g * NCH + n0) * CU + t * units + u
                    pe.wait_ge(phi_ready, i * (2 * CU) + (at + 1))
                    slot = 2 * (at % 2)
                    flat = ps[:, slot:slot + 2, :].rearrange("p a n -> p (a n)")
                    for c0 in range(0, UW, 512):
                        nc.tensor.matmul(flat[:, c0:c0 + 512], ones3[:], m3row[:, u * UW + c0:u * UW + c0 + 512],
                                         start=True, stop=False, skip_group_check=True)
                    keys_of = slice(t * P, (t + 1) * P)
                    for k in range(DT) if units == 1 else [u]:
                        for kk, qq in ((khi, qh), (klo, qh), (khi, ql)):
                            for c0 in range(0, hq, 512):
                                w = min(512, hq)
                                at0 = c0 + (k * hq if units == 1 else 0)
                                last = nc.tensor.matmul(flat[:, at0:at0 + w], kk[:, b, k, keys_of],
                                                        qq[:, k, c0:c0 + w], start=False, stop=True,
                                                        skip_group_check=True)
                    last.then_inc(st_full, 1)

            def sums(i, g, n0, t):
                b = n0 % 2
                at = (g * NCH + n0) * TPC + t
                pe.wait_ge(v_ready, i * (2 * TPC) + (at + 1 + RING))
                for u in range(units):
                    pe.wait_ge(plo_ready, i * (2 * CU) + (at * units + u + 1 + RING))
                    for h in range(u * heads // units, (u + 1) * heads // units):
                        out = ps[:, 4 + h // per, (h % per) * HW:(h % per + 1) * HW]
                        nc.tensor.matmul(out, phi[:, at % 2, h * P:(h + 1) * P], v[:, b, t, h, :],
                                         start=False, stop=True, skip_group_check=True)
                        last = nc.tensor.matmul(out[:, 0:2 * dh + 1], plo[:, at % 2, h * P:(h + 1) * P],
                                                v[:, b, t, h, 0:2 * dh + 1], start=False, stop=True,
                                                skip_group_check=True)
                    last.then_inc(pv_done, 1)

            for g in range(groups):
                pe.wait_ge(norm.xT_ready, 1)
                if g:
                    pe.wait_ge(oT_ready, g)
                for hf in range(DT):
                    last = products(ps[:, 4, hf * P:(hf + 1) * P],
                                    [(wq(g, k, hf), norm.xnT[:, k, :]) for k in range(DT)])
                last.then_inc(q_in_psum, 1)
                pe.wait_ge(weights_split, g + 1)
                load0 = 2 * g * NCH

                def body_a(i, b, project):
                    pe.wait_ge(khi_ready, i * 8 + (4 * (load0 + b + 1) + RING))
                    for h in range(heads):
                        if project and h % (heads // 4) == 0:
                            key_upper(i, load0 + b + 1, h // (heads // 4))
                        score_upper(i, g, b, h)

                for hb in range(4):
                    key_upper(0, load0, hb)
                pe.wait_ge(q_ready, g + 1)
                with pe.Fori(0, PAIRS - 1) as i:
                    for b in range(2):
                        body_a(i, b, True)
                body_a(PAIRS - 1, 0, True)
                body_a(PAIRS - 1, 1, False)
                pe.wait_ge(hi_ready, (2 * g + 1) * NCH + 1)
                key(0, g, 0, 0)
                pe.wait_ge(neg_ready, g + 1)
                nc.tensor.transpose(ps[0:3 * heads, 5, 0:P], m3f[:], ident).then_inc(m3_in_psum, 1)
                for hb in range(1, 4):
                    key(0, g, 0, hb)
                for t in range(TPC):
                    value(0, g, 0, t)
                pe.wait_ge(m3_rows, 16 * (g + 1))
                for bank in (4, 5):
                    nc.tensor.matmul(ps[:, bank, 0:BW], zeros3[:], m3row[:, 0:BW], start=True, stop=False,
                                     skip_group_check=True)
                scores(0, g, 0, 0)

                def body_b(i, b, project):
                    for t in range(TPC):
                        if project:
                            if t < 4:
                                key(i, g, b + 1, t)
                            value(i, g, b + 1, t)
                        if t + 1 < TPC:
                            scores(i, g, b, t + 1)
                        elif project:
                            scores(i, g, b + 1, 0)
                        sums(i, g, b, t)

                with pe.Fori(0, PAIRS - 1) as i:
                    for b in range(2):
                        body_b(i, b, True)
                body_b(PAIRS - 1, 0, True)
                body_b(PAIRS - 1, 1, False)
                pe.wait_ge(o_ready, g + 1)
                for k in range(DT):
                    last = nc.tensor.transpose(ps[:, 4, k * P:(k + 1) * P], o[:, k * P:(k + 1) * P], ident)
                last.then_inc(oT_in_psum, 1)
                pe.wait_ge(oT_ready, g + 1)
                products(ps[:, 5, 0:D], [(oT[:, k, :], wo(g, k)) for k in range(DT)]).then_inc(y_in_psum, 1)



class RowSoftmax:

    def __init__(self, core, scope, heads, width, per_bank, scale, mask):
        self.nc, self.ps, self.ident = core.nc, core.psum, core.ident()
        self.heads, self.width, self.per_bank, self.scale, self.mask = heads, width, per_bank, scale, mask
        self.p = scope.sb("p", [P, heads, width])
        self.top = scope.sb("top", [P, heads])
        self.pT = scope.sb("pT", [P, heads, P])
        self.s_in_psum, self.shifted, self.exp_done, self.p_ready, self.pT_in_psum, self.pT_ready = scope.signals(
            "s_in_psum shifted exp_done p_ready pT_in_psum pT_ready")

    def bc(self, a, width):
        return a.unsqueeze(2).to_broadcast([P, self.heads, width])

    def vector(self, dve, chain):
        nc = self.nc
        dve.wait_ge(self.s_in_psum, 1)
        for h in range(0, self.heads, self.per_bank):
            n = min(self.per_bank, self.heads - h)
            src = self.ps[:, h // self.per_bank, 0:n * self.width].rearrange("p (h c) -> p h c", h=n)
            last = nc.vector.scalar_tensor_tensor(self.p[:, h:h + n], src, self.scale,
                                                  self.mask.unsqueeze(1).to_broadcast([P, n, self.width]),
                                                  ALU.mult, ALU.add)
        chain(last)
        chain(nc.vector.tensor_reduce(self.top[:], self.p[:], AX.X, ALU.max))
        nc.vector.tensor_tensor(self.p[:], self.p[:], self.bc(self.top[:], self.width), ALU.subtract).then_inc(
            self.shifted, 1)
        dve.wait_ge(self.exp_done, 1)
        chain(nc.vector.tensor_reduce(self.top[:], self.p[:], AX.X, ALU.add))
        chain(nc.vector.reciprocal(self.top[:], self.top[:]))
        nc.vector.tensor_tensor(self.p[:], self.p[:], self.bc(self.top[:], self.width), ALU.mult).then_inc(
            self.p_ready, 1)
        dve.wait_ge(self.pT_in_psum, 1)
        for b in range(0, self.heads // 4, 2):
            last = nc.vector.tensor_copy(self.pT[:, 4 * b:4 * b + 8].rearrange("p h q -> p (h q)"),
                                         self.ps[:, b:b + 2, :].rearrange("p b n -> p (b n)"))
        last.then_inc(self.pT_ready, 1)

    def scalar(self, act):
        act.wait_ge(self.shifted, 1)
        flat = self.p[:].rearrange("p h c -> p (h c)")
        self.nc.scalar.activation(flat, flat, ACT.Exp).then_inc(self.exp_done, 1)

    def tensor(self, pe):
        pe.wait_ge(self.p_ready, 1)
        for h in range(self.heads):
            last = self.nc.tensor.transpose(self.ps[:, h // 4, (h % 4) * P:(h % 4 + 1) * P],
                                            self.p[:, h, 0:P], self.ident)
        last.then_inc(self.pT_in_psum, 1)


def transposed(nc, ps, bank, src, tiles, ident, signal):
    for k in range(tiles):
        last = nc.tensor.transpose(ps[:, bank + k // 4, (k % 4) * P:(k % 4 + 1) * P],
                                   src[:, k * P:(k + 1) * P], ident)
    last.then_inc(signal, 1)


def projected(nc, out, xT, w, tiles, signal, start=True):
    for k in range(tiles):
        last = nc.tensor.matmul(out, xT[:, k, :], w[:, k], start=(k == 0), stop=(k == tiles - 1))
    if signal is not None:
        last.then_inc(signal, 1)


def l0_attn(core):
    nc, ps, ident = core.nc, core.psum, core.ident()
    H, DH = 16, 64
    with Scope(core, "l0a") as s:
        outer = Norm(core, s)
        inner = Norm(core, s, outer.xn[:], core.weight("gamma"), "inner")
        order = [h for n in range(2) for h in range(n, H, 2)]
        soft = RowSoftmax(core, s, H, P + 2, 2, 8.0, core.constant("prefix_mask"))
        q, sq, qT = s.sb("q", [P, H, DH]), s.sb("sq", [P, H, DH]), s.sb("qT", [P, 8, P])
        k, v = s.sb("k", [P, DH]), s.sb("v", [P, DH])
        kk, nk = s.sb("kk", [P, 2, DH]), s.sb("nk", [2, 2, DH])
        kT = s.sb("kT", [P, P + 2])
        ss, rn = s.sb("ss", [P, H + 2]), s.sb("rn", [P, H + 2])
        pn, pnT = s.sb("pn", [P, 2 * H]), s.sb("pnT", [2 * H, P])
        o, oT = s.sb("o", [P, H * DH]), s.sb("oT", [P, 8, P])
        (chain_sem, kv_in_psum, q_in_psum, squares, norms, qk_ready, qkT_in_psum, qkT_ready, pn_ready,
         pnT_in_psum, pnT_ready, o_in_psum, o_ready, oT_in_psum, oT_ready, y_in_psum) = s.signals(
            "chain_sem kv_in_psum q_in_psum squares norms qk_ready qkT_in_psum qkT_ready pn_ready "
            "pnT_in_psum pnT_ready o_in_psum o_ready oT_in_psum oT_ready y_in_psum")
        block = s.ctx.enter_context(nc.Block())

        @block.vector
        def _(dve):
            chain = Chain(dve, chain_sem)
            outer.vector(dve, chain)
            inner.vector(dve, chain)
            null_k = core.weight("null_k")[0:2, :]
            chain(nc.vector.memset(ss[:], 1.0))
            dve.wait_ge(kv_in_psum, 1)
            nc.vector.tensor_copy(k[:], ps[:, 0, 0:DH])
            chain(nc.vector.tensor_copy(v[:], ps[:, 0, DH:2 * DH]))
            dve.wait_ge(q_in_psum, 1)
            chain(nc.vector.tensor_copy(q[:].rearrange("p h d -> p (h d)"),
                                        ps[:, 1:3, :].rearrange("p b n -> p (b n)")))
            chain(nc.vector.tensor_tensor(sq[:], q[:], q[:], ALU.mult))
            chain(nc.vector.tensor_reduce(ss[:, 0:H], sq[:], AX.X, ALU.add))
            chain(nc.vector.tensor_tensor(sq[:, 0], k[:], k[:], ALU.mult))
            chain(nc.vector.tensor_reduce(ss[:, H:H + 1], sq[:, 0], AX.X, ALU.add))
            chain(nc.vector.tensor_tensor(sq[0:2, 1], null_k, null_k, ALU.mult))
            nc.vector.tensor_reduce(ss[0:2, H + 1:H + 2], sq[0:2, 1], AX.X, ALU.add).then_inc(squares, 1)
            dve.wait_ge(norms, 1)
            chain(nc.vector.tensor_scalar(rn[:], rn[:], 1e-12, None, ALU.max))
            chain(nc.vector.reciprocal(rn[:], rn[:]))
            chain(nc.vector.tensor_tensor(q[:], q[:], rn[:, 0:H].unsqueeze(2).to_broadcast([P, H, DH]), ALU.mult))
            nc.vector.tensor_tensor(q[:], q[:], core.weight("qs").unsqueeze(1).to_broadcast([P, H, DH]), ALU.mult)
            for n in range(2):
                nc.vector.scalar_tensor_tensor(kk[:, n], k[:], rn[:, H:H + 1], core.weight("ks"), ALU.mult, ALU.mult)
                last = nc.vector.scalar_tensor_tensor(nk[:, n], null_k, rn[0:2, H + 1:H + 2],
                                                      core.weight("ks")[0:2, :], ALU.mult, ALU.mult)
            last.then_inc(qk_ready, 1)
            dve.wait_ge(qkT_in_psum, 1)
            nc.vector.tensor_copy(qT[:].rearrange("p t n -> p (t n)"), ps[:, 0:2, :].rearrange("p b n -> p (b n)"))
            nc.vector.tensor_copy(kT[:], ps[:, 3, 0:P + 2]).then_inc(qkT_ready, 1)
            soft.vector(dve, chain)
            nc.vector.tensor_copy(pn[:].rearrange("p (h n) -> p h n", h=H), soft.p[:, :, P:P + 2]).then_inc(
                pn_ready, 1)
            dve.wait_ge(pnT_in_psum, 1)
            nc.vector.tensor_copy(pnT[:], ps[0:2 * H, 4, 0:P]).then_inc(pnT_ready, 1)
            dve.wait_ge(o_in_psum, 1)
            nc.vector.tensor_copy(o[:], ps[:, 5:7, :].rearrange("p b n -> p (b n)")).then_inc(o_ready, 1)
            dve.wait_ge(oT_in_psum, 1)
            nc.vector.tensor_copy(oT[:].rearrange("p t n -> p (t n)"),
                                  ps[:, 0:2, :].rearrange("p b n -> p (b n)")).then_inc(oT_ready, 1)
            dve.wait_ge(y_in_psum, 1)
            nc.vector.tensor_tensor(core.x[:], core.x[:], ps[:, 2, 0:D], ALU.add)

        @block.scalar
        def _(act):
            outer.scalar(act)
            inner.scalar(act)
            act.wait_ge(squares, 1)
            nc.scalar.activation(rn[:], ss[:], ACT.Sqrt).then_inc(norms, 1)
            soft.scalar(act)

        @block.tensor
        def _(pe):
            outer.tensor(pe)
            pe.wait_ge(outer.xT_ready, 1)
            projected(nc, ps[:, 0, 0:2 * DH], outer.xnT, core.kxn("akv"), DT, kv_in_psum)
            inner.tensor(pe)
            pe.wait_ge(inner.xT_ready, 1)
            wq = core.kxn("aq")
            for n in range(2):
                projected(nc, ps[:, 1 + n, :], inner.xnT, wq[:, :, n * 512:(n + 1) * 512], DT,
                          q_in_psum if n else None)
            pe.wait_ge(qk_ready, 1)
            for t in range(8):
                nc.tensor.transpose(ps[:, t // 4, (t % 4) * P:(t % 4 + 1) * P],
                                    q[:].rearrange("p h d -> p (h d)")[:, t * P:(t + 1) * P], ident)
            nc.tensor.transpose(ps[:, 3, 0:P], kk[:].rearrange("p n d -> p (n d)"), ident)
            nc.tensor.transpose(ps[:, 3, P:P + 2], nk[:].rearrange("p n d -> p (n d)"),
                                core.ident(2)).then_inc(qkT_in_psum, 1)
            pe.wait_ge(qkT_ready, 1)
            for n, h in enumerate(order):
                at = DH * (h % 2)
                last = nc.tensor.matmul(ps[:, n // 2, (n % 2) * (P + 2):(n % 2 + 1) * (P + 2)],
                                        qT[at:at + DH, h // 2, :], kT[at:at + DH, :], start=True, stop=True)
            last.then_inc(soft.s_in_psum, 1)
            soft.tensor(pe)
            pe.wait_ge(pn_ready, 1)
            nc.tensor.transpose(ps[0:2 * H, 4, 0:P], pn[:], ident).then_inc(pnT_in_psum, 1)
            pe.wait_ge(pnT_ready, 1)
            pe.wait_ge(soft.pT_ready, 1)
            nv = core.weight("null_v")[0:2 * H, :]
            for n in range(2):
                nc.tensor.matmul(ps[:, 5 + n, :], pnT[:], nv[:, n * 512:(n + 1) * 512], start=True, stop=False,
                                 skip_group_check=True)
                for h in range(8 * n, 8 * n + 8):
                    last = nc.tensor.matmul(ps[:, 5 + n, (h % 8) * DH:(h % 8 + 1) * DH], soft.pT[:, order.index(h), :], v[:],
                                            start=False, stop=(h % 8 == 7), skip_group_check=True)
            last.then_inc(o_in_psum, 1)
            pe.wait_ge(o_ready, 1)
            transposed(nc, ps, 0, o, 8, ident, oT_in_psum)
            pe.wait_ge(oT_ready, 1)
            projected(nc, ps[:, 2, 0:D], oT, core.kxn("ao", 8), 8, y_in_psum)


def l0_ffn(core):
    nc, ps = core.nc, core.psum
    with Scope(core, "l0f") as s:
        norm = Norm(core, s)
        mix = s.sb("mix", [P, 2, DT, P])
        omu = s.sb("omu", [P, 2 * DT])
        kact = s.sb("kact", [P, DT, P])
        r, y = s.sb("r", [P, D]), s.sb("y", [P, D])
        chain_sem, mixed, r_in_psum, k_in_psum, k_ready, r_ready, y_in_psum = s.signals(
            "chain_sem mixed r_in_psum k_in_psum k_ready r_ready y_in_psum")
        block = s.ctx.enter_context(nc.Block())

        @block.vector
        def _(dve):
            chain = Chain(dve, chain_sem)
            norm.vector(dve, chain)
            for n, mu in enumerate((core.weight("mu_r"), core.weight("mu_k"))):
                nc.vector.tensor_scalar(omu[:, 2 * n:2 * n + 2], mu, -1.0, 1.0, ALU.mult, ALU.add)
                for k in range(DT):
                    last = nc.vector.tensor_scalar(mix[:, n, k], norm.xnT[:, k], mu[:, k:k + 1], None, ALU.mult)
            chain(last)
            for n in range(2):
                for k in range(DT):
                    last = nc.vector.scalar_tensor_tensor(
                        mix[:, n, k, 1:P], norm.xnT[:, k, 0:P - 1], omu[:, 2 * n + k:2 * n + k + 1],
                        mix[:, n, k, 1:P], ALU.mult, ALU.add)
            last.then_inc(mixed, 1)
            dve.wait_ge(k_in_psum, 1)
            kflat = kact[:].rearrange("p k t -> p (k t)")
            chain(nc.vector.tensor_scalar(kflat, ps[:, 1, 0:D], 0.0, None, ALU.max))
            nc.vector.tensor_tensor(kflat, kflat, kflat, ALU.mult).then_inc(k_ready, 1)
            dve.wait_ge(y_in_psum, 1)
            dve.wait_ge(r_ready, 1)
            chain(nc.vector.tensor_tensor(y[:], ps[:, 2, 0:D], r[:], ALU.mult))
            nc.vector.tensor_tensor(core.x[:], core.x[:], y[:], ALU.add)

        @block.scalar
        def _(act):
            norm.scalar(act)
            act.wait_ge(r_in_psum, 1)
            nc.scalar.activation(r[:], ps[:, 0, 0:D], ACT.Sigmoid).then_inc(r_ready, 1)

        @block.tensor
        def _(pe):
            norm.tensor(pe)
            pe.wait_ge(mixed, 1)
            projected(nc, ps[:, 0, 0:D], mix[:, 0], core.kxn("fr"), DT, r_in_psum)
            wk = core.kxn("fk")
            for half in range(DT):
                for k in range(DT):
                    last = nc.tensor.matmul(ps[:, 1, half * P:(half + 1) * P], wk[:, k, half * P:(half + 1) * P],
                                            mix[:, 1, k], start=(k == 0), stop=(k == DT - 1))
            last.then_inc(k_in_psum, 1)
            pe.wait_ge(k_ready, 1)
            projected(nc, ps[:, 2, 0:D], kact, core.kxn("fv"), DT, y_in_psum)


def l1_attn(core):
    nc, ps, ident = core.nc, core.psum, core.ident()
    H, DK, DV, C = 4, 64, 128, 64
    with Scope(core, "l1a") as s:
        norm = Norm(core, s)
        qT, kT = s.sb("qT", [P, DT, P]), s.sb("kT", [P, DT, P])
        low = s.sb("low", [16, P])
        z, az, g = s.sb("z", [P, DT, P]), s.sb("az", [P, DT, P]), s.sb("g", [P, DT, P])
        b, eb, enb, blast = s.sb("b", [P, DT, P]), s.sb("eb", [P, DT, P]), s.sb("enb", [P, DT, P]), s.sb("bl", [P, DT, C])
        qg, kg, kh = s.sb("qg", [P, DT, P]), s.sb("kg", [P, DT, P]), s.sb("kh", [P, DT, C])
        ones = s.sb("ones", [P, C])
        v, gate, sig = s.sb("v", [P, H * DV]), s.sb("gate", [P, H * DV]), s.sb("sig", [P, H * DV])
        at = s.sb("at", [P, H, P])
        o, sq = s.sb("o", [P, H, DV]), s.sb("sq", [P, H, DV])
        ms, rms = s.sb("ms", [P, H]), s.sb("rms", [P, H])
        oT = s.sb("oT", [P, H, P])
        (chain_sem, low_in_psum, low_ready, z_in_psum, az_ready, soft_ready, b_ready, eb_ready, qk_in_psum, qk_ready,
         gates_ready, v_in_psum, v_ready, g_in_psum, g_ready, a_in_psum, a_ready, o_in_psum, ms_ready, rms_ready,
         o_ready, oT_in_psum, oT_ready, y_in_psum) = s.signals(
            "chain_sem low_in_psum low_ready z_in_psum az_ready soft_ready b_ready eb_ready qk_in_psum qk_ready "
            "gates_ready v_in_psum v_ready g_in_psum g_ready a_in_psum a_ready o_in_psum ms_ready rms_ready "
            "o_ready oT_in_psum oT_ready y_in_psum")
        flat = lambda t: t[:].rearrange("p k t -> p (k t)")
        block = s.ctx.enter_context(nc.Block())

        @block.vector
        def _(dve):
            chain = Chain(dve, chain_sem)
            norm.vector(dve, chain)
            chain(nc.vector.memset(ones[:], 1.0))
            dve.wait_ge(low_in_psum, 1)
            nc.vector.tensor_copy(low[:], ps[0:16, 0, 0:P]).then_inc(low_ready, 1)
            dve.wait_ge(z_in_psum, 1)
            for k in range(DT):
                last = nc.vector.tensor_scalar(z[:, k], ps[:, 1, k * P:(k + 1) * P], core.weight("gkb")[:, k:k + 1],
                                               None, ALU.add)
            chain(last)
            chain(nc.vector.tensor_scalar(az[:], z[:], -1.0, None, ALU.mult))
            nc.vector.tensor_tensor(az[:], az[:], z[:], ALU.min).then_inc(az_ready, 1)
            dve.wait_ge(az_ready, 1)
            chain(nc.vector.tensor_scalar(z[:], z[:], 0.0, None, ALU.min))
            dve.wait_ge(soft_ready, 1)
            chain(nc.vector.tensor_tensor(g[:], z[:], az[:], ALU.subtract))
            chain(nc.vector.tensor_scalar(g[:], g[:], 1.0 / 16.0, None, ALU.mult))
            for k in range(DT):
                for c in range(2):
                    last = nc.vector.tensor_tensor_scan(b[:, k, c * C:(c + 1) * C], ones[:],
                                                        g[:, k, c * C:(c + 1) * C], 0.0, ALU.mult, ALU.add)
            chain(last)
            for k in range(DT):
                last = nc.vector.tensor_scalar(blast[:, k], b[:, k, 0:C], -1.0, b[:, k, C - 1:C], ALU.mult, ALU.add)
            last.then_inc(b_ready, 1)
            dve.wait_ge(qk_in_psum, 1)
            chain(nc.vector.tensor_copy(flat(kT), ps[:, 3, 0:D]))
            dve.wait_ge(eb_ready, 1)
            chain(nc.vector.scalar_tensor_tensor(flat(qg), ps[:, 2, 0:D], DK ** -0.5, flat(eb), ALU.mult, ALU.mult))
            nc.vector.tensor_tensor(kg[:], kT[:], enb[:], ALU.mult)
            nc.vector.tensor_tensor(kh[:], kT[:, :, 0:C], blast[:], ALU.mult).then_inc(gates_ready, 1)
            dve.wait_ge(a_in_psum, 1)
            mask = core.constant("chunk_mask").unsqueeze(1).to_broadcast([P, 2, P])
            for n in range(2):
                last = nc.vector.tensor_tensor(at[:, n:H:2], ps[:, n, 0:2 * P].rearrange("p (h t) -> p h t", h=2),
                                               mask, ALU.mult)
            chain(last)
            for n in range(2):
                last = nc.vector.tensor_copy(at[0:C, n:H:2, C:P],
                                             ps[0:C, 2 + n, 0:2 * C].rearrange("p (h t) -> p h t", h=2))
            last.then_inc(a_ready, 1)
            dve.wait_ge(o_in_psum, 1)
            chain(nc.vector.tensor_copy(o[:].rearrange("p h d -> p (h d)"), ps[:, 6, :]))
            chain(nc.vector.tensor_tensor(sq[:], o[:], o[:], ALU.mult))
            chain(nc.vector.tensor_reduce(ms[:], sq[:], AX.X, ALU.add))
            nc.vector.tensor_scalar(ms[:], ms[:], 1.0 / DV, 1e-5, ALU.mult, ALU.add).then_inc(ms_ready, 1)
            dve.wait_ge(rms_ready, 1)
            chain(nc.vector.reciprocal(rms[:], rms[:]))
            chain(nc.vector.tensor_tensor(o[:], o[:], rms[:].unsqueeze(2).to_broadcast([P, H, DV]), ALU.mult))
            chain(nc.vector.tensor_tensor(o[:], o[:], core.weight("gn").unsqueeze(1).to_broadcast([P, H, DV]),
                                          ALU.mult))
            dve.wait_ge(g_ready, 2)
            oflat = o[:].rearrange("p h d -> p (h d)")
            chain(nc.vector.tensor_tensor(oflat, oflat, gate[:], ALU.mult))
            nc.vector.tensor_tensor(oflat, oflat, sig[:], ALU.mult).then_inc(o_ready, 1)
            dve.wait_ge(oT_in_psum, 1)
            nc.vector.tensor_copy(oT[:].rearrange("p h t -> p (h t)"), ps[:, 2, :]).then_inc(oT_ready, 1)
            dve.wait_ge(y_in_psum, 1)
            nc.vector.tensor_tensor(core.x[:], core.x[:], ps[:, 3, 0:D], ALU.add)

        @block.scalar
        def _(act):
            chain = Chain(act, qk_ready)
            norm.scalar(act)
            act.wait_ge(az_ready, 1)
            chain(nc.scalar.activation(az[:], az[:], ACT.Exp))
            nc.scalar.activation(az[:], az[:], ACT.Ln, bias=core.constant("one")).then_inc(soft_ready, 1)
            act.wait_ge(v_in_psum, 1)
            nc.scalar.activation(v[:], ps[:, 4, :], ACT.Copy).then_inc(v_ready, 1)
            act.wait_ge(g_in_psum, 1)
            nc.scalar.activation(gate[:], ps[:, 5, :], ACT.Copy).then_inc(g_ready, 1)
            act.wait_ge(b_ready, 1)
            chain(nc.scalar.activation(flat(eb), flat(b), ACT.Exp))
            nc.scalar.activation(flat(enb), flat(b), ACT.Exp, scale=-1.0)
            nc.scalar.activation(blast[:].rearrange("p k t -> p (k t)"), blast[:].rearrange("p k t -> p (k t)"),
                                 ACT.Exp).then_inc(eb_ready, 1)
            nc.scalar.activation(sig[:], ps[:, 5, :], ACT.Sigmoid).then_inc(g_ready, 1)
            act.wait_ge(ms_ready, 1)
            nc.scalar.activation(rms[:], ms[:], ACT.Sqrt).then_inc(rms_ready, 1)

        @block.tensor
        def _(pe):
            norm.tensor(pe)
            pe.wait_ge(norm.xT_ready, 1)
            for k in range(DT):
                last = nc.tensor.matmul(ps[0:16, 0, 0:P], core.kxn("gk1")[:, k, :], norm.xnT[:, k, :],
                                        start=(k == 0), stop=(k == DT - 1))
            last.then_inc(low_in_psum, 1)
            for name, bank in (("gq", 2), ("gk", 3)):
                w = core.kxn(name)
                for half in range(DT):
                    for k in range(DT):
                        last = nc.tensor.matmul(ps[:, bank, half * P:(half + 1) * P],
                                                w[:, k, half * P:(half + 1) * P], norm.xnT[:, k, :],
                                                start=(k == 0), stop=(k == DT - 1))
            last.then_inc(qk_in_psum, 1)
            projected(nc, ps[:, 4, :], norm.xnT, core.kxn("gv"), DT, v_in_psum)
            projected(nc, ps[:, 5, :], norm.xnT, core.kxn("gg"), DT, g_in_psum)
            pe.wait_ge(low_ready, 1)
            for half in range(DT):
                last = nc.tensor.matmul(ps[:, 1, half * P:(half + 1) * P],
                                        core.weight("gk2")[0:16, half * P:(half + 1) * P], low[:],
                                        start=True, stop=True)
            last.then_inc(z_in_psum, 1)
            pe.wait_ge(gates_ready, 1)
            for h in range(H):
                r = slice(DK * (h % 2), DK * (h % 2) + DK)
                nc.tensor.matmul(ps[:, h % 2, (h // 2) * P:(h // 2 + 1) * P], kg[r, h // 2, :], qg[r, h // 2, :],
                                 start=True, stop=True)
            for h in range(H):
                r = slice(DK * (h % 2), DK * (h % 2) + DK)
                last = nc.tensor.matmul(ps[0:C, 2 + h % 2, (h // 2) * C:(h // 2 + 1) * C], kh[r, h // 2, :], qg[r, h // 2, C:P],
                                        start=True, stop=True)
            last.then_inc(a_in_psum, 1)
            pe.wait_ge(a_ready, 1)
            pe.wait_ge(v_ready, 1)
            for h in range(H):
                last = nc.tensor.matmul(ps[:, 6, h * DV:(h + 1) * DV], at[:, h, :], v[:, h * DV:(h + 1) * DV],
                                        start=True, stop=True)
            last.then_inc(o_in_psum, 1)
            pe.wait_ge(o_ready, 1)
            transposed(nc, ps, 2, o[:].rearrange("p h d -> p (h d)"), H, ident, oT_in_psum)
            pe.wait_ge(oT_ready, 1)
            projected(nc, ps[:, 3, 0:D], oT, core.kxn("go", 4), 4, y_in_psum)


def l0_xattn(core):
    cross_attention(core, "l0x", 16, 1, *cross_weights(core, 1), 0.25)


def l1_xattn(core):
    cross_attention(core, "l1x", 16, 1, *cross_weights(core, 1), 0.25)


def l2_xattn(core):
    cross_attention_plain(core, "l2x", 1, 1, *cross_weights(core, 1), 1.0 / 16.0)


def l3_xattn(core):
    cross_attention(core, "l3x", 4, 4, *cross_weights(core, 4), 0.125)


def cross_weights(core, groups):
    def columns(name):
        m = core.kxn(name)
        return lambda g, k, half=None: (m[:, k, g * D:(g + 1) * D] if half is None
                                        else m[:, k, g * D + half * P:g * D + (half + 1) * P])

    has = core.cols[core.layer]
    col = lambda name: (lambda g, k: core.weight(name)[:, k:k + 1]) if name in has else (
        lambda g, k: core.constant("zero")[:, 0:1])
    row = lambda name: (lambda g: core.weight(name)) if name in has else None
    wo = None
    if "xo" in has:
        rows = core.kxn("xo", DT * groups)
        wo = lambda g, k: rows[:, DT * g + k, :]
    return (columns("xq"), columns("xk"), columns("xv"), wo, col("xbq"), col("xbk"), row("xbv"),
            core.weight("xbo") if "xbo" in has else None)




def l1_ffn(core):
    nc, ps, ident = core.nc, core.psum, core.ident()
    E, G, CAP, SLOTS, INTER, AI = 32, 16, 5, 32, 512, 128
    PER = P // SLOTS
    GROUPS = E // PER
    RING = 6
    with Scope(core, "l1f") as s:
        norm = Norm(core, s)
        stats, sq = s.sb("stats", [P, 8]), s.sb("sq", [P, D])
        statsT = s.sb("statsT", [6, P])
        hT = s.sb("hT", [P, P])
        logits, probs = s.sb("logits", [P, E]), s.sb("probs", [P, E])
        top, topi, topf = s.sb("top", [P, 8]), s.sb("topi", [P, 8], U32), s.sb("topf", [P, 8])
        small = s.sb("small", [P, 4])
        hit, wc, score = s.sb("hit", [P, 2, E]), s.sb("wc", [P, E]), s.sb("score", [P, E])
        scoreT = s.sb("scoreT", [E, P])
        best, besti, bestf = s.sb("best", [E, 8]), s.sb("besti", [E, 8], U32), s.sb("bestf", [E, 8])
        pick = s.sb("pick", [E, CAP, P])
        sel, wsel = s.sb("sel", [P, E, SLOTS]), s.sb("wsel", [P, E, SLOTS])
        wmask, gw = s.sb("wmask", [P, E]), s.sb("gw", [P, G])
        xeT = s.sb("xeT", [P, DT, E * SLOTS])
        wselT = s.sb("wselT", [P, GROUPS, P])
        up = s.sb("up", [P, RING, DT, 2 * INTER])
        down = s.sb("down", [P, RING, INTER // P, D])
        sg, hact = s.sb("sg", [P, INTER]), s.sb("hact", [P, INTER])
        hactT = s.sb("hactT", [P, INTER // P, P])
        ye = s.sb("ye", [P, GROUPS, D])
        aup = s.sb("aup", [P, 2, DT, 2 * AI])
        adown = s.sb("adown", [P, 2, D])
        asg, ah = s.sb("asg", [P, 2, P]), s.sb("ah", [P, 2, P])
        acc = s.sb("acc", [P, D])
        (chain_sem, sums_ready, sqrt_ready, stats_ready, statsT_in_psum, statsT_ready, h_in_psum, h_ready,
         logits_in_psum, shifted, exp_done, score_ready, scoreT_in_psum, scoreT_ready, pick_ready, sel_in_psum,
         sel_ready, xe_in_psum, xe_ready, up_used, down_used, sig_done, hact_ready, hactT_in_psum,
         hactT_ready, ye_ready, a_in_psum, asig_done, ah_ready, ay_in_psum, ay_added,
         out_in_psum) = s.signals(
            "chain_sem sums_ready sqrt_ready stats_ready statsT_in_psum statsT_ready h_in_psum h_ready "
            "logits_in_psum shifted exp_done score_ready scoreT_in_psum scoreT_ready pick_ready sel_in_psum "
            "sel_ready xe_in_psum xe_ready up_used down_used sig_done hact_ready hactT_in_psum "
            "hactT_ready ye_ready a_in_psum asig_done ah_ready ay_in_psum ay_added out_in_psum")
        up_in = s.signals(" ".join(f"up_in{n}" for n in range(RING)))
        down_in = s.signals(" ".join(f"down_in{n}" for n in range(RING)))
        a_in = s.signals("a_in0 a_in1")
        block = s.ctx.enter_context(nc.Block())

        @block.sync
        def _(sp):
            for e in range(E):
                if e >= RING:
                    sp.wait_ge(up_used, e - RING + 1)
                sp.dma_start(up[:, e % RING], core.dram["w_up"][e]).then_inc(up_in[e % RING], 16)
                if e >= RING:
                    sp.wait_ge(down_used, e - RING + 1)
                sp.dma_start(down[:, e % RING], core.dram["w_down"][e]).then_inc(down_in[e % RING], 16)

        @block.gpsimd
        def _(pool):
            for n in range(G):
                if n >= 2:
                    pool.wait_ge(ay_in_psum, n - 1)
                pool.dma_start(aup[:, n % 2], core.dram["a_up"][n]).then_inc(a_in[n % 2], 16)
                pool.dma_start(adown[:, n % 2], core.dram["a_down"][n]).then_inc(a_in[n % 2], 16)

        @block.vector
        def _(dve):
            chain = Chain(dve, chain_sem)
            norm.vector(dve, chain)
            xn = norm.xn[:]
            chain(nc.vector.memset(stats[:], 0.0))
            chain(nc.vector.bn_stats(norm.stats[:], xn))
            chain(nc.vector.bn_aggr(norm.mv[:], norm.stats[:]))
            nc.vector.tensor_copy(stats[:, 0:1], norm.mv[:, 0:1])
            nc.vector.tensor_scalar(stats[:, 6:7], norm.mv[:, 1:2], D / (D - 1.0), None, ALU.mult)
            nc.vector.tensor_reduce(stats[:, 2:3], xn, AX.X, ALU.min)
            nc.vector.tensor_reduce(stats[:, 3:4], xn, AX.X, ALU.max)
            chain(nc.vector.tensor_tensor(sq[:], xn, xn, ALU.mult))
            nc.vector.tensor_reduce(stats[:, 7:8], sq[:], AX.X, ALU.add).then_inc(sums_ready, 1)
            dve.wait_ge(sums_ready, 1)
            chain(nc.vector.tensor_scalar(sq[:], xn, 1e-6, None, ALU.is_lt))
            chain(nc.vector.scalar_tensor_tensor(sq[:], xn, -1e-6, sq[:], ALU.is_gt, ALU.mult))
            chain(nc.vector.tensor_reduce(stats[:, 5:6], sq[:], AX.X, ALU.add))
            nc.vector.tensor_scalar(stats[:, 5:6], stats[:, 5:6], 1.0 / D, None, ALU.mult).then_inc(stats_ready, 1)
            dve.wait_ge(statsT_in_psum, 1)
            nc.vector.tensor_copy(statsT[:], ps[0:6, 0, 0:P]).then_inc(statsT_ready, 1)
            dve.wait_ge(logits_in_psum, 1)
            chain(nc.vector.tensor_reduce(small[:, 0:1], ps[:, 2, 0:E], AX.X, ALU.max))
            nc.vector.tensor_scalar(logits[:], ps[:, 2, 0:E], small[:, 0:1], None, ALU.subtract).then_inc(shifted, 1)
            dve.wait_ge(exp_done, 1)
            chain(nc.vector.tensor_reduce(small[:, 1:2], logits[:], AX.X, ALU.add))
            chain(nc.vector.reciprocal(small[:, 1:2], small[:, 1:2]))
            chain(nc.vector.tensor_scalar(probs[:], logits[:], small[:, 1:2], None, ALU.mult))
            chain(nc.vector.max(top[:], probs[:]))
            chain(nc.vector.max_index(topi[:], top[:], probs[:]))
            chain(nc.vector.tensor_copy(topf[:], topi[:]))
            chain(nc.vector.tensor_tensor(small[:, 0:1], top[:, 0:1], top[:, 1:2], ALU.add))
            chain(nc.vector.reciprocal(small[:, 0:1], small[:, 0:1]))
            for n in range(2):
                last = nc.vector.tensor_scalar(hit[:, n], core.constant("iota")[:, 0:E], topf[:, n:n + 1], None,
                                               ALU.is_equal)
            chain(last)
            chain(nc.vector.tensor_tensor(score[:], hit[:, 0], hit[:, 1], ALU.add))
            chain(nc.vector.tensor_scalar(wc[:], probs[:], small[:, 0:1], None, ALU.mult))
            chain(nc.vector.tensor_tensor(wc[:], wc[:], score[:], ALU.mult))
            chain(nc.vector.tensor_tensor(logits[:], probs[:], score[:], ALU.mult))
            chain(nc.vector.tensor_scalar(score[:], score[:], 1.0, None, ALU.subtract))
            nc.vector.tensor_tensor(score[:], score[:], logits[:], ALU.add).then_inc(score_ready, 1)
            dve.wait_ge(scoreT_in_psum, 1)
            nc.vector.tensor_copy(scoreT[:], ps[0:E, 3, 0:P]).then_inc(scoreT_ready, 1)
            dve.wait_ge(scoreT_ready, 1)
            chain(nc.vector.max(best[:], scoreT[:]))
            chain(nc.vector.max_index(besti[:], best[:], scoreT[:]))
            chain(nc.vector.tensor_copy(bestf[:], besti[:]))
            for c in range(CAP):
                last = nc.vector.tensor_scalar(pick[:, c], core.constant("iota")[0:E, :], bestf[:, c:c + 1], None,
                                               ALU.is_equal)
            last.then_inc(pick_ready, 1)
            chain(nc.vector.memset(sel[:], 0.0))
            dve.wait_ge(sel_in_psum, 1)
            chain(nc.vector.tensor_copy(sel[:, :, 0:CAP].rearrange("p e c -> p c e"),
                                        ps[:, 4, 0:CAP * E].rearrange("p (c e) -> p c e", c=CAP)))
            nc.vector.tensor_tensor(wsel[:], sel[:], wc[:].unsqueeze(2).to_broadcast([P, E, SLOTS]),
                                    ALU.mult).then_inc(sel_ready, 1)
            dve.wait_ge(sel_ready, 1)
            chain(nc.vector.tensor_reduce(wmask[:], wsel[:, :, 0:CAP], AX.X, ALU.add))
            chain(nc.vector.tensor_reduce(gw[:], wmask[:].rearrange("p (g e) -> p g e", g=G), AX.X, ALU.add))
            chain(nc.vector.tensor_scalar(gw[:], gw[:], 0.05, None, ALU.mult))
            chain(nc.vector.memset(acc[:], 0.0))
            dve.wait_ge(xe_in_psum, 1)
            nc.vector.tensor_copy(xeT[:].rearrange("p k n -> p (k n)"),
                                  ps[:, 0:4, :].rearrange("p b n -> p (b n)")).then_inc(xe_ready, 1)
            dve.wait_ge(xe_in_psum, 2)
            nc.vector.tensor_copy(wselT[:].rearrange("p g n -> p (g n)"),
                                  ps[:, 4:6, :].rearrange("p b n -> p (b n)")).then_inc(xe_ready, 1)
            for q in range(GROUPS):
                dve.wait_ge(sig_done, q + 1)
                chain(nc.vector.tensor_tensor(sg[:], sg[:], ps[:, 0, :], ALU.mult))
                if q:
                    dve.wait_ge(hactT_in_psum, q)
                nc.vector.tensor_tensor(hact[:], sg[:], ps[:, 1, :], ALU.mult).then_inc(hact_ready, 1)
                dve.wait_ge(hactT_in_psum, q + 1)
                nc.vector.tensor_copy(hactT[:].rearrange("p k n -> p (k n)"), ps[:, 2, :]).then_inc(hactT_ready, 1)
                for n in range(2 * q, 2 * q + 2):
                    dve.wait_ge(asig_done, n + 1)
                    chain(nc.vector.tensor_tensor(asg[:, n % 2], asg[:, n % 2], ps[:, 4, 0:P], ALU.mult))
                    nc.vector.tensor_tensor(ah[:, n % 2], asg[:, n % 2], ps[:, 4, P:2 * P], ALU.mult).then_inc(
                        ah_ready, 1)
                    dve.wait_ge(ay_in_psum, n + 1)
                    nc.vector.scalar_tensor_tensor(acc[:], ps[:, 5, 0:D], gw[:, n:n + 1], acc[:], ALU.mult,
                                                   ALU.add).then_inc(ay_added, 1)
                    dve.wait_ge(ay_added, n + 1)
                dve.wait_ge(down_used, PER * (q + 1))
                nc.vector.tensor_copy(ye[:, q], ps[:, 3, 0:D]).then_inc(ye_ready, 1)
            chain(nc.vector.tensor_tensor(core.x[:], core.x[:], acc[:], ALU.add))
            dve.wait_ge(out_in_psum, 1)
            nc.vector.tensor_tensor(core.x[:], core.x[:], ps[:, 7, 0:D], ALU.add)

        @block.scalar
        def _(act):
            norm.scalar(act)
            act.wait_ge(sums_ready, 1)
            nc.scalar.activation(stats[:, 1:2], stats[:, 6:7], ACT.Sqrt).then_inc(sqrt_ready, 1)
            nc.scalar.activation(stats[:, 4:5], stats[:, 7:8], ACT.Sqrt).then_inc(sqrt_ready, 1)
            act.wait_ge(h_in_psum, 1)
            nc.scalar.activation(hT[:], ps[:, 1, 0:P], ACT.Gelu, bias=core.weight("r1b")).then_inc(h_ready, 1)
            act.wait_ge(shifted, 1)
            nc.scalar.activation(logits[:], logits[:], ACT.Exp).then_inc(exp_done, 1)
            for q in range(GROUPS):
                act.wait_ge(up_used, PER * (q + 1))
                if q:
                    act.wait_ge(hact_ready, q)
                nc.scalar.activation(sg[:], ps[:, 0, :], ACT.Sigmoid).then_inc(sig_done, 1)
                for n in range(2 * q, 2 * q + 2):
                    act.wait_ge(a_in_psum, n + 1)
                    if n >= 2:
                        act.wait_ge(ah_ready, n - 1)
                    nc.scalar.activation(asg[:, n % 2], ps[:, 4, 0:P], ACT.Sigmoid).then_inc(asig_done, 1)

        @block.tensor
        def _(pe):
            norm.tensor(pe)
            pe.wait_ge(stats_ready, 1)
            pe.wait_ge(sqrt_ready, 2)
            nc.tensor.transpose(ps[0:6, 0, 0:P], stats[:, 0:6], ident).then_inc(statsT_in_psum, 1)
            pe.wait_ge(norm.xT_ready, 1)
            pe.wait_ge(statsT_ready, 1)
            r1 = core.kxn("r1")
            for k in range(DT):
                nc.tensor.matmul(ps[:, 1, 0:P], r1[:, k, :], norm.xnT[:, k, :], start=(k == 0), stop=False)
            nc.tensor.matmul(ps[:, 1, 0:P], core.weight("r1s")[0:6, :], statsT[:], start=False,
                             stop=True).then_inc(h_in_psum, 1)
            pe.wait_ge(h_ready, 1)
            nc.tensor.matmul(ps[:, 2, 0:E], hT[:], core.weight("r2"), start=True, stop=True).then_inc(
                logits_in_psum, 1)
            pe.wait_ge(score_ready, 1)
            nc.tensor.transpose(ps[0:E, 3, 0:P], score[:], ident).then_inc(scoreT_in_psum, 1)
            pe.wait_ge(pick_ready, 1)
            for c in range(CAP):
                last = nc.tensor.transpose(ps[:, 4, c * E:(c + 1) * E], pick[:, c], core.ident(E))
            last.then_inc(sel_in_psum, 1)
            pe.wait_ge(sel_ready, 1)
            flat = sel[:].rearrange("p e c -> p (e c)")
            for k in range(DT):
                for n in range(2):
                    last = nc.tensor.matmul(ps[:, 2 * k + n, :], norm.xn[:, k * P:(k + 1) * P],
                                            flat[:, n * 512:(n + 1) * 512], start=True, stop=True)
            last.then_inc(xe_in_psum, 1)
            transposed(nc, ps, 4, wsel[:].rearrange("p e c -> p (e c)"), GROUPS, ident, xe_in_psum)
            pe.wait_ge(xe_ready, 2)
            for q in range(GROUPS):
                for j in range(PER):
                    e = q * PER + j
                    pe.wait_ge(up_in[e % RING], 16 * (e // RING + 1))
                    if q and j == 0:
                        pe.wait_ge(hact_ready, q)
                    for n in range(2):
                        for k in range(DT):
                            last = nc.tensor.matmul(ps[j * SLOTS:(j + 1) * SLOTS, n, :],
                                                    xeT[:, k, e * SLOTS:(e + 1) * SLOTS],
                                                    up[:, e % RING, k, n * INTER:(n + 1) * INTER],
                                                    start=(k == 0), stop=(k == DT - 1))
                    last.then_inc(up_used, 1)
                pe.wait_ge(hact_ready, q + 1)
                if q:
                    pe.wait_ge(hactT_ready, q)
                transposed(nc, ps, 2, hact, INTER // P, ident, hactT_in_psum)
                for n in range(2 * q, 2 * q + 2):
                    pe.wait_ge(a_in[n % 2], 32 * (n // 2 + 1))
                    if n:
                        pe.wait_ge(ah_ready, n)
                    for m in range(2):
                        for k in range(DT):
                            last = nc.tensor.matmul(ps[:, 4, m * P:(m + 1) * P],
                                                    aup[:, n % 2, k, m * AI:(m + 1) * AI], norm.xnT[:, k, :],
                                                    start=(k == 0), stop=(k == DT - 1))
                    last.then_inc(a_in_psum, 1)
                    pe.wait_ge(ah_ready, n + 1)
                    if n:
                        pe.wait_ge(ay_added, n)
                    nc.tensor.matmul(ps[:, 5, 0:D], ah[:, n % 2], adown[:, n % 2], start=True,
                                     stop=True).then_inc(ay_in_psum, 1)
                pe.wait_ge(hactT_ready, q + 1)
                if q:
                    pe.wait_ge(ye_ready, q)
                for j in range(PER):
                    e = q * PER + j
                    pe.wait_ge(down_in[e % RING], 16 * (e // RING + 1))
                    for k in range(INTER // P):
                        last = nc.tensor.matmul(ps[j * SLOTS:(j + 1) * SLOTS, 3, 0:D],
                                                hactT[:, k, j * SLOTS:(j + 1) * SLOTS], down[:, e % RING, k, :],
                                                start=(k == 0), stop=(k == INTER // P - 1))
                    last.then_inc(down_used, 1)
            pe.wait_ge(ye_ready, GROUPS)
            for q in range(GROUPS):
                last = nc.tensor.matmul(ps[:, 7, 0:D], wselT[:, q, :], ye[:, q, :], start=(q == 0),
                                        stop=(q == GROUPS - 1))
            last.then_inc(out_in_psum, 1)


def rotary(nc, src, even, odd, cos, sin, tmp, chain):
    x1, x2 = src
    nc.vector.tensor_tensor(tmp[0], x1, cos, ALU.mult)
    nc.vector.tensor_tensor(tmp[1], x2, sin, ALU.mult)
    nc.vector.tensor_tensor(tmp[2], x1, sin, ALU.mult)
    chain(nc.vector.tensor_tensor(tmp[3], x2, cos, ALU.mult))
    nc.vector.tensor_tensor(even, tmp[0], tmp[1], ALU.subtract)
    return nc.vector.tensor_tensor(odd, tmp[2], tmp[3], ALU.add)


def l2_attn(core):
    nc, ps, ident = core.nc, core.psum, core.ident()
    H, KV, DH, QL, KL, PAD = 16, 4, 16, 64, 32, 32
    with Scope(core, "l2a") as s:
        norm = Norm(core, s)
        soft = RowSoftmax(core, s, H, P, 4, DH ** -0.5, core.constant("causal_mask"))
        qaT, kvaT = s.sb("qaT", [QL, P]), s.sb("kvaT", [KL, P])
        qk, v = s.sb("qk", [P, H + KV, DH]), s.sb("v", [P, KV * DH])
        tmp = s.sb("tmp", [P, 4, H + KV, DH // 2])
        rot = s.sb("rot", [P, H + KV, DH])
        qp, kp = s.sb("qp", [P, H // KV, KV, PAD]), s.sb("kp", [P, KV, PAD])
        qT, kT = s.sb("qT", [P, H // KV, P]), s.sb("kT", [P, P])
        o, oT = s.sb("o", [P, D]), s.sb("oT", [P, DT, P])
        (chain_sem, low_in_psum, low_ready, qkv_in_psum, qk_ready, qkT_in_psum, qkT_ready, o_in_psum, o_ready,
         oT_in_psum, oT_ready, y_in_psum) = s.signals(
            "chain_sem low_in_psum low_ready qkv_in_psum qk_ready qkT_in_psum qkT_ready o_in_psum o_ready "
            "oT_in_psum oT_ready y_in_psum")
        block = s.ctx.enter_context(nc.Block())

        @block.vector
        def _(dve):
            chain = Chain(dve, chain_sem)
            norm.vector(dve, chain)
            nc.vector.memset(qp[:], 0.0)
            chain(nc.vector.memset(kp[:], 0.0))
            dve.wait_ge(low_in_psum, 1)
            nc.vector.tensor_copy(qaT[:], ps[0:QL, 0, 0:P])
            nc.vector.tensor_copy(kvaT[:], ps[0:KL, 0, P:2 * P]).then_inc(low_ready, 1)
            dve.wait_ge(qkv_in_psum, 1)
            nc.vector.tensor_copy(qk[:, 0:H].rearrange("p h d -> p (h d)"), ps[:, 1, 0:D])
            nc.vector.tensor_copy(qk[:, H:].rearrange("p h d -> p (h d)"), ps[:, 2, 0:KV * DH])
            chain(nc.vector.tensor_copy(v[:], ps[:, 2, KV * DH:2 * KV * DH]))
            table = lambda n: core.constant(n).unsqueeze(1).to_broadcast([P, H + KV, DH // 2])
            chain(rotary(nc, (qk[:, :, 0::2], qk[:, :, 1::2]), rot[:, :, 0::2], rot[:, :, 1::2], table("rope_cos"),
                         table("rope_sin"), [tmp[:, n] for n in range(4)], chain))
            nc.vector.tensor_copy(qp[:, :, :, 0:DH].rearrange("p i g d -> p g i d"),
                                  rot[:, 0:H].rearrange("p (g i) d -> p g i d", g=KV))
            nc.vector.tensor_copy(kp[:, :, 0:DH], rot[:, H:]).then_inc(qk_ready, 1)
            dve.wait_ge(qkT_in_psum, 1)
            nc.vector.tensor_copy(qT[:].rearrange("p i q -> p (i q)"), ps[:, 3, :])
            nc.vector.tensor_copy(kT[:], ps[:, 4, 0:P]).then_inc(qkT_ready, 1)
            soft.vector(dve, chain)
            dve.wait_ge(o_in_psum, 1)
            nc.vector.tensor_copy(o[:], ps[:, 5, 0:D]).then_inc(o_ready, 1)
            dve.wait_ge(oT_in_psum, 1)
            nc.vector.tensor_copy(oT[:].rearrange("p k t -> p (k t)"), ps[:, 6, 0:D]).then_inc(oT_ready, 1)
            chain(nc.vector.tensor_tensor(core.x[:], core.x[:], core.weight("bout"), ALU.add))
            dve.wait_ge(y_in_psum, 1)
            nc.vector.tensor_tensor(core.x[:], core.x[:], ps[:, 4, 0:D], ALU.add)

        @block.scalar
        def _(act):
            norm.scalar(act)
            soft.scalar(act)

        @block.tensor
        def _(pe):
            norm.tensor(pe)
            pe.wait_ge(norm.xT_ready, 1)
            for k in range(DT):
                nc.tensor.matmul(ps[0:QL, 0, 0:P], core.kxn("qa")[:, k, :], norm.xnT[:, k, :], start=(k == 0),
                                 stop=(k == DT - 1))
            for k in range(DT):
                last = nc.tensor.matmul(ps[0:KL, 0, P:2 * P], core.kxn("kva")[:, k, :], norm.xnT[:, k, :],
                                        start=(k == 0), stop=(k == DT - 1))
            last.then_inc(low_in_psum, 1)
            pe.wait_ge(low_ready, 1)
            nc.tensor.matmul(ps[:, 1, 0:D], qaT[:], core.weight("qb")[0:QL, :], start=True, stop=True)
            nc.tensor.matmul(ps[:, 2, 0:2 * KV * DH], kvaT[:], core.weight("kvb")[0:KL, :], start=True,
                             stop=True).then_inc(qkv_in_psum, 1)
            pe.wait_ge(qk_ready, 1)
            for i in range(H // KV):
                nc.tensor.transpose(ps[:, 3, i * P:(i + 1) * P], qp[:, i].rearrange("p g d -> p (g d)"), ident)
            nc.tensor.transpose(ps[:, 4, 0:P], kp[:].rearrange("p g d -> p (g d)"), ident).then_inc(qkT_in_psum, 1)
            pe.wait_ge(qkT_ready, 1)
            for g in range(KV):
                for i in range(H // KV):
                    last = nc.tensor.matmul(ps[:, g, i * P:(i + 1) * P], qT[PAD * g:PAD * (g + 1), i, :],
                                            kT[PAD * g:PAD * (g + 1), :], start=True, stop=True)
            last.then_inc(soft.s_in_psum, 1)
            soft.tensor(pe)
            pe.wait_ge(soft.pT_ready, 1)
            for h in range(H):
                g = h // (H // KV)
                last = nc.tensor.matmul(ps[:, 5, h * DH:(h + 1) * DH], soft.pT[:, h, :], v[:, g * DH:(g + 1) * DH],
                                        start=True, stop=True)
            last.then_inc(o_in_psum, 1)
            pe.wait_ge(o_ready, 1)
            transposed(nc, ps, 6, o, DT, ident, oT_in_psum)
            pe.wait_ge(oT_ready, 1)
            projected(nc, ps[:, 4, 0:D], oT, core.kxn("aout"), DT, y_in_psum)


def quantised(nc, chain, src, out, blocks, top, inv, scaled):
    wide = [P, blocks, 32]
    top, inv = top[:, 0:blocks], inv[:, 0:blocks]
    chain(nc.vector.tensor_reduce(top, src, AX.X, ALU.max, apply_absolute_value=True))
    chain(nc.vector.tensor_scalar(top, top, 2.0 ** -120, None, ALU.max))
    chain(nc.vector.tensor_scalar(top.bitcast(I32), top.bitcast(I32), 0x7F800000, None, ALU.bitwise_and))
    chain(nc.vector.tensor_scalar(top, top, 0.125, None, ALU.mult))
    chain(nc.vector.reciprocal(inv, top))
    chain(nc.vector.tensor_tensor(scaled, src, inv.unsqueeze(2).to_broadcast(wide), ALU.mult))
    chain(nc.vector.tensor_scalar(scaled, scaled, 1.5 * 2.0 ** 23, None, ALU.add))
    chain(nc.vector.tensor_scalar(scaled, scaled, 1.5 * 2.0 ** 23, None, ALU.subtract))
    return nc.vector.tensor_tensor(out, scaled, top.unsqueeze(2).to_broadcast(wide), ALU.mult)


def l2_ffn(core):
    nc, ps = core.nc, core.psum
    F = 1024
    FT = F // P
    with Scope(core, "l2f") as s:
        norm = Norm(core, s)
        identb = s.sb("identb", [P, P], BF16)
        top, inv, scaled = s.sb("top", [P, 64]), s.sb("inv", [P, 64]), s.sb("scaled", [P, 64, 32])
        wfq, wpq = s.sb("wfq", [P, FT, D], BF16), s.sb("wpq", [P, DT, F], BF16)
        wfT, wpT = s.sb("wfT", [P, DT, F], BF16), s.sb("wpT", [P, FT, D], BF16)
        xq, xqT = s.sb("xq", [P, D], BF16), s.sb("xqT", [P, DT, P], BF16)
        h = s.sb("h", [P, F])
        hq, hqT = s.sb("hq", [P, F], BF16), s.sb("hqT", [P, FT, P], BF16)
        (chain_sem, wf_ready, wp_ready, wfT_in_psum, wpT_in_psum, wT_ready, xq_ready, xqT_in_psum, xqT_ready,
         h_in_psum, h_ready, gelu_done, hq_ready, hqT_in_psum, hqT_ready, y_in_psum) = s.signals(
            "chain_sem wf_ready wp_ready wfT_in_psum wpT_in_psum wT_ready xq_ready xqT_in_psum xqT_ready "
            "h_in_psum h_ready gelu_done hq_ready hqT_in_psum hqT_ready y_in_psum")
        blocks = lambda a: a.rearrange("p (b k) -> p b k", k=32)
        half_words = lambda bank, n: ps[:, bank, :].bitcast(BF16)[:, 0:n]
        block = s.ctx.enter_context(nc.Block())

        @block.vector
        def _(dve):
            chain = Chain(dve, chain_sem)
            nc.vector.tensor_copy(identb[:], core.ident())
            quantised(nc, chain, blocks(core.weight("fc")), blocks(wfq[:].rearrange("p n k -> p (n k)")), 64, top,
                      inv, scaled[:]).then_inc(wf_ready, 1)
            dve.wait_ge(wf_ready, 1)
            quantised(nc, chain, blocks(core.weight("proj")), blocks(wpq[:].rearrange("p n k -> p (n k)")), 64,
                      top, inv, scaled[:]).then_inc(wp_ready, 1)
            dve.wait_ge(wp_ready, 1)
            norm.vector(dve, chain)
            quantised(nc, chain, blocks(norm.xn[:]), blocks(xq[:]), 8, top, inv, scaled[:, 0:8]).then_inc(
                xq_ready, 1)
            dve.wait_ge(xq_ready, 1)
            dve.wait_ge(wfT_in_psum, 1)
            for k in range(DT):
                nc.vector.tensor_copy(wfT[:, k], half_words(k, F))
            dve.wait_ge(wpT_in_psum, 1)
            for n in range(2):
                last = nc.vector.tensor_copy(wpT[:, 4 * n:4 * n + 4].rearrange("p k o -> p (k o)"),
                                             half_words(2 + n, F))
            last.then_inc(wT_ready, 1)
            dve.wait_ge(xqT_in_psum, 1)
            nc.vector.tensor_copy(xqT[:].rearrange("p k t -> p (k t)"), half_words(4, D)).then_inc(xqT_ready, 1)
            dve.wait_ge(h_in_psum, 1)
            nc.vector.tensor_tensor(h[:], ps[:, 5:7, :].rearrange("p b n -> p (b n)"), core.weight("bfc"),
                                    ALU.add).then_inc(h_ready, 1)
            dve.wait_ge(gelu_done, 1)
            quantised(nc, chain, blocks(h[:]), blocks(hq[:]), 32, top, inv, scaled[:, 0:32]).then_inc(hq_ready, 1)
            dve.wait_ge(hqT_in_psum, 1)
            nc.vector.tensor_copy(hqT[:].rearrange("p k t -> p (k t)"), half_words(0, F)).then_inc(hqT_ready, 1)
            chain(nc.vector.tensor_tensor(core.x[:], core.x[:], core.weight("bproj"), ALU.add))
            dve.wait_ge(y_in_psum, 1)
            nc.vector.tensor_tensor(core.x[:], core.x[:], ps[:, 1, 0:D], ALU.add)

        @block.scalar
        def _(act):
            norm.scalar(act)
            act.wait_ge(h_ready, 1)
            nc.scalar.activation(h[:], h[:], ACT.Gelu).then_inc(gelu_done, 1)

        @block.tensor
        def _(pe):
            pe.wait_ge(wf_ready, 1)
            for k in range(DT):
                for n in range(FT):
                    last = nc.tensor.transpose(half_words(k, F)[:, n * P:(n + 1) * P],
                                               wfq[:, n, k * P:(k + 1) * P], identb[:])
            last.then_inc(wfT_in_psum, 1)
            pe.wait_ge(wp_ready, 1)
            for k in range(FT):
                for n in range(DT):
                    at = (k % 4) * D + n * P
                    last = nc.tensor.transpose(half_words(2 + k // 4, F)[:, at:at + P],
                                               wpq[:, n, k * P:(k + 1) * P], identb[:])
            last.then_inc(wpT_in_psum, 1)
            norm.tensor(pe)
            pe.wait_ge(xq_ready, 1)
            for k in range(DT):
                last = nc.tensor.transpose(half_words(4, D)[:, k * P:(k + 1) * P], xq[:, k * P:(k + 1) * P],
                                           identb[:])
            last.then_inc(xqT_in_psum, 1)
            pe.wait_ge(wT_ready, 1)
            pe.wait_ge(xqT_ready, 1)
            for n in range(2):
                projected(nc, ps[:, 5 + n, :], xqT, wfT[:, :, n * 512:(n + 1) * 512], DT, h_in_psum if n else None)
            pe.wait_ge(hq_ready, 1)
            for k in range(FT):
                last = nc.tensor.transpose(half_words(0, F)[:, k * P:(k + 1) * P], hq[:, k * P:(k + 1) * P],
                                           identb[:])
            last.then_inc(hqT_in_psum, 1)
            pe.wait_ge(hqT_ready, 1)
            projected(nc, ps[:, 1, 0:D], hqT, wpT, FT, y_in_psum)


def l3_attn(core):
    nc, ps, ident = core.nc, core.psum, core.ident()
    H, DH = 8, 32
    with Scope(core, "l3a") as s:
        norm = Norm(core, s)
        q, k, v = s.sb("q", [P, H, DH]), s.sb("k", [P, H, DH]), s.sb("v", [P, D])
        tmp = s.sb("tmp", [P, 4, H, DH // 2])
        qr, kr = s.sb("qr", [P, H, DH]), s.sb("kr", [P, H, DH])
        qT, kT = s.sb("qT", [P, DT, P]), s.sb("kT", [P, DT, P])
        st = s.sb("st", [P, H, P])
        y, sq = s.sb("y", [P, H, DH]), s.sb("sq", [P, H, DH])
        mean, var, std = s.sb("mean", [P, H]), s.sb("var", [P, H]), s.sb("std", [P, H])
        sig, gate = s.sb("sig", [P, D]), s.sb("gate", [P, D])
        yT = s.sb("yT", [P, DT, P])
        (chain_sem, qkv_in_psum, g_in_psum, gate_ready, rot_ready, qkT_in_psum, qkT_ready, s_in_psum, s_ready,
         y_in_psum, var_ready, std_ready, y_ready, yT_in_psum, yT_ready, out_in_psum) = s.signals(
            "chain_sem qkv_in_psum g_in_psum gate_ready rot_ready qkT_in_psum qkT_ready s_in_psum s_ready "
            "y_in_psum var_ready std_ready y_ready yT_in_psum yT_ready out_in_psum")
        flat = lambda t: t[:].rearrange("p h d -> p (h d)")
        wide = lambda t: t[:].unsqueeze(2).to_broadcast([P, H, DH])
        block = s.ctx.enter_context(nc.Block())

        @block.vector
        def _(dve):
            chain = Chain(dve, chain_sem)
            norm.vector(dve, chain)
            dve.wait_ge(qkv_in_psum, 1)
            nc.vector.tensor_copy(flat(q), ps[:, 0, 0:D])
            nc.vector.tensor_copy(flat(k), ps[:, 1, 0:D])
            chain(nc.vector.tensor_copy(v[:], ps[:, 2, 0:D]))
            for src, dst, tag in ((q, qr, "q"), (k, kr, "k")):
                table = lambda n: core.constant(n).unsqueeze(1).to_broadcast([P, H, DH // 2])
                last = rotary(nc, (src[:, :, 0::2], src[:, :, 1::2]), dst[:, :, 0::2], dst[:, :, 1::2],
                              table(f"xpos_cos_{tag}"), table(f"xpos_sin_{tag}"), [tmp[:, n] for n in range(4)],
                              chain)
                if tag == "q":
                    chain(last)
            last.then_inc(rot_ready, 1)
            dve.wait_ge(qkT_in_psum, 1)
            nc.vector.tensor_copy(flat(qT), ps[:, 4, 0:D])
            nc.vector.tensor_copy(flat(kT), ps[:, 5, 0:D]).then_inc(qkT_ready, 1)
            dve.wait_ge(s_in_psum, 1)
            decay = core.constant("decay").rearrange("p (h t) -> p h t", h=H)
            for g in range(4):
                last = nc.vector.tensor_tensor(st[:, g:H:4], ps[:, g, 0:2 * P].rearrange("p (h t) -> p h t", h=2),
                                               decay[:, g:H:4], ALU.mult)
            last.then_inc(s_ready, 1)
            dve.wait_ge(y_in_psum, 1)
            chain(nc.vector.tensor_copy(flat(y), ps[:, 4, 0:D]))
            chain(nc.vector.tensor_reduce(mean[:], y[:], AX.X, ALU.add))
            chain(nc.vector.tensor_scalar(mean[:], mean[:], 1.0 / DH, None, ALU.mult))
            chain(nc.vector.tensor_tensor(y[:], y[:], wide(mean), ALU.subtract))
            chain(nc.vector.tensor_tensor(sq[:], y[:], y[:], ALU.mult))
            chain(nc.vector.tensor_reduce(var[:], sq[:], AX.X, ALU.add))
            nc.vector.tensor_scalar(var[:], var[:], 1.0 / DH, LN_EPS, ALU.mult, ALU.add).then_inc(var_ready, 1)
            dve.wait_ge(std_ready, 1)
            chain(nc.vector.reciprocal(std[:], std[:]))
            chain(nc.vector.tensor_tensor(y[:], y[:], wide(std), ALU.mult))
            chain(nc.vector.tensor_tensor(flat(y), flat(y), core.weight("gnw"), ALU.mult))
            chain(nc.vector.tensor_tensor(flat(y), flat(y), core.weight("gnb"), ALU.add))
            dve.wait_ge(gate_ready, 2)
            chain(nc.vector.tensor_tensor(flat(y), flat(y), sig[:], ALU.mult))
            nc.vector.tensor_tensor(flat(y), flat(y), gate[:], ALU.mult).then_inc(y_ready, 1)
            dve.wait_ge(yT_in_psum, 1)
            nc.vector.tensor_copy(flat(yT), ps[:, 0, 0:D]).then_inc(yT_ready, 1)
            dve.wait_ge(out_in_psum, 1)
            nc.vector.tensor_tensor(core.x[:], core.x[:], ps[:, 1, 0:D], ALU.add)

        @block.scalar
        def _(act):
            norm.scalar(act)
            act.wait_ge(g_in_psum, 1)
            nc.scalar.activation(sig[:], ps[:, 3, 0:D], ACT.Sigmoid).then_inc(gate_ready, 1)
            nc.scalar.activation(gate[:], ps[:, 3, 0:D], ACT.Copy).then_inc(gate_ready, 1)
            act.wait_ge(var_ready, 1)
            nc.scalar.activation(std[:], var[:], ACT.Sqrt).then_inc(std_ready, 1)

        @block.tensor
        def _(pe):
            norm.tensor(pe)
            pe.wait_ge(norm.xT_ready, 1)
            for bank, name in enumerate(("rq", "rk", "rv")):
                projected(nc, ps[:, bank, 0:D], norm.xnT, core.kxn(name), DT, qkv_in_psum if bank == 2 else None)
            projected(nc, ps[:, 3, 0:D], norm.xnT, core.kxn("rg"), DT, g_in_psum)
            pe.wait_ge(rot_ready, 1)
            for bank, r in ((4, qr), (5, kr)):
                for n in range(DT):
                    last = nc.tensor.transpose(ps[:, bank, n * P:(n + 1) * P], flat(r)[:, n * P:(n + 1) * P], ident)
            last.then_inc(qkT_in_psum, 1)
            pe.wait_ge(qkT_ready, 1)
            pe.wait_ge(gate_ready, 2)
            for h in range(H):
                r = slice(DH * (h % 4), DH * (h % 4) + DH)
                last = nc.tensor.matmul(ps[:, h % 4, (h // 4) * P:(h // 4 + 1) * P], kT[r, h // 4, :],
                                        qT[r, h // 4, :], start=True, stop=True)
            last.then_inc(s_in_psum, 1)
            pe.wait_ge(s_ready, 1)
            for h in range(H):
                last = nc.tensor.matmul(ps[:, 4, h * DH:(h + 1) * DH], st[:, h, :], v[:, h * DH:(h + 1) * DH],
                                        start=True, stop=True)
            last.then_inc(y_in_psum, 1)
            pe.wait_ge(y_ready, 1)
            transposed(nc, ps, 0, flat(y), DT, ident, yT_in_psum)
            pe.wait_ge(yT_ready, 1)
            projected(nc, ps[:, 1, 0:D], yT, core.kxn("ro"), DT, out_in_psum)


def l3_ffn(core):
    nc, ps = core.nc, core.psum
    E, F = 8, 1024
    FT = F // P
    W1, W2, B1, B2 = 0, DT * F, DT * F + FT * D, DT * F + FT * D + FT
    WIDE = B2 + D
    with Scope(core, "l3f") as s:
        norm = Norm(core, s)
        w = s.sb("w", [P, 2, WIDE])
        hT = s.sb("hT", [P, 2, FT, P])
        mean, g = s.sb("mean", [P, DT, 1]), s.sb("g", [1, E])
        one = s.sb("one", [1, 4])
        top, topi = s.sb("top", [1, 8]), s.sb("topi", [1, 8], U32)
        pair, ones = s.sb("pair", [1, 2]), s.sb("ones", [1, P])
        coef = s.sb("coef", [P, 4])
        y, b2a = s.sb("y", [P, D]), s.sb("b2a", [P, D])
        (chain_sem, mean_ready, g_in_psum, shifted, exp_done, chosen, pair_ready, pair_in_psum, h_in_psum, h_ready,
         y_in_psum, y_added, coef_ready) = s.signals(
            "chain_sem mean_ready g_in_psum shifted exp_done chosen pair_ready pair_in_psum h_in_psum h_ready "
            "y_in_psum y_added coef_ready")
        w_in = s.signals("w_in0 w_in1")
        block = s.ctx.enter_context(nc.Block())

        @block.sync
        def _(sp):
            sp.dma_start(w[:, 0], core.dram["mlps"][E]).then_inc(w_in[0], 16)
            sp.wait_ge(chosen, 1)
            first = sp.value_load(topi[0:1, 0:1], min_val=0, max_val=E - 1)
            sp.dma_start(w[:, 1], core.dram["mlps"][bass.ds(first, 1)].squeeze(0)).then_inc(w_in[1], 16)
            second = sp.value_load(topi[0:1, 1:2], min_val=0, max_val=E - 1)
            sp.wait_ge(y_added, 1)
            sp.dma_start(w[:, 0], core.dram["mlps"][bass.ds(second, 1)].squeeze(0)).then_inc(w_in[0], 16)

        @block.vector
        def _(dve):
            chain = Chain(dve, chain_sem)
            nc.vector.memset(ones[:], 1.0)
            norm.vector(dve, chain)
            chain(nc.vector.tensor_reduce(mean[:], norm.xnT[:], AX.X, ALU.add))
            nc.vector.tensor_scalar(mean[:], mean[:], 1.0 / P, None, ALU.mult).then_inc(mean_ready, 1)
            dve.wait_ge(g_in_psum, 1)
            chain(nc.vector.tensor_tensor(g[:], ps[0:1, 0, 0:E], core.weight("bgate")[0:1, :], ALU.add))
            chain(nc.vector.tensor_reduce(one[:, 0:1], g[:], AX.X, ALU.max))
            nc.vector.tensor_scalar(g[:], g[:], one[:, 0:1], None, ALU.subtract).then_inc(shifted, 1)
            dve.wait_ge(exp_done, 1)
            chain(nc.vector.tensor_reduce(one[:, 1:2], g[:], AX.X, ALU.add))
            chain(nc.vector.reciprocal(one[:, 1:2], one[:, 1:2]))
            chain(nc.vector.tensor_scalar(g[:], g[:], one[:, 1:2], None, ALU.mult))
            chain(nc.vector.max(top[:], g[:]))
            nc.vector.max_index(topi[:], top[:], g[:]).then_inc(chosen, 1)
            chain(nc.vector.tensor_tensor(one[:, 2:3], top[:, 0:1], top[:, 1:2], ALU.add))
            chain(nc.vector.reciprocal(one[:, 2:3], one[:, 2:3]))
            nc.vector.tensor_scalar(pair[:], top[:, 0:2], one[:, 2:3], None, ALU.mult).then_inc(pair_ready, 1)
            chain(nc.vector.tensor_scalar(coef[:, 0:1], core.weight("alpha"), 0.1, 1.0, ALU.max, ALU.min))
            chain(nc.vector.tensor_scalar(coef[:, 3:4], coef[:, 0:1], -1.0, 1.0, ALU.mult, ALU.add))
            dve.wait_ge(pair_in_psum, 1)
            chain(nc.vector.tensor_scalar(coef[:, 1:3], ps[:, 1, 0:2], coef[:, 3:4], None, ALU.mult))
            for n in range(3):
                dve.wait_ge(y_in_psum, n + 1)
                chain(nc.vector.tensor_tensor(y[:], ps[:, 2, 0:D], w[:, n % 2, B2:B2 + D], ALU.add))
                nc.vector.scalar_tensor_tensor(core.x[:], y[:], coef[:, n:n + 1], core.x[:], ALU.mult,
                                               ALU.add).then_inc(y_added, 1)
                dve.wait_ge(y_added, n + 1)

        @block.scalar
        def _(act):
            norm.scalar(act)
            act.wait_ge(shifted, 1)
            nc.scalar.activation(g[:], g[:], ACT.Exp).then_inc(exp_done, 1)
            for n in range(3):
                for t in range(FT):
                    act.wait_ge(h_in_psum, n * FT + t + 1)
                    nc.scalar.activation(hT[:, n % 2, t], ps[:, 3 + t % 4, 0:P], ACT.Gelu_apprx_tanh,
                                         bias=w[:, n % 2, B1 + t:B1 + t + 1]).then_inc(h_ready, 1)

        @block.tensor
        def _(pe):
            norm.tensor(pe)
            pe.wait_ge(mean_ready, 1)
            wg = core.kxn("gate")
            for k in range(DT):
                last = nc.tensor.matmul(ps[0:1, 0, 0:E], mean[:, k, :], wg[:, k, :], start=(k == 0),
                                        stop=(k == DT - 1))
            last.then_inc(g_in_psum, 1)
            pe.wait_ge(pair_ready, 1)
            nc.tensor.matmul(ps[:, 1, 0:2], ones[:], pair[:], start=True, stop=True).then_inc(pair_in_psum, 1)
            for n in range(3):
                pe.wait_ge(w_in[n % 2], 16 * (n // 2 + 1))
                w1 = w[:, n % 2, W1:W2].rearrange("p (k f) -> p k f", k=DT)
                w2 = w[:, n % 2, W2:B1].rearrange("p (k o) -> p k o", k=FT)
                for t in range(FT):
                    if n * FT + t >= 4:
                        pe.wait_ge(h_ready, n * FT + t - 3)
                    for k in range(DT):
                        last = nc.tensor.matmul(ps[:, 3 + t % 4, 0:P], w1[:, k, t * P:(t + 1) * P],
                                                norm.xnT[:, k, :], start=(k == 0), stop=(k == DT - 1))
                    last.then_inc(h_in_psum, 1)
                if n:
                    pe.wait_ge(y_added, n)
                pe.wait_ge(h_ready, (n + 1) * FT)
                projected(nc, ps[:, 2, 0:D], hT[:, n % 2], w2, FT, y_in_psum)


LAYERS = [[l0_xattn, l0_attn, l0_ffn], [l1_xattn, l1_attn, l1_ffn], [l2_xattn, l2_attn, l2_ffn],
          [l3_xattn, l3_attn, l3_ffn]]


def program(nc, dram, cols, out):
    with ExitStack() as ctx:
        core = Core(nc, ctx, dram, cols)
        x_in = nc.alloc_semaphore("x_in")
        const_in = nc.alloc_semaphore("const_in")
        weights_in = nc.alloc_semaphore("weights_in")
        stored = nc.alloc_semaphore("stored")
        with nc.Block() as block:
            @block.sync
            def _(sp):
                sp.dma_start(core.x[:], dram["x"]).then_inc(x_in, 16)
                sp.dma_start(core.const[:], dram["const"]).then_inc(const_in, 16)
                sp.wait_ge(x_in, 16)
                sp.wait_ge(const_in, 16)
        for layer in range(4):
            core.layer = f"w{layer}"
            with nc.sbuf_tensor(f"weights{layer}", [P, cols[core.layer]["_"]], F32) as w:
                core.w = w
                with nc.Block() as block:
                    @block.sync
                    def _(sp):
                        sp.dma_start(w[:], dram[core.layer]).then_inc(weights_in, 16)
                        sp.wait_ge(weights_in, 16 * (layer + 1))
                for sub in LAYERS[layer]:
                    sub(core)
        with nc.Block() as block:
            @block.sync
            def _(sp):
                sp.dma_start(out, core.x[:]).then_inc(stored, 16)
                sp.wait_ge(stored, 16)



def _constants():
    p = np.arange(P)
    t = {"ident": np.eye(P)}
    t["head16"] = (p[:, None] // 16 == np.arange(8)[None, :])
    t["head64"] = (p[:, None] // 64 == np.arange(2)[None, :])
    t["zero"] = np.zeros((P, D))
    t["one"] = np.ones((P, 1))
    i, j = p[:, None], p[None, :]
    masked = (j > i) & ~((i < 64) & (j < 64))
    t["prefix_mask"] = np.concatenate([np.where(masked, -1e30, 0.0), np.zeros((P, 2))], 1)
    t["causal_mask"] = np.where(j > i, -1e30, 0.0)
    t["chunk_mask"] = (j >= i) & (i // 64 == j // 64)
    t["iota"] = np.broadcast_to(p[None, :], (P, P))
    freq = p[:, None].astype(np.float32) * (1.0 / 10000.0 ** (np.arange(0, 16, 2, dtype=np.float32) / 16))[None, :]
    t["rope_cos"], t["rope_sin"] = np.cos(freq), np.sin(freq)
    pos = p.astype(np.float32)
    base = (np.arange(0, 32, 2, dtype=np.float32) + np.float32(0.4 * 32)) / np.float32(1.4 * 32)
    scale = base[None, :] ** (pos[:, None] / np.float32(512.0))
    turn = pos[:, None] * (1.0 / 10000.0 ** (np.arange(16, dtype=np.float32) / 16))[None, :]
    t["xpos_cos_q"], t["xpos_sin_q"] = np.cos(turn) * scale, np.sin(turn) * scale
    t["xpos_cos_k"], t["xpos_sin_k"] = np.cos(turn) / scale, np.sin(turn) / scale
    gamma = 1.0 - np.exp(np.linspace(np.log(1.0 / 32.0), np.log(1.0 / 512.0), 8))
    apart = (j - i)[:, None, :]
    t["decay"] = np.where(apart >= 0, np.exp(np.maximum(apart, 0) * np.log(gamma)[None, :, None]),
                          0.0).reshape(P, 8 * P)
    return t


def _kxn(w):
    k = w.shape[0] // P
    return w.reshape(k, P, -1).transpose(1, 0, 2).reshape(P, -1)


def _col(b):
    return b.reshape(-1, P).T


def _row(b):
    return np.broadcast_to(b.reshape(1, -1), (P, b.size))


def _pad(a):
    return np.concatenate([a, np.zeros((P - a.shape[0], a.shape[1]), a.dtype)], 0)


def _null_values(null_v, heads):
    z = np.zeros((P, heads * null_v.shape[1]), null_v.dtype)
    for n, h in enumerate([h for m in range(2) for h in range(m, heads, 2)]):
        z[2 * n:2 * n + 2, h * null_v.shape[1]:(h + 1) * null_v.shape[1]] = null_v
    return z


def _packs(a):
    w0 = {
        "xq": _kxn(a["L0_xattn_Wq"]), "xk": _kxn(a["L0_xattn_Wk"]), "xv": _kxn(a["L0_xattn_Wv"]),
        "xo": _kxn(a["L0_xattn_Wo"]), "xbq": _col(a["L0_xattn_bq"]), "xbk": _col(a["L0_xattn_bk"]),
        "xbv": _row(a["L0_xattn_bv"]), "xbo": _row(a["L0_xattn_bo"]),
        "gamma": _row(a["L0_attn_gamma"]), "aq": _kxn(a["L0_attn_Wq"]), "akv": _kxn(a["L0_attn_Wkv"]),
        "qs": _row(a["L0_attn_q_scale"]), "ks": _row(a["L0_attn_k_scale"]),
        "null_k": _pad(a["L0_attn_null_kv"][0]), "null_v": _null_values(a["L0_attn_null_kv"][1], 16),
        "ao": _kxn(a["L0_attn_Wout"]),
        "fr": _kxn(a["L0_ffn_W_r"].T), "fk": _kxn(a["L0_ffn_W_k"].T), "fv": _kxn(a["L0_ffn_W_v"].T),
        "mu_r": _col(a["L0_ffn_mu_r"]), "mu_k": _col(a["L0_ffn_mu_k"]),
    }
    w1 = {
        "xq": _kxn(a["L1_xattn_wq"].T), "xk": _kxn(a["L1_xattn_wk"].T), "xv": _kxn(a["L1_xattn_wv"].T),
        "xo": _kxn(a["L1_xattn_wo"].T), "xbq": _col(a["L1_xattn_bq"]), "xbk": _col(a["L1_xattn_bk"]),
        "xbv": _row(a["L1_xattn_bv"]), "xbo": _row(a["L1_xattn_bo"]),
        "gq": _kxn(a["L1_attn_Wq"]), "gk": _kxn(a["L1_attn_Wk"]), "gv": _kxn(a["L1_attn_Wv"]),
        "gg": _kxn(a["L1_attn_Wg"]), "gk1": _kxn(a["L1_attn_gk_w1"]), "gk2": _pad(a["L1_attn_gk_w2"]),
        "gkb": _col(a["L1_attn_gk_b2"]), "gn": _row(a["L1_attn_g_norm_w"]), "go": _kxn(a["L1_attn_Wo"]),
    }
    w1.update({
        "r1": _kxn(np.ascontiguousarray(a["L1_ffn_r1_w"].T)[0:D]), "r1s": _pad(a["L1_ffn_r1_w"].T[D:]),
        "r1b": _col(a["L1_ffn_r1_b"]), "r2": a["L1_ffn_r2_w"].T,
    })
    kvb = a["L2_attn_Wkvb"].reshape(32, 64, 2)
    w2 = {
        "xq": _kxn(a["L2_xattn_Wq"].T), "xk": _kxn(a["L2_xattn_Wk"].T), "xv": _kxn(a["L2_xattn_Wv"].T),
        "xbq": _col(a["L2_xattn_bq"]), "xbk": _col(a["L2_xattn_bk"]), "xbv": _row(a["L2_xattn_bv"]),
        "qa": _kxn(a["L2_attn_Wqa"]), "qb": _pad(a["L2_attn_Wqb"]), "kva": _kxn(a["L2_attn_Wkva"]),
        "kvb": _pad(np.concatenate([kvb[:, :, 0], kvb[:, :, 1]], 1)), "aout": _kxn(a["L2_attn_Wout"]),
        "bout": _row(a["L2_attn_bout"]),
        "fc": _kxn(a["L2_ffn_w_fc"]), "bfc": _row(a["L2_ffn_b_fc"]), "proj": _kxn(a["L2_ffn_w_proj"]),
        "bproj": _row(a["L2_ffn_b_proj"]),
    }
    heads = lambda m: _kxn(m.transpose(1, 0, 2).reshape(D, -1))
    w3 = {
        "xq": _kxn(a["L3_xattn_Wq"]), "xk": _kxn(a["L3_xattn_Wk"]), "xv": _kxn(a["L3_xattn_Wv"]),
        "xo": _kxn(a["L3_xattn_Wo"]),
        "rq": heads(a["L3_attn_W_Q"]), "rk": heads(a["L3_attn_W_K"]), "rv": heads(a["L3_attn_W_V"]),
        "rg": _kxn(a["L3_attn_W_G"]), "ro": _kxn(a["L3_attn_W_O"]), "gnw": _row(a["L3_attn_gn_weight"]),
        "gnb": _row(a["L3_attn_gn_bias"]),
        "gate": _kxn(a["L3_ffn_w_gate"]), "bgate": _row(a["L3_ffn_b_gate"]),
        "alpha": _row(a["L3_ffn_alpha"].reshape(1)),
    }
    return [w0, w1, w2, w3]


def _each(w):
    return np.stack([_kxn(m) for m in w])


def _big(a):
    mlp = lambda w1, w2, b1, b2: np.concatenate([_kxn(w1), _kxn(w2), _col(b1), _row(b2)], 1)
    mlps = [mlp(a["L3_ffn_W1e"][e], a["L3_ffn_W2e"][e], a["L3_ffn_b1e"][e], a["L3_ffn_b2e"][e]) for e in range(8)]
    mlps.append(mlp(a["L3_ffn_W1m"], a["L3_ffn_W2m"], a["L3_ffn_b1m"], a["L3_ffn_b2m"]))
    return {
        "w_up": _each(a["L1_ffn_w_up"].transpose(0, 2, 1)), "w_down": _each(a["L1_ffn_w_down"].transpose(0, 2, 1)),
        "a_up": _each(a["L1_ffn_a_up"].transpose(0, 2, 1)), "a_down": _each(a["L1_ffn_a_down"].transpose(0, 2, 1)),
        "mlps": np.stack(mlps),
    }


def kernel(**inputs):
    import concourse.bacc as bacc
    from concourse.bass_utils import run_bass_kernel_spmd

    a = {n: np.asarray(v) for n, v in inputs.items()}
    arrays, cols = {}, {}
    packs = {f"w{n}": pack for n, pack in enumerate(_packs(a))}
    packs["const"] = {n: t.astype(np.float32) for n, t in _constants().items()}
    for name, pack in packs.items():
        at, where = 0, {}
        for n, piece in pack.items():
            where[n] = (at, at + piece.shape[1])
            at += piece.shape[1]
        where["_"] = at
        cols[name] = where
        arrays[name] = np.ascontiguousarray(np.concatenate(list(pack.values()), 1))
    arrays["x"] = a["x"][0]
    arrays["ctxT"] = np.ascontiguousarray(a["ctx_1024"][0].T)
    arrays.update(_big(a))

    nc = bacc.Bacc("TRN2", target_bir_lowering=False, num_devices=1)
    dram = {n: nc.dram_tensor(n, v.shape, mybir.dt.from_np(v.dtype), kind="ExternalInput").ap()
            for n, v in arrays.items()}
    out = nc.dram_tensor("out_0_dram", (P, D), F32, kind="ExternalOutput").ap()
    program(nc, dram, cols, out)
    r = run_bass_kernel_spmd(nc, [arrays], core_ids=[0])
    return r.results[0]["out_0_dram"].reshape(1, P, D)
```

```python
from contextlib import ExitStack

import numpy as np

import concourse.bass as bass
from concourse import mybir

F32 = mybir.dt.float32
BF16 = mybir.dt.bfloat16
F16 = mybir.dt.float16
F32R = mybir.dt.float32r
I32 = mybir.dt.int32
U32 = mybir.dt.uint32
ALU = mybir.AluOpType
ACT = mybir.ActivationFunctionType
AX = mybir.AxisListType

P = 128
D = 256
DT = D // P
KEYS = 12544
CH = 896
BLK = CH // 2
TPC = CH // P
NCH = KEYS // CH
LN_EPS = 1e-5
P_SHIFT = float(8 * np.log(2))
AHEAD = 4


class Chain:

    def __init__(self, eng, sem):
        self.eng, self.sem, self.n = eng, sem, 0

    def __call__(self, ins):
        self.n += 1
        ins.then_inc(self.sem, 1)
        self.eng.wait_ge(self.sem, self.n)


class Core:

    def __init__(self, nc, ctx, dram, cols):
        self.nc, self.ctx, self.dram, self.cols = nc, ctx, dram, cols
        self.x = ctx.enter_context(nc.sbuf_tensor("rows", [P, D], F32))
        self.const = ctx.enter_context(nc.sbuf_tensor("consts", [P, cols["const"]["_"]], F32))
        self.psum = ctx.enter_context(nc.psum_tensor("psum", [P, 8, 512], F32))
        self.w = None
        self.behind_first_chunks = None

    def constant(self, name):
        a, b = self.cols["const"][name]
        return self.const[:, a:b]

    def weight(self, name):
        a, b = self.cols[self.layer][name]
        return self.w[:, a:b]

    def kxn(self, name, k=DT):
        return self.weight(name).rearrange("p (k n) -> p k n", k=k)

    def ident(self, n=P):
        return self.constant("ident")[0:n, 0:n]


class Scope:

    def __init__(self, core, name):
        self.nc, self.name, self.ctx, self.sems = core.nc, name, ExitStack(), []

    def __enter__(self):
        return self

    def __exit__(self, *e):
        self.ctx.__exit__(*e)
        if e[0] is None:
            self.nc.clear_and_free_semaphores(self.sems)
            self.nc.all_engine_barrier(sem_only=True)

    def sb(self, name, shape, dt=F32):
        return self.ctx.enter_context(self.nc.sbuf_tensor(f"{self.name}_{name}", shape, dt))

    def signals(self, names):
        made = [self.nc.alloc_semaphore(f"{self.name}_{n}") for n in names.split()]
        self.sems += made
        return made


class Norm:

    def __init__(self, core, scope, src=None, gamma=None, tag="ln"):
        self.nc, self.ident, self.gamma = core.nc, core.ident(), gamma
        self.src = core.x[:] if src is None else src
        self.stats = scope.sb(f"{tag}_stats", [P, 6])
        self.mv = scope.sb(f"{tag}_mv", [P, 2])
        self.std = scope.sb(f"{tag}_std", [P, 1])
        self.rstd = scope.sb(f"{tag}_rstd", [P, 1])
        self.xn = scope.sb(f"{tag}_xn", [P, D])
        self.xnT = scope.sb(f"{tag}_xnT", [P, DT, P])
        self.ps = core.psum[:, 7, 0:DT * P]
        self.var_ready, self.std_ready, self.xn_ready, self.xT_in_psum, self.xT_ready = scope.signals(
            f"{tag}_var_ready {tag}_std_ready {tag}_xn_ready {tag}_xT_in_psum {tag}_xT_ready")

    def vector(self, dve, chain):
        nc = self.nc
        chain(nc.vector.bn_stats(self.stats[:], self.src))
        chain(nc.vector.bn_aggr(self.mv[:], self.stats[:]))
        nc.vector.tensor_scalar(self.rstd[:], self.mv[:, 1:2], LN_EPS, None, ALU.add).then_inc(self.var_ready, 1)
        dve.wait_ge(self.std_ready, 1)
        chain(nc.vector.reciprocal(self.rstd[:], self.std[:]))
        last = nc.vector.tensor_scalar(self.xn[:], self.src, self.mv[:, 0:1], self.rstd[:], ALU.subtract, ALU.mult)
        if self.gamma is not None:
            chain(last)
            last = nc.vector.tensor_tensor(self.xn[:], self.xn[:], self.gamma, ALU.mult)
        last.then_inc(self.xn_ready, 1)
        dve.wait_ge(self.xT_in_psum, 1)
        nc.vector.tensor_copy(self.xnT[:].rearrange("p k t -> p (k t)"), self.ps).then_inc(self.xT_ready, 1)
        dve.wait_ge(self.xT_ready, 1)

    def scalar(self, act):
        act.wait_ge(self.var_ready, 1)
        self.nc.scalar.activation(self.std[:], self.rstd[:], ACT.Sqrt).then_inc(self.std_ready, 1)

    def tensor(self, pe):
        pe.wait_ge(self.xn_ready, 1)
        for k in range(DT):
            last = self.nc.tensor.transpose(self.ps[:, k * P:(k + 1) * P], self.xn[:, k * P:(k + 1) * P],
                                            self.ident)
        last.then_inc(self.xT_in_psum, 1)


def split(nc, out_hi, out_lo, src, chain):
    chain(nc.vector.tensor_copy(out_hi, src))
    return nc.vector.tensor_tensor(out_lo, src, out_hi.bitcast(F32), ALU.subtract)


def cross_attention(core, name, heads, groups, wq, wk, wv, wo, bq, bk, bv, bo, scale):
    nc = core.nc
    dh = D // heads
    per = heads // DT
    hq = per * P
    units = 2 if heads == 16 else 1
    UW = heads * P // units
    HW = 3 * dh + 1
    BW = per * HW
    CU = TPC * units
    PAIRS = NCH // 2
    K_BANK, V_BANK = 7, 6
    SIDE = groups > 1
    HALVES = 2 * heads
    WB = 2 if SIDE else 1

    def first_pieces(h):
        pieces = [piece for t in range(TPC) for piece in ([("key", t)] if t < 4 else []) + [("value", t)]]
        return pieces[h * len(pieces) // heads:(h + 1) * len(pieces) // heads]

    def ahead(i, g, b, more):
        if more:
            return i, g, b + 1
        return (0, g + 1, 0) if g + 1 < groups else None

    def side_halves(t):
        return range(t, t + 1) if t + 1 < TPC else range(t, HALVES)
    with Scope(core, name) as s:
        norm = Norm(core, s)
        ctxb = s.sb("ctx", [P, 2, DT, CH])
        chi, clo = s.sb("chi", [P, 2, DT, CH], F32R), s.sb("clo", [P, 2, DT, CH], F32R)
        khi, klo = s.sb("khi", [P, 2, DT, CH], F32R), s.sb("klo", [P, 2, DT, CH], F32R)
        v = s.sb("v", [P, 2, TPC, heads, HW], BF16)
        vrest = s.sb("vrest", [P, 2, D])
        p32 = s.sb("p32", [P, 2, UW])
        phi, plo = s.sb("phi", [P, 2, heads * P], F16), s.sb("plo", [P, 2, heads * P], F16)
        wkh, wkl = s.sb("wkh", [P, WB, DT, D], F32R), s.sb("wkl", [P, WB, DT, D], F32R)
        wvh, wvl = s.sb("wvh", [P, WB, DT, D], F32R), s.sb("wvl", [P, WB, DT, D], F32R)
        qT = s.sb("qT", [P, DT, P])
        qh, ql = s.sb("qh", [P, WB, DT, per * P], F32R), s.sb("ql", [P, WB, DT, per * P], F32R)
        chunk_max = s.sb("chunk_max", [P, 2, heads])
        run_max = s.sb("run_max", [P, heads])
        if SIDE:
            side_k = s.sb("side_k", [P, 2, DT, CH], F32R)
            side_max, side_run = s.sb("side_max", [P, 2, HALVES]), s.sb("side_run", [P, HALVES])
        neg = s.sb("neg", [P, 2, heads])
        m3b = s.sb("m3b", [P, 3, heads], BF16)
        m3f = s.sb("m3f", [P, 3 * heads])
        m3T = s.sb("m3T", [3 * heads, P], BF16)
        m3row = s.sb("m3row", [3, heads * P], BF16)
        ones3, zeros3 = s.sb("ones3", [3, P], BF16), s.sb("zeros3", [3, P], BF16)
        oa = s.sb("oa", [P, heads, HW])
        rden = s.sb("rden", [P, heads, 1])
        o = s.sb("o", [P, D])
        wide = o[:] if SIDE else p32[:, 0]
        oT = s.sb("oT", [P, DT, P])
        ps = core.psum
        ident = core.ident()
        m3_dram = nc.dram_tensor(f"{name}_m3", [3 * heads, P], BF16).ap()

        (weights_split, hi_ready, lo_ready, k_in_psum, khi_ready, klo_ready, q_in_psum, q_ready, s_full,
         s_free, max_step, neg_ready, m3_in_psum, m3T_ready, m3_stored, m3_rows, v_in_psum, v1_ready,
         rest_ready, v2_ready, v_ready, st_full, phi_ready, plo_ready, pv_done, o_ready,
         oT_in_psum, oT_ready, y_in_psum, chain_sem, side_k_in_psum, side_k_ready, side_full, side_free,
         side_step) = s.signals(
            "weights_split hi_ready lo_ready k_in_psum khi_ready klo_ready q_in_psum q_ready s_full "
            "s_free max_step neg_ready m3_in_psum m3T_ready m3_stored m3_rows v_in_psum v1_ready "
            "rest_ready v2_ready v_ready st_full phi_ready plo_ready pv_done o_ready "
            "oT_in_psum oT_ready y_in_psum chain_sem side_k_in_psum side_k_ready side_full side_free "
            "side_step")
        ctx_in = s.signals("ctx_in0 ctx_in1")
        RING = 2

        ctxT = core.dram["ctxT"].rearrange("(k p) n -> p k n", p=P)
        block = s.ctx.enter_context(nc.Block())

        @block.sync
        def _(sp):
            def load(i, n0, b):
                sp.dma_start(ctxb[:, b], ctxT[:, :, bass.ds(i * (2 * CH) + (n0 + b) * CH, CH)]).then_inc(
                    ctx_in[b], 16)

            for b in range(2):
                load(0, 0, b)
            if core.behind_first_chunks is not None:
                core.behind_first_chunks(sp, core.w)
            with sp.Fori(0, PAIRS - 1) as i:
                for b in range(2):
                    sp.wait_ge(hi_ready, i * (2 * DT) + DT * (b + 1))
                    load(i, 2, b)
            for g in range(groups):
                for b in range(2):
                    if g:
                        sp.wait_ge(lo_ready, DT * (g * NCH - 1 + b))
                    else:
                        sp.wait_ge(hi_ready, DT * (NCH - 1 + b))
                    load(0, 0, b)
                with sp.Fori(0, PAIRS - 1) as i:
                    for b in range(2):
                        sp.wait_ge(lo_ready, i * (2 * DT) + DT * (g * NCH + b + 1))
                        load(i, 2, b)

        @block.gpsimd
        def _(pool):
            for sem in (khi_ready, s_free, rest_ready, v_ready, phi_ready, plo_ready, side_free):
                pool.sem_inc(sem, RING)

            def lower(i, g, n0, k):
                b = n0 % 2
                if g or n0 > 1:
                    pool.wait_ge(v_in_psum, i * (2 * TPC) + TPC * (g * NCH + n0 - 1))
                pool.wait_ge(hi_ready, i * (2 * DT) + (DT * ((g + 1) * NCH + n0) + k + 1))
                nc.gpsimd.tensor_tensor(clo[:, b, k], ctxb[:, b, k], chi[:, b, k].bitcast(F32),
                                        ALU.subtract).then_inc(lo_ready, 1)

            def third(i, g, n0, t):
                at = (g * NCH + n0) * TPC + t
                b = n0 % 2
                rest = vrest[:, at % 2].rearrange("p (h w) -> p h w", h=heads)
                pool.wait_ge(v2_ready, i * (2 * TPC) + (at + 1))
                nc.gpsimd.tensor_tensor(v[:, b, t, :, 2 * dh + 1:HW], rest, v[:, b, t, :, dh + 1:2 * dh + 1],
                                        ALU.subtract).then_inc(v_ready, 1)

            for k in range(DT):
                lower(0, 0, 0, k)
            for t in range(TPC):
                third(0, 0, 0, t)
            for k in range(DT):
                lower(0, 0, 1, k)
            for g in range(groups):
                with pool.Fori(0, PAIRS - 1) as i:
                    for b in range(2):
                        for t in range(TPC):
                            if 0 <= t - AHEAD < DT:
                                lower(i, g, b + 2, t - AHEAD)
                            third(i, g, b + 1, t)
                for b in range(2):
                    to = ahead(PAIRS - 1, g, b, b == 0)
                    for t in range(TPC if to else 0):
                        if g + 1 < groups and 0 <= t - AHEAD < DT:
                            lower(0, g + 1, b, t - AHEAD)
                        third(*to, t)

        @block.scalar
        def _(act):
            norm.scalar(act)

            def upper(i, load, k, freed, count):
                b = load % 2
                act.wait_ge(ctx_in[b], i * 16 + (load // 2 + 1) * 16)
                if freed is not None:
                    act.wait_ge(freed, count)
                nc.scalar.activation(chi[:, b, k], ctxb[:, b, k], ACT.Copy).then_inc(hi_ready, 1)

            def key(i, g, load, hb, bank):
                hf, blk = hb // 2, hb % 2
                act.wait_ge(k_in_psum, i * 8 + (4 * load + hb + 1))
                nc.scalar.activation(khi[:, load % 2, hf, blk * BLK:(blk + 1) * BLK], ps[:, bank, 0:BLK],
                                     ACT.Identity, bias=bk(g, hf)).then_inc(khi_ready, 1)

            def first(i, g, n0, t):
                at = (g * NCH + n0) * TPC + t
                act.wait_ge(v_in_psum, i * (2 * TPC) + (at + 1))
                nc.scalar.activation(v[:, n0 % 2, t, :, 0:dh],
                                     ps[:, V_BANK, 0:D].rearrange("p (h w) -> p h w", h=heads),
                                     ACT.Copy).then_inc(v1_ready, 1)

            def probs(i, g, n0, t):
                for u in range(units):
                    at = (g * NCH + n0) * CU + t * units + u
                    tile = ((g * NCH + n0) * TPC + t) % 2
                    src = ps[:, 2 * (at % 2):2 * (at % 2) + 2, :].rearrange("p a n -> p (a n)")[:, 0:UW]
                    act.wait_ge(st_full, i * (2 * CU) + (at + 1))
                    act.wait_ge(plo_ready, i * (2 * CU) + (at + 1))
                    nc.scalar.activation(p32[:, at % 2], src, ACT.Exp)
                    nc.scalar.activation(phi[:, tile, u * UW:(u + 1) * UW], src, ACT.Exp).then_inc(phi_ready, 1)

            def side_key(i, g, n0, hb):
                hf, blk = hb // 2, hb % 2
                act.wait_ge(side_k_in_psum, i * 8 + (4 * (g * NCH + n0) + hb + 1))
                nc.scalar.activation(side_k[:, n0 % 2, hf, blk * BLK:(blk + 1) * BLK], ps[:, K_BANK, 0:BLK],
                                     ACT.Identity, bias=bk(g + 1, hf)).then_inc(side_k_ready, 1)

            for b in range(2):
                for k in range(DT):
                    upper(0, b, k, None, 0)

            def body_a(i, b):
                for hb in range(4):
                    if hb < DT:
                        upper(i, b + 2, hb, k_in_psum, i * 8 + 4 * (b + 1))
                    key(i, 0, b + 1, hb, 6 + hb % 2)

            for hb in range(4):
                key(0, 0, 0, hb, 6 + hb % 2)
            with act.Fori(0, PAIRS - 1) as i:
                for b in range(2):
                    body_a(i, b)
            i = PAIRS - 1
            body_a(i, 0)
            for k in range(DT):
                upper(i, 3, k, k_in_psum, i * 8 + 8)
            for h in range(heads):
                for kind, n in first_pieces(h):
                    if kind == "key":
                        key(0, 0, NCH, n, K_BANK)
                    else:
                        first(0, 0, 0, n)
            for g in range(groups):
                load0 = (g + 1) * NCH
                act.wait_ge(m3T_ready, g + 1)
                act.dma_start(m3_dram[:, :], m3T[:]).then_inc(m3_stored, 16)
                act.wait_ge(m3_stored, 16 * (g + 1))
                act.dma_start(m3row[:], m3_dram.rearrange("(k h) q -> k (h q)", k=3)).then_inc(m3_rows, 16)
                side = g + 1 < groups
                if side:
                    for hb in range(4):
                        side_key(0, g, 0, hb)
                probs(0, g, 0, 0)

                def body_b(i, b, split, project):
                    to = ahead(i, g, b, project)
                    for t in range(TPC):
                        if split and 0 <= t - AHEAD < DT:
                            upper(i, load0 + b + 2, t - AHEAD, v_in_psum, i * (2 * TPC) + TPC * (g * NCH + b + 1))
                        if to:
                            if t < 4:
                                key(to[0], to[1], (to[1] + 1) * NCH + to[2], t, K_BANK)
                            first(*to, t)
                        if t + 1 < TPC:
                            probs(i, g, b, t + 1)
                        elif project:
                            probs(i, g, b + 1, 0)
                        if side and project and t >= 3:
                            side_key(i, g, b + 1, t - 3)

                with act.Fori(0, PAIRS - 1) as i:
                    for b in range(2):
                        body_b(i, b, True, True)
                body_b(PAIRS - 1, 0, g + 1 < groups, True)
                body_b(PAIRS - 1, 1, g + 1 < groups, False)

        @block.vector
        def _(dve):
            chain = Chain(dve, chain_sem)
            chain(nc.vector.memset(ones3[:], 1.0))
            chain(nc.vector.memset(zeros3[:], 0.0))
            chain(nc.vector.memset(v[:, :, :, :, dh:dh + 1].rearrange("p a t h w -> p (a t h) w"), 1.0))
            norm.vector(dve, chain)

            def key_rest(i, g, n0, hb):
                hf, cols = hb // 2, slice((hb % 2) * BLK, (hb % 2 + 1) * BLK)
                load = (g + 1) * NCH + n0
                dve.wait_ge(khi_ready, i * 8 + (4 * load + hb + 1 + RING))
                nc.vector.scalar_tensor_tensor(klo[:, n0 % 2, hf, cols], ps[:, K_BANK, 0:BLK], bk(g, hf),
                                               khi[:, n0 % 2, hf, cols].bitcast(F32), ALU.add,
                                               ALU.subtract).then_inc(klo_ready, 1)

            def value_rest(i, g, n0, t):
                at = (g * NCH + n0) * TPC + t
                dve.wait_ge(v1_ready, i * (2 * TPC) + (at + 1))
                dve.wait_ge(v_ready, i * (2 * TPC) + (at + 1))
                nc.vector.tensor_tensor(vrest[:, at % 2].rearrange("p (h w) -> p h w", h=heads),
                                        ps[:, V_BANK, 0:D].rearrange("p (h w) -> p h w", h=heads),
                                        v[:, n0 % 2, t, :, 0:dh], ALU.subtract).then_inc(rest_ready, 1)

            def value_second(i, g, n0, t):
                at = (g * NCH + n0) * TPC + t
                dve.wait_ge(rest_ready, i * (2 * TPC) + (at + 1 + RING))
                nc.vector.tensor_copy(v[:, n0 % 2, t, :, dh + 1:2 * dh + 1],
                                      vrest[:, at % 2].rearrange("p (h w) -> p h w", h=heads)).then_inc(v2_ready, 1)

            def prob_rest(i, g, n0, t):
                for u in range(units):
                    at = (g * NCH + n0) * CU + t * units + u
                    tile = ((g * NCH + n0) * TPC + t) % 2
                    cols = slice(u * UW, (u + 1) * UW)
                    dve.wait_ge(phi_ready, i * (2 * CU) + (at + 1 + RING))
                    nc.vector.tensor_tensor(plo[:, tile, cols], p32[:, at % 2], phi[:, tile, cols],
                                            ALU.subtract).then_inc(plo_ready, 1)

            def prepare(g):
                m = g % WB
                for hi, lo, w in ((wkh, wkl, wk), (wvh, wvl, wv)):
                    for k in range(DT):
                        last = split(nc, hi[:, m, k], lo[:, m, k], w(g, k), chain)
                    if w is wk:
                        chain(last)
                last.then_inc(weights_split, 1)
                dve.wait_ge(q_in_psum, g + 1)
                for k in range(DT):
                    last = nc.vector.tensor_scalar(qT[:, k, :], ps[:, 1 if g else 4, k * P:(k + 1) * P], bq(g, k),
                                                   scale, ALU.add, ALU.mult)
                chain(last)
                mask = core.constant(f"head{dh}")
                for k in range(DT):
                    chain(nc.vector.tensor_tensor(
                        wide[:, 0:hq].rearrange("p (j q) -> p j q", j=per),
                        qT[:, k, :].unsqueeze(1).to_broadcast([P, per, P]),
                        mask.unsqueeze(2).to_broadcast([P, per, P]), ALU.mult))
                    last = split(nc, qh[:, m, k], ql[:, m, k], wide[:, 0:hq], chain)
                    if k == 0:
                        chain(last)
                last.then_inc(q_ready, 1)

            def side_max_of(i, g, n0, t):
                b = n0 % 2
                for u in side_halves(t):
                    at = (g * NCH + n0) * HALVES + u
                    dve.wait_ge(side_full, i * (2 * HALVES) + (at + 1))
                    nc.vector.tensor_reduce(side_max[:, b, u:u + 1], ps[:, 1 + 2 * (u % 2), 0:BLK], AX.X,
                                            ALU.max).then_inc(side_free, 1)
                if t + 1 == TPC:
                    dve.wait_ge(side_free, i * (2 * HALVES) + ((g * NCH + n0 + 1) * HALVES + RING))
                    if b:
                        dve.wait_ge(side_step, i * 2 + (g * NCH + 1))
                    nc.vector.tensor_tensor(side_run[:], side_run[:], side_max[:, b], ALU.max).then_inc(
                        side_step, 1)
                    if b:
                        dve.wait_ge(side_step, i * 2 + (g * NCH + 2))

            prepare(0)
            chain(nc.vector.memset(run_max[:], -3.0e38))

            def body_a(i, b, last):
                for h in range(heads):
                    at = b * heads + h
                    dve.wait_ge(s_full, i * (2 * heads) + (at + 1))
                    bank = 2 * (at % 2)
                    nc.vector.tensor_reduce(chunk_max[:, b, h:h + 1], ps[:, bank:bank + 2, 0:BLK],
                                            AX.XY, ALU.max).then_inc(s_free, 1)
                    for kind, n in first_pieces(h) if last else ():
                        if kind == "key":
                            key_rest(0, 0, 0, n)
                        else:
                            value_rest(0, 0, 0, n)
                            value_second(0, 0, 0, n)
                dve.wait_ge(s_free, i * (2 * heads) + ((b + 1) * heads + RING))
                if b:
                    dve.wait_ge(max_step, i * 2 + 1)
                nc.vector.tensor_tensor(run_max[:], run_max[:], chunk_max[:, b], ALU.max).then_inc(max_step, 1)
                if b:
                    dve.wait_ge(max_step, i * 2 + 2)

            with dve.Fori(0, PAIRS - 1) as i:
                for b in range(2):
                    body_a(i, b, False)
            for b in range(2):
                body_a(PAIRS - 1, b, b == 1)
            for g in range(groups):
                side = g + 1 < groups
                if g:
                    halves = side_run[:].rearrange("p (h a) -> p h a", a=2)
                    chain(nc.vector.tensor_tensor(run_max[:], halves[:, :, 0], halves[:, :, 1], ALU.max))
                if side:
                    chain(nc.vector.memset(side_run[:], -3.0e38))
                chain(nc.vector.tensor_scalar(neg[:, 0], run_max[:], -1.0, P_SHIFT, ALU.mult, ALU.add))
                for k in range(3):
                    chain(nc.vector.tensor_copy(m3b[:, k], neg[:, k % 2]))
                    if k < 2:
                        chain(nc.vector.tensor_tensor(neg[:, (k + 1) % 2], neg[:, k % 2], m3b[:, k],
                                                      ALU.subtract))
                nc.vector.tensor_copy(m3f[:], m3b[:].rearrange("p a h -> p (a h)")).then_inc(neg_ready, 1)
                dve.wait_ge(m3_in_psum, g + 1)
                nc.vector.tensor_copy(m3T[:], ps[0:3 * heads, 5, 0:P]).then_inc(m3T_ready, 1)
                if side:
                    prepare(g + 1)
                prob_rest(0, g, 0, 0)

                def body_b(i, b, project):
                    to = ahead(i, g, b, project)
                    for t in range(TPC):
                        if to:
                            if t < 4:
                                key_rest(*to, t)
                            value_rest(*to, t)
                        if t + 1 < TPC:
                            prob_rest(i, g, b, t + 1)
                        elif project:
                            prob_rest(i, g, b + 1, 0)
                        if to:
                            value_second(*to, t)
                        if side:
                            side_max_of(i, g, b, t)

                with dve.Fori(0, PAIRS - 1) as i:
                    for b in range(2):
                        body_b(i, b, True)
                body_b(PAIRS - 1, 0, True)
                body_b(PAIRS - 1, 1, False)
                dve.wait_ge(pv_done, (g + 1) * NCH * CU)
                chain(nc.vector.tensor_copy(oa[:].rearrange("p (a j) w -> p a (j w)", a=DT), ps[:, 4:6, 0:BW]))
                o3 = o[:].rearrange("p (h w) -> p h w", h=heads)
                nc.vector.reciprocal(rden[:], oa[:, :, dh:dh + 1])
                chain(nc.vector.tensor_tensor(o3, oa[:, :, 0:dh], oa[:, :, dh + 1:2 * dh + 1], ALU.add))
                chain(nc.vector.tensor_tensor(o3, o3, oa[:, :, 2 * dh + 1:HW], ALU.add))
                last = nc.vector.tensor_tensor(o3, o3, rden[:].to_broadcast([P, heads, dh]), ALU.mult)
                if bv is not None:
                    chain(last)
                    last = nc.vector.tensor_tensor(o[:], o[:], bv(g), ALU.add)
                last.then_inc(o_ready, 1)
                dve.wait_ge(oT_in_psum, g + 1)
                nc.vector.tensor_copy(oT[:].rearrange("p k t -> p (k t)"), ps[:, 4, 0:D]).then_inc(oT_ready, 1)
                dve.wait_ge(y_in_psum, g + 1)
                chain(nc.vector.tensor_tensor(core.x[:], core.x[:], ps[:, 5, 0:D], ALU.add))
                if bo is not None and g == 0:
                    chain(nc.vector.tensor_tensor(core.x[:], core.x[:], bo, ALU.add))

        @block.tensor
        def _(pe):
            norm.tensor(pe)

            def products(out, pairs):
                for n, (lhsT, rhs) in enumerate(pairs):
                    last = nc.tensor.matmul(out, lhsT, rhs, start=(n == 0), stop=(n == len(pairs) - 1))
                return last

            def key_upper(i, load, hb):
                b = load % 2
                hf, cols = slice((hb // 2) * P, (hb // 2 + 1) * P), slice((hb % 2) * BLK, (hb % 2 + 1) * BLK)
                if hb == 0:
                    pe.wait_ge(hi_ready, i * (2 * DT) + DT * (load + 1))
                pe.wait_ge(khi_ready, i * 8 + (4 * load + hb + 1))
                products(ps[:, 6 + hb % 2, 0:BLK],
                         [(wkh[:, 0, k, hf], chi[:, b, k, cols]) for k in range(DT)]).then_inc(k_in_psum, 1)

            def score_upper(i, g, n0, h):
                at = (g * NCH + n0) * heads + h
                pe.wait_ge(s_free, i * (2 * heads) + (at + 1))
                for blk in range(2):
                    last = nc.tensor.matmul(ps[:, 2 * (at % 2) + blk, 0:BLK],
                                            qh[:, 0, h // per, (h % per) * P:(h % per + 1) * P],
                                            khi[:, n0 % 2, h // per, blk * BLK:(blk + 1) * BLK],
                                            start=True, stop=True)
                last.then_inc(s_full, 1)

            def key(i, g, n0, hb):
                b, m = n0 % 2, g % WB
                hf, cols = slice((hb // 2) * P, (hb // 2 + 1) * P), slice((hb % 2) * BLK, (hb % 2 + 1) * BLK)
                if hb == 0:
                    pe.wait_ge(lo_ready, i * (2 * DT) + DT * (g * NCH + n0 + 1))
                if hb == 0 and (g or (n0 and g + 1 < groups)):
                    sided = g + 1 < groups
                    pe.wait_ge(side_k_ready, (i * 8 if sided else 0) + 4 * (g * NCH + (n0 if sided else 0)))
                if g or n0 or hb:
                    pe.wait_ge(klo_ready, i * 8 + (4 * (g * NCH + n0) + hb))
                pairs = []
                for k in range(DT):
                    pairs += [(wkh[:, m, k, hf], chi[:, b, k, cols]), (wkl[:, m, k, hf], chi[:, b, k, cols]),
                              (wkh[:, m, k, hf], clo[:, b, k, cols])]
                products(ps[:, K_BANK, 0:BLK], pairs).then_inc(k_in_psum, 1)

            def value(i, g, n0, t):
                at = (g * NCH + n0) * TPC + t
                b, m = n0 % 2, g % WB
                rows = slice(t * P, (t + 1) * P)
                pe.wait_ge(rest_ready, i * (2 * TPC) + (at + RING))
                pairs = []
                for k in range(DT):
                    pairs += [(chi[:, b, k, rows], wvh[:, m, k]), (clo[:, b, k, rows], wvh[:, m, k]),
                              (chi[:, b, k, rows], wvl[:, m, k])]
                products(ps[:, V_BANK, 0:D], pairs).then_inc(v_in_psum, 1)

            def scores(i, g, n0, t):
                b = n0 % 2
                if t == 0:
                    pe.wait_ge(klo_ready, i * 8 + 4 * (g * NCH + n0 + 1))
                for u in range(units):
                    at = (g * NCH + n0) * CU + t * units + u
                    pe.wait_ge(phi_ready, i * (2 * CU) + (at + 1))
                    slot = 2 * (at % 2)
                    flat = ps[:, slot:slot + 2, :].rearrange("p a n -> p (a n)")
                    for c0 in range(0, UW, 512):
                        nc.tensor.matmul(flat[:, c0:c0 + 512], ones3[:], m3row[:, u * UW + c0:u * UW + c0 + 512],
                                         start=True, stop=False, skip_group_check=True)
                    keys_of = slice(t * P, (t + 1) * P)
                    for k in range(DT) if units == 1 else [u]:
                        for kk, qq in ((khi, qh), (klo, qh), (khi, ql)):
                            for c0 in range(0, hq, 512):
                                w = min(512, hq)
                                at0 = c0 + (k * hq if units == 1 else 0)
                                last = nc.tensor.matmul(flat[:, at0:at0 + w], kk[:, b, k, keys_of],
                                                        qq[:, g % WB, k, c0:c0 + w], start=False, stop=True,
                                                        skip_group_check=True)
                    last.then_inc(st_full, 1)

            def sums(i, g, n0, t):
                b = n0 % 2
                at = (g * NCH + n0) * TPC + t
                pe.wait_ge(v_ready, i * (2 * TPC) + (at + 1 + RING))
                for u in range(units):
                    pe.wait_ge(plo_ready, i * (2 * CU) + (at * units + u + 1 + RING))
                    for h in range(u * heads // units, (u + 1) * heads // units):
                        out = ps[:, 4 + h // per, (h % per) * HW:(h % per + 1) * HW]
                        nc.tensor.matmul(out, phi[:, at % 2, h * P:(h + 1) * P], v[:, b, t, h, :],
                                         start=False, stop=True, skip_group_check=True)
                        last = nc.tensor.matmul(out[:, 0:2 * dh + 1], plo[:, at % 2, h * P:(h + 1) * P],
                                                v[:, b, t, h, 0:2 * dh + 1], start=False, stop=True,
                                                skip_group_check=True)
                    last.then_inc(pv_done, 1)

            def side_key(i, g, n0, hb):
                hf, cols = slice((hb // 2) * P, (hb // 2 + 1) * P), slice((hb % 2) * BLK, (hb % 2 + 1) * BLK)
                if hb:
                    pe.wait_ge(side_k_ready, i * 8 + (4 * (g * NCH + n0) + hb))
                else:
                    pe.wait_ge(klo_ready, i * 8 + 4 * (g * NCH + n0 + 1))
                products(ps[:, K_BANK, 0:BLK], [(wkh[:, (g + 1) % WB, k, hf], chi[:, n0 % 2, k, cols])
                                                for k in range(DT)]).then_inc(side_k_in_psum, 1)

            def side_scores(i, g, n0, t):
                for u in side_halves(t):
                    h, blk = u // 2, u % 2
                    at = (g * NCH + n0) * HALVES + u
                    if u == 0:
                        pe.wait_ge(side_k_ready, i * 8 + 4 * (g * NCH + n0 + 1))
                    pe.wait_ge(side_free, i * (2 * HALVES) + (at + 1))
                    nc.tensor.matmul(ps[:, 1 + 2 * (u % 2), 0:BLK],
                                     qh[:, (g + 1) % WB, h // per, (h % per) * P:(h % per + 1) * P],
                                     side_k[:, n0 % 2, h // per, blk * BLK:(blk + 1) * BLK],
                                     start=True, stop=True).then_inc(side_full, 1)

            def query(g, bank):
                for hf in range(DT):
                    last = products(ps[:, bank, hf * P:(hf + 1) * P],
                                    [(wq(g, k, hf), norm.xnT[:, k, :]) for k in range(DT)])
                last.then_inc(q_in_psum, 1)

            pe.wait_ge(norm.xT_ready, 1)
            query(0, 4)
            pe.wait_ge(weights_split, 1)

            def body_a(i, b, project):
                pe.wait_ge(khi_ready, i * 8 + (4 * (b + 1) + RING))
                for h in range(heads):
                    if project and h % (heads // 4) == 0:
                        key_upper(i, b + 1, h // (heads // 4))
                    score_upper(i, 0, b, h)
                    for kind, n in () if project else first_pieces(h):
                        (key if kind == "key" else value)(0, 0, 0, n)

            for hb in range(4):
                key_upper(0, 0, hb)
            pe.wait_ge(q_ready, 1)
            with pe.Fori(0, PAIRS - 1) as i:
                for b in range(2):
                    body_a(i, b, True)
            body_a(PAIRS - 1, 0, True)
            body_a(PAIRS - 1, 1, False)
            for g in range(groups):
                side = g + 1 < groups
                pe.wait_ge(hi_ready, DT * ((g + 1) * NCH + 1))
                pe.wait_ge(neg_ready, g + 1)
                nc.tensor.transpose(ps[0:3 * heads, 5, 0:P], m3f[:], ident).then_inc(m3_in_psum, 1)
                if side:
                    query(g + 1, 1)
                    pe.wait_ge(weights_split, g + 2)
                    for hb in range(4):
                        side_key(0, g, 0, hb)
                    pe.wait_ge(q_ready, g + 2)
                pe.wait_ge(m3_rows, 16 * (g + 1))
                for bank in (4, 5):
                    nc.tensor.matmul(ps[:, bank, 0:BW], zeros3[:], m3row[:, 0:BW], start=True, stop=False,
                                     skip_group_check=True)
                scores(0, g, 0, 0)

                def body_b(i, b, project):
                    to = ahead(i, g, b, project)
                    for t in range(TPC):
                        if to:
                            if t < 4:
                                key(*to, t)
                            value(*to, t)
                        if t + 1 < TPC:
                            scores(i, g, b, t + 1)
                        elif project:
                            scores(i, g, b + 1, 0)
                        if side and project and t >= 3:
                            side_key(i, g, b + 1, t - 3)
                        sums(i, g, b, t)
                        if side:
                            side_scores(i, g, b, t)

                with pe.Fori(0, PAIRS - 1) as i:
                    for b in range(2):
                        body_b(i, b, True)
                body_b(PAIRS - 1, 0, True)
                body_b(PAIRS - 1, 1, False)
                pe.wait_ge(o_ready, g + 1)
                for k in range(DT):
                    last = nc.tensor.transpose(ps[:, 4, k * P:(k + 1) * P], o[:, k * P:(k + 1) * P], ident)
                last.then_inc(oT_in_psum, 1)
                pe.wait_ge(oT_ready, g + 1)
                products(ps[:, 5, 0:D], [(oT[:, k, :], wo(g, k)) for k in range(DT)]).then_inc(y_in_psum, 1)



class RowSoftmax:

    def __init__(self, core, scope, heads, width, per_bank, scale, mask):
        self.nc, self.ps, self.ident = core.nc, core.psum, core.ident()
        self.heads, self.width, self.per_bank, self.scale, self.mask = heads, width, per_bank, scale, mask
        self.p = scope.sb("p", [P, heads, width])
        self.top = scope.sb("top", [P, heads])
        self.pT = scope.sb("pT", [P, heads, P])
        self.s_in_psum, self.shifted, self.exp_done, self.pT_in_psum, self.pT_ready = scope.signals(
            "s_in_psum shifted exp_done pT_in_psum pT_ready")

    def bc(self, a, width):
        return a.unsqueeze(2).to_broadcast([P, self.heads, width])

    def vector(self, dve, chain):
        nc = self.nc
        dve.wait_ge(self.s_in_psum, 1)
        for h in range(0, self.heads, self.per_bank):
            n = min(self.per_bank, self.heads - h)
            src = self.ps[:, h // self.per_bank, 0:n * self.width].rearrange("p (h c) -> p h c", h=n)
            last = nc.vector.scalar_tensor_tensor(self.p[:, h:h + n], src, self.scale,
                                                  self.mask.unsqueeze(1).to_broadcast([P, n, self.width]),
                                                  ALU.mult, ALU.add)
        chain(last)
        chain(nc.vector.tensor_reduce(self.top[:], self.p[:], AX.X, ALU.max))
        nc.vector.tensor_tensor(self.p[:], self.p[:], self.bc(self.top[:], self.width), ALU.subtract).then_inc(
            self.shifted, 1)
        dve.wait_ge(self.exp_done, 1)
        chain(nc.vector.tensor_reduce(self.top[:], self.p[:], AX.X, ALU.add))
        chain(nc.vector.reciprocal(self.top[:], self.top[:]))
        dve.wait_ge(self.pT_in_psum, 1)
        for b in range(0, self.heads // 4, 2):
            last = nc.vector.tensor_copy(self.pT[:, 4 * b:4 * b + 8].rearrange("p h q -> p (h q)"),
                                         self.ps[:, b:b + 2, :].rearrange("p b n -> p (b n)"))
        last.then_inc(self.pT_ready, 1)

    def scalar(self, act):
        act.wait_ge(self.shifted, 1)
        flat = self.p[:].rearrange("p h c -> p (h c)")
        self.nc.scalar.activation(flat, flat, ACT.Exp).then_inc(self.exp_done, 1)

    def tensor(self, pe):
        pe.wait_ge(self.exp_done, 1)
        for h in range(self.heads):
            last = self.nc.tensor.transpose(self.ps[:, h // 4, (h % 4) * P:(h % 4 + 1) * P],
                                            self.p[:, h, 0:P], self.ident)
        last.then_inc(self.pT_in_psum, 1)


def transposed(nc, ps, bank, src, tiles, ident, signal):
    for k in range(tiles):
        last = nc.tensor.transpose(ps[:, bank + k // 4, (k % 4) * P:(k % 4 + 1) * P],
                                   src[:, k * P:(k + 1) * P], ident)
    last.then_inc(signal, 1)


def projected(nc, out, xT, w, tiles, signal, start=True):
    for k in range(tiles):
        last = nc.tensor.matmul(out, xT[:, k, :], w[:, k], start=(k == 0), stop=(k == tiles - 1))
    if signal is not None:
        last.then_inc(signal, 1)


def l0_attn(core):
    nc, ps, ident = core.nc, core.psum, core.ident()
    H, DH = 16, 64
    with Scope(core, "l0a") as s:
        outer = Norm(core, s)
        inner = Norm(core, s, outer.xn[:], core.weight("gamma"), "inner")
        order = [h for n in range(2) for h in range(n, H, 2)]
        soft = RowSoftmax(core, s, H, P + 2, 2, 8.0, core.constant("prefix_mask"))
        q, sq, qT = s.sb("q", [P, H, DH]), s.sb("sq", [P, H, DH]), s.sb("qT", [P, 8, P])
        k, v = s.sb("k", [P, DH]), s.sb("v", [P, DH])
        kk, nk = s.sb("kk", [P, 2, DH]), s.sb("nk", [2, 2, DH])
        kT = s.sb("kT", [P, P + 2])
        ss, rn = s.sb("ss", [P, H + 2]), s.sb("rn", [P, H + 2])
        pn, pnT = s.sb("pn", [P, 2 * H]), s.sb("pnT", [2 * H, P])
        o, oT = s.sb("o", [P, H * DH]), s.sb("oT", [P, 8, P])
        (chain_sem, kv_in_psum, q_in_psum, squares, norms, qk_ready, qkT_in_psum, qkT_ready, pn_ready,
         pnT_in_psum, pnT_ready, o_in_psum, o_ready, oT_in_psum, oT_ready, y_in_psum) = s.signals(
            "chain_sem kv_in_psum q_in_psum squares norms qk_ready qkT_in_psum qkT_ready pn_ready "
            "pnT_in_psum pnT_ready o_in_psum o_ready oT_in_psum oT_ready y_in_psum")
        block = s.ctx.enter_context(nc.Block())

        @block.vector
        def _(dve):
            chain = Chain(dve, chain_sem)
            outer.vector(dve, chain)
            inner.vector(dve, chain)
            null_k = core.weight("null_k")[0:2, :]
            chain(nc.vector.memset(ss[:], 1.0))
            dve.wait_ge(kv_in_psum, 1)
            nc.vector.tensor_copy(k[:], ps[:, 0, 0:DH])
            chain(nc.vector.tensor_copy(v[:], ps[:, 0, DH:2 * DH]))
            dve.wait_ge(q_in_psum, 1)
            chain(nc.vector.tensor_copy(q[:].rearrange("p h d -> p (h d)"),
                                        ps[:, 1:3, :].rearrange("p b n -> p (b n)")))
            chain(nc.vector.tensor_tensor(sq[:], q[:], q[:], ALU.mult))
            chain(nc.vector.tensor_reduce(ss[:, 0:H], sq[:], AX.X, ALU.add))
            chain(nc.vector.tensor_tensor(sq[:, 0], k[:], k[:], ALU.mult))
            chain(nc.vector.tensor_reduce(ss[:, H:H + 1], sq[:, 0], AX.X, ALU.add))
            chain(nc.vector.tensor_tensor(sq[0:2, 1], null_k, null_k, ALU.mult))
            nc.vector.tensor_reduce(ss[0:2, H + 1:H + 2], sq[0:2, 1], AX.X, ALU.add).then_inc(squares, 1)
            dve.wait_ge(norms, 1)
            chain(nc.vector.tensor_scalar(rn[:], rn[:], 1e-12, None, ALU.max))
            chain(nc.vector.reciprocal(rn[:], rn[:]))
            chain(nc.vector.tensor_tensor(q[:], q[:], rn[:, 0:H].unsqueeze(2).to_broadcast([P, H, DH]), ALU.mult))
            nc.vector.tensor_tensor(q[:], q[:], core.weight("qs").unsqueeze(1).to_broadcast([P, H, DH]), ALU.mult)
            for n in range(2):
                nc.vector.scalar_tensor_tensor(kk[:, n], k[:], rn[:, H:H + 1], core.weight("ks"), ALU.mult, ALU.mult)
                last = nc.vector.scalar_tensor_tensor(nk[:, n], null_k, rn[0:2, H + 1:H + 2],
                                                      core.weight("ks")[0:2, :], ALU.mult, ALU.mult)
            last.then_inc(qk_ready, 1)
            dve.wait_ge(qkT_in_psum, 1)
            nc.vector.tensor_copy(qT[:].rearrange("p t n -> p (t n)"), ps[:, 0:2, :].rearrange("p b n -> p (b n)"))
            nc.vector.tensor_copy(kT[:], ps[:, 3, 0:P + 2]).then_inc(qkT_ready, 1)
            soft.vector(dve, chain)
            nc.vector.tensor_copy(pn[:].rearrange("p (h n) -> p h n", h=H), soft.p[:, :, P:P + 2]).then_inc(
                pn_ready, 1)
            dve.wait_ge(pnT_in_psum, 1)
            nc.vector.tensor_copy(pnT[:], ps[0:2 * H, 4, 0:P]).then_inc(pnT_ready, 1)
            dve.wait_ge(o_in_psum, 1)
            heads = lambda a: a.rearrange("p (m n d) -> p n m d", n=2, d=DH)
            for n in range(2):
                last = nc.vector.tensor_tensor(
                    heads(o[:])[:, n], heads(ps[:, 5:7, :].rearrange("p b n -> p (b n)"))[:, n],
                    soft.top[:, 8 * n:8 * n + 8].unsqueeze(2).to_broadcast([P, 8, DH]), ALU.mult)
            last.then_inc(o_ready, 1)
            dve.wait_ge(oT_in_psum, 1)
            nc.vector.tensor_copy(oT[:].rearrange("p t n -> p (t n)"),
                                  ps[:, 0:2, :].rearrange("p b n -> p (b n)")).then_inc(oT_ready, 1)
            dve.wait_ge(y_in_psum, 1)
            nc.vector.tensor_tensor(core.x[:], core.x[:], ps[:, 2, 0:D], ALU.add)

        @block.scalar
        def _(act):
            outer.scalar(act)
            inner.scalar(act)
            act.wait_ge(squares, 1)
            nc.scalar.activation(rn[:], ss[:], ACT.Sqrt).then_inc(norms, 1)
            soft.scalar(act)

        @block.tensor
        def _(pe):
            outer.tensor(pe)
            pe.wait_ge(outer.xT_ready, 1)
            projected(nc, ps[:, 0, 0:2 * DH], outer.xnT, core.kxn("akv"), DT, kv_in_psum)
            inner.tensor(pe)
            pe.wait_ge(inner.xT_ready, 1)
            wq = core.kxn("aq")
            for n in range(2):
                projected(nc, ps[:, 1 + n, :], inner.xnT, wq[:, :, n * 512:(n + 1) * 512], DT,
                          q_in_psum if n else None)
            pe.wait_ge(qk_ready, 1)
            for t in range(8):
                nc.tensor.transpose(ps[:, t // 4, (t % 4) * P:(t % 4 + 1) * P],
                                    q[:].rearrange("p h d -> p (h d)")[:, t * P:(t + 1) * P], ident)
            nc.tensor.transpose(ps[:, 3, 0:P], kk[:].rearrange("p n d -> p (n d)"), ident)
            nc.tensor.transpose(ps[:, 3, P:P + 2], nk[:].rearrange("p n d -> p (n d)"),
                                core.ident(2)).then_inc(qkT_in_psum, 1)
            pe.wait_ge(qkT_ready, 1)
            for n, h in enumerate(order):
                at = DH * (h % 2)
                last = nc.tensor.matmul(ps[:, n // 2, (n % 2) * (P + 2):(n % 2 + 1) * (P + 2)],
                                        qT[at:at + DH, h // 2, :], kT[at:at + DH, :], start=True, stop=True)
            last.then_inc(soft.s_in_psum, 1)
            soft.tensor(pe)
            pe.wait_ge(pn_ready, 1)
            nc.tensor.transpose(ps[0:2 * H, 4, 0:P], pn[:], ident).then_inc(pnT_in_psum, 1)
            pe.wait_ge(pnT_ready, 1)
            pe.wait_ge(soft.pT_ready, 1)
            nv = core.weight("null_v")[0:2 * H, :]
            for n in range(2):
                nc.tensor.matmul(ps[:, 5 + n, :], pnT[:], nv[:, n * 512:(n + 1) * 512], start=True, stop=False,
                                 skip_group_check=True)
                for h in range(8 * n, 8 * n + 8):
                    last = nc.tensor.matmul(ps[:, 5 + n, (h % 8) * DH:(h % 8 + 1) * DH], soft.pT[:, order.index(h), :], v[:],
                                            start=False, stop=(h % 8 == 7), skip_group_check=True)
            last.then_inc(o_in_psum, 1)
            pe.wait_ge(o_ready, 1)
            transposed(nc, ps, 0, o, 8, ident, oT_in_psum)
            pe.wait_ge(oT_ready, 1)
            projected(nc, ps[:, 2, 0:D], oT, core.kxn("ao", 8), 8, y_in_psum)


def l0_ffn(core):
    nc, ps = core.nc, core.psum
    with Scope(core, "l0f") as s:
        norm = Norm(core, s)
        mix = s.sb("mix", [P, 2, DT, P])
        omu = s.sb("omu", [P, 2 * DT])
        kact = s.sb("kact", [P, DT, P])
        r, y = s.sb("r", [P, D]), s.sb("y", [P, D])
        chain_sem, mixed, r_in_psum, k_in_psum, k_ready, r_ready, y_in_psum = s.signals(
            "chain_sem mixed r_in_psum k_in_psum k_ready r_ready y_in_psum")
        block = s.ctx.enter_context(nc.Block())

        @block.vector
        def _(dve):
            chain = Chain(dve, chain_sem)
            norm.vector(dve, chain)
            for n, mu in enumerate((core.weight("mu_r"), core.weight("mu_k"))):
                nc.vector.tensor_scalar(omu[:, 2 * n:2 * n + 2], mu, -1.0, 1.0, ALU.mult, ALU.add)
                for k in range(DT):
                    last = nc.vector.tensor_scalar(mix[:, n, k], norm.xnT[:, k], mu[:, k:k + 1], None, ALU.mult)
            chain(last)
            for n in range(2):
                for k in range(DT):
                    last = nc.vector.scalar_tensor_tensor(
                        mix[:, n, k, 1:P], norm.xnT[:, k, 0:P - 1], omu[:, 2 * n + k:2 * n + k + 1],
                        mix[:, n, k, 1:P], ALU.mult, ALU.add)
            last.then_inc(mixed, 1)
            dve.wait_ge(k_in_psum, 1)
            kflat = kact[:].rearrange("p k t -> p (k t)")
            chain(nc.vector.tensor_scalar(kflat, ps[:, 1, 0:D], 0.0, None, ALU.max))
            nc.vector.tensor_tensor(kflat, kflat, kflat, ALU.mult).then_inc(k_ready, 1)
            dve.wait_ge(y_in_psum, 1)
            dve.wait_ge(r_ready, 1)
            chain(nc.vector.tensor_tensor(y[:], ps[:, 2, 0:D], r[:], ALU.mult))
            nc.vector.tensor_tensor(core.x[:], core.x[:], y[:], ALU.add)

        @block.scalar
        def _(act):
            norm.scalar(act)
            act.wait_ge(r_in_psum, 1)
            nc.scalar.activation(r[:], ps[:, 0, 0:D], ACT.Sigmoid).then_inc(r_ready, 1)

        @block.tensor
        def _(pe):
            norm.tensor(pe)
            pe.wait_ge(mixed, 1)
            projected(nc, ps[:, 0, 0:D], mix[:, 0], core.kxn("fr"), DT, r_in_psum)
            wk = core.kxn("fk")
            for half in range(DT):
                for k in range(DT):
                    last = nc.tensor.matmul(ps[:, 1, half * P:(half + 1) * P], wk[:, k, half * P:(half + 1) * P],
                                            mix[:, 1, k], start=(k == 0), stop=(k == DT - 1))
            last.then_inc(k_in_psum, 1)
            pe.wait_ge(k_ready, 1)
            projected(nc, ps[:, 2, 0:D], kact, core.kxn("fv"), DT, y_in_psum)


def l1_attn(core):
    nc, ps, ident = core.nc, core.psum, core.ident()
    H, DK, DV, C = 4, 64, 128, 64
    with Scope(core, "l1a") as s:
        norm = Norm(core, s)
        qT, kT = s.sb("qT", [P, DT, P]), s.sb("kT", [P, DT, P])
        low = s.sb("low", [16, P])
        z, az, g = s.sb("z", [P, DT, P]), s.sb("az", [P, DT, P]), s.sb("g", [P, DT, P])
        b, eb, enb, blast = s.sb("b", [P, DT, P]), s.sb("eb", [P, DT, P]), s.sb("enb", [P, DT, P]), s.sb("bl", [P, DT, C])
        qg, kg, kh = s.sb("qg", [P, DT, P]), s.sb("kg", [P, DT, P]), s.sb("kh", [P, DT, C])
        ones = s.sb("ones", [P, C])
        v, gate, sig = s.sb("v", [P, H * DV]), s.sb("gate", [P, H * DV]), s.sb("sig", [P, H * DV])
        at = s.sb("at", [P, H, P])
        o, sq = s.sb("o", [P, H, DV]), s.sb("sq", [P, H, DV])
        ms, rms = s.sb("ms", [P, H]), s.sb("rms", [P, H])
        oT = s.sb("oT", [P, H, P])
        (chain_sem, low_in_psum, low_ready, z_in_psum, az_ready, soft_ready, b_ready, eb_ready, qk_in_psum, qk_ready,
         gates_ready, v_in_psum, v_ready, g_in_psum, g_ready, a_in_psum, a_ready, o_in_psum, ms_ready, rms_ready,
         o_ready, oT_in_psum, oT_ready, y_in_psum) = s.signals(
            "chain_sem low_in_psum low_ready z_in_psum az_ready soft_ready b_ready eb_ready qk_in_psum qk_ready "
            "gates_ready v_in_psum v_ready g_in_psum g_ready a_in_psum a_ready o_in_psum ms_ready rms_ready "
            "o_ready oT_in_psum oT_ready y_in_psum")
        flat = lambda t: t[:].rearrange("p k t -> p (k t)")
        block = s.ctx.enter_context(nc.Block())

        @block.vector
        def _(dve):
            chain = Chain(dve, chain_sem)
            norm.vector(dve, chain)
            chain(nc.vector.memset(ones[:], 1.0))
            dve.wait_ge(low_in_psum, 1)
            nc.vector.tensor_copy(low[:], ps[0:16, 0, 0:P]).then_inc(low_ready, 1)
            dve.wait_ge(z_in_psum, 1)
            for k in range(DT):
                last = nc.vector.tensor_scalar(z[:, k], ps[:, 1, k * P:(k + 1) * P], core.weight("gkb")[:, k:k + 1],
                                               None, ALU.add)
            chain(last)
            chain(nc.vector.tensor_scalar(az[:], z[:], -1.0, None, ALU.mult))
            nc.vector.tensor_tensor(az[:], az[:], z[:], ALU.min).then_inc(az_ready, 1)
            dve.wait_ge(az_ready, 1)
            chain(nc.vector.tensor_scalar(z[:], z[:], 0.0, None, ALU.min))
            dve.wait_ge(soft_ready, 1)
            chain(nc.vector.tensor_tensor(g[:], z[:], az[:], ALU.subtract))
            chain(nc.vector.tensor_scalar(g[:], g[:], 1.0 / 16.0, None, ALU.mult))
            for k in range(DT):
                for c in range(2):
                    last = nc.vector.tensor_tensor_scan(b[:, k, c * C:(c + 1) * C], ones[:],
                                                        g[:, k, c * C:(c + 1) * C], 0.0, ALU.mult, ALU.add)
            chain(last)
            for k in range(DT):
                last = nc.vector.tensor_scalar(blast[:, k], b[:, k, 0:C], -1.0, b[:, k, C - 1:C], ALU.mult, ALU.add)
            last.then_inc(b_ready, 1)
            dve.wait_ge(qk_in_psum, 1)
            chain(nc.vector.tensor_copy(flat(kT), ps[:, 3, 0:D]))
            dve.wait_ge(eb_ready, 1)
            chain(nc.vector.scalar_tensor_tensor(flat(qg), ps[:, 2, 0:D], DK ** -0.5, flat(eb), ALU.mult, ALU.mult))
            nc.vector.tensor_tensor(kg[:], kT[:], enb[:], ALU.mult)
            nc.vector.tensor_tensor(kh[:], kT[:, :, 0:C], blast[:], ALU.mult).then_inc(gates_ready, 1)
            dve.wait_ge(a_in_psum, 1)
            mask = core.constant("chunk_mask").unsqueeze(1).to_broadcast([P, 2, P])
            for n in range(2):
                last = nc.vector.tensor_tensor(at[:, n:H:2], ps[:, n, 0:2 * P].rearrange("p (h t) -> p h t", h=2),
                                               mask, ALU.mult)
            chain(last)
            for n in range(2):
                last = nc.vector.tensor_copy(at[0:C, n:H:2, C:P],
                                             ps[0:C, 2 + n, 0:2 * C].rearrange("p (h t) -> p h t", h=2))
            last.then_inc(a_ready, 1)
            dve.wait_ge(o_in_psum, 1)
            chain(nc.vector.tensor_copy(o[:].rearrange("p h d -> p (h d)"), ps[:, 6, :]))
            chain(nc.vector.tensor_tensor(sq[:], o[:], o[:], ALU.mult))
            chain(nc.vector.tensor_reduce(ms[:], sq[:], AX.X, ALU.add))
            nc.vector.tensor_scalar(ms[:], ms[:], 1.0 / DV, 1e-5, ALU.mult, ALU.add).then_inc(ms_ready, 1)
            dve.wait_ge(rms_ready, 1)
            chain(nc.vector.reciprocal(rms[:], rms[:]))
            chain(nc.vector.tensor_tensor(o[:], o[:], rms[:].unsqueeze(2).to_broadcast([P, H, DV]), ALU.mult))
            chain(nc.vector.tensor_tensor(o[:], o[:], core.weight("gn").unsqueeze(1).to_broadcast([P, H, DV]),
                                          ALU.mult))
            dve.wait_ge(g_ready, 2)
            oflat = o[:].rearrange("p h d -> p (h d)")
            chain(nc.vector.tensor_tensor(oflat, oflat, gate[:], ALU.mult))
            nc.vector.tensor_tensor(oflat, oflat, sig[:], ALU.mult).then_inc(o_ready, 1)
            dve.wait_ge(oT_in_psum, 1)
            nc.vector.tensor_copy(oT[:].rearrange("p h t -> p (h t)"), ps[:, 2, :]).then_inc(oT_ready, 1)
            dve.wait_ge(y_in_psum, 1)
            nc.vector.tensor_tensor(core.x[:], core.x[:], ps[:, 3, 0:D], ALU.add)

        @block.scalar
        def _(act):
            chain = Chain(act, qk_ready)
            norm.scalar(act)
            act.wait_ge(az_ready, 1)
            chain(nc.scalar.activation(az[:], az[:], ACT.Exp))
            nc.scalar.activation(az[:], az[:], ACT.Ln, bias=core.constant("one")).then_inc(soft_ready, 1)
            act.wait_ge(v_in_psum, 1)
            nc.scalar.activation(v[:], ps[:, 4, :], ACT.Copy).then_inc(v_ready, 1)
            act.wait_ge(g_in_psum, 1)
            nc.scalar.activation(gate[:], ps[:, 5, :], ACT.Copy).then_inc(g_ready, 1)
            act.wait_ge(b_ready, 1)
            chain(nc.scalar.activation(flat(eb), flat(b), ACT.Exp))
            nc.scalar.activation(flat(enb), flat(b), ACT.Exp, scale=-1.0)
            nc.scalar.activation(blast[:].rearrange("p k t -> p (k t)"), blast[:].rearrange("p k t -> p (k t)"),
                                 ACT.Exp).then_inc(eb_ready, 1)
            nc.scalar.activation(sig[:], ps[:, 5, :], ACT.Sigmoid).then_inc(g_ready, 1)
            act.wait_ge(ms_ready, 1)
            nc.scalar.activation(rms[:], ms[:], ACT.Sqrt).then_inc(rms_ready, 1)

        @block.tensor
        def _(pe):
            norm.tensor(pe)
            pe.wait_ge(norm.xT_ready, 1)
            for k in range(DT):
                last = nc.tensor.matmul(ps[0:16, 0, 0:P], core.kxn("gk1")[:, k, :], norm.xnT[:, k, :],
                                        start=(k == 0), stop=(k == DT - 1))
            last.then_inc(low_in_psum, 1)
            for name, bank in (("gq", 2), ("gk", 3)):
                w = core.kxn(name)
                for half in range(DT):
                    for k in range(DT):
                        last = nc.tensor.matmul(ps[:, bank, half * P:(half + 1) * P],
                                                w[:, k, half * P:(half + 1) * P], norm.xnT[:, k, :],
                                                start=(k == 0), stop=(k == DT - 1))
            last.then_inc(qk_in_psum, 1)
            projected(nc, ps[:, 4, :], norm.xnT, core.kxn("gv"), DT, v_in_psum)
            projected(nc, ps[:, 5, :], norm.xnT, core.kxn("gg"), DT, g_in_psum)
            pe.wait_ge(low_ready, 1)
            for half in range(DT):
                last = nc.tensor.matmul(ps[:, 1, half * P:(half + 1) * P],
                                        core.weight("gk2")[0:16, half * P:(half + 1) * P], low[:],
                                        start=True, stop=True)
            last.then_inc(z_in_psum, 1)
            pe.wait_ge(gates_ready, 1)
            for h in range(H):
                r = slice(DK * (h % 2), DK * (h % 2) + DK)
                nc.tensor.matmul(ps[:, h % 2, (h // 2) * P:(h // 2 + 1) * P], kg[r, h // 2, :], qg[r, h // 2, :],
                                 start=True, stop=True)
            for h in range(H):
                r = slice(DK * (h % 2), DK * (h % 2) + DK)
                last = nc.tensor.matmul(ps[0:C, 2 + h % 2, (h // 2) * C:(h // 2 + 1) * C], kh[r, h // 2, :], qg[r, h // 2, C:P],
                                        start=True, stop=True)
            last.then_inc(a_in_psum, 1)
            pe.wait_ge(a_ready, 1)
            pe.wait_ge(v_ready, 1)
            for h in range(H):
                last = nc.tensor.matmul(ps[:, 6, h * DV:(h + 1) * DV], at[:, h, :], v[:, h * DV:(h + 1) * DV],
                                        start=True, stop=True)
            last.then_inc(o_in_psum, 1)
            pe.wait_ge(o_ready, 1)
            transposed(nc, ps, 2, o[:].rearrange("p h d -> p (h d)"), H, ident, oT_in_psum)
            pe.wait_ge(oT_ready, 1)
            projected(nc, ps[:, 3, 0:D], oT, core.kxn("go", 4), 4, y_in_psum)


def l0_xattn(core):
    cross_attention(core, "l0x", 16, 1, *cross_weights(core, 1), 0.25)


def l1_xattn(core):
    cross_attention(core, "l1x", 16, 1, *cross_weights(core, 1), 0.25)


def l2_xattn(core):
    nc, ps, ident = core.nc, core.psum, core.ident()
    PAIRS = NCH // 2
    RING = 2
    with Scope(core, "l2x") as s:
        norm = Norm(core, s)
        ctxb = s.sb("ctx", [P, 2, 2, CH])
        chi, clo = s.sb("chi", [P, 2, DT * CH], F32R), s.sb("clo", [P, 2, DT * CH], F32R)
        scores = s.sb("scores", [P, KEYS])
        p32 = s.sb("p32", [P, 2, CH])
        pThi, pTlo = s.sb("pThi", [P, 2, CH], F32R), s.sb("pTlo", [P, 2, CH], F32R)
        qT, qk = s.sb("qT", [P, DT, P]), s.sb("qk", [P, DT, P])
        qh, ql = s.sb("qh", [P, DT, P], F32R), s.sb("ql", [P, DT, P], F32R)
        qb = s.sb("qb", [P, 1])
        part, run = s.sb("part", [P, 2, 1]), s.sb("run", [P, 2])
        neg, rden = s.sb("neg", [P, 1]), s.sb("rden", [P, 1])
        zeros = s.sb("zeros", [3, D], BF16)
        o, oT = s.sb("o", [P, D]), s.sb("oT", [P, DT, P])
        (q_in_psum, qT_ready, qk_in_psum, qk_ready, hi_ready, lo_ready, lo2_ready, used, kept, part_ready, step, neg_ready,
         exp_ready, pT_in_psum, pThi_ready, pTlo_ready, o_ready, oT_in_psum, oT_ready, y_in_psum,
         chain_sem) = s.signals(
            "q_in_psum qT_ready qk_in_psum qk_ready hi_ready lo_ready lo2_ready used kept part_ready step neg_ready "
            "exp_ready pT_in_psum pThi_ready pTlo_ready o_ready oT_in_psum oT_ready y_in_psum chain_sem")
        ctx_in = s.signals("ctx_in00 ctx_in01 ctx_in10 ctx_in11")
        split_by = (lo_ready, lo2_ready)
        ctxT = core.dram["ctxT"].rearrange("(k p) n -> p k n", p=P)
        ctxN = core.dram["ctx"].rearrange("(p t) d -> p (t d)", p=P)
        by_tile = scores[:].rearrange("q (p t) -> q t p", p=P)

        def pT_psum(b):
            return ps[:, 2 * b:2 * b + 2, :].rearrange("p a n -> p (a n)")[:, 0:CH]

        block = s.ctx.enter_context(nc.Block())

        @block.sync
        def _(sp):
            with sp.Fori(0, PAIRS) as i:
                for b in range(2):
                    for k in range(2):
                        sp.wait_ge(split_by[k], i * 2 + (b + 1))
                        sp.dma_start(ctxb[:, b, k], ctxT[:, k, bass.ds(i * (2 * CH) + b * CH, CH)]).then_inc(
                            ctx_in[2 * b + k], 16)
            with sp.Fori(0, PAIRS) as i:
                for b in range(2):
                    for k in range(2):
                        sp.wait_ge(split_by[k], i * 2 + (NCH + b + 1))
                        sp.dma_start(ctxb[:, b, k], ctxN[:, bass.ds(i * (4 * CH) + (2 * b + k) * CH, CH)]).then_inc(
                            ctx_in[2 * b + k], 16)

        @block.gpsimd
        def _(pool):
            pool.sem_inc(lo_ready, RING)
            pool.sem_inc(lo2_ready, RING)
            pool.sem_inc(used, RING)
            pool.sem_inc(kept, RING)
            pool.sem_inc(pTlo_ready, RING)
            with pool.Fori(0, NCH) as i:
                for b in range(2):
                    pool.wait_ge(hi_ready, i * 4 + (2 * b + 1))
                    nc.gpsimd.tensor_tensor(clo[:, b, 0:CH], ctxb[:, b, 0], chi[:, b, 0:CH].bitcast(F32),
                                            ALU.subtract).then_inc(lo_ready, 1)

        @block.scalar
        def _(act):
            norm.scalar(act)

            def upper(i, load):
                b = load % 2
                act.wait_ge(used, i * 2 + (load + 1))
                for k in range(2):
                    act.wait_ge(ctx_in[2 * b + k], i * 16 + (load // 2 + 1) * 16)
                    nc.scalar.activation(chi[:, b, k * CH:(k + 1) * CH], ctxb[:, b, k], ACT.Copy).then_inc(
                        hi_ready, 1)

            def exps(i, n0):
                b = n0 % 2
                if n0 > 1:
                    act.wait_ge(part_ready, i * 2 + (NCH + n0 - 1))
                nc.scalar.activation(p32[:, b].rearrange("q (t p) -> q t p", t=TPC),
                                     by_tile[:, bass.ds(i * (2 * TPC) + n0 * TPC, TPC), :], ACT.Exp,
                                     bias=neg[:]).then_inc(exp_ready, 1)

            def body_b(i, b, more):
                if more:
                    exps(i, b + 1)
                act.wait_ge(pT_in_psum, i * 2 + (b + 1))
                nc.scalar.activation(pThi[:, b], pT_psum(b), ACT.Copy).then_inc(pThi_ready, 1)
                if more:
                    upper(i, NCH + b + 1)

            upper(0, 0)
            act.wait_ge(qk_ready, 1)
            with act.Fori(0, PAIRS) as i:
                for b in range(2):
                    upper(i, b + 1)
                    act.wait_ge(used, i * 2 + (b + 1 + RING))
                    nc.scalar.activation(
                        scores[:, bass.ds(i * (2 * CH) + b * CH, CH)].rearrange("p (a n) -> p a n", a=2),
                        ps[:, 2 * b:2 * b + 2, 0:BLK], ACT.Identity, bias=qb[:]).then_inc(kept, 1)
            act.wait_ge(neg_ready, 1)
            exps(0, 0)
            with act.Fori(0, PAIRS - 1) as i:
                for b in range(2):
                    body_b(i, b, True)
            body_b(PAIRS - 1, 0, True)
            body_b(PAIRS - 1, 1, False)

        @block.vector
        def _(dve):
            chain = Chain(dve, chain_sem)
            norm.vector(dve, chain)
            nc.vector.memset(zeros[:], 0.0)
            nc.vector.memset(run[:, 1:2], 0.0)
            chain(nc.vector.memset(run[:, 0:1], -3.0e38))
            dve.wait_ge(q_in_psum, 1)
            for k in range(DT):
                last = nc.vector.tensor_scalar(qT[:, k, :], ps[:, 4, k * P:(k + 1) * P],
                                               core.weight("xbq")[:, k:k + 1], D ** -0.5, ALU.add, ALU.mult)
            last.then_inc(qT_ready, 1)
            dve.wait_ge(qk_in_psum, 1)
            nc.vector.tensor_copy(qb[:], ps[:, 5, D:D + 1])
            qk_flat, qh_flat, ql_flat = (t[:].rearrange("p k t -> p (k t)") for t in (qk, qh, ql))
            chain(nc.vector.tensor_copy(qk_flat, ps[:, 5, 0:D]))
            split(nc, qh_flat, ql_flat, qk_flat, chain).then_inc(qk_ready, 1)

            def joined(i, count, col, b, op):
                dve.wait_ge(part_ready, i * 2 + (count + 1))
                if b:
                    dve.wait_ge(step, i * 2 + count)
                nc.vector.tensor_tensor(run[:, col:col + 1], run[:, col:col + 1], part[:, b], op).then_inc(step, 1)
                if b:
                    dve.wait_ge(step, i * 2 + (count + 1))

            def lower(i, load):
                b = load % 2
                dve.wait_ge(hi_ready, i * 4 + 2 * (load + 1))
                nc.vector.tensor_tensor(clo[:, b, CH:2 * CH], ctxb[:, b, 1], chi[:, b, CH:2 * CH].bitcast(F32),
                                        ALU.subtract).then_inc(lo2_ready, 1)

            lower(0, 0)
            with dve.Fori(0, PAIRS) as i:
                for b in range(2):
                    lower(i, b + 1)
                    dve.wait_ge(kept, i * 2 + (b + 1 + RING))
                    nc.vector.tensor_reduce(part[:, b], scores[:, bass.ds(i * (2 * CH) + b * CH, CH)], AX.X,
                                            ALU.max).then_inc(part_ready, 1)
                    joined(i, b, 0, b, ALU.max)
            nc.vector.tensor_scalar(neg[:], run[:, 0:1], -1.0, None, ALU.mult).then_inc(neg_ready, 1)

            def summed(i, n0):
                dve.wait_ge(exp_ready, i * 2 + (n0 + 1))
                nc.vector.tensor_reduce(part[:, n0 % 2], p32[:, n0 % 2], AX.X, ALU.add).then_inc(part_ready, 1)
                joined(i, NCH + n0, 1, n0 % 2, ALU.add)

            def body_b(i, b, more):
                if more:
                    summed(i, b + 1)
                dve.wait_ge(pThi_ready, i * 2 + (b + 1))
                nc.vector.tensor_tensor(pTlo[:, b], pT_psum(b), pThi[:, b].bitcast(F32),
                                        ALU.subtract).then_inc(pTlo_ready, 1)
                if more:
                    lower(i, NCH + b + 1)

            summed(0, 0)
            with dve.Fori(0, PAIRS - 1) as i:
                for b in range(2):
                    body_b(i, b, True)
            body_b(PAIRS - 1, 0, True)
            body_b(PAIRS - 1, 1, False)
            chain(nc.vector.reciprocal(rden[:], run[:, 1:2]))
            dve.wait_ge(used, 2 * NCH + RING)
            nc.vector.tensor_scalar(o[:], ps[:, 4, 0:D], rden[:], None, ALU.mult).then_inc(o_ready, 1)
            dve.wait_ge(oT_in_psum, 1)
            nc.vector.tensor_copy(oT[:].rearrange("p k t -> p (k t)"), ps[:, 5, 0:D]).then_inc(oT_ready, 1)
            chain(nc.vector.tensor_tensor(core.x[:], core.x[:], core.weight("xbv"), ALU.add))
            dve.wait_ge(y_in_psum, 1)
            nc.vector.tensor_tensor(core.x[:], core.x[:], ps[:, 6, 0:D], ALU.add)

        @block.tensor
        def _(pe):
            norm.tensor(pe)
            pe.wait_ge(norm.xT_ready, 1)
            wq, wk, bk = core.kxn("xq"), core.kxn("xk"), core.weight("xbk")
            for half in range(DT):
                for k in range(DT):
                    last = nc.tensor.matmul(ps[:, 4, half * P:(half + 1) * P], wq[:, k, half * P:(half + 1) * P],
                                            norm.xnT[:, k, :], start=(k == 0), stop=(k == DT - 1))
            last.then_inc(q_in_psum, 1)
            pe.wait_ge(qT_ready, 1)
            for half in range(DT):
                for k in range(DT):
                    nc.tensor.matmul(ps[:, 5, half * P:(half + 1) * P], wk[:, k, half * P:(half + 1) * P],
                                     qT[:, k, :], start=(k == 0), stop=(k == DT - 1))
            for k in range(DT):
                last = nc.tensor.matmul(ps[:, 5, D:D + 1], qT[:, k, :], bk[:, k:k + 1], start=(k == 0),
                                        stop=(k == DT - 1))
            last.then_inc(qk_in_psum, 1)
            pe.wait_ge(qk_ready, 1)
            with pe.Fori(0, PAIRS) as i:
                for b in range(2):
                    pe.wait_ge(lo_ready, i * 2 + (b + 1 + RING))
                    pe.wait_ge(lo2_ready, i * 2 + (b + 1 + RING))
                    pe.wait_ge(kept, i * 2 + (b + 1))
                    hi, lo = (t[:, b].rearrange("p (k n) -> p k n", k=DT) for t in (chi, clo))
                    for blk in range(2):
                        cols = slice(blk * BLK, (blk + 1) * BLK)
                        pairs = []
                        for k in range(DT):
                            pairs += [(qh[:, k], hi[:, k, cols]), (ql[:, k], hi[:, k, cols]),
                                      (qh[:, k], lo[:, k, cols])]
                        for n, (lhsT, rhs) in enumerate(pairs):
                            last = nc.tensor.matmul(ps[:, 2 * b + blk, 0:BLK], lhsT, rhs, start=(n == 0),
                                                    stop=(n == len(pairs) - 1))
                    last.then_inc(used, 1)

            def turned(i, n0):
                b = n0 % 2
                pe.wait_ge(exp_ready, i * 2 + (n0 + 1))
                pe.wait_ge(pTlo_ready, i * 2 + (n0 + 1))
                for t in range(TPC):
                    last = nc.tensor.transpose(ps[:, 2 * b + t // 4, (t % 4) * P:(t % 4 + 1) * P], p32[:, b, t * P:(t + 1) * P],
                                               ident)
                last.then_inc(pT_in_psum, 1)

            def body_b(i, b, more):
                if more:
                    turned(i, b + 1)
                pe.wait_ge(lo_ready, i * 2 + (NCH + b + 1 + RING))
                pe.wait_ge(lo2_ready, i * 2 + (NCH + b + 1 + RING))
                pe.wait_ge(pTlo_ready, i * 2 + (b + 1 + RING))
                for t in range(TPC):
                    keys, d = slice(t * P, (t + 1) * P), slice(t * D, (t + 1) * D)
                    for p, c in ((pThi, chi), (pTlo, chi), (pThi, clo)):
                        last = nc.tensor.matmul(ps[:, 4, 0:D], p[:, b, keys], c[:, b, d], start=False, stop=True,
                                                skip_group_check=True)
                last.then_inc(used, 1)

            nc.tensor.matmul(ps[:, 4, 0:D], zeros[:, 0:P], zeros[:], start=True, stop=False, skip_group_check=True)
            turned(0, 0)
            with pe.Fori(0, PAIRS - 1) as i:
                for b in range(2):
                    body_b(i, b, True)
            body_b(PAIRS - 1, 0, True)
            body_b(PAIRS - 1, 1, False)
            pe.wait_ge(o_ready, 1)
            for k in range(DT):
                last = nc.tensor.transpose(ps[:, 5, k * P:(k + 1) * P], o[:, k * P:(k + 1) * P], ident)
            last.then_inc(oT_in_psum, 1)
            pe.wait_ge(oT_ready, 1)
            projected(nc, ps[:, 6, 0:D], oT, core.kxn("xv"), DT, y_in_psum)


def l3_xattn(core):
    cross_attention(core, "l3x", 4, 4, *cross_weights(core, 4), 0.125)


def cross_weights(core, groups):
    def columns(name):
        m = core.kxn(name)
        return lambda g, k, half=None: (m[:, k, g * D:(g + 1) * D] if half is None
                                        else m[:, k, g * D + half * P:g * D + (half + 1) * P])

    has = core.cols[core.layer]
    col = lambda name: (lambda g, k: core.weight(name)[:, k:k + 1]) if name in has else (
        lambda g, k: core.constant("zero")[:, 0:1])
    row = lambda name: (lambda g: core.weight(name)) if name in has else None
    wo = None
    if "xo" in has:
        rows = core.kxn("xo", DT * groups)
        wo = lambda g, k: rows[:, DT * g + k, :]
    return (columns("xq"), columns("xk"), columns("xv"), wo, col("xbq"), col("xbk"), row("xbv"),
            core.weight("xbo") if "xbo" in has else None)




def l1_ffn(core):
    nc, ps, ident = core.nc, core.psum, core.ident()
    E, G, CAP, SLOTS, INTER, AI = 32, 16, 5, 32, 512, 128
    PER = P // SLOTS
    GROUPS = E // PER
    RING = 8
    with Scope(core, "l1f") as s:
        norm = Norm(core, s)
        stats, sq = s.sb("stats", [P, 8]), s.sb("sq", [P, D])
        statsT = s.sb("statsT", [6, P])
        hT = s.sb("hT", [P, P])
        logits, probs = s.sb("logits", [P, E]), s.sb("probs", [P, E])
        top, topi, topf = s.sb("top", [P, 8]), s.sb("topi", [P, 8], U32), s.sb("topf", [P, 8])
        small = s.sb("small", [P, 4])
        hit, wc, score = s.sb("hit", [P, 2, E]), s.sb("wc", [P, E]), s.sb("score", [P, E])
        scoreT = s.sb("scoreT", [E, P])
        best, besti, bestf = s.sb("best", [E, 8]), s.sb("besti", [E, 8], U32), s.sb("bestf", [E, 8])
        shared = s.sb("shared", [P, CAP, P])
        pick, asg, ah = shared[0:E], shared[:, 0:2], shared[:, 2:4]
        sels = s.sb("sels", [P, 2, E, SLOTS])
        sel, wsel = sels[:, 0], sels[:, 1]
        ye = sels[:].rearrange("p a e c -> p (a e c)").rearrange("p (g d) -> p g d", d=D)
        wmask, gw = s.sb("wmask", [P, E]), s.sb("gw", [P, G])
        xeT = s.sb("xeT", [P, DT, E * SLOTS])
        wselT = s.sb("wselT", [P, GROUPS, P])
        up = s.sb("up", [P, RING, DT, 2 * INTER])
        down = s.sb("down", [P, RING, INTER // P, D])
        sg, hact = s.sb("sg", [P, INTER]), s.sb("hact", [P, INTER])
        hactT = s.sb("hactT", [P, INTER // P, P])
        aup = s.sb("aup", [P, 2, DT, 2 * AI])
        adown = s.sb("adown", [P, 2, D])
        acc = sq
        (chain_sem, sums_ready, sqrt_ready, stats_ready, statsT_in_psum, statsT_ready, h_in_psum, h_ready,
         logits_in_psum, shifted, exp_done, score_ready, scoreT_in_psum, scoreT_ready, pick_ready, sel_in_psum,
         sel_ready, xe_in_psum, xe_ready, up_used, down_used, sig_done, hact_ready, hactT_in_psum,
         hactT_ready, ye_ready, a_in_psum, asig_done, ah_ready, ay_in_psum, ay_added,
         out_in_psum) = s.signals(
            "chain_sem sums_ready sqrt_ready stats_ready statsT_in_psum statsT_ready h_in_psum h_ready "
            "logits_in_psum shifted exp_done score_ready scoreT_in_psum scoreT_ready pick_ready sel_in_psum "
            "sel_ready xe_in_psum xe_ready up_used down_used sig_done hact_ready hactT_in_psum "
            "hactT_ready ye_ready a_in_psum asig_done ah_ready ay_in_psum ay_added out_in_psum")
        up_in = s.signals(" ".join(f"up_in{n}" for n in range(RING)))
        down_in = s.signals(" ".join(f"down_in{n}" for n in range(RING)))
        a_in = s.signals("a_in0 a_in1")
        block = s.ctx.enter_context(nc.Block())

        @block.sync
        def _(sp):
            for e in range(E):
                if e >= RING:
                    sp.wait_ge(up_used, e - RING + 1)
                sp.dma_start(up[:, e % RING], core.dram["w_up"][e]).then_inc(up_in[e % RING], 16)
                if e >= RING:
                    sp.wait_ge(down_used, e - RING + 1)
                sp.dma_start(down[:, e % RING], core.dram["w_down"][e]).then_inc(down_in[e % RING], 16)

        @block.gpsimd
        def _(pool):
            for n in range(G):
                if n >= 2:
                    pool.wait_ge(ay_in_psum, n - 1)
                pool.dma_start(aup[:, n % 2], core.dram["a_up"][n]).then_inc(a_in[n % 2], 16)
                pool.dma_start(adown[:, n % 2], core.dram["a_down"][n]).then_inc(a_in[n % 2], 16)

        @block.vector
        def _(dve):
            chain = Chain(dve, chain_sem)
            norm.vector(dve, chain)
            xn = norm.xn[:]
            chain(nc.vector.memset(stats[:], 0.0))
            chain(nc.vector.bn_stats(norm.stats[:], xn))
            chain(nc.vector.bn_aggr(norm.mv[:], norm.stats[:]))
            nc.vector.tensor_copy(stats[:, 0:1], norm.mv[:, 0:1])
            nc.vector.tensor_scalar(stats[:, 6:7], norm.mv[:, 1:2], D / (D - 1.0), None, ALU.mult)
            nc.vector.tensor_reduce(stats[:, 2:3], xn, AX.X, ALU.min)
            nc.vector.tensor_reduce(stats[:, 3:4], xn, AX.X, ALU.max)
            chain(nc.vector.tensor_tensor(sq[:], xn, xn, ALU.mult))
            nc.vector.tensor_reduce(stats[:, 7:8], sq[:], AX.X, ALU.add).then_inc(sums_ready, 1)
            dve.wait_ge(sums_ready, 1)
            chain(nc.vector.tensor_scalar(sq[:], xn, 1e-6, None, ALU.is_lt))
            chain(nc.vector.scalar_tensor_tensor(sq[:], xn, -1e-6, sq[:], ALU.is_gt, ALU.mult))
            chain(nc.vector.tensor_reduce(stats[:, 5:6], sq[:], AX.X, ALU.add))
            nc.vector.tensor_scalar(stats[:, 5:6], stats[:, 5:6], 1.0 / D, None, ALU.mult).then_inc(stats_ready, 1)
            dve.wait_ge(statsT_in_psum, 1)
            nc.vector.tensor_copy(statsT[:], ps[0:6, 0, 0:P]).then_inc(statsT_ready, 1)
            dve.wait_ge(logits_in_psum, 1)
            chain(nc.vector.tensor_reduce(small[:, 0:1], ps[:, 2, 0:E], AX.X, ALU.max))
            nc.vector.tensor_scalar(logits[:], ps[:, 2, 0:E], small[:, 0:1], None, ALU.subtract).then_inc(shifted, 1)
            dve.wait_ge(exp_done, 1)
            chain(nc.vector.tensor_reduce(small[:, 1:2], logits[:], AX.X, ALU.add))
            chain(nc.vector.reciprocal(small[:, 1:2], small[:, 1:2]))
            chain(nc.vector.tensor_scalar(probs[:], logits[:], small[:, 1:2], None, ALU.mult))
            chain(nc.vector.max(top[:], probs[:]))
            chain(nc.vector.max_index(topi[:], top[:], probs[:]))
            chain(nc.vector.tensor_copy(topf[:], topi[:]))
            chain(nc.vector.tensor_tensor(small[:, 0:1], top[:, 0:1], top[:, 1:2], ALU.add))
            chain(nc.vector.reciprocal(small[:, 0:1], small[:, 0:1]))
            for n in range(2):
                last = nc.vector.tensor_scalar(hit[:, n], core.constant("iota")[:, 0:E], topf[:, n:n + 1], None,
                                               ALU.is_equal)
            chain(last)
            chain(nc.vector.tensor_tensor(score[:], hit[:, 0], hit[:, 1], ALU.add))
            chain(nc.vector.tensor_scalar(wc[:], probs[:], small[:, 0:1], None, ALU.mult))
            chain(nc.vector.tensor_tensor(wc[:], wc[:], score[:], ALU.mult))
            chain(nc.vector.tensor_tensor(logits[:], probs[:], score[:], ALU.mult))
            chain(nc.vector.tensor_scalar(score[:], score[:], 1.0, None, ALU.subtract))
            nc.vector.tensor_tensor(score[:], score[:], logits[:], ALU.add).then_inc(score_ready, 1)
            dve.wait_ge(scoreT_in_psum, 1)
            nc.vector.tensor_copy(scoreT[:], ps[0:E, 3, 0:P]).then_inc(scoreT_ready, 1)
            dve.wait_ge(scoreT_ready, 1)
            chain(nc.vector.max(best[:], scoreT[:]))
            chain(nc.vector.max_index(besti[:], best[:], scoreT[:]))
            chain(nc.vector.tensor_copy(bestf[:], besti[:]))
            for c in range(CAP):
                last = nc.vector.tensor_scalar(pick[:, c], core.constant("iota")[0:E, :], bestf[:, c:c + 1], None,
                                               ALU.is_equal)
            last.then_inc(pick_ready, 1)
            chain(nc.vector.memset(sel, 0.0))
            dve.wait_ge(sel_in_psum, 1)
            chain(nc.vector.tensor_copy(sel[:, :, 0:CAP].rearrange("p e c -> p c e"),
                                        ps[:, 4, 0:CAP * E].rearrange("p (c e) -> p c e", c=CAP)))
            nc.vector.tensor_tensor(wsel, sel, wc[:].unsqueeze(2).to_broadcast([P, E, SLOTS]),
                                    ALU.mult).then_inc(sel_ready, 1)
            dve.wait_ge(sel_ready, 1)
            chain(nc.vector.tensor_reduce(wmask[:], wsel[:, :, 0:CAP], AX.X, ALU.add))
            chain(nc.vector.tensor_reduce(gw[:], wmask[:].rearrange("p (g e) -> p g e", g=G), AX.X, ALU.add))
            chain(nc.vector.tensor_scalar(gw[:], gw[:], 0.05, None, ALU.mult))
            chain(nc.vector.memset(acc[:], 0.0))
            dve.wait_ge(xe_in_psum, 1)
            nc.vector.tensor_copy(xeT[:].rearrange("p k n -> p (k n)"),
                                  ps[:, 0:4, :].rearrange("p b n -> p (b n)")).then_inc(xe_ready, 1)
            dve.wait_ge(xe_in_psum, 2)
            nc.vector.tensor_copy(wselT[:].rearrange("p g n -> p (g n)"),
                                  ps[:, 4:6, :].rearrange("p b n -> p (b n)")).then_inc(xe_ready, 1)
            for q in range(GROUPS):
                dve.wait_ge(sig_done, q + 1)
                chain(nc.vector.tensor_tensor(sg[:], sg[:], ps[:, 0, :], ALU.mult))
                if q:
                    dve.wait_ge(hactT_in_psum, q)
                nc.vector.tensor_tensor(hact[:], sg[:], ps[:, 1, :], ALU.mult).then_inc(hact_ready, 1)
                dve.wait_ge(hactT_in_psum, q + 1)
                nc.vector.tensor_copy(hactT[:].rearrange("p k n -> p (k n)"), ps[:, 2, :]).then_inc(hactT_ready, 1)
                for n in range(2 * q, 2 * q + 2):
                    dve.wait_ge(asig_done, n + 1)
                    chain(nc.vector.tensor_tensor(asg[:, n % 2], asg[:, n % 2], ps[:, 4, 0:P], ALU.mult))
                    nc.vector.tensor_tensor(ah[:, n % 2], asg[:, n % 2], ps[:, 4, P:2 * P], ALU.mult).then_inc(
                        ah_ready, 1)
                    dve.wait_ge(ay_in_psum, n + 1)
                    nc.vector.scalar_tensor_tensor(acc[:], ps[:, 5, 0:D], gw[:, n:n + 1], acc[:], ALU.mult,
                                                   ALU.add).then_inc(ay_added, 1)
                    dve.wait_ge(ay_added, n + 1)
                dve.wait_ge(down_used, PER * (q + 1))
                nc.vector.tensor_copy(ye[:, q], ps[:, 3, 0:D]).then_inc(ye_ready, 1)
            chain(nc.vector.tensor_tensor(core.x[:], core.x[:], acc[:], ALU.add))
            dve.wait_ge(out_in_psum, 1)
            nc.vector.tensor_tensor(core.x[:], core.x[:], ps[:, 7, 0:D], ALU.add)

        @block.scalar
        def _(act):
            norm.scalar(act)
            act.wait_ge(sums_ready, 1)
            nc.scalar.activation(stats[:, 1:2], stats[:, 6:7], ACT.Sqrt).then_inc(sqrt_ready, 1)
            nc.scalar.activation(stats[:, 4:5], stats[:, 7:8], ACT.Sqrt).then_inc(sqrt_ready, 1)
            act.wait_ge(h_in_psum, 1)
            nc.scalar.activation(hT[:], ps[:, 1, 0:P], ACT.Gelu, bias=core.weight("r1b")).then_inc(h_ready, 1)
            act.wait_ge(shifted, 1)
            nc.scalar.activation(logits[:], logits[:], ACT.Exp).then_inc(exp_done, 1)
            for q in range(GROUPS):
                act.wait_ge(up_used, PER * (q + 1))
                if q:
                    act.wait_ge(hact_ready, q)
                nc.scalar.activation(sg[:], ps[:, 0, :], ACT.Sigmoid).then_inc(sig_done, 1)
                for n in range(2 * q, 2 * q + 2):
                    act.wait_ge(a_in_psum, n + 1)
                    if n >= 2:
                        act.wait_ge(ah_ready, n - 1)
                    nc.scalar.activation(asg[:, n % 2], ps[:, 4, 0:P], ACT.Sigmoid).then_inc(asig_done, 1)

        @block.tensor
        def _(pe):
            norm.tensor(pe)
            pe.wait_ge(stats_ready, 1)
            pe.wait_ge(sqrt_ready, 2)
            nc.tensor.transpose(ps[0:6, 0, 0:P], stats[:, 0:6], ident).then_inc(statsT_in_psum, 1)
            pe.wait_ge(norm.xT_ready, 1)
            pe.wait_ge(statsT_ready, 1)
            r1 = core.kxn("r1")
            for k in range(DT):
                nc.tensor.matmul(ps[:, 1, 0:P], r1[:, k, :], norm.xnT[:, k, :], start=(k == 0), stop=False)
            nc.tensor.matmul(ps[:, 1, 0:P], core.weight("r1s")[0:6, :], statsT[:], start=False,
                             stop=True).then_inc(h_in_psum, 1)
            pe.wait_ge(h_ready, 1)
            nc.tensor.matmul(ps[:, 2, 0:E], hT[:], core.weight("r2"), start=True, stop=True).then_inc(
                logits_in_psum, 1)
            pe.wait_ge(score_ready, 1)
            nc.tensor.transpose(ps[0:E, 3, 0:P], score[:], ident).then_inc(scoreT_in_psum, 1)
            pe.wait_ge(pick_ready, 1)
            for c in range(CAP):
                last = nc.tensor.transpose(ps[:, 4, c * E:(c + 1) * E], pick[:, c], core.ident(E))
            last.then_inc(sel_in_psum, 1)
            pe.wait_ge(sel_ready, 1)
            flat = sel.rearrange("p e c -> p (e c)")
            for k in range(DT):
                for n in range(2):
                    last = nc.tensor.matmul(ps[:, 2 * k + n, :], norm.xn[:, k * P:(k + 1) * P],
                                            flat[:, n * 512:(n + 1) * 512], start=True, stop=True)
            last.then_inc(xe_in_psum, 1)
            transposed(nc, ps, 4, wsel.rearrange("p e c -> p (e c)"), GROUPS, ident, xe_in_psum)
            pe.wait_ge(xe_ready, 2)
            for q in range(GROUPS):
                for j in range(PER):
                    e = q * PER + j
                    pe.wait_ge(up_in[e % RING], 16 * (e // RING + 1))
                    if q and j == 0:
                        pe.wait_ge(hact_ready, q)
                    for n in range(2):
                        for k in range(DT):
                            last = nc.tensor.matmul(ps[j * SLOTS:(j + 1) * SLOTS, n, :],
                                                    xeT[:, k, e * SLOTS:(e + 1) * SLOTS],
                                                    up[:, e % RING, k, n * INTER:(n + 1) * INTER],
                                                    start=(k == 0), stop=(k == DT - 1))
                    last.then_inc(up_used, 1)
                pe.wait_ge(hact_ready, q + 1)
                if q:
                    pe.wait_ge(hactT_ready, q)
                transposed(nc, ps, 2, hact, INTER // P, ident, hactT_in_psum)
                for n in range(2 * q, 2 * q + 2):
                    pe.wait_ge(a_in[n % 2], 32 * (n // 2 + 1))
                    if n:
                        pe.wait_ge(ah_ready, n)
                    for m in range(2):
                        for k in range(DT):
                            last = nc.tensor.matmul(ps[:, 4, m * P:(m + 1) * P],
                                                    aup[:, n % 2, k, m * AI:(m + 1) * AI], norm.xnT[:, k, :],
                                                    start=(k == 0), stop=(k == DT - 1))
                    last.then_inc(a_in_psum, 1)
                    pe.wait_ge(ah_ready, n + 1)
                    if n:
                        pe.wait_ge(ay_added, n)
                    nc.tensor.matmul(ps[:, 5, 0:D], ah[:, n % 2], adown[:, n % 2], start=True,
                                     stop=True).then_inc(ay_in_psum, 1)
                pe.wait_ge(hactT_ready, q + 1)
                if q:
                    pe.wait_ge(ye_ready, q)
                for j in range(PER):
                    e = q * PER + j
                    pe.wait_ge(down_in[e % RING], 16 * (e // RING + 1))
                    for k in range(INTER // P):
                        last = nc.tensor.matmul(ps[j * SLOTS:(j + 1) * SLOTS, 3, 0:D],
                                                hactT[:, k, j * SLOTS:(j + 1) * SLOTS], down[:, e % RING, k, :],
                                                start=(k == 0), stop=(k == INTER // P - 1))
                    last.then_inc(down_used, 1)
            pe.wait_ge(ye_ready, GROUPS)
            for q in range(GROUPS):
                last = nc.tensor.matmul(ps[:, 7, 0:D], wselT[:, q, :], ye[:, q, :], start=(q == 0),
                                        stop=(q == GROUPS - 1))
            last.then_inc(out_in_psum, 1)


def rotary(nc, src, even, odd, cos, sin, tmp, chain):
    x1, x2 = src
    nc.vector.tensor_tensor(tmp[0], x1, cos, ALU.mult)
    nc.vector.tensor_tensor(tmp[1], x2, sin, ALU.mult)
    nc.vector.tensor_tensor(tmp[2], x1, sin, ALU.mult)
    chain(nc.vector.tensor_tensor(tmp[3], x2, cos, ALU.mult))
    nc.vector.tensor_tensor(even, tmp[0], tmp[1], ALU.subtract)
    return nc.vector.tensor_tensor(odd, tmp[2], tmp[3], ALU.add)


def l2_attn(core):
    nc, ps, ident = core.nc, core.psum, core.ident()
    H, KV, DH, QL, KL, PAD = 16, 4, 16, 64, 32, 32
    with Scope(core, "l2a") as s:
        norm = Norm(core, s)
        soft = RowSoftmax(core, s, H, P, 4, DH ** -0.5, core.constant("causal_mask"))
        qaT, kvaT = s.sb("qaT", [QL, P]), s.sb("kvaT", [KL, P])
        qk, v = s.sb("qk", [P, H + KV, DH]), s.sb("v", [P, KV * DH])
        tmp = s.sb("tmp", [P, 4, H + KV, DH // 2])
        rot = s.sb("rot", [P, H + KV, DH])
        qp, kp = s.sb("qp", [P, H // KV, KV, PAD]), s.sb("kp", [P, KV, PAD])
        qT, kT = s.sb("qT", [P, H // KV, P]), s.sb("kT", [P, P])
        o, oT = s.sb("o", [P, D]), s.sb("oT", [P, DT, P])
        (chain_sem, low_in_psum, low_ready, qkv_in_psum, qk_ready, qkT_in_psum, qkT_ready, o_in_psum, o_ready,
         oT_in_psum, oT_ready, y_in_psum) = s.signals(
            "chain_sem low_in_psum low_ready qkv_in_psum qk_ready qkT_in_psum qkT_ready o_in_psum o_ready "
            "oT_in_psum oT_ready y_in_psum")
        block = s.ctx.enter_context(nc.Block())

        @block.vector
        def _(dve):
            chain = Chain(dve, chain_sem)
            norm.vector(dve, chain)
            nc.vector.memset(qp[:], 0.0)
            chain(nc.vector.memset(kp[:], 0.0))
            dve.wait_ge(low_in_psum, 1)
            nc.vector.tensor_copy(qaT[:], ps[0:QL, 0, 0:P])
            nc.vector.tensor_copy(kvaT[:], ps[0:KL, 0, P:2 * P]).then_inc(low_ready, 1)
            dve.wait_ge(qkv_in_psum, 1)
            nc.vector.tensor_copy(qk[:, 0:H].rearrange("p h d -> p (h d)"), ps[:, 1, 0:D])
            nc.vector.tensor_copy(qk[:, H:].rearrange("p h d -> p (h d)"), ps[:, 2, 0:KV * DH])
            chain(nc.vector.tensor_copy(v[:], ps[:, 2, KV * DH:2 * KV * DH]))
            table = lambda n: core.constant(n).unsqueeze(1).to_broadcast([P, H + KV, DH // 2])
            chain(rotary(nc, (qk[:, :, 0::2], qk[:, :, 1::2]), rot[:, :, 0::2], rot[:, :, 1::2], table("rope_cos"),
                         table("rope_sin"), [tmp[:, n] for n in range(4)], chain))
            nc.vector.tensor_copy(qp[:, :, :, 0:DH].rearrange("p i g d -> p g i d"),
                                  rot[:, 0:H].rearrange("p (g i) d -> p g i d", g=KV))
            nc.vector.tensor_copy(kp[:, :, 0:DH], rot[:, H:]).then_inc(qk_ready, 1)
            dve.wait_ge(qkT_in_psum, 1)
            nc.vector.tensor_copy(qT[:].rearrange("p i q -> p (i q)"), ps[:, 3, :])
            nc.vector.tensor_copy(kT[:], ps[:, 4, 0:P]).then_inc(qkT_ready, 1)
            soft.vector(dve, chain)
            dve.wait_ge(o_in_psum, 1)
            heads = lambda a: a.rearrange("p (h d) -> p h d", d=DH)
            nc.vector.tensor_tensor(heads(o[:]), heads(ps[:, 5, 0:D]), soft.bc(soft.top[:], DH),
                                    ALU.mult).then_inc(o_ready, 1)
            dve.wait_ge(oT_in_psum, 1)
            nc.vector.tensor_copy(oT[:].rearrange("p k t -> p (k t)"), ps[:, 6, 0:D]).then_inc(oT_ready, 1)
            chain(nc.vector.tensor_tensor(core.x[:], core.x[:], core.weight("bout"), ALU.add))
            dve.wait_ge(y_in_psum, 1)
            nc.vector.tensor_tensor(core.x[:], core.x[:], ps[:, 4, 0:D], ALU.add)

        @block.scalar
        def _(act):
            norm.scalar(act)
            soft.scalar(act)

        @block.tensor
        def _(pe):
            norm.tensor(pe)
            pe.wait_ge(norm.xT_ready, 1)
            for k in range(DT):
                nc.tensor.matmul(ps[0:QL, 0, 0:P], core.kxn("qa")[:, k, :], norm.xnT[:, k, :], start=(k == 0),
                                 stop=(k == DT - 1))
            for k in range(DT):
                last = nc.tensor.matmul(ps[0:KL, 0, P:2 * P], core.kxn("kva")[:, k, :], norm.xnT[:, k, :],
                                        start=(k == 0), stop=(k == DT - 1))
            last.then_inc(low_in_psum, 1)
            pe.wait_ge(low_ready, 1)
            nc.tensor.matmul(ps[:, 1, 0:D], qaT[:], core.weight("qb")[0:QL, :], start=True, stop=True)
            nc.tensor.matmul(ps[:, 2, 0:2 * KV * DH], kvaT[:], core.weight("kvb")[0:KL, :], start=True,
                             stop=True).then_inc(qkv_in_psum, 1)
            pe.wait_ge(qk_ready, 1)
            for i in range(H // KV):
                nc.tensor.transpose(ps[:, 3, i * P:(i + 1) * P], qp[:, i].rearrange("p g d -> p (g d)"), ident)
            nc.tensor.transpose(ps[:, 4, 0:P], kp[:].rearrange("p g d -> p (g d)"), ident).then_inc(qkT_in_psum, 1)
            pe.wait_ge(qkT_ready, 1)
            for g in range(KV):
                for i in range(H // KV):
                    last = nc.tensor.matmul(ps[:, g, i * P:(i + 1) * P], qT[PAD * g:PAD * (g + 1), i, :],
                                            kT[PAD * g:PAD * (g + 1), :], start=True, stop=True)
            last.then_inc(soft.s_in_psum, 1)
            soft.tensor(pe)
            pe.wait_ge(soft.pT_ready, 1)
            for h in range(H):
                g = h // (H // KV)
                last = nc.tensor.matmul(ps[:, 5, h * DH:(h + 1) * DH], soft.pT[:, h, :], v[:, g * DH:(g + 1) * DH],
                                        start=True, stop=True)
            last.then_inc(o_in_psum, 1)
            pe.wait_ge(o_ready, 1)
            transposed(nc, ps, 6, o, DT, ident, oT_in_psum)
            pe.wait_ge(oT_ready, 1)
            projected(nc, ps[:, 4, 0:D], oT, core.kxn("aout"), DT, y_in_psum)


def quantised(nc, chain, src, out, blocks, top, inv, scaled):
    wide = [P, blocks, 32]
    top, inv = top[:, 0:blocks], inv[:, 0:blocks]
    chain(nc.vector.tensor_reduce(top, src, AX.X, ALU.max, apply_absolute_value=True))
    chain(nc.vector.tensor_scalar(top, top, 2.0 ** -120, None, ALU.max))
    chain(nc.vector.tensor_scalar(top.bitcast(I32), top.bitcast(I32), 0x7F800000, None, ALU.bitwise_and))
    chain(nc.vector.tensor_scalar(top, top, 0.125, None, ALU.mult))
    chain(nc.vector.reciprocal(inv, top))
    chain(nc.vector.tensor_tensor(scaled, src, inv.unsqueeze(2).to_broadcast(wide), ALU.mult))
    chain(nc.vector.tensor_scalar(scaled, scaled, 1.5 * 2.0 ** 23, None, ALU.add))
    chain(nc.vector.tensor_scalar(scaled, scaled, 1.5 * 2.0 ** 23, None, ALU.subtract))
    return nc.vector.tensor_tensor(out, scaled, top.unsqueeze(2).to_broadcast(wide), ALU.mult)


def l2_ffn(core):
    nc, ps = core.nc, core.psum
    F = 1024
    FT = F // P
    with Scope(core, "l2f") as s:
        norm = Norm(core, s)
        identb = s.sb("identb", [P, P], BF16)
        top, inv, scaled = s.sb("top", [P, 64]), s.sb("inv", [P, 64]), s.sb("scaled", [P, 64, 32])
        wfq, wpq = s.sb("wfq", [P, FT, D], BF16), s.sb("wpq", [P, DT, F], BF16)
        wfT, wpT = s.sb("wfT", [P, DT, F], BF16), s.sb("wpT", [P, FT, D], BF16)
        xq, xqT = s.sb("xq", [P, D], BF16), s.sb("xqT", [P, DT, P], BF16)
        h = s.sb("h", [P, F])
        hq, hqT = s.sb("hq", [P, F], BF16), s.sb("hqT", [P, FT, P], BF16)
        (chain_sem, wf_ready, wp_ready, wfT_in_psum, wpT_in_psum, wT_ready, xq_ready, xqT_in_psum, xqT_ready,
         h_in_psum, h_ready, gelu_done, hq_ready, hqT_in_psum, hqT_ready, y_in_psum) = s.signals(
            "chain_sem wf_ready wp_ready wfT_in_psum wpT_in_psum wT_ready xq_ready xqT_in_psum xqT_ready "
            "h_in_psum h_ready gelu_done hq_ready hqT_in_psum hqT_ready y_in_psum")
        blocks = lambda a: a.rearrange("p (b k) -> p b k", k=32)
        half_words = lambda bank, n: ps[:, bank, :].bitcast(BF16)[:, 0:n]
        block = s.ctx.enter_context(nc.Block())

        @block.vector
        def _(dve):
            chain = Chain(dve, chain_sem)
            nc.vector.tensor_copy(identb[:], core.ident())
            quantised(nc, chain, blocks(core.weight("fc")), blocks(wfq[:].rearrange("p n k -> p (n k)")), 64, top,
                      inv, scaled[:]).then_inc(wf_ready, 1)
            dve.wait_ge(wf_ready, 1)
            quantised(nc, chain, blocks(core.weight("proj")), blocks(wpq[:].rearrange("p n k -> p (n k)")), 64,
                      top, inv, scaled[:]).then_inc(wp_ready, 1)
            dve.wait_ge(wp_ready, 1)
            norm.vector(dve, chain)
            quantised(nc, chain, blocks(norm.xn[:]), blocks(xq[:]), 8, top, inv, scaled[:, 0:8]).then_inc(
                xq_ready, 1)
            dve.wait_ge(xq_ready, 1)
            dve.wait_ge(wfT_in_psum, 1)
            for k in range(DT):
                nc.vector.tensor_copy(wfT[:, k], half_words(k, F))
            dve.wait_ge(wpT_in_psum, 1)
            for n in range(2):
                last = nc.vector.tensor_copy(wpT[:, 4 * n:4 * n + 4].rearrange("p k o -> p (k o)"),
                                             half_words(2 + n, F))
            last.then_inc(wT_ready, 1)
            dve.wait_ge(xqT_in_psum, 1)
            nc.vector.tensor_copy(xqT[:].rearrange("p k t -> p (k t)"), half_words(4, D)).then_inc(xqT_ready, 1)
            dve.wait_ge(h_in_psum, 1)
            nc.vector.tensor_tensor(h[:], ps[:, 5:7, :].rearrange("p b n -> p (b n)"), core.weight("bfc"),
                                    ALU.add).then_inc(h_ready, 1)
            dve.wait_ge(gelu_done, 1)
            quantised(nc, chain, blocks(h[:]), blocks(hq[:]), 32, top, inv, scaled[:, 0:32]).then_inc(hq_ready, 1)
            dve.wait_ge(hqT_in_psum, 1)
            nc.vector.tensor_copy(hqT[:].rearrange("p k t -> p (k t)"), half_words(0, F)).then_inc(hqT_ready, 1)
            chain(nc.vector.tensor_tensor(core.x[:], core.x[:], core.weight("bproj"), ALU.add))
            dve.wait_ge(y_in_psum, 1)
            nc.vector.tensor_tensor(core.x[:], core.x[:], ps[:, 1, 0:D], ALU.add)

        @block.scalar
        def _(act):
            norm.scalar(act)
            act.wait_ge(h_ready, 1)
            nc.scalar.activation(h[:], h[:], ACT.Gelu).then_inc(gelu_done, 1)

        @block.tensor
        def _(pe):
            pe.wait_ge(wf_ready, 1)
            for k in range(DT):
                for n in range(FT):
                    last = nc.tensor.transpose(half_words(k, F)[:, n * P:(n + 1) * P],
                                               wfq[:, n, k * P:(k + 1) * P], identb[:])
            last.then_inc(wfT_in_psum, 1)
            pe.wait_ge(wp_ready, 1)
            for k in range(FT):
                for n in range(DT):
                    at = (k % 4) * D + n * P
                    last = nc.tensor.transpose(half_words(2 + k // 4, F)[:, at:at + P],
                                               wpq[:, n, k * P:(k + 1) * P], identb[:])
            last.then_inc(wpT_in_psum, 1)
            norm.tensor(pe)
            pe.wait_ge(xq_ready, 1)
            for k in range(DT):
                last = nc.tensor.transpose(half_words(4, D)[:, k * P:(k + 1) * P], xq[:, k * P:(k + 1) * P],
                                           identb[:])
            last.then_inc(xqT_in_psum, 1)
            pe.wait_ge(wT_ready, 1)
            pe.wait_ge(xqT_ready, 1)
            for n in range(2):
                projected(nc, ps[:, 5 + n, :], xqT, wfT[:, :, n * 512:(n + 1) * 512], DT, h_in_psum if n else None)
            pe.wait_ge(hq_ready, 1)
            for k in range(FT):
                last = nc.tensor.transpose(half_words(0, F)[:, k * P:(k + 1) * P], hq[:, k * P:(k + 1) * P],
                                           identb[:])
            last.then_inc(hqT_in_psum, 1)
            pe.wait_ge(hqT_ready, 1)
            projected(nc, ps[:, 1, 0:D], hqT, wpT, FT, y_in_psum)


def l3_attn(core):
    nc, ps, ident = core.nc, core.psum, core.ident()
    H, DH = 8, 32
    with Scope(core, "l3a") as s:
        norm = Norm(core, s)
        q, k, v = s.sb("q", [P, H, DH]), s.sb("k", [P, H, DH]), s.sb("v", [P, D])
        tmp = s.sb("tmp", [P, 4, H, DH // 2])
        qr, kr = s.sb("qr", [P, H, DH]), s.sb("kr", [P, H, DH])
        qT, kT = s.sb("qT", [P, DT, P]), s.sb("kT", [P, DT, P])
        st = s.sb("st", [P, H, P])
        y, sq = s.sb("y", [P, H, DH]), s.sb("sq", [P, H, DH])
        mean, var, std = s.sb("mean", [P, H]), s.sb("var", [P, H]), s.sb("std", [P, H])
        sig, gate = s.sb("sig", [P, D]), s.sb("gate", [P, D])
        yT = s.sb("yT", [P, DT, P])
        (chain_sem, qkv_in_psum, g_in_psum, gate_ready, rot_ready, qkT_in_psum, qkT_ready, s_in_psum, s_ready,
         y_in_psum, var_ready, std_ready, y_ready, yT_in_psum, yT_ready, out_in_psum) = s.signals(
            "chain_sem qkv_in_psum g_in_psum gate_ready rot_ready qkT_in_psum qkT_ready s_in_psum s_ready "
            "y_in_psum var_ready std_ready y_ready yT_in_psum yT_ready out_in_psum")
        flat = lambda t: t[:].rearrange("p h d -> p (h d)")
        wide = lambda t: t[:].unsqueeze(2).to_broadcast([P, H, DH])
        block = s.ctx.enter_context(nc.Block())

        @block.vector
        def _(dve):
            chain = Chain(dve, chain_sem)
            norm.vector(dve, chain)
            dve.wait_ge(qkv_in_psum, 1)
            nc.vector.tensor_copy(flat(q), ps[:, 0, 0:D])
            nc.vector.tensor_copy(flat(k), ps[:, 1, 0:D])
            chain(nc.vector.tensor_copy(v[:], ps[:, 2, 0:D]))
            for src, dst, tag in ((q, qr, "q"), (k, kr, "k")):
                table = lambda n: core.constant(n).unsqueeze(1).to_broadcast([P, H, DH // 2])
                last = rotary(nc, (src[:, :, 0::2], src[:, :, 1::2]), dst[:, :, 0::2], dst[:, :, 1::2],
                              table(f"xpos_cos_{tag}"), table(f"xpos_sin_{tag}"), [tmp[:, n] for n in range(4)],
                              chain)
                if tag == "q":
                    chain(last)
            last.then_inc(rot_ready, 1)
            dve.wait_ge(qkT_in_psum, 1)
            nc.vector.tensor_copy(flat(qT), ps[:, 4, 0:D])
            nc.vector.tensor_copy(flat(kT), ps[:, 5, 0:D]).then_inc(qkT_ready, 1)
            dve.wait_ge(s_in_psum, 1)
            decay = core.constant("decay").rearrange("p (h t) -> p h t", h=H)
            for g in range(4):
                last = nc.vector.tensor_tensor(st[:, g:H:4], ps[:, g, 0:2 * P].rearrange("p (h t) -> p h t", h=2),
                                               decay[:, g:H:4], ALU.mult)
            last.then_inc(s_ready, 1)
            dve.wait_ge(y_in_psum, 1)
            chain(nc.vector.tensor_copy(flat(y), ps[:, 4, 0:D]))
            chain(nc.vector.tensor_reduce(mean[:], y[:], AX.X, ALU.add))
            chain(nc.vector.tensor_scalar(mean[:], mean[:], 1.0 / DH, None, ALU.mult))
            chain(nc.vector.tensor_tensor(y[:], y[:], wide(mean), ALU.subtract))
            chain(nc.vector.tensor_tensor(sq[:], y[:], y[:], ALU.mult))
            chain(nc.vector.tensor_reduce(var[:], sq[:], AX.X, ALU.add))
            nc.vector.tensor_scalar(var[:], var[:], 1.0 / DH, LN_EPS, ALU.mult, ALU.add).then_inc(var_ready, 1)
            dve.wait_ge(std_ready, 1)
            chain(nc.vector.reciprocal(std[:], std[:]))
            chain(nc.vector.tensor_tensor(y[:], y[:], wide(std), ALU.mult))
            chain(nc.vector.tensor_tensor(flat(y), flat(y), core.weight("gnw"), ALU.mult))
            chain(nc.vector.tensor_tensor(flat(y), flat(y), core.weight("gnb"), ALU.add))
            dve.wait_ge(gate_ready, 2)
            chain(nc.vector.tensor_tensor(flat(y), flat(y), sig[:], ALU.mult))
            nc.vector.tensor_tensor(flat(y), flat(y), gate[:], ALU.mult).then_inc(y_ready, 1)
            dve.wait_ge(yT_in_psum, 1)
            nc.vector.tensor_copy(flat(yT), ps[:, 0, 0:D]).then_inc(yT_ready, 1)
            dve.wait_ge(out_in_psum, 1)
            nc.vector.tensor_tensor(core.x[:], core.x[:], ps[:, 1, 0:D], ALU.add)

        @block.scalar
        def _(act):
            norm.scalar(act)
            act.wait_ge(g_in_psum, 1)
            nc.scalar.activation(sig[:], ps[:, 3, 0:D], ACT.Sigmoid).then_inc(gate_ready, 1)
            nc.scalar.activation(gate[:], ps[:, 3, 0:D], ACT.Copy).then_inc(gate_ready, 1)
            act.wait_ge(var_ready, 1)
            nc.scalar.activation(std[:], var[:], ACT.Sqrt).then_inc(std_ready, 1)

        @block.tensor
        def _(pe):
            norm.tensor(pe)
            pe.wait_ge(norm.xT_ready, 1)
            for bank, name in enumerate(("rq", "rk", "rv")):
                projected(nc, ps[:, bank, 0:D], norm.xnT, core.kxn(name), DT, qkv_in_psum if bank == 2 else None)
            projected(nc, ps[:, 3, 0:D], norm.xnT, core.kxn("rg"), DT, g_in_psum)
            pe.wait_ge(rot_ready, 1)
            for bank, r in ((4, qr), (5, kr)):
                for n in range(DT):
                    last = nc.tensor.transpose(ps[:, bank, n * P:(n + 1) * P], flat(r)[:, n * P:(n + 1) * P], ident)
            last.then_inc(qkT_in_psum, 1)
            pe.wait_ge(qkT_ready, 1)
            pe.wait_ge(gate_ready, 2)
            for h in range(H):
                r = slice(DH * (h % 4), DH * (h % 4) + DH)
                last = nc.tensor.matmul(ps[:, h % 4, (h // 4) * P:(h // 4 + 1) * P], kT[r, h // 4, :],
                                        qT[r, h // 4, :], start=True, stop=True)
            last.then_inc(s_in_psum, 1)
            pe.wait_ge(s_ready, 1)
            for h in range(H):
                last = nc.tensor.matmul(ps[:, 4, h * DH:(h + 1) * DH], st[:, h, :], v[:, h * DH:(h + 1) * DH],
                                        start=True, stop=True)
            last.then_inc(y_in_psum, 1)
            pe.wait_ge(y_ready, 1)
            transposed(nc, ps, 0, flat(y), DT, ident, yT_in_psum)
            pe.wait_ge(yT_ready, 1)
            projected(nc, ps[:, 1, 0:D], yT, core.kxn("ro"), DT, out_in_psum)


def l3_ffn(core):
    nc, ps = core.nc, core.psum
    E, F = 8, 1024
    FT = F // P
    W1, W2, B1, B2 = 0, DT * F, DT * F + FT * D, DT * F + FT * D + FT
    WIDE = B2 + D
    with Scope(core, "l3f") as s:
        norm = Norm(core, s)
        w = s.sb("w", [P, 2, WIDE])
        hT = s.sb("hT", [P, 2, FT, P])
        mean, g = s.sb("mean", [P, DT, 1]), s.sb("g", [1, E])
        one = s.sb("one", [1, 4])
        top, topi = s.sb("top", [1, 8]), s.sb("topi", [1, 8], U32)
        pair, ones = s.sb("pair", [1, 2]), s.sb("ones", [1, P])
        coef = s.sb("coef", [P, 4])
        y, b2a = s.sb("y", [P, D]), s.sb("b2a", [P, D])
        (chain_sem, mean_ready, g_in_psum, shifted, exp_done, chosen, pair_ready, pair_in_psum, h_in_psum, h_ready,
         y_in_psum, y_added, coef_ready) = s.signals(
            "chain_sem mean_ready g_in_psum shifted exp_done chosen pair_ready pair_in_psum h_in_psum h_ready "
            "y_in_psum y_added coef_ready")
        w_in = s.signals("w_in0 w_in1")
        block = s.ctx.enter_context(nc.Block())

        @block.sync
        def _(sp):
            sp.dma_start(w[:, 0], core.dram["mlps"][E]).then_inc(w_in[0], 16)
            sp.wait_ge(chosen, 1)
            first = sp.value_load(topi[0:1, 0:1], min_val=0, max_val=E - 1)
            sp.dma_start(w[:, 1], core.dram["mlps"][bass.ds(first, 1)].squeeze(0)).then_inc(w_in[1], 16)
            second = sp.value_load(topi[0:1, 1:2], min_val=0, max_val=E - 1)
            sp.wait_ge(y_added, 1)
            sp.dma_start(w[:, 0], core.dram["mlps"][bass.ds(second, 1)].squeeze(0)).then_inc(w_in[0], 16)

        @block.vector
        def _(dve):
            chain = Chain(dve, chain_sem)
            nc.vector.memset(ones[:], 1.0)
            norm.vector(dve, chain)
            chain(nc.vector.tensor_reduce(mean[:], norm.xnT[:], AX.X, ALU.add))
            nc.vector.tensor_scalar(mean[:], mean[:], 1.0 / P, None, ALU.mult).then_inc(mean_ready, 1)
            dve.wait_ge(g_in_psum, 1)
            chain(nc.vector.tensor_tensor(g[:], ps[0:1, 0, 0:E], core.weight("bgate")[0:1, :], ALU.add))
            chain(nc.vector.tensor_reduce(one[:, 0:1], g[:], AX.X, ALU.max))
            nc.vector.tensor_scalar(g[:], g[:], one[:, 0:1], None, ALU.subtract).then_inc(shifted, 1)
            dve.wait_ge(exp_done, 1)
            chain(nc.vector.tensor_reduce(one[:, 1:2], g[:], AX.X, ALU.add))
            chain(nc.vector.reciprocal(one[:, 1:2], one[:, 1:2]))
            chain(nc.vector.tensor_scalar(g[:], g[:], one[:, 1:2], None, ALU.mult))
            chain(nc.vector.max(top[:], g[:]))
            nc.vector.max_index(topi[:], top[:], g[:]).then_inc(chosen, 1)
            chain(nc.vector.tensor_tensor(one[:, 2:3], top[:, 0:1], top[:, 1:2], ALU.add))
            chain(nc.vector.reciprocal(one[:, 2:3], one[:, 2:3]))
            nc.vector.tensor_scalar(pair[:], top[:, 0:2], one[:, 2:3], None, ALU.mult).then_inc(pair_ready, 1)
            chain(nc.vector.tensor_scalar(coef[:, 0:1], core.weight("alpha"), 0.1, 1.0, ALU.max, ALU.min))
            chain(nc.vector.tensor_scalar(coef[:, 3:4], coef[:, 0:1], -1.0, 1.0, ALU.mult, ALU.add))
            dve.wait_ge(pair_in_psum, 1)
            chain(nc.vector.tensor_scalar(coef[:, 1:3], ps[:, 1, 0:2], coef[:, 3:4], None, ALU.mult))
            for n in range(3):
                dve.wait_ge(y_in_psum, n + 1)
                chain(nc.vector.tensor_tensor(y[:], ps[:, 2, 0:D], w[:, n % 2, B2:B2 + D], ALU.add))
                nc.vector.scalar_tensor_tensor(core.x[:], y[:], coef[:, n:n + 1], core.x[:], ALU.mult,
                                               ALU.add).then_inc(y_added, 1)
                dve.wait_ge(y_added, n + 1)

        @block.scalar
        def _(act):
            norm.scalar(act)
            act.wait_ge(shifted, 1)
            nc.scalar.activation(g[:], g[:], ACT.Exp).then_inc(exp_done, 1)
            for n in range(3):
                for t in range(FT):
                    act.wait_ge(h_in_psum, n * FT + t + 1)
                    nc.scalar.activation(hT[:, n % 2, t], ps[:, 3 + t % 4, 0:P], ACT.Gelu_apprx_tanh,
                                         bias=w[:, n % 2, B1 + t:B1 + t + 1]).then_inc(h_ready, 1)

        @block.tensor
        def _(pe):
            norm.tensor(pe)
            pe.wait_ge(mean_ready, 1)
            wg = core.kxn("gate")
            for k in range(DT):
                last = nc.tensor.matmul(ps[0:1, 0, 0:E], mean[:, k, :], wg[:, k, :], start=(k == 0),
                                        stop=(k == DT - 1))
            last.then_inc(g_in_psum, 1)
            pe.wait_ge(pair_ready, 1)
            nc.tensor.matmul(ps[:, 1, 0:2], ones[:], pair[:], start=True, stop=True).then_inc(pair_in_psum, 1)
            for n in range(3):
                pe.wait_ge(w_in[n % 2], 16 * (n // 2 + 1))
                w1 = w[:, n % 2, W1:W2].rearrange("p (k f) -> p k f", k=DT)
                w2 = w[:, n % 2, W2:B1].rearrange("p (k o) -> p k o", k=FT)
                for t in range(FT):
                    if n * FT + t >= 4:
                        pe.wait_ge(h_ready, n * FT + t - 3)
                    for k in range(DT):
                        last = nc.tensor.matmul(ps[:, 3 + t % 4, 0:P], w1[:, k, t * P:(t + 1) * P],
                                                norm.xnT[:, k, :], start=(k == 0), stop=(k == DT - 1))
                    last.then_inc(h_in_psum, 1)
                if n:
                    pe.wait_ge(y_added, n)
                pe.wait_ge(h_ready, (n + 1) * FT)
                projected(nc, ps[:, 2, 0:D], hT[:, n % 2], w2, FT, y_in_psum)


LAYERS = [[l0_xattn, l0_attn, l0_ffn], [l1_xattn, l1_attn, l1_ffn], [l2_xattn, l2_attn, l2_ffn],
          [l3_xattn, l3_attn, l3_ffn]]


def program(nc, dram, cols, out):
    with ExitStack() as ctx:
        core = Core(nc, ctx, dram, cols)
        x_in = nc.alloc_semaphore("x_in")
        const_in = nc.alloc_semaphore("const_in")
        cross_in, weights_in = nc.alloc_semaphore("cross_in"), nc.alloc_semaphore("weights_in")
        stored = nc.alloc_semaphore("stored")

        def load(layer):
            held = ExitStack()
            w = held.enter_context(nc.sbuf_tensor(f"weights{layer}", [P, cols[f"w{layer}"]["_"]], F32,
                                                  side="right" if layer % 2 else "left"))
            with nc.Block() as block:
                @block.sync
                def _(sp):
                    at = cross_columns(layer)
                    sp.dma_start(w[:, 0:at], dram[f"w{layer}"][:, 0:at]).then_inc(cross_in, 16)
                    if layer:
                        load_rest(sp, layer, w)
            return held, w

        def cross_columns(layer):
            return max(where[1] for name, where in cols[f"w{layer}"].items() if name.startswith("x"))

        def load_rest(sp, layer, w):
            at = cross_columns(layer)
            sp.dma_start(w[:, at:], dram[f"w{layer}"][:, at:]).then_inc(weights_in, 16)

        with nc.Block() as block:
            @block.sync
            def _(sp):
                sp.dma_start(core.x[:], dram["x"]).then_inc(x_in, 16)
                sp.dma_start(core.const[:], dram["const"]).then_inc(const_in, 16)
        held, core.w = load(0)
        for layer in range(4):
            core.layer = f"w{layer}"
            with nc.Block() as block:
                @block.sync
                def _(sp):
                    if layer == 0:
                        sp.wait_ge(x_in, 16)
                        sp.wait_ge(const_in, 16)
                    sp.wait_ge(cross_in, 16 * (layer + 1))
            core.behind_first_chunks = (lambda sp, w: load_rest(sp, 0, w)) if layer == 0 else None
            for n, sub in enumerate(LAYERS[layer]):
                sub(core)
                if n == 0:
                    with nc.Block() as block:
                        @block.sync
                        def _(sp):
                            sp.wait_ge(weights_in, 16 * (layer + 1))
                    if layer < 3:
                        next_held, next_w = load(layer + 1)
            held.close()
            if layer < 3:
                held, core.w = next_held, next_w
        with nc.Block() as block:
            @block.sync
            def _(sp):
                sp.dma_start(out, core.x[:]).then_inc(stored, 16)
                sp.wait_ge(stored, 16)



def _constants():
    p = np.arange(P)
    t = {"ident": np.eye(P)}
    t["head16"] = (p[:, None] // 16 == np.arange(8)[None, :])
    t["head64"] = (p[:, None] // 64 == np.arange(2)[None, :])
    t["zero"] = np.zeros((P, D))
    t["one"] = np.ones((P, 1))
    i, j = p[:, None], p[None, :]
    masked = (j > i) & ~((i < 64) & (j < 64))
    t["prefix_mask"] = np.concatenate([np.where(masked, -1e30, 0.0), np.zeros((P, 2))], 1)
    t["causal_mask"] = np.where(j > i, -1e30, 0.0)
    t["chunk_mask"] = (j >= i) & (i // 64 == j // 64)
    t["iota"] = np.broadcast_to(p[None, :], (P, P))
    freq = p[:, None].astype(np.float32) * (1.0 / 10000.0 ** (np.arange(0, 16, 2, dtype=np.float32) / 16))[None, :]
    t["rope_cos"], t["rope_sin"] = np.cos(freq), np.sin(freq)
    pos = p.astype(np.float32)
    base = (np.arange(0, 32, 2, dtype=np.float32) + np.float32(0.4 * 32)) / np.float32(1.4 * 32)
    scale = base[None, :] ** (pos[:, None] / np.float32(512.0))
    turn = pos[:, None] * (1.0 / 10000.0 ** (np.arange(16, dtype=np.float32) / 16))[None, :]
    t["xpos_cos_q"], t["xpos_sin_q"] = np.cos(turn) * scale, np.sin(turn) * scale
    t["xpos_cos_k"], t["xpos_sin_k"] = np.cos(turn) / scale, np.sin(turn) / scale
    gamma = 1.0 - np.exp(np.linspace(np.log(1.0 / 32.0), np.log(1.0 / 512.0), 8))
    apart = (j - i)[:, None, :]
    t["decay"] = np.where(apart >= 0, np.exp(np.maximum(apart, 0) * np.log(gamma)[None, :, None]),
                          0.0).reshape(P, 8 * P)
    return t


def _kxn(w):
    k = w.shape[0] // P
    return w.reshape(k, P, -1).transpose(1, 0, 2).reshape(P, -1)


def _col(b):
    return b.reshape(-1, P).T


def _row(b):
    return np.broadcast_to(b.reshape(1, -1), (P, b.size))


def _pad(a):
    return np.concatenate([a, np.zeros((P - a.shape[0], a.shape[1]), a.dtype)], 0)


def _null_values(null_v, heads):
    z = np.zeros((P, heads * null_v.shape[1]), null_v.dtype)
    for n, h in enumerate([h for m in range(2) for h in range(m, heads, 2)]):
        z[2 * n:2 * n + 2, h * null_v.shape[1]:(h + 1) * null_v.shape[1]] = null_v
    return z


def _packs(a):
    w0 = {
        "xq": _kxn(a["L0_xattn_Wq"]), "xk": _kxn(a["L0_xattn_Wk"]), "xv": _kxn(a["L0_xattn_Wv"]),
        "xo": _kxn(a["L0_xattn_Wo"]), "xbq": _col(a["L0_xattn_bq"]), "xbk": _col(a["L0_xattn_bk"]),
        "xbv": _row(a["L0_xattn_bv"]), "xbo": _row(a["L0_xattn_bo"]),
        "gamma": _row(a["L0_attn_gamma"]), "aq": _kxn(a["L0_attn_Wq"]), "akv": _kxn(a["L0_attn_Wkv"]),
        "qs": _row(a["L0_attn_q_scale"]), "ks": _row(a["L0_attn_k_scale"]),
        "null_k": _pad(a["L0_attn_null_kv"][0]), "null_v": _null_values(a["L0_attn_null_kv"][1], 16),
        "ao": _kxn(a["L0_attn_Wout"]),
        "fr": _kxn(a["L0_ffn_W_r"].T), "fk": _kxn(a["L0_ffn_W_k"].T), "fv": _kxn(a["L0_ffn_W_v"].T),
        "mu_r": _col(a["L0_ffn_mu_r"]), "mu_k": _col(a["L0_ffn_mu_k"]),
    }
    w1 = {
        "xq": _kxn(a["L1_xattn_wq"].T), "xk": _kxn(a["L1_xattn_wk"].T), "xv": _kxn(a["L1_xattn_wv"].T),
        "xo": _kxn(a["L1_xattn_wo"].T), "xbq": _col(a["L1_xattn_bq"]), "xbk": _col(a["L1_xattn_bk"]),
        "xbv": _row(a["L1_xattn_bv"]), "xbo": _row(a["L1_xattn_bo"]),
        "gq": _kxn(a["L1_attn_Wq"]), "gk": _kxn(a["L1_attn_Wk"]), "gv": _kxn(a["L1_attn_Wv"]),
        "gg": _kxn(a["L1_attn_Wg"]), "gk1": _kxn(a["L1_attn_gk_w1"]), "gk2": _pad(a["L1_attn_gk_w2"]),
        "gkb": _col(a["L1_attn_gk_b2"]), "gn": _row(a["L1_attn_g_norm_w"]), "go": _kxn(a["L1_attn_Wo"]),
    }
    w1.update({
        "r1": _kxn(np.ascontiguousarray(a["L1_ffn_r1_w"].T)[0:D]), "r1s": _pad(a["L1_ffn_r1_w"].T[D:]),
        "r1b": _col(a["L1_ffn_r1_b"]), "r2": a["L1_ffn_r2_w"].T,
    })
    kvb = a["L2_attn_Wkvb"].reshape(32, 64, 2)
    w2 = {
        "xq": _kxn(a["L2_xattn_Wq"].T), "xk": _kxn(a["L2_xattn_Wk"]), "xv": _kxn(a["L2_xattn_Wv"].T),
        "xbq": _col(a["L2_xattn_bq"]), "xbk": _col(a["L2_xattn_bk"]), "xbv": _row(a["L2_xattn_bv"]),
        "qa": _kxn(a["L2_attn_Wqa"]), "qb": _pad(a["L2_attn_Wqb"]), "kva": _kxn(a["L2_attn_Wkva"]),
        "kvb": _pad(np.concatenate([kvb[:, :, 0], kvb[:, :, 1]], 1)), "aout": _kxn(a["L2_attn_Wout"]),
        "bout": _row(a["L2_attn_bout"]),
        "fc": _kxn(a["L2_ffn_w_fc"]), "bfc": _row(a["L2_ffn_b_fc"]), "proj": _kxn(a["L2_ffn_w_proj"]),
        "bproj": _row(a["L2_ffn_b_proj"]),
    }
    heads = lambda m: _kxn(m.transpose(1, 0, 2).reshape(D, -1))
    w3 = {
        "xq": _kxn(a["L3_xattn_Wq"]), "xk": _kxn(a["L3_xattn_Wk"]), "xv": _kxn(a["L3_xattn_Wv"]),
        "xo": _kxn(a["L3_xattn_Wo"]),
        "rq": heads(a["L3_attn_W_Q"]), "rk": heads(a["L3_attn_W_K"]), "rv": heads(a["L3_attn_W_V"]),
        "rg": _kxn(a["L3_attn_W_G"]), "ro": _kxn(a["L3_attn_W_O"]), "gnw": _row(a["L3_attn_gn_weight"]),
        "gnb": _row(a["L3_attn_gn_bias"]),
        "gate": _kxn(a["L3_ffn_w_gate"]), "bgate": _row(a["L3_ffn_b_gate"]),
        "alpha": _row(a["L3_ffn_alpha"].reshape(1)),
    }
    return [w0, w1, w2, w3]


def _each(w):
    return np.stack([_kxn(m) for m in w])


def _big(a):
    mlp = lambda w1, w2, b1, b2: np.concatenate([_kxn(w1), _kxn(w2), _col(b1), _row(b2)], 1)
    mlps = [mlp(a["L3_ffn_W1e"][e], a["L3_ffn_W2e"][e], a["L3_ffn_b1e"][e], a["L3_ffn_b2e"][e]) for e in range(8)]
    mlps.append(mlp(a["L3_ffn_W1m"], a["L3_ffn_W2m"], a["L3_ffn_b1m"], a["L3_ffn_b2m"]))
    return {
        "w_up": _each(a["L1_ffn_w_up"].transpose(0, 2, 1)), "w_down": _each(a["L1_ffn_w_down"].transpose(0, 2, 1)),
        "a_up": _each(a["L1_ffn_a_up"].transpose(0, 2, 1)), "a_down": _each(a["L1_ffn_a_down"].transpose(0, 2, 1)),
        "mlps": np.stack(mlps),
    }


def kernel(**inputs):
    import concourse.bacc as bacc
    from concourse.bass_utils import run_bass_kernel_spmd

    a = {n: np.asarray(v) for n, v in inputs.items()}
    arrays, cols = {}, {}
    packs = {f"w{n}": pack for n, pack in enumerate(_packs(a))}
    packs["const"] = {n: t.astype(np.float32) for n, t in _constants().items()}
    for name, pack in packs.items():
        at, where = 0, {}
        for n, piece in pack.items():
            where[n] = (at, at + piece.shape[1])
            at += piece.shape[1]
        where["_"] = at
        cols[name] = where
        arrays[name] = np.ascontiguousarray(np.concatenate(list(pack.values()), 1))
    arrays["x"] = a["x"][0]
    arrays["ctxT"] = np.ascontiguousarray(a["ctx_1024"][0].T)
    arrays["ctx"] = a["ctx_1024"][0]
    arrays.update(_big(a))

    nc = bacc.Bacc("TRN2", target_bir_lowering=False, num_devices=1)
    dram = {n: nc.dram_tensor(n, v.shape, mybir.dt.from_np(v.dtype), kind="ExternalInput").ap()
            for n, v in arrays.items()}
    out = nc.dram_tensor("out_0_dram", (P, D), F32, kind="ExternalOutput").ap()
    program(nc, dram, cols, out)
    r = run_bass_kernel_spmd(nc, [arrays], core_ids=[0])
    return r.results[0]["out_0_dram"].reshape(1, P, D)
```
